# Optimizing a Trainium2 kernel written in Bass

```python
import numpy as np
import jax
import jax.numpy as jnp

def _softmax(x, axis=-1):
    return jax.nn.softmax(x, axis=axis)

def _gelu(x):
    return jax.nn.gelu(x, approximate=True)

def _silu(x):
    return jax.nn.silu(x)

def _sigmoid(x):
    return jax.nn.sigmoid(x)

def _layernorm(x, axis=-1, eps=1e-05):
    m = jnp.mean(x, axis=axis, keepdims=True)
    v = jnp.var(x, axis=axis, keepdims=True)
    return (x - m) / jnp.sqrt(v + eps)

def _scatter_add(tgt, idx, src, axis=0):
    return tgt.at[idx].add(src)

def _segment_sum(src, seg, n):
    return jax.ops.segment_sum(src, seg, n)
kernel_name = 'mk_audio_tower_d4_tok_audfeat768_r4_a8b6ac'

def setup_inputs(seed: int=0):
    np.random.seed(seed)
    _w = jnp.asarray

    def _rec_inputs():
        import jax
        import jax.numpy as jnp
        _rk = jax.random.key(seed)
        x = -0.000147625 + 0.999875 * jax.random.normal(jax.random.fold_in(_rk, 1), (64, 64, 192), jnp.float32)
        return x
    x = _rec_inputs()

    def _L0_tok_setup():
        import jax, jax.numpy as jnp
        import numpy as np
        CURRENT_FRAME = 16

        def quick_gelu(x):
            return x * jax.nn.sigmoid(1.702 * x)
        key = jax.random.key(seed)
        ks = jax.random.split(key, 7)
        D, D2, K = (192, 96, 4)
        N, B, T = (196, 16, CURRENT_FRAME)
        x = jax.random.normal(ks[0], (N, B * T, D), dtype=jnp.float32)
        s = 0.02
        return {'x': x, 'w_down': jax.random.normal(ks[1], (D, D2), dtype=jnp.float32) * s, 'b_down': jax.random.normal(ks[2], (D2,), dtype=jnp.float32) * s, 'w_conv': jax.random.normal(ks[3], (D2, 1, K), dtype=jnp.float32) * s, 'b_conv': jax.random.normal(ks[4], (D2,), dtype=jnp.float32) * s, 'w_up': jax.random.normal(ks[5], (D2, D), dtype=jnp.float32) * s, 'b_up': jax.random.normal(ks[6], (D,), dtype=jnp.float32) * s}
    _L0_tok_all = _L0_tok_setup()
    _L0_tok_in = {k: v for k, v in _L0_tok_all.items() if k in ('w_down', 'b_down', 'w_conv', 'b_conv', 'w_up', 'b_up')}
    del _L0_tok_all

    def _L0_attn_setup():
        import jax, jax.numpy as jnp
        import numpy as np
        import math
        H = 12
        LOGIT_SCALE_MAX = math.log(1.0 / 0.01)

        def _normalize(t, eps=1e-12):
            n = jnp.linalg.norm(t, axis=-1, keepdims=True)
            return t / jnp.maximum(n, eps)
        key = jax.random.key(seed)
        ks = jax.random.split(key, 4)
        L, N, C = (256, 8, 192)
        scale = (C // H) ** (-0.5)
        return {'x': jax.random.normal(ks[0], (L, N, C), jnp.float32), 'in_proj_weight': jax.random.normal(ks[1], (3 * C, C), jnp.float32) * scale, 'in_proj_bias': jnp.zeros((3 * C,), jnp.float32), 'logit_scale': jnp.full((H, 1, 1), jnp.log(10.0), jnp.float32), 'head_scale': jnp.ones((H, 1, 1), jnp.float32), 'out_w': jax.random.normal(ks[2], (C, C), jnp.float32) * scale, 'out_b': jnp.zeros((C,), jnp.float32)}
    _L0_attn_all = _L0_attn_setup()
    _L0_attn_in = {k: v for k, v in _L0_attn_all.items() if k in ('in_proj_weight', 'in_proj_bias', 'logit_scale', 'head_scale', 'out_w', 'out_b')}
    del _L0_attn_all

    def _L0_ffn_setup():
        import jax, jax.numpy as jnp
        import numpy as np
        B, S, D, E = (8, 256, 192, 8)
        F = 4 * D
        key = jax.random.key(seed)
        ks = jax.random.split(key, 5)
        scale = 0.02
        x = jax.random.normal(ks[0], (B, S, D), jnp.float32)
        gate_w = jax.random.normal(ks[1], (D, E), jnp.float32) * scale
        gate_b = jnp.zeros((E,), jnp.float32)
        w1 = jax.random.normal(ks[2], (E, D, F), jnp.float32) * scale
        b1 = jnp.zeros((E, F), jnp.float32)
        w2 = jax.random.normal(ks[3], (E, F, D), jnp.float32) * scale
        b2 = jnp.zeros((E, D), jnp.float32)
        return {'x': x, 'gate_w': gate_w, 'gate_b': gate_b, 'w1': w1, 'b1': b1, 'w2': w2, 'b2': b2}
    _L0_ffn_all = _L0_ffn_setup()
    _L0_ffn_in = {k: v for k, v in _L0_ffn_all.items() if k in ('gate_w', 'gate_b', 'w1', 'b1', 'w2', 'b2')}
    del _L0_ffn_all

    def _L1_attn_setup():
        import math
        import jax, jax.numpy as jnp
        import numpy as np
        HIDDEN = 192
        NUM_HEADS = 12
        HEAD_DIM = HIDDEN // NUM_HEADS
        THETA = 10000.0
        BATCH, SEQ = (2, 512)

        def _rope(x):
            S, D = (x.shape[1], x.shape[-1])
            inv_freq = 1.0 / THETA ** (jnp.arange(0, D, 2, dtype=jnp.float32) / D)
            angles = jnp.arange(S, dtype=jnp.float32)[:, None] * inv_freq[None, :]
            sin = jnp.sin(angles)[None, :, None, :].astype(x.dtype)
            cos = jnp.cos(angles)[None, :, None, :].astype(x.dtype)
            x_even = x[..., 0::2]
            x_odd = x[..., 1::2]
            rotated = jnp.stack((x_even * cos - x_odd * sin, x_even * sin + x_odd * cos), axis=-1)
            return rotated.reshape(x.shape)
        key = jax.random.key(seed)
        k0, k1, k2 = jax.random.split(key, 3)
        scale = 0.02
        x = jax.random.normal(k0, (BATCH, SEQ, HIDDEN), dtype=jnp.float32)
        qkv_w = jax.random.normal(k1, (3 * HIDDEN, HIDDEN), dtype=jnp.float32) * scale
        qkv_b = jnp.zeros((3 * HIDDEN,), dtype=jnp.float32)
        proj_w = jax.random.normal(k2, (HIDDEN, HIDDEN), dtype=jnp.float32) * scale
        proj_b = jnp.zeros((HIDDEN,), dtype=jnp.float32)
        return {'x': x, 'qkv_w': qkv_w, 'qkv_b': qkv_b, 'proj_w': proj_w, 'proj_b': proj_b}
    _L1_attn_all = _L1_attn_setup()
    _L1_attn_in = {k: v for k, v in _L1_attn_all.items() if k in ('qkv_w', 'qkv_b', 'proj_w', 'proj_b')}
    del _L1_attn_all

    def _L1_ffn_setup():
        import jax, jax.numpy as jnp
        import numpy as np
        import math
        B, T, C = (8, 512, 192)
        E = 3
        HD = C // E
        TOPK = 2
        NGLOB = 4

        def _masked_softmax(att, mask):
            att = jnp.where(mask, -jnp.inf, att)
            return jax.nn.softmax(att, axis=-1)
        key = jax.random.key(seed)
        ks = jax.random.split(key, 16)
        s = 0.02
        return {'x': jax.random.normal(ks[0], (B, T, C), jnp.float32), 'Wqk': jax.random.normal(ks[1], (C, 2 * C), jnp.float32) * s, 'bqk': jnp.zeros((2 * C,), jnp.float32), 'Wv': jax.random.normal(ks[2], (E, C, HD), jnp.float32) * s, 'bv': jnp.zeros((E, HD), jnp.float32), 'conv_w': jax.random.normal(ks[3], (HD, 1, 3), jnp.float32) * s, 'conv_b': jnp.zeros((HD,), jnp.float32), 'glob': jax.random.normal(ks[4], (NGLOB, HD), jnp.float32) * 0.02, 'pos_bias': jnp.zeros((64, 64), jnp.float32), 'Wg1': jax.random.normal(ks[5], (C, 32), jnp.float32) * s, 'bg1': jnp.zeros((32,), jnp.float32), 'Wg2': jax.random.normal(ks[6], (32, E), jnp.float32) * s, 'bg2': jnp.zeros((E,), jnp.float32), 'Wp': jax.random.normal(ks[7], (C, C), jnp.float32) * s, 'bp': jnp.zeros((C,), jnp.float32)}
    _L1_ffn_all = _L1_ffn_setup()
    _L1_ffn_in = {k: v for k, v in _L1_ffn_all.items() if k in ('Wqk', 'bqk', 'Wv', 'bv', 'conv_w', 'conv_b', 'glob', 'pos_bias', 'Wg1', 'bg1', 'Wg2', 'bg2', 'Wp', 'bp')}
    del _L1_ffn_all

    def _L2_attn_setup():
        import jax, jax.numpy as jnp
        import numpy as np
        EPS_NORM = 1e-12

        def _normalize(re, im, axis=-1):
            n = jnp.sqrt(jnp.sum(re * re + im * im, axis=axis, keepdims=True))
            n = jnp.maximum(n, EPS_NORM)
            return (re / n, im / n)
        B, N, D = (4, 512, 192)
        H, d, S = (8, 32, 64)
        Sr, dr = (32, 32)
        K = 3
        key = jax.random.key(seed)
        ks = jax.random.split(key, 40)
        g = lambda i, shape, s=1.0: jax.random.normal(ks[i], shape, dtype=jnp.float32) * s
        scale = 1.0 / d ** 0.5
        inp = {'h': g(0, (B, N, D)), 'W_real': g(1, (H, D, d), 0.02), 'W_imag': g(2, (H, D, d), 0.02), 'pw1': g(3, (H, 16, D), D ** (-0.5)), 'pb1': jnp.zeros((H, 16), jnp.float32), 'pw2': g(4, (H, 16), 0.25), 'pb2': jnp.zeros((H,), jnp.float32), 'm_real': g(5, (H, S, d), scale), 'm_imag': g(6, (H, S, d), scale), 'values': g(7, (H, S, D), 0.02), 'gate_w': g(8, (H, H * D), (H * D) ** (-0.5)), 'gate_b': jnp.zeros((H,), jnp.float32), 'out_w': g(9, (D, D), D ** (-0.5)), 'out_b': jnp.zeros((D,), jnp.float32), 'beta': jnp.float32(0.3), 'P_real': g(10, (Sr, dr), scale), 'P_imag': g(11, (Sr, dr), scale), 'C_real': g(12, (Sr, dr), scale), 'C_imag': g(13, (Sr, dr), scale), 'enc_r_w': g(14, (dr, D), D ** (-0.5)), 'enc_i_w': g(15, (dr, D), D ** (-0.5)), 'r_out_w': g(16, (D, 2 * Sr), 0.05), 'r_out_b': jnp.zeros((D,), jnp.float32), 'ew1': g(17, (K, D, D), D ** (-0.5)), 'eb1': jnp.zeros((K, D), jnp.float32), 'eg': jnp.ones((K, D), jnp.float32), 'ebt': jnp.zeros((K, D), jnp.float32), 'ew2': g(18, (K, D, D), D ** (-0.5)), 'eb2': jnp.zeros((K, D), jnp.float32), 'rw1': g(19, (16, D), D ** (-0.5)), 'rb1': jnp.zeros((16,), jnp.float32), 'rw2': g(20, (K, 16), 0.25), 'rb2': jnp.zeros((K,), jnp.float32)}
        return inp
    _L2_attn_all = _L2_attn_setup()
    _L2_attn_in = {k: v for k, v in _L2_attn_all.items() if k in ('W_real', 'W_imag', 'pw1', 'pb1', 'pw2', 'pb2', 'm_real', 'm_imag', 'values', 'gate_w', 'gate_b', 'out_w', 'out_b', 'beta', 'P_real', 'P_imag', 'C_real', 'C_imag', 'enc_r_w', 'enc_i_w', 'r_out_w', 'r_out_b', 'ew1', 'eb1', 'eg', 'ebt', 'ew2', 'eb2', 'rw1', 'rb1', 'rw2', 'rb2')}
    del _L2_attn_all

    def _L2_ffn_setup():
        import jax, jax.numpy as jnp
        import numpy as np
        DECAY = 0.9
        EPS = 0.01
        TOP_K = 2
        key = jax.random.key(seed)
        k1, k2, k3, k4 = jax.random.split(key, 4)
        B, S, H, I, E = (4, 512, 192, 512, 8)
        return {'hidden_states': jax.random.normal(k1, (B, S, H), jnp.float32), 'router_w': jax.random.normal(k2, (E, H), jnp.float32) * 0.02, 'w1': jax.random.normal(k3, (E, I, H), jnp.float32) * 0.02, 'w2': jax.random.normal(k4, (E, H, I), jnp.float32) * 0.02}
    _L2_ffn_all = _L2_ffn_setup()
    _L2_ffn_in = {k: v for k, v in _L2_ffn_all.items() if k in ('router_w', 'w1', 'w2')}
    del _L2_ffn_all

    def _L3_attn_setup():
        import jax, jax.numpy as jnp
        import numpy as np
        NUM_HEADS = 12
        OT_REG = 0.1
        SINKHORN_ITERS = 10
        DIAG_VAL = 1000.0

        def _sot(q):
            N = q.shape[-2]
            qn = q / (jnp.linalg.norm(q, axis=-1, keepdims=True) + 1e-08)
            C = 1.0 - jnp.einsum('bhnd,bhmd->bhnm', qn, qn)
            eye = jnp.eye(N, dtype=bool)
            C = jnp.where(eye, DIAG_VAL, C)
            log_K = -C / OT_REG
            log_marg = -jnp.log(jnp.float32(N))
            log_v = jnp.zeros(q.shape[:2] + (N,), dtype=q.dtype)
            for _ in range(SINKHORN_ITERS):
                log_u = log_marg - jax.nn.logsumexp(log_K + log_v[..., None, :], axis=-1)
                log_v = log_marg - jax.nn.logsumexp(log_K + log_u[..., :, None], axis=-2)
            log_T = log_u[..., :, None] + log_K + log_v[..., None, :]
            z = jnp.exp(log_T)
            z = z / jnp.max(z, axis=(-2, -1), keepdims=True)
            z = jnp.where(eye, 1.0, z)
            return z
        key = jax.random.key(seed)
        k1, k2, k3 = jax.random.split(key, 3)
        B, N, C = (64, 64, 192)
        x = jax.random.normal(k1, (B, N, C), dtype=jnp.float32)
        w_qkv = jax.random.normal(k2, (3 * C, C), dtype=jnp.float32) * C ** (-0.5)
        w_proj = jax.random.normal(k3, (C, C), dtype=jnp.float32) * C ** (-0.5)
        b_proj = jnp.zeros((C,), dtype=jnp.float32)
        return {'x': x, 'w_qkv': w_qkv, 'w_proj': w_proj, 'b_proj': b_proj}
    _L3_attn_all = _L3_attn_setup()
    _L3_attn_in = {k: v for k, v in _L3_attn_all.items() if k in ('w_qkv', 'w_proj', 'b_proj')}
    del _L3_attn_all

    def _L3_ffn_setup():
        import jax, jax.numpy as jnp
        import numpy as np
        E, H, I = (5, 192, 256)
        TOP_K = 2
        key = jax.random.key(seed)
        ks = jax.random.split(key, 6)
        s = 0.02
        return {'x': jax.random.normal(ks[0], (4, 512, H), dtype=jnp.float32), 'router_w': jax.random.normal(ks[1], (E, H), dtype=jnp.float32) * s, 'router_b': jnp.zeros((E,), dtype=jnp.float32), 'gate_w': jax.random.normal(ks[2], (E, H, I), dtype=jnp.float32) * s, 'up_w': jax.random.normal(ks[3], (E, H, I), dtype=jnp.float32) * s, 'down_w': jax.random.normal(ks[4], (E, I, H), dtype=jnp.float32) * s}
    _L3_ffn_all = _L3_ffn_setup()
    _L3_ffn_in = {k: v for k, v in _L3_ffn_all.items() if k in ('router_w', 'router_b', 'gate_w', 'up_w', 'down_w')}
    del _L3_ffn_all
    return {'x': x, 'L0_tok_w_down': _L0_tok_in['w_down'], 'L0_tok_b_down': _L0_tok_in['b_down'], 'L0_tok_w_conv': _L0_tok_in['w_conv'], 'L0_tok_b_conv': _L0_tok_in['b_conv'], 'L0_tok_w_up': _L0_tok_in['w_up'], 'L0_tok_b_up': _L0_tok_in['b_up'], 'L0_attn_in_proj_weight': _L0_attn_in['in_proj_weight'], 'L0_attn_in_proj_bias': _L0_attn_in['in_proj_bias'], 'L0_attn_logit_scale': _L0_attn_in['logit_scale'], 'L0_attn_head_scale': _L0_attn_in['head_scale'], 'L0_attn_out_w': _L0_attn_in['out_w'], 'L0_attn_out_b': _L0_attn_in['out_b'], 'L0_ffn_gate_w': _L0_ffn_in['gate_w'], 'L0_ffn_gate_b': _L0_ffn_in['gate_b'], 'L0_ffn_w1': _L0_ffn_in['w1'], 'L0_ffn_b1': _L0_ffn_in['b1'], 'L0_ffn_w2': _L0_ffn_in['w2'], 'L0_ffn_b2': _L0_ffn_in['b2'], 'L1_attn_qkv_w': _L1_attn_in['qkv_w'], 'L1_attn_qkv_b': _L1_attn_in['qkv_b'], 'L1_attn_proj_w': _L1_attn_in['proj_w'], 'L1_attn_proj_b': _L1_attn_in['proj_b'], 'L1_ffn_Wqk': _L1_ffn_in['Wqk'], 'L1_ffn_bqk': _L1_ffn_in['bqk'], 'L1_ffn_Wv': _L1_ffn_in['Wv'], 'L1_ffn_bv': _L1_ffn_in['bv'], 'L1_ffn_conv_w': _L1_ffn_in['conv_w'], 'L1_ffn_conv_b': _L1_ffn_in['conv_b'], 'L1_ffn_glob': _L1_ffn_in['glob'], 'L1_ffn_pos_bias': _L1_ffn_in['pos_bias'], 'L1_ffn_Wg1': _L1_ffn_in['Wg1'], 'L1_ffn_bg1': _L1_ffn_in['bg1'], 'L1_ffn_Wg2': _L1_ffn_in['Wg2'], 'L1_ffn_bg2': _L1_ffn_in['bg2'], 'L1_ffn_Wp': _L1_ffn_in['Wp'], 'L1_ffn_bp': _L1_ffn_in['bp'], 'L2_attn_W_real': _L2_attn_in['W_real'], 'L2_attn_W_imag': _L2_attn_in['W_imag'], 'L2_attn_pw1': _L2_attn_in['pw1'], 'L2_attn_pb1': _L2_attn_in['pb1'], 'L2_attn_pw2': _L2_attn_in['pw2'], 'L2_attn_pb2': _L2_attn_in['pb2'], 'L2_attn_m_real': _L2_attn_in['m_real'], 'L2_attn_m_imag': _L2_attn_in['m_imag'], 'L2_attn_values': _L2_attn_in['values'], 'L2_attn_gate_w': _L2_attn_in['gate_w'], 'L2_attn_gate_b': _L2_attn_in['gate_b'], 'L2_attn_out_w': _L2_attn_in['out_w'], 'L2_attn_out_b': _L2_attn_in['out_b'], 'L2_attn_beta': _L2_attn_in['beta'], 'L2_attn_P_real': _L2_attn_in['P_real'], 'L2_attn_P_imag': _L2_attn_in['P_imag'], 'L2_attn_C_real': _L2_attn_in['C_real'], 'L2_attn_C_imag': _L2_attn_in['C_imag'], 'L2_attn_enc_r_w': _L2_attn_in['enc_r_w'], 'L2_attn_enc_i_w': _L2_attn_in['enc_i_w'], 'L2_attn_r_out_w': _L2_attn_in['r_out_w'], 'L2_attn_r_out_b': _L2_attn_in['r_out_b'], 'L2_attn_ew1': _L2_attn_in['ew1'], 'L2_attn_eb1': _L2_attn_in['eb1'], 'L2_attn_eg': _L2_attn_in['eg'], 'L2_attn_ebt': _L2_attn_in['ebt'], 'L2_attn_ew2': _L2_attn_in['ew2'], 'L2_attn_eb2': _L2_attn_in['eb2'], 'L2_attn_rw1': _L2_attn_in['rw1'], 'L2_attn_rb1': _L2_attn_in['rb1'], 'L2_attn_rw2': _L2_attn_in['rw2'], 'L2_attn_rb2': _L2_attn_in['rb2'], 'L2_ffn_router_w': _L2_ffn_in['router_w'], 'L2_ffn_w1': _L2_ffn_in['w1'], 'L2_ffn_w2': _L2_ffn_in['w2'], 'L3_attn_w_qkv': _L3_attn_in['w_qkv'], 'L3_attn_w_proj': _L3_attn_in['w_proj'], 'L3_attn_b_proj': _L3_attn_in['b_proj'], 'L3_ffn_router_w': _L3_ffn_in['router_w'], 'L3_ffn_router_b': _L3_ffn_in['router_b'], 'L3_ffn_gate_w': _L3_ffn_in['gate_w'], 'L3_ffn_up_w': _L3_ffn_in['up_w'], 'L3_ffn_down_w': _L3_ffn_in['down_w']}

def reference(x, L0_tok_w_down, L0_tok_b_down, L0_tok_w_conv, L0_tok_b_conv, L0_tok_w_up, L0_tok_b_up, L0_attn_in_proj_weight, L0_attn_in_proj_bias, L0_attn_logit_scale, L0_attn_head_scale, L0_attn_out_w, L0_attn_out_b, L0_ffn_gate_w, L0_ffn_gate_b, L0_ffn_w1, L0_ffn_b1, L0_ffn_w2, L0_ffn_b2, L1_attn_qkv_w, L1_attn_qkv_b, L1_attn_proj_w, L1_attn_proj_b, L1_ffn_Wqk, L1_ffn_bqk, L1_ffn_Wv, L1_ffn_bv, L1_ffn_conv_w, L1_ffn_conv_b, L1_ffn_glob, L1_ffn_pos_bias, L1_ffn_Wg1, L1_ffn_bg1, L1_ffn_Wg2, L1_ffn_bg2, L1_ffn_Wp, L1_ffn_bp, L2_attn_W_real, L2_attn_W_imag, L2_attn_pw1, L2_attn_pb1, L2_attn_pw2, L2_attn_pb2, L2_attn_m_real, L2_attn_m_imag, L2_attn_values, L2_attn_gate_w, L2_attn_gate_b, L2_attn_out_w, L2_attn_out_b, L2_attn_beta, L2_attn_P_real, L2_attn_P_imag, L2_attn_C_real, L2_attn_C_imag, L2_attn_enc_r_w, L2_attn_enc_i_w, L2_attn_r_out_w, L2_attn_r_out_b, L2_attn_ew1, L2_attn_eb1, L2_attn_eg, L2_attn_ebt, L2_attn_ew2, L2_attn_eb2, L2_attn_rw1, L2_attn_rb1, L2_attn_rw2, L2_attn_rb2, L2_ffn_router_w, L2_ffn_w1, L2_ffn_w2, L3_attn_w_qkv, L3_attn_w_proj, L3_attn_b_proj, L3_ffn_router_w, L3_ffn_router_b, L3_ffn_gate_w, L3_ffn_up_w, L3_ffn_down_w):
    import jax
    import jax.numpy as jnp

    def _L0_tok_ref(x, w_down, b_down, w_conv, b_conv, w_up, b_up):
        import jax, jax.numpy as jnp
        import numpy as np
        CURRENT_FRAME = 16

        def quick_gelu(x):
            return x * jax.nn.sigmoid(1.702 * x)
        N, BT, D = x.shape
        T = CURRENT_FRAME
        B = BT // T
        h = x @ w_down + b_down
        D2 = h.shape[-1]
        h = h.reshape(N, B, T, D2).transpose(1, 3, 2, 0)
        h = h.transpose(0, 3, 1, 2).reshape(B * N, D2, T)
        y = jax.lax.conv_general_dilated(h, w_conv, window_strides=(2,), padding=[(1, 1)], feature_group_count=D2, dimension_numbers=('NCH', 'OIH', 'NCH'))
        y = y + b_conv[None, :, None]
        T2 = y.shape[-1]
        y = y.reshape(B, N, D2, T2).transpose(2, 0, 3, 1)
        y = y.reshape(N, B * T2, D2)
        return quick_gelu(y) @ w_up + b_up

    def _L0_attn_ref(x, in_proj_weight, in_proj_bias, logit_scale, head_scale, out_w, out_b):
        import jax, jax.numpy as jnp
        import numpy as np
        import math
        H = 12
        LOGIT_SCALE_MAX = math.log(1.0 / 0.01)

        def _normalize(t, eps=1e-12):
            n = jnp.linalg.norm(t, axis=-1, keepdims=True)
            return t / jnp.maximum(n, eps)
        L, N, C = x.shape
        D = C // H
        qkv = x @ in_proj_weight.T + in_proj_bias
        q, k, v = jnp.split(qkv, 3, axis=-1)

        def to_heads(t):
            return t.reshape(L, N, H, D).transpose(1, 2, 0, 3)
        q, k, v = (to_heads(q), to_heads(k), to_heads(v))
        attn = jnp.einsum('nhld,nhmd->nhlm', _normalize(q), _normalize(k))
        ls = jnp.exp(jnp.minimum(logit_scale, LOGIT_SCALE_MAX))
        attn = attn * ls[None]
        attn = jax.nn.softmax(attn, axis=-1)
        o = jnp.einsum('nhlm,nhmd->nhld', attn, v)
        o = o * head_scale[None]
        o = o.transpose(2, 0, 1, 3).reshape(L, N, C)
        return o @ out_w.T + out_b

    def _L0_ffn_ref(x, gate_w, gate_b, w1, b1, w2, b2):
        import jax, jax.numpy as jnp
        import numpy as np
        B, S, D, E = (8, 256, 192, 8)
        F = 4 * D
        orig_shape = x.shape
        xt = x.reshape(-1, x.shape[-1])
        gates = jax.nn.softmax(xt @ gate_w + gate_b, axis=-1)
        expert_idx = jnp.argmax(gates, axis=-1)
        out = jnp.zeros_like(xt)
        n_experts = w1.shape[0]
        for e in range(n_experts):
            h = jax.nn.gelu(xt @ w1[e] + b1[e], approximate=False)
            y = h @ w2[e] + b2[e]
            out = jnp.where((expert_idx == e)[:, None], y, out)
        return out.reshape(orig_shape)

    def _L1_attn_ref(x, qkv_w, qkv_b, proj_w, proj_b):
        import math
        import jax, jax.numpy as jnp
        import numpy as np
        HIDDEN = 192
        NUM_HEADS = 12
        HEAD_DIM = HIDDEN // NUM_HEADS
        THETA = 10000.0
        BATCH, SEQ = (2, 512)

        def _rope(x):
            S, D = (x.shape[1], x.shape[-1])
            inv_freq = 1.0 / THETA ** (jnp.arange(0, D, 2, dtype=jnp.float32) / D)
            angles = jnp.arange(S, dtype=jnp.float32)[:, None] * inv_freq[None, :]
            sin = jnp.sin(angles)[None, :, None, :].astype(x.dtype)
            cos = jnp.cos(angles)[None, :, None, :].astype(x.dtype)
            x_even = x[..., 0::2]
            x_odd = x[..., 1::2]
            rotated = jnp.stack((x_even * cos - x_odd * sin, x_even * sin + x_odd * cos), axis=-1)
            return rotated.reshape(x.shape)
        B, S, H = x.shape
        qkv = (x @ qkv_w.T + qkv_b).reshape(B, S, 3, NUM_HEADS, HEAD_DIM)
        q, k, v = (qkv[:, :, 0], qkv[:, :, 1], qkv[:, :, 2])
        q = _rope(q).transpose(0, 2, 1, 3)
        k = _rope(k).transpose(0, 2, 1, 3)
        v = v.transpose(0, 2, 1, 3)
        scores = jnp.einsum('bhqd,bhkd->bhqk', q, k) / math.sqrt(HEAD_DIM)
        weights = jax.nn.softmax(scores, axis=-1)
        context = jnp.einsum('bhqk,bhkd->bhqd', weights, v)
        context = context.transpose(0, 2, 1, 3).reshape(B, S, H)
        return context @ proj_w.T + proj_b

    def _L1_ffn_ref(x, Wqk, bqk, Wv, bv, conv_w, conv_b, glob, pos_bias, Wg1, bg1, Wg2, bg2, Wp, bp):
        import jax, jax.numpy as jnp
        import numpy as np
        import math
        B, T, C = (8, 512, 192)
        E = 3
        HD = C // E
        TOPK = 2
        NGLOB = 4

        def _masked_softmax(att, mask):
            att = jnp.where(mask, -jnp.inf, att)
            return jax.nn.softmax(att, axis=-1)
        Bx, Tx, Cx = x.shape
        scale = 1.0 / math.sqrt(HD)
        gate = jax.nn.softmax(jax.nn.relu(x @ Wg1 + bg1) @ Wg2 + bg2, axis=-1)
        top_w, top_i = jax.lax.top_k(gate, TOPK)
        top_w = jax.nn.softmax(top_w, axis=-1)
        qk = x @ Wqk + bqk
        q, k = (qk[..., :Cx], qk[..., Cx:])
        q = q.reshape(Bx, Tx, E, HD)
        k = k.reshape(Bx, Tx, E, HD)
        rows = jnp.arange(Tx)[:, None]
        ys = []
        for e in range(E):
            qe = q[:, :, e]
            ke = k[:, :, e]
            ve = x @ Wv[e] + bv[e]
            if e == 0:
                qc = jnp.transpose(qe, (0, 2, 1))
                qc = jax.lax.conv_general_dilated(qc, conv_w, window_strides=(1,), padding=((1, 1),), feature_group_count=HD, dimension_numbers=('NCH', 'OIH', 'NCH'))
                qe = jnp.transpose(qc + conv_b[None, :, None], (0, 2, 1))
            elif e == 1:
                gb = jnp.broadcast_to(glob[None], (Bx, NGLOB, HD))
                ke = jnp.concatenate([ke, gb], axis=1)
                ve = jnp.concatenate([ve, gb], axis=1)
            att = jnp.einsum('btd,bsd->bts', qe, ke) * scale
            if e == 2 and Tx <= 64:
                att = att + pos_bias[:Tx, :Tx][None]
            S = att.shape[-1]
            mask = jnp.arange(S)[None, :] > rows
            att = _masked_softmax(att, mask[None])
            ys.append(jnp.einsum('bts,bsd->btd', att, ve))
        ys = jnp.stack(ys, axis=2)
        w_e = jnp.sum(jax.nn.one_hot(top_i, E, dtype=x.dtype) * top_w[..., None], axis=-2)
        combined = (ys * w_e[..., None]).reshape(Bx, Tx, Cx)
        return combined @ Wp + bp

    def _L2_attn_ref(h, W_real, W_imag, pw1, pb1, pw2, pb2, m_real, m_imag, values, gate_w, gate_b, out_w, out_b, beta, P_real, P_imag, C_real, C_imag, enc_r_w, enc_i_w, r_out_w, r_out_b, ew1, eb1, eg, ebt, ew2, eb2, rw1, rb1, rw2, rb2):
        import jax, jax.numpy as jnp
        import numpy as np
        EPS_NORM = 1e-12

        def _normalize(re, im, axis=-1):
            n = jnp.sqrt(jnp.sum(re * re + im * im, axis=axis, keepdims=True))
            n = jnp.maximum(n, EPS_NORM)
            return (re / n, im / n)
        B, N, D = h.shape
        H, _, d = W_real.shape
        pr = jnp.einsum('bnD,hDd->bhnd', h, W_real)
        pi = jnp.einsum('bnD,hDd->bhnd', h, W_imag)
        pr, pi = _normalize(pr, pi)
        z = jax.nn.silu(jnp.einsum('bnD,hkD->bhnk', h, pw1) + pb1[None, :, None, :])
        p = jax.nn.sigmoid(jnp.einsum('bhnk,hk->bhn', z, pw2) + pb2[None, :, None]) * 0.95
        mr, mi = _normalize(m_real, m_imag)
        ov_re = jnp.einsum('bhnd,hsd->bhns', pr, mr) + jnp.einsum('bhnd,hsd->bhns', pi, mi)
        ov_im = jnp.einsum('bhnd,hsd->bhns', pi, mr) - jnp.einsum('bhnd,hsd->bhns', pr, mi)
        raw = (1.0 - p)[..., None] * (ov_re * ov_re + ov_im * ov_im) + p[..., None] / d
        attn = raw / (raw.sum(axis=-1, keepdims=True) + 1e-08)
        out_h = jnp.einsum('bhns,hsD->bhnD', attn, values)
        concat = jnp.transpose(out_h, (0, 2, 1, 3)).reshape(B, N, H * D)
        gates = jax.nn.softmax(concat @ gate_w.T + gate_b, axis=-1)
        combined = jnp.einsum('bhnD,bnh->bnD', out_h, gates)
        attn_out = combined @ out_w.T + out_b
        p_tok = p.mean(axis=1)
        h1 = h + attn_out
        coupling = jax.nn.softmax(jnp.einsum('bnD,bmD->bnm', h1, h1) * D ** (-0.5), axis=-1)
        neigh = jnp.einsum('bnm,bm->bn', coupling, 1.0 - p_tok)
        p_new = jnp.clip(p_tok * (1.0 - jax.nn.sigmoid(beta) * neigh), 0.0, 0.95)
        qr, qi = _normalize(h1 @ enc_r_w.T, h1 @ enc_i_w.T)
        Pr, Pi = _normalize(P_real, P_imag)
        Cr, Ci = _normalize(C_real, C_imag)
        a_re = qr @ Pr.T + qi @ Pi.T
        a_im = qr @ Pi.T - qi @ Pr.T
        b_re = qr @ Cr.T + qi @ Ci.T
        b_im = qr @ Ci.T - qi @ Cr.T
        g_re = (Pr * Cr + Pi * Ci).sum(-1)
        g_im = (Pr * Ci - Pi * Cr).sum(-1)
        t_re = a_re * g_re - a_im * g_im
        t_im = a_re * g_im + a_im * g_re
        R_re = t_re * b_re + t_im * b_im
        R_im = t_im * b_re - t_re * b_im
        feats = jnp.concatenate([R_re, R_im], axis=-1)
        reason = feats @ r_out_w.T + r_out_b
        h2 = h1 + (1.0 - p_new)[..., None] * reason
        x = jnp.einsum('bnD,kED->bnkE', h2, ew1) + eb1
        mu = x.mean(axis=-1, keepdims=True)
        var = ((x - mu) ** 2).mean(axis=-1, keepdims=True)
        x = (x - mu) / jnp.sqrt(var + 1e-05) * eg + ebt
        x = jax.nn.gelu(x, approximate=False)
        y = jnp.einsum('bnkE,kDE->bnkD', x, ew2) + eb2
        rg = jax.nn.softmax(jax.nn.gelu(h2 @ rw1.T + rb1, approximate=False) @ rw2.T + rb2, axis=-1)
        route = jnp.einsum('bnkD,bnk->bnD', y, rg)
        return h2 + route

    def _L2_ffn_ref(hidden_states, router_w, w1, w2):
        import jax, jax.numpy as jnp
        import numpy as np
        DECAY = 0.9
        EPS = 0.01
        TOP_K = 2
        B, S, H = hidden_states.shape
        E = router_w.shape[0]
        flat = hidden_states.reshape(B * S, H)
        logits = flat @ router_w.T
        probs = jax.nn.softmax(logits, axis=-1)
        topk_probs, topk_idx = jax.lax.top_k(probs, TOP_K)
        importance = jax.lax.stop_gradient(probs).sum(axis=0)
        running = jnp.ones((E,), dtype=flat.dtype)
        blended = running + (1.0 - DECAY) * (importance - running)
        running = blended + EPS
        balance = running[topk_idx]
        balanced = topk_probs / balance
        balanced = balanced / balanced.sum(axis=-1, keepdims=True)
        h = jnp.einsum('th,eih->tei', flat, w1)
        h = jax.nn.silu(h)
        outs = jnp.einsum('tei,ehi->teh', h, w2)
        sel = jnp.take_along_axis(outs, topk_idx[:, :, None], axis=1)
        combined = (sel * balanced[..., None]).sum(axis=1)
        return combined.reshape(B, S, H)

    def _L3_attn_ref(x, w_qkv, w_proj, b_proj):
        import jax, jax.numpy as jnp
        import numpy as np
        NUM_HEADS = 12
        OT_REG = 0.1
        SINKHORN_ITERS = 10
        DIAG_VAL = 1000.0

        def _sot(q):
            N = q.shape[-2]
            qn = q / (jnp.linalg.norm(q, axis=-1, keepdims=True) + 1e-08)
            C = 1.0 - jnp.einsum('bhnd,bhmd->bhnm', qn, qn)
            eye = jnp.eye(N, dtype=bool)
            C = jnp.where(eye, DIAG_VAL, C)
            log_K = -C / OT_REG
            log_marg = -jnp.log(jnp.float32(N))
            log_v = jnp.zeros(q.shape[:2] + (N,), dtype=q.dtype)
            for _ in range(SINKHORN_ITERS):
                log_u = log_marg - jax.nn.logsumexp(log_K + log_v[..., None, :], axis=-1)
                log_v = log_marg - jax.nn.logsumexp(log_K + log_u[..., :, None], axis=-2)
            log_T = log_u[..., :, None] + log_K + log_v[..., None, :]
            z = jnp.exp(log_T)
            z = z / jnp.max(z, axis=(-2, -1), keepdims=True)
            z = jnp.where(eye, 1.0, z)
            return z
        B, N, C = x.shape
        H = NUM_HEADS
        hd = C // H
        scale = hd ** (-0.5)
        qkv = jnp.einsum('bnc,oc->bno', x, w_qkv)
        qkv = qkv.reshape(B, N, 3, H, hd).transpose(2, 0, 3, 1, 4)
        q, k, v = (qkv[0], qkv[1], qkv[2])
        attn = _sot(q)
        attn = jax.nn.softmax(attn * scale, axis=-1)
        out = jnp.einsum('bhnm,bhmd->bhnd', attn, v)
        out = out.transpose(0, 2, 1, 3).reshape(B, N, C)
        out = jnp.einsum('bnc,oc->bno', out, w_proj) + b_proj
        return out

    def _L3_ffn_ref(x, router_w, router_b, gate_w, up_w, down_w):
        import jax, jax.numpy as jnp
        import numpy as np
        E, H, I = (5, 192, 256)
        TOP_K = 2
        B, S, Hd = x.shape
        xf = x.reshape(-1, Hd)
        T = xf.shape[0]
        logits = xf @ router_w.T + router_b
        scores = jax.nn.softmax(logits, axis=-1)
        vals, idx = jax.lax.top_k(scores, TOP_K)
        vals = vals / jnp.sum(vals, axis=-1, keepdims=True)
        comb = jnp.zeros((T, gate_w.shape[0]), dtype=x.dtype)
        comb = comb.at[jnp.arange(T)[:, None], idx].add(vals)
        g = jnp.einsum('th,ehi->tei', xf, gate_w)
        u = jnp.einsum('th,ehi->tei', xf, up_w)
        y = jnp.einsum('tei,eih->teh', jax.nn.silu(g) * u, down_w)
        out = jnp.einsum('teh,te->th', y, comb)
        return out.reshape(B, S, Hd)
    h = _L0_tok_ref(x, L0_tok_w_down, L0_tok_b_down, L0_tok_w_conv, L0_tok_b_conv, L0_tok_w_up, L0_tok_b_up)
    h = h + _L0_attn_ref(_layernorm(h, axis=-1), L0_attn_in_proj_weight, L0_attn_in_proj_bias, L0_attn_logit_scale, L0_attn_head_scale, L0_attn_out_w, L0_attn_out_b)
    h = h + _L0_ffn_ref(_layernorm(h, axis=-1), L0_ffn_gate_w, L0_ffn_gate_b, L0_ffn_w1, L0_ffn_b1, L0_ffn_w2, L0_ffn_b2)
    h = h + _L1_attn_ref(_layernorm(h, axis=-1), L1_attn_qkv_w, L1_attn_qkv_b, L1_attn_proj_w, L1_attn_proj_b)
    h = h + _L1_ffn_ref(_layernorm(h, axis=-1), L1_ffn_Wqk, L1_ffn_bqk, L1_ffn_Wv, L1_ffn_bv, L1_ffn_conv_w, L1_ffn_conv_b, L1_ffn_glob, L1_ffn_pos_bias, L1_ffn_Wg1, L1_ffn_bg1, L1_ffn_Wg2, L1_ffn_bg2, L1_ffn_Wp, L1_ffn_bp)
    h = h + _L2_attn_ref(_layernorm(h, axis=-1), L2_attn_W_real, L2_attn_W_imag, L2_attn_pw1, L2_attn_pb1, L2_attn_pw2, L2_attn_pb2, L2_attn_m_real, L2_attn_m_imag, L2_attn_values, L2_attn_gate_w, L2_attn_gate_b, L2_attn_out_w, L2_attn_out_b, L2_attn_beta, L2_attn_P_real, L2_attn_P_imag, L2_attn_C_real, L2_attn_C_imag, L2_attn_enc_r_w, L2_attn_enc_i_w, L2_attn_r_out_w, L2_attn_r_out_b, L2_attn_ew1, L2_attn_eb1, L2_attn_eg, L2_attn_ebt, L2_attn_ew2, L2_attn_eb2, L2_attn_rw1, L2_attn_rb1, L2_attn_rw2, L2_attn_rb2)
    h = h + _L2_ffn_ref(_layernorm(h, axis=-1), L2_ffn_router_w, L2_ffn_w1, L2_ffn_w2)
    h = h + _L3_attn_ref(_layernorm(h, axis=-1), L3_attn_w_qkv, L3_attn_w_proj, L3_attn_b_proj)
    h = h + _L3_ffn_ref(_layernorm(h, axis=-1), L3_ffn_router_w, L3_ffn_router_b, L3_ffn_gate_w, L3_ffn_up_w, L3_ffn_down_w)
    return h

_drawn_inputs = setup_inputs


def setup_inputs(seed=0):
    import zlib

    import numpy as np

    out = dict(_drawn_inputs(seed))
    spreads = {'L0_attn_in_proj_bias': (0.0, 0.322),
     'L0_attn_logit_scale': (2.3025851249694824, 0.6),
     'L0_attn_head_scale': (1.0, 0.2),
     'L0_attn_out_b': (0.0, 0.8),
     'L0_ffn_gate_b': (0.0, 0.496),
     'L0_ffn_b1': (0.0, 0.8),
     'L0_ffn_b2': (0.0, 0.8),
     'L1_attn_qkv_b': (0.0, 0.8),
     'L1_attn_proj_b': (0.0, 0.8),
     'L1_ffn_bqk': (0.0, 0.8),
     'L1_ffn_bv': (0.0, 0.8),
     'L1_ffn_conv_b': (0.0, 0.8),
     'L1_ffn_pos_bias': (0.0, 2.0),
     'L1_ffn_bg1': (0.0, 0.8),
     'L1_ffn_bg2': (0.0, 0.8),
     'L1_ffn_bp': (0.0, 0.8),
     'L2_attn_pb1': (0.0, 2.0),
     'L2_attn_pb2': (0.0, 2.0),
     'L2_attn_gate_b': (0.0, 2.0),
     'L2_attn_out_b': (0.0, 0.8),
     'L2_attn_r_out_b': (0.0, 0.8),
     'L2_attn_eb1': (0.0, 0.8),
     'L2_attn_eg': (1.0, 0.6),
     'L2_attn_ebt': (0.0, 0.8),
     'L2_attn_eb2': (0.0, 0.8),
     'L2_attn_rb1': (0.0, 2.0),
     'L2_attn_rb2': (0.0, 0.8),
     'L3_attn_b_proj': (0.0, 0.8),
     'L3_ffn_router_b': (0.0, 0.8)}
    factors = {'x': 8.0,
     'L0_tok_w_down': 8.0,
     'L0_tok_b_down': 8.0,
     'L0_tok_w_conv': 8.0,
     'L0_tok_b_conv': 8.0,
     'L0_ffn_gate_w': 5.037,
     'L0_ffn_w1': 8.0,
     'L0_ffn_w2': 8.0,
     'L1_attn_qkv_w': 8.0,
     'L1_attn_proj_w': 8.0,
     'L1_ffn_Wqk': 8.0,
     'L1_ffn_Wv': 8.0,
     'L1_ffn_conv_w': 8.0,
     'L1_ffn_Wg1': 8.0,
     'L1_ffn_Wg2': 8.0,
     'L1_ffn_Wp': 8.0,
     'L2_attn_W_real': 8.0,
     'L2_attn_W_imag': 8.0,
     'L2_attn_pw1': 8.0,
     'L2_attn_pw2': 8.0,
     'L2_attn_m_real': 8.0,
     'L2_attn_m_imag': 8.0,
     'L2_attn_values': 8.0,
     'L2_attn_gate_w': 45.216,
     'L2_attn_out_w': 8.0,
     'L2_attn_P_real': 61.943,
     'L2_attn_P_imag': 64.0,
     'L2_attn_C_real': 47.28,
     'L2_attn_C_imag': 48.201,
     'L2_attn_enc_r_w': 43.848,
     'L2_attn_enc_i_w': 41.162,
     'L2_attn_r_out_w': 40.254,
     'L2_attn_rw1': 3.479,
     'L2_attn_rw2': 3.568,
     'L2_ffn_router_w': 8.0,
     'L2_ffn_w1': 8.0,
     'L2_ffn_w2': 8.0,
     'L3_ffn_router_w': 8.0,
     'L3_ffn_gate_w': 8.0,
     'L3_ffn_up_w': 8.0,
     'L3_ffn_down_w': 8.0}
    for name, (base, spread) in spreads.items():
        noise = np.random.default_rng([zlib.crc32(name.encode()), seed]).standard_normal(out[name].shape)
        drawn = base * np.exp(spread * noise) if base else spread * noise
        out[name] = jnp.asarray(drawn.astype(out[name].dtype))
    for name, factor in factors.items():
        out[name] = (out[name] * factor).astype(out[name].dtype)
    return out
```

```python
from contextlib import ExitStack

import numpy as np

import concourse.bass as bass
from concourse import mybir
from concourse.alu_op_type import AluOpType as ALU

F32 = mybir.dt.float32
ACT = mybir.ActivationFunctionType
AX = mybir.AxisListType

P = 128
D = 192
C = 96
NC = D // C
TOK = 2048
T = TOK // P
U = 4
BANK = 512
HEADS = 12
HP = 32
HW = HEADS * HP
EPS = 1e-5


class Count:

    def __init__(self, nc, ctx, name, primed=0):
        self.sem = ctx.enter_context(nc.semaphore(name))
        self.primed, self.base = primed, 0

    def after(self, n):
        return self.base + self.primed + n

    def room(self, n):
        return self.base + n

    def passed(self, n):
        self.base += n


class Chain:

    def __init__(self, nc, ctx, name):
        self.sem = ctx.enter_context(nc.semaphore(name))
        self.base, self.turn, self.per, self.steps = 0, 0, 0, 0

    def start(self, turn=0, per=0):
        self.turn, self.per, self.steps = turn, per, 0

    def __call__(self, eng, ins):
        self.steps += 1
        ins.then_inc(self.sem, 1)
        eng.wait_ge(self.sem, self.turn * self.per + (self.base + self.steps))

    def apart(self, eng, ins):
        self(eng, ins)
        self.steps += 1
        eng.sem_inc(self.sem, 1)

    def end(self, turns=1):
        if turns > 1:
            assert self.steps == self.per, (self.steps, self.per)
        self.base += turns * self.steps


class Core:

    def __init__(self, nc, ctx, dram):
        self.nc, self.ctx, self.dram = nc, ctx, dram
        self.counts = {}
        self.buffers = 0
        self.H = self.keep("residual", [P, T, D])
        self.ident = self.keep("identity", [P, P])
        self.ones = self.keep("ones", [P, P])
        self.ps = ctx.enter_context(nc.psum_tensor("psum", [P, 8, BANK], F32))
        self.dve, self.act, self.pool = (Chain(nc, ctx, f"{e}_step_done") for e in ("vector", "scalar", "gpsimd"))

    def keep(self, name, shape):
        return self.ctx.enter_context(self.nc.sbuf_tensor(name, shape, F32))

    def buffer(self, mem, name, shape):
        self.buffers += 1
        return mem.enter_context(self.nc.sbuf_tensor(f"{name}_{self.buffers}", shape, F32))

    def count(self, name, primed=0):
        if name not in self.counts:
            self.counts[name] = Count(self.nc, self.ctx, name, primed)
        assert self.counts[name].primed == primed
        return self.counts[name]


def bcast(ap, shape):
    return ap.broadcast_to(shape)


def load(k, pairs):
    loaded = k.count("weights_loaded")
    with k.nc.Block() as block:
        @block.sync
        def _(sp):
            for n, (dst, name) in enumerate(pairs):
                sp.dma_start(dst, k.dram[name]).then_inc(loaded.sem, 16)
            sp.wait_ge(loaded.sem, loaded.after(16 * len(pairs)))
    loaded.passed(16 * len(pairs))


def begin(k):
    nc = k.nc
    loaded = k.count("weights_loaded")
    with nc.Block() as block:
        @block.sync
        def _(sp):
            sp.dma_start(k.ident[:, :], k.dram["identity"]).then_inc(loaded.sem, 16)
            for s in k.all_primed:
                sp.sem_inc(s.sem, s.primed)
            sp.wait_ge(loaded.sem, loaded.after(16))

        @block.gpsimd
        def _(pool):
            pool.memset(k.ones[:, :], 1.0)
    loaded.passed(16)


def front(k, outs, xt_big=None, xn_big=None, src=None):
    nc, ps = k.nc, k.ps
    norm = src is None
    xn_ready = k.count("xn_ready")
    var_ready = k.count("var_ready")
    std_ready = k.count("std_ready")
    xn_transposed = k.count("xn_transposed", U)
    xt_ready = k.count("xt_ready")
    xt_spread = k.count("xt_spread", U)
    projected = k.count("projected")
    projection_read = k.count("projection_read", 2)
    with ExitStack() as mem:
        XN = k.buffer(mem, "xn_tiles", [P, U, D])
        XT = k.buffer(mem, "xt_tiles", [C + 1, U, NC, P])
        stats = k.buffer(mem, "bn_stats", [P, U, 6])
        mv = k.buffer(mem, "mean_var", [P, U, 2])
        rstd = k.buffer(mem, "rstd", [P, U])
        spreads = xt_big is not None or xn_big is not None
        with nc.Block() as block:
            @block.vector
            def _(dve):
                dve.memset(XT[C:C + 1, :, :, :], 1.0).then_inc(k.dve.sem, 1)
                dve.wait_ge(k.dve.sem, k.dve.base + 1)
                k.dve.base += 1
                def normalise(i):
                    k.dve.start(i, 5)
                    for u in range(U):
                        last = dve.bn_stats(stats[:, u, :], k.H[:, bass.ds(i * U + u, 1), :])
                    k.dve.apart(dve, last)
                    for u in range(U):
                        last = dve.bn_aggr(mv[:, u, :], stats[:, u, :])
                    k.dve(dve, last)
                    k.dve(dve, dve.tensor_scalar(rstd[:, :], mv[:, :, 1], EPS, None, ALU.add))
                    dve.sem_inc(var_ready.sem, 1)
                    dve.wait_ge(std_ready.sem, i + std_ready.after(1))
                    k.dve(dve, dve.reciprocal(rstd[:, :], rstd[:, :]))
                    for u in range(U):
                        t = i * U + u
                        dve.wait_ge(xn_transposed.sem, i * U + xn_transposed.room(u + 1))
                        if spreads:
                            dve.wait_ge(xt_spread.sem, i * U + xt_spread.room(u + 1))
                        dve.tensor_scalar(XN[:, u, :], k.H[:, bass.ds(t, 1), :], mv[:, u, 0:1], rstd[:, u:u + 1],
                                          ALU.subtract, ALU.mult).then_inc(xn_ready.sem, 1)
                    dve.wait_ge(xn_ready.sem, i * U + xn_ready.after(U))

                with dve.Fori(0, T // U) as i:
                    if not norm:
                        for u in range(U):
                            dve.wait_ge(xn_transposed.sem, i * U + xn_transposed.room(u + 1))
                            dve.tensor_copy(XN[:, u, :], src[:, bass.ds(i * U + u, 1), :]).then_inc(xn_ready.sem, 1)
                    else:
                        normalise(i)
                if norm:
                    k.dve.end(T // U)

            @block.tensor
            def _(pe):
                with pe.Fori(0, T // U) as i:
                    for u in range(U):
                        pe.wait_ge(xn_ready.sem, i * U + xn_ready.after(u + 1))
                        for c in range(NC):
                            last = pe.transpose(ps[0:C, u // 2, (2 * (u % 2) + c) * P:(2 * (u % 2) + c + 1) * P],
                                                XN[:, u, c * C:(c + 1) * C], k.ident[:, :])
                        last.then_inc(xn_transposed.sem, 1)
                    for u in range(U):
                        if not outs:
                            break
                        if u % 2 == 0:
                            pe.wait_ge(xt_ready.sem, i * (U // 2) + xt_ready.after(u // 2 + 1))
                        pe.wait_ge(projection_read.sem, i * U + projection_read.room(u + 1))
                        for n, (w, dst) in enumerate(outs):
                            width = dst.shape[2]
                            for c in range(NC):
                                r = C + 1 - c
                                last = pe.matmul(ps[:, 2 + 2 * (u % 2) + n, 0:width], XT[0:r, u, c, :],
                                                 w[0:r, c, :], start=(c == 0), stop=(c == NC - 1))
                        last.then_inc(projected.sem, 1)

            @block.scalar
            def _(act):
                with act.Fori(0, T // U) as i:
                    if norm:
                        act.wait_ge(var_ready.sem, i + var_ready.after(1))
                        act.activation(rstd[:, :], rstd[:, :], ACT.Sqrt).then_inc(std_ready.sem, 1)
                    for h in range(U // 2):
                        act.wait_ge(xn_transposed.sem, i * U + xn_transposed.after(2 * h + 2))
                        if spreads:
                            act.wait_ge(xt_spread.sem, i * U + xt_spread.room(2 * h + 2))
                        act.copy(XT[0:C, 2 * h:2 * h + 2, :, :], ps[0:C, h, :]).then_inc(xt_ready.sem, 1)
                    for u in range(U):
                        if not outs:
                            break
                        act.wait_ge(projected.sem, i * U + projected.after(u + 1))
                        for n, (w, dst) in enumerate(outs):
                            width = dst.shape[2]
                            last = act.copy(dst[:, bass.ds(i * U + u, 1), :], ps[:, 2 + 2 * (u % 2) + n, 0:width])
                        last.then_inc(projection_read.sem, 1)

            @block.gpsimd
            def _(pool):
                if not spreads:
                    return
                if xt_big is not None:
                    k.pool.start()
                    k.pool(pool, pool.memset(xt_big[C:C + 1, :, :], 1.0))
                    k.pool.end()
                with pool.Fori(0, T // U) as i:
                    for u in range(U):
                        if xn_big is not None:
                            pool.wait_ge(xn_ready.sem, i * U + xn_ready.after(u + 1))
                            last = pool.tensor_copy(xn_big[:, bass.ds(i * U + u, 1), :], XN[:, u, :])
                        if xt_big is not None:
                            pool.wait_ge(xt_ready.sem, i * (U // 2) + xt_ready.after(u // 2 + 1))
                            last = pool.tensor_copy(xt_big[0:C, :, bass.ds((i * U + u) * P, P)], XT[0:C, u, :, :])
                        last.then_inc(xt_spread.sem, 1)
    if norm:
        var_ready.passed(T // U)
        std_ready.passed(T // U)
    xn_ready.passed(T)
    xn_transposed.passed(T)
    xt_ready.passed(T // 2)
    if spreads:
        xt_spread.passed(T)
    if outs:
        projected.passed(T)
        projection_read.passed(T)


def route(k, L, E, kind, mem, lower=None, top=1, gates=None):
    nc, ps = k.nc, k.ps
    scores_ready = k.count("scores_ready")
    exps_ready = k.count("exps_ready")
    load_ready = k.count("load_ready")
    load_summed = k.count("load_summed")
    st = k.buffer(mem, "route_stat", [P, T])
    beats = k.buffer(mem, "route_beats", [P, T, E, E])
    ties = k.buffer(mem, "route_ties", [P, T, E, E])
    sel = k.buffer(mem, "route_selected", [P, T, E])
    load_e = k.buffer(mem, "route_load", [P, E])
    per_token = [P, T, E]
    pair = [P, T, E, E]
    row = lambda a: a[:, :].unsqueeze(2).broadcast_to(per_token)
    passes = 2 if kind == "softmax_top" else 1
    with nc.Block() as block:
        @block.vector
        def _(dve):
            link = lambda ins: k.dve(dve, ins)
            k.dve.start()

            def normalise(W):
                link(dve.tensor_reduce(st[:, :], W, AX.X, ALU.add))
                link(dve.reciprocal(st[:, :], st[:, :]))
                link(dve.tensor_tensor(W, W, row(st), ALU.mult))

            link(dve.tensor_reduce(st[:, :], L, AX.X, ALU.max))
            dve.tensor_tensor(L, L, row(st), ALU.subtract).then_inc(scores_ready.sem, 1)
            dve.wait_ge(exps_ready.sem, exps_ready.after(1))
            normalise(L)
            link(dve.tensor_tensor(beats[:, :, :, :], L.unsqueeze(2).broadcast_to(pair),
                                   L.unsqueeze(3).broadcast_to(pair), ALU.is_gt))
            link(dve.tensor_tensor(ties[:, :, :, :], L.unsqueeze(2).broadcast_to(pair),
                                   L.unsqueeze(3).broadcast_to(pair), ALU.is_equal))
            tri = lower[:, 0:E * E].rearrange("p (e j) -> p e j", e=E).unsqueeze(1).broadcast_to(pair)
            link(dve.tensor_tensor(ties[:, :, :, :], ties[:, :, :, :], tri, ALU.mult))
            link(dve.tensor_tensor(beats[:, :, :, :], beats[:, :, :, :], ties[:, :, :, :], ALU.add))
            link(dve.tensor_reduce(sel[:, :, :], beats[:, :, :, :], AX.X, ALU.add))
            if kind == "argmax":
                link(dve.tensor_scalar(L, sel[:, :, :], float(top), None, ALU.is_lt))
                return k.dve.end()
            link(dve.tensor_scalar(sel[:, :, :], sel[:, :, :], float(top), None, ALU.is_lt))
            if kind == "balanced":
                dve.tensor_reduce(load_e[:, :], L.rearrange("p t e -> p e t"), AX.X,
                                  ALU.add).then_inc(load_ready.sem, 1)
                dve.wait_ge(load_summed.sem, load_summed.after(1))
                link(dve.tensor_scalar(load_e[:, :], ps[:, 0, 0:E], -1.0, 1.0 - 0.9, ALU.add, ALU.mult))
                link(dve.tensor_scalar(load_e[:, :], load_e[:, :], 1.0, 0.01, ALU.add, ALU.add))
                link(dve.reciprocal(load_e[:, :], load_e[:, :]))
                link(dve.tensor_tensor(L, L, load_e[:, :].unsqueeze(1).broadcast_to(per_token), ALU.mult))
            if kind == "softmax_top":
                link(dve.tensor_reduce(st[:, :], L, AX.X, ALU.max))
                dve.tensor_tensor(L, L, row(st), ALU.subtract).then_inc(scores_ready.sem, 1)
                dve.wait_ge(exps_ready.sem, exps_ready.after(2))
            link(dve.tensor_tensor(L, L, sel[:, :, :], ALU.mult))
            normalise(L)
            k.dve.end()

        @block.scalar
        def _(act):
            for n in range(passes):
                act.wait_ge(scores_ready.sem, scores_ready.after(n + 1))
                act.activation(L, L, ACT.Exp).then_inc(exps_ready.sem, 1)

        @block.tensor
        def _(pe):
            if kind == "balanced":
                pe.wait_ge(load_ready.sem, load_ready.after(1))
                pe.matmul(ps[:, 0, 0:E], k.ones[:, :], load_e[:, :], start=True,
                          stop=True).then_inc(load_summed.sem, 1)
    scores_ready.passed(passes)
    exps_ready.passed(passes)
    if kind == "balanced":
        load_ready.passed(1)
        load_summed.passed(1)


def experts(k, E, F, xt, w1, w2, W, func, w1_up=None, b2=None):
    nc, ps = k.nc, k.ps
    NF = F // P
    G = TOK // BANK
    J = BANK // P
    hidden_in = k.count("hidden_in")
    hidden_ready = k.count("hidden_ready", 4)
    expert_out = k.count("expert_out", 2 * J)
    expert_added = k.count("expert_added", J)
    gate_ready = k.count("gate_ready", 2)
    per_chunk = 1 if w1_up is None else 2
    ring = 4 // per_chunk
    with ExitStack() as mem:
        hid = k.buffer(mem, "hidden", [P, 2, NF, BANK])
        gate = k.buffer(mem, "gate", [P, 2, BANK]) if w1_up is not None else None
        with nc.Block() as block:
            @block.tensor
            def _(pe):
                with pe.Fori(0, G) as g:
                    def first(e):
                        for f in range(NF):
                            n = e * NF + f
                            pe.wait_ge(hidden_ready.sem, g * (E * NF) + (hidden_ready.base + hidden_ready.primed - ring + n + 1))
                            for m, w in enumerate((w1,) if w1_up is None else (w1, w1_up)):
                                for c in range(NC):
                                    r = C + 1 - c
                                    last = pe.matmul(ps[:, (n % ring) * per_chunk + m, :], w[0:r, e, c, f * P:(f + 1) * P],
                                                     xt[0:r, c, bass.ds(g * BANK, BANK)], start=(c == 0), stop=(c == NC - 1))
                            last.then_inc(hidden_in.sem, 1)

                    def second(e):
                        pe.wait_ge(hidden_ready.sem, g * (E * NF) + hidden_ready.after((e + 1) * NF))
                        for j in range(J):
                            pe.wait_ge(expert_added.sem, g * (E * J) + expert_added.room(e * J + j + 1))
                            for f in range(NF):
                                last = pe.matmul(ps[:, 4 + j, 0:D], hid[:, e % 2, f, j * P:(j + 1) * P], w2[:, e, f, :],
                                                 start=(f == 0), stop=(f == NF - 1))
                            last.then_inc(expert_out.sem, 1)

                    first(0)
                    for e in range(E):
                        if e + 1 < E:
                            first(e + 1)
                        second(e)

            @block.scalar
            def _(act):
                with act.Fori(0, G) as g:
                    for e in range(E):
                        if w1_up is None:
                            act.wait_ge(expert_out.sem, g * (E * J) + expert_out.room((e + 1) * J))
                        for f in range(NF):
                            n = e * NF + f
                            act.wait_ge(hidden_in.sem, g * (E * NF) + hidden_in.after(n + 1))
                            if w1_up is None:
                                act.activation(hid[:, e % 2, f, :], ps[:, n % ring, :], func).then_inc(hidden_ready.sem, 1)
                            else:
                                act.wait_ge(hidden_ready.sem, g * (E * NF) + (hidden_ready.base + hidden_ready.primed - 2 + n + 1))
                                act.activation(gate[:, n % 2, :], ps[:, (n % ring) * 2, :], func).then_inc(gate_ready.sem, 1)

            @block.vector
            def _(dve):
                with dve.Fori(0, G) as g:
                    def up(e):
                        dve.wait_ge(expert_out.sem, g * (E * J) + expert_out.room((e + 1) * J))
                        for f in range(NF):
                            n = e * NF + f
                            dve.wait_ge(gate_ready.sem, g * (E * NF) + gate_ready.after(n + 1))
                            dve.tensor_tensor(hid[:, e % 2, f, :], gate[:, n % 2, :], ps[:, (n % ring) * 2 + 1, :],
                                              ALU.mult).then_inc(hidden_ready.sem, 1)

                    def add(e):
                        for j in range(J):
                            t = g * J + j
                            h = k.H[:, bass.ds(t, 1), :]
                            dve.wait_ge(expert_added.sem, g * (E * J) + expert_added.room(e * J + j + 1))
                            if b2 is not None:
                                k.dve(dve, dve.scalar_tensor_tensor(h, b2[:, e, :], W[:, bass.ds(t, 1), e:e + 1], h, ALU.mult, ALU.add))
                            dve.wait_ge(expert_out.sem, g * (E * J) + expert_out.after(e * J + j + 1))
                            dve.scalar_tensor_tensor(h, ps[:, 4 + j, 0:D], W[:, bass.ds(t, 1), e:e + 1], h, ALU.mult,
                                                     ALU.add).then_inc(expert_added.sem, 1)
                    k.dve.start(g, E * J if b2 is not None else 0)
                    if w1_up is not None:
                        up(0)
                    for e in range(E):
                        if w1_up is not None and e + 1 < E:
                            up(e + 1)
                        add(e)
                k.dve.end(G)
    hidden_in.passed(G * E * NF)
    hidden_ready.passed(G * E * NF)
    expert_out.passed(G * E * J)
    expert_added.passed(G * E * J)
    if w1_up is not None:
        gate_ready.passed(G * E * NF)


def moe(k, tag, E, F, kind, top, func, gated=False, bias2=False):
    nc = k.nc
    with ExitStack() as mem:
        sb = lambda name, shape: mem.enter_context(nc.sbuf_tensor(f"{tag}_{name}", shape, F32))
        router, w1, w2 = sb("router", [C + 1, NC, E]), sb("w1", [C + 1, E, NC, F]), sb("w2", [P, E, F // P, D])
        up = sb("up", [C + 1, E, NC, F]) if gated else None
        b2 = sb("b2", [P, E, D]) if bias2 else None
        lower = sb("lower", [P, E * E])
        pairs = [(router[:, :, :], f"{tag}_router"), (w1[:, :, :, :], f"{tag}_w1"), (w2[:, :, :, :], f"{tag}_w2"), (lower[:, :], f"lower{E}")]
        if gated:
            pairs.append((up[:, :, :, :], f"{tag}_up"))
        if bias2:
            pairs.append((b2[:, :, :], f"{tag}_b2"))
        xt = sb("xt", [C + 1, NC, TOK])
        W = sb("weights", [P, T, E])
        load(k, pairs)
        front(k, [(router, W)], xt_big=xt)
        with ExitStack() as inner:
            route(k, W[:, :, :], E, kind, inner, lower, top)
        experts(k, E, F, xt, w1, w2, W, func, w1_up=up, b2=b2)


def diagonal_blocks(ps, bank, NJ, L, eng_copy, dst_of, blocks):
    for b in blocks:
        rows = slice(b * L, (b + 1) * L)
        src = ps[rows, bank:bank + NJ, 0:3 * P].rearrange("p j (g m) -> p j g m", m=P)[:, :, :, b * L:(b + 1) * L]
        dst = dst_of(rows)
        if NJ == 1:
            src = src[:, 0, :, :]
        else:
            dst = dst.rearrange("p (j g) m -> p j g m", j=NJ)
        last = eng_copy(dst, src)
    return last


class Attention:

    G = 3

    def __init__(self, k, mem, tag, NJ, M, L, scale, values, wo=None, bo=None, ot_big=None, mask=None, head_w=None,
                 score_bank=4, out_bank=0):
        self.k, self.NJ, self.M, self.L, self.scale, self.values = k, NJ, M, L, scale, values
        self.S, self.mask, self.head_w = NJ * self.G, mask, head_w
        self.wo, self.bo, self.ot_big, self.score_bank, self.out_bank = wo, bo, ot_big, score_bank, out_bank
        sb = lambda name, shape: mem.enter_context(k.nc.sbuf_tensor(f"{tag}_{name}", shape, F32))
        S = self.S
        self.SC = sb("scores", [P, 2, S, L])
        self.PT = sb("probs_t", [P, 2, S, P])
        self.V = sb("values", [P, 2, S * M])
        self.OT = sb("out_t", [NJ * M, 2, self.G, P])
        self.stat = sb("row_stat", [P, 2, S])
        self.scores_in = k.count("scores_in")
        self.scores_out = k.count("scores_out", 2)
        self.shifted = k.count("shifted")
        self.exped = k.count("exped")
        self.probs_ready = k.count("probs_ready", 2)
        self.v_staged = k.count("v_staged")
        self.pv_done = k.count("pv_done", 2)
        self.ot_ready = k.count("ot_ready", 1)
        self.out_ready = k.count("out_ready")
        self.out_added = k.count("out_added", 1)

    def finished(self, n=T, scores=True, staged=True):
        for s in (self.exped, self.probs_ready, self.pv_done, self.ot_ready):
            s.passed(n)
        if staged:
            self.v_staged.passed(n)
        if scores:
            self.scores_in.passed(n)
            self.shifted.passed(n)
            self.scores_out.passed(2 * n)
        if self.wo is not None:
            self.out_ready.passed(n)
            self.out_added.passed(n)

    def zero(self, dve):
        self.k.dve.start()
        self.k.dve(dve, dve.memset(self.PT[:, :, :, :], 0.0))
        self.k.dve.end()

    def _blocks(self, eng_copy, p, blocks):
        dst = lambda rows: self.SC[rows, p, :, :]
        diagonal_blocks(self.k.ps, self.score_bank, self.NJ, self.L, eng_copy, dst, blocks).then_inc(self.scores_out.sem, 1)

    def act_extract(self, act, i, p):
        half = range(0, P // self.L // 2)
        act.wait_ge(self.scores_in.sem, 2 * i + self.scores_in.after(p + 1))
        act.wait_ge(self.probs_ready.sem, 2 * i + self.probs_ready.room(p + 1))
        self._blocks(act.copy, p, half)

    def dve_extract(self, dve, i, p):
        half = range(P // self.L // 2, P // self.L)
        dve.wait_ge(self.scores_in.sem, 2 * i + self.scores_in.after(p + 1))
        self._blocks(dve.tensor_copy, p, half)

    SHIFT_STEPS, PROB_STEPS = 1, 3

    def dve_shift(self, dve, i, p):
        k, sc = self.k, self.SC[:, p, :, :]
        dve.wait_ge(self.scores_out.sem, 4 * i + self.scores_out.after(2 * p + 2))
        if self.mask is not None:
            k.dve(dve, dve.scalar_tensor_tensor(sc, sc, self.scale, self.mask[:, :, :], ALU.mult, ALU.add))
        st = self.stat[:, p, :]
        k.dve(dve, dve.tensor_reduce(st, sc, AX.X, ALU.max))
        dve.tensor_tensor(sc, sc, st.unsqueeze(2).broadcast_to([P, self.S, self.L]), ALU.subtract).then_inc(self.shifted.sem, 1)

    def act_exp(self, act, i, p):
        act.wait_ge(self.shifted.sem, 2 * i + self.shifted.after(p + 1))
        sc = self.SC[:, p, :, :]
        act.activation(sc, sc, ACT.Exp, scale=1.0 if self.mask is not None else self.scale).then_inc(self.exped.sem, 1)

    def dve_probs(self, dve, i, p):
        k, L, sc, st = self.k, self.L, self.SC[:, p, :, :], self.stat[:, p, :]
        dve.wait_ge(self.exped.sem, 2 * i + self.exped.after(p + 1))
        k.dve(dve, dve.tensor_reduce(st, sc, AX.X, ALU.add))
        k.dve(dve, dve.reciprocal(st, st))
        if self.head_w is not None:
            k.dve(dve, dve.tensor_tensor(st, st, self.head_w[:, bass.ds(2 * i + p, 1), :], ALU.mult))
        k.dve(dve, dve.tensor_tensor(sc, sc, st.unsqueeze(2).broadcast_to([P, self.S, L]), ALU.mult))
        dve.wait_ge(self.pv_done.sem, 2 * i + self.pv_done.room(p + 1))
        n = L // 32
        for b in range(P // L):
            for r in range(n):
                for c in range(n):
                    rows = slice(b * L + 32 * r, b * L + 32 * r + 32)
                    out_rows = slice(b * L + 32 * c, b * L + 32 * c + 32)
                    last = dve.transpose(self.PT[out_rows, p, :, b * L + 32 * r:b * L + 32 * r + 32],
                                         self.SC[rows, p, :, 32 * c:32 * c + 32])
        last.then_inc(self.probs_ready.sem, 1)

    def pool_values(self, pool, i, p):
        pool.wait_ge(self.pv_done.sem, 2 * i + self.pv_done.room(p + 1))
        pool.tensor_copy(self.V[:, p, :], self.values[:, bass.ds(2 * i + p, 1), :]).then_inc(self.v_staged.sem, 1)

    def pe_values(self, pe, i, p):
        k, M = self.k, self.M
        if self.values is not None:
            pe.wait_ge(self.v_staged.sem, 2 * i + self.v_staged.after(p + 1))
        pe.wait_ge(self.probs_ready.sem, 2 * i + self.probs_ready.after(p + 1))
        pe.wait_ge(self.ot_ready.sem, 2 * i + self.ot_ready.room(p + 1))
        for g in range(self.G):
            for j in range(self.NJ):
                h = self.NJ * g + j
                last = pe.matmul(k.ps[j * M:(j + 1) * M, self.out_bank, g * P:(g + 1) * P], self.V[:, p, h * M:(h + 1) * M],
                                 self.PT[:, p, j * self.G + g, :], start=True, stop=True)
        last.then_inc(self.pv_done.sem, 1)

    def act_out(self, act, i, p):
        act.wait_ge(self.pv_done.sem, 2 * i + self.pv_done.after(p + 1))
        src = self.k.ps[0:self.NJ * self.M, self.out_bank, 0:self.G * P]
        if self.ot_big is not None:
            src = src.rearrange("p (g n l) -> p g n l", g=self.G, l=self.L)
            dst = self.ot_big[:, :, :].rearrange("p g (l n) -> p g n l", l=self.L)
            n = P // self.L
            for g in range(self.G):
                last = act.copy(dst[:, g, bass.ds((2 * i + p) * n, n), :], src[:, g, :, :])
            last.then_inc(self.ot_ready.sem, 1)
            return
        act.copy(self.OT[:, p, :, :], src).then_inc(self.ot_ready.sem, 1)

    def pe_project(self, pe, i, p):
        k = self.k
        pe.wait_ge(self.ot_ready.sem, 2 * i + self.ot_ready.after(p + 1))
        pe.wait_ge(self.out_added.sem, 2 * i + self.out_added.room(p + 1))
        dst = k.ps[:, self.out_bank + 1, 0:D]
        pe.matmul(dst, k.ones[0:1, :], self.bo[0:1, :], start=True, stop=False)
        for g in range(self.G):
            last = pe.matmul(dst, self.OT[:, p, g, :], self.wo[:, g, :], start=False, stop=(g == self.G - 1))
        last.then_inc(self.out_ready.sem, 1)

    def dve_add(self, dve, i, p):
        k = self.k
        h = k.H[:, bass.ds(2 * i + p, 1), :]
        dve.wait_ge(self.out_ready.sem, 2 * i + self.out_ready.after(p + 1))
        dve.tensor_tensor(h, h, k.ps[:, self.out_bank + 1, 0:D], ALU.add).then_inc(self.out_added.sem, 1)


def head_scores(pe, ps, q, kk):
    for g in range(3):
        for j in range(4):
            rows = slice(32 * j, 32 * j + 32)
            cols = slice(g * P, (g + 1) * P)
            last = pe.matmul(ps[:, 4 + j, cols], q[rows, cols], kk[rows, cols], start=True, stop=True)
    return last


def rotary_attention(k):
    nc, ps = k.nc, k.ps
    with ExitStack() as mem:
        sb = lambda name, shape: mem.enter_context(nc.sbuf_tensor(f"a1_{name}", shape, F32))
        wqk, wv = sb("wqk", [C + 1, NC, 4, HW]), sb("wv", [C + 1, NC, HW])
        wo, bo = sb("wo", [P, 3, D]), sb("bo", [1, D])
        turn = sb("turn", [P, 2, 32])
        xt, V = sb("xt", [C + 1, NC, TOK]), sb("v", [P, T, HW])
        load(k, [(wqk[:, :, :, :], "a1_wqk"), (wv[:, :, :], "a1_wv"), (wo[:, :, :], "a1_wo"), (bo[:, :], "a1_bo"), (turn[:, :, :], "a1_turn")])
        front(k, [(wv, V)], xt_big=xt)
        a = Attention(k, mem, "a1", 4, HP, 32, 0.25, V, wo, bo)
        QK = sb("qk", [P, 2, 2, HW])
        by_cos, by_sin = sb("by_cos", [P, 2, HW]), sb("by_sin", [P, 2, HW])
        qk_in = k.count("qk_in")
        qk_ready = k.count("qk_ready", 1)
        with nc.Block() as block:
            @block.tensor
            def _(pe):
                with pe.Fori(0, T // 2) as i:
                    for p in range(2):
                        pe.wait_ge(qk_ready.sem, 2 * i + qk_ready.room(p + 1))
                        pe.wait_ge(a.out_added.sem, 2 * i + a.out_added.room(1))
                        pe.wait_ge(a.ot_ready.sem, 2 * i + a.ot_ready.room(1))
                        for m in range(4):
                            for g in range(3):
                                for c in range(NC):
                                    r = C + 1 - c
                                    last = pe.matmul(ps[:, m, g * P:(g + 1) * P], wqk[0:r, c, m, g * P:(g + 1) * P],
                                                     xt[0:r, c, bass.ds((2 * i + p) * P, P)], start=(c == 0), stop=(c == NC - 1))
                        last.then_inc(qk_in.sem, 1)
                        pe.wait_ge(qk_ready.sem, 2 * i + qk_ready.after(p + 1))
                        pe.wait_ge(a.scores_out.sem, 4 * i + a.scores_out.room(2 * p + 2))
                        head_scores(pe, ps, QK[:, p, 0, :], QK[:, p, 1, :]).then_inc(a.scores_in.sem, 1)
                    for p in range(2):
                        a.pe_values(pe, i, p)
                        a.pe_project(pe, i, p)

            @block.vector
            def _(dve):
                a.zero(dve)
                with dve.Fori(0, T // 2) as i:
                    k.dve.start(i, 2 * (1 + 1 + 3))
                    for p in range(2):
                        dve.wait_ge(qk_in.sem, 2 * i + qk_in.after(p + 1))
                        rep = lambda n: turn[:, n, :].unsqueeze(1).unsqueeze(1).broadcast_to([P, 2, HEADS, 32])
                        part = lambda n: ps[:, n:4:2, 0:HW].rearrange("p m (h d) -> p m h d", d=32)
                        as4 = lambda b: b[:, :, :].rearrange("p m (h d) -> p m h d", d=32)
                        dve.tensor_tensor(as4(by_cos), part(0), rep(0), ALU.mult)
                        k.dve(dve, dve.tensor_tensor(as4(by_sin), part(1), rep(1), ALU.mult))
                        dve.tensor_tensor(QK[:, p, :, :], by_cos[:, :, :], by_sin[:, :, :], ALU.add).then_inc(qk_ready.sem, 1)
                        a.dve_extract(dve, i, p)
                        a.dve_shift(dve, i, p)
                    for p in range(2):
                        a.dve_probs(dve, i, p)
                    for p in range(2):
                        a.dve_add(dve, i, p)
                k.dve.end(T // 2)

            @block.scalar
            def _(act):
                with act.Fori(0, T // 2) as i:
                    for p in range(2):
                        a.act_extract(act, i, p)
                    for p in range(2):
                        a.act_exp(act, i, p)
                    for p in range(2):
                        a.act_out(act, i, p)

            @block.gpsimd
            def _(pool):
                with pool.Fori(0, T // 2) as i:
                    for p in range(2):
                        a.pool_values(pool, i, p)
        a.finished()
        qk_in.passed(T)
        qk_ready.passed(T)


def causal_mixture(k):
    nc, ps = k.nc, k.ps
    E, HD = 3, 64
    with ExitStack() as mem:
        sb = lambda name, shape: mem.enter_context(nc.sbuf_tensor(f"f1_{name}", shape, F32))
        wqk, wvg = sb("wqk", [C + 1, NC, 2 * D]), sb("wvg", [C + 1, NC, D + 32])
        wo, bo = sb("wo", [HD, E, D]), sb("bo", [1, D])
        conv = sb("conv", [HD, 4])
        mask, pos = sb("mask", [P, E, 32]), sb("pos", [P, E, 32])
        wg2, bg2, lower = sb("wg2", [P, E, 32]), sb("bg2", [P, E]), sb("lower", [P, E * E])
        xt, VG = sb("xt", [C + 1, NC, TOK]), sb("vg", [P, T, D + 32])
        W = sb("w", [P, T, E])
        load(k, [(wqk[:, :, :], "f1_wqk"), (wvg[:, :, :], "f1_wvg"), (wo[:, :, :], "f1_wo"), (bo[:, :], "f1_bo"),
                 (conv[:, :], "f1_conv"), (mask[:, :, :], "f1_mask"), (pos[:, :, :], "f1_pos"),
                 (wg2[:, :, :], "f1_wg2"), (bg2[:, :], "f1_bg2"), (lower[:, :], "lower3")])
        front(k, [(wvg, VG)], xt_big=xt)
        with ExitStack() as inner:
            prod = inner.enter_context(nc.sbuf_tensor("f1_prod", [P, T, E, 32], F32))
            with nc.Block() as block:
                @block.vector
                def _(dve):
                    link = lambda ins: k.dve(dve, ins)
                    k.dve.start()
                    g1 = VG[:, :, D:D + 32]
                    link(dve.tensor_scalar(g1, g1, 0.0, None, ALU.max))
                    link(dve.tensor_tensor(prod[:, :, :, :], g1.unsqueeze(2).broadcast_to([P, T, E, 32]),
                                           wg2[:, :, :].unsqueeze(1).broadcast_to([P, T, E, 32]), ALU.mult))
                    link(dve.tensor_reduce(W[:, :, :], prod[:, :, :, :], AX.X, ALU.add))
                    link(dve.tensor_tensor(W[:, :, :], W[:, :, :], bg2[:, :].unsqueeze(1).broadcast_to([P, T, E]), ALU.add))
                    link(dve.tensor_tensor(mask[:, :, :], mask[:, :, :], pos[:, :, :], ALU.add))
                    k.dve.end()
            route(k, W[:, :, :], E, "softmax_top", inner, lower, 2)
        a = Attention(k, mem, "f1", 1, HD, 32, 0.125, VG[:, :, 0:D], wo, bo, mask=mask, head_w=W, out_bank=2)
        Q, K = sb("q", [HD, 2, E, P]), sb("k", [HD, 2, E, P])
        qk_in = k.count("qk_in")
        qk_ready = k.count("qk_ready", 1)
        keys_ready = k.count("keys_ready", 1)
        with nc.Block() as block:
            @block.tensor
            def _(pe):
                with pe.Fori(0, T // 2) as i:
                    for p in range(2):
                        pe.wait_ge(qk_ready.sem, 2 * i + qk_ready.room(p + 1))
                        pe.wait_ge(keys_ready.sem, 2 * i + keys_ready.room(p + 1))
                        for m in range(2):
                            for e in range(E):
                                cols = slice(m * D + e * HD, m * D + (e + 1) * HD)
                                for c in range(NC):
                                    r = C + 1 - c
                                    last = pe.matmul(ps[0:HD, m, e * P:(e + 1) * P], wqk[0:r, c, cols],
                                                     xt[0:r, c, bass.ds((2 * i + p) * P, P)], start=(c == 0), stop=(c == NC - 1))
                        last.then_inc(qk_in.sem, 1)
                        pe.wait_ge(qk_ready.sem, 2 * i + qk_ready.after(p + 1))
                        pe.wait_ge(keys_ready.sem, 2 * i + keys_ready.after(p + 1))
                        pe.wait_ge(a.scores_out.sem, 4 * i + a.scores_out.room(2 * p + 2))
                        for e in range(E):
                            last = pe.matmul(ps[:, 4, e * P:(e + 1) * P], Q[:, p, e, :], K[:, p, e, :], start=True, stop=True)
                        last.then_inc(a.scores_in.sem, 1)
                    for p in range(2):
                        a.pe_values(pe, i, p)
                        a.pe_project(pe, i, p)

            @block.vector
            def _(dve):
                a.zero(dve)
                with dve.Fori(0, T // 2) as i:
                    k.dve.start(i, 2 * (2 + 2 + 4))
                    for p in range(2):
                        dve.wait_ge(qk_in.sem, 2 * i + qk_in.after(p + 1))
                        q, src = Q[:, p, 0, :], ps[0:HD, 0, 0:P]
                        k.dve(dve, dve.tensor_scalar(q, src, conv[:, 1:2], conv[:, 3:4], ALU.mult, ALU.add))
                        seq = lambda x, a0, a1: x.rearrange("p (b s) -> p b s", s=32)[:, :, a0:a1]
                        k.dve(dve, dve.scalar_tensor_tensor(seq(q, 1, 32), seq(src, 0, 31), conv[:, 0:1], seq(q, 1, 32), ALU.mult, ALU.add))
                        dve.scalar_tensor_tensor(seq(q, 0, 31), seq(src, 1, 32), conv[:, 2:3], seq(q, 0, 31), ALU.mult,
                                                 ALU.add).then_inc(qk_ready.sem, 1)
                        a.dve_extract(dve, i, p)
                        a.dve_shift(dve, i, p)
                    for p in range(2):
                        a.dve_probs(dve, i, p)
                    for p in range(2):
                        a.dve_add(dve, i, p)
                k.dve.end(T // 2)

            @block.scalar
            def _(act):
                with act.Fori(0, T // 2) as i:
                    for p in range(2):
                        act.wait_ge(qk_in.sem, 2 * i + qk_in.after(p + 1))
                        act.wait_ge(qk_ready.sem, 2 * i + qk_ready.after(p + 1))
                        act.copy(Q[:, p, 1:E, :], ps[0:HD, 0, P:E * P])
                        act.copy(K[:, p, :, :], ps[0:HD, 1, 0:E * P]).then_inc(keys_ready.sem, 1)
                        a.act_extract(act, i, p)
                    for p in range(2):
                        a.act_exp(act, i, p)
                    for p in range(2):
                        a.act_out(act, i, p)

            @block.gpsimd
            def _(pool):
                with pool.Fori(0, T // 2) as i:
                    for p in range(2):
                        a.pool_values(pool, i, p)
        a.finished()
        for s in (qk_in, qk_ready, keys_ready):
            s.passed(T)


SINKHORN = 10
GT = 4
GW = GT * HW


def transport_attention(k):
    nc, ps = k.nc, k.ps
    with ExitStack() as mem:
        sb = lambda name, shape: mem.enter_context(nc.sbuf_tensor(f"a3_{name}", shape, F32))
        wq, wv = sb("wq", [C + 1, NC, HW]), sb("wv", [C + 1, NC, HW])
        wo, bo = sb("wo", [P, 3, D]), sb("bo", [1, D])
        eye, off, blocks = sb("eye", [P, 32]), sb("off", [P, 32]), sb("blocks", [P, P])
        V, K = sb("v", [P, T, HW]), sb("kernel", [P, T, HEADS, 32])
        load(k, [(wq[:, :, :], "a3_wq"), (wv[:, :, :], "a3_wv"), (wo[:, :, :], "a3_wo"), (bo[:, :], "a3_bo"),
                 (eye[:, :], "eye32"), (off[:, :], "off32"), (blocks[:, :], "blocks32")])
        with ExitStack() as inner:
            Q = inner.enter_context(nc.sbuf_tensor("a3_q", [P, T, HW], F32))
            front(k, [(wq, Q), (wv, V)])
            transport_kernel(k, inner, Q, K, off)
        Z = sb("z", [P, T, HEADS, 32])
        with ExitStack() as inner:
            scale_kernel(k, inner, K, Z, blocks, eye)
        a = Attention(k, mem, "a3", 4, HP, 32, 0.25, V, wo, bo)
        with nc.Block() as block:
            @block.tensor
            def _(pe):
                with pe.Fori(0, T // 2) as i:
                    for p in range(2):
                        a.pe_values(pe, i, p)
                        a.pe_project(pe, i, p)

            @block.vector
            def _(dve):
                a.zero(dve)
                with dve.Fori(0, T // 2) as i:
                    k.dve.start(i, 2 * 3)
                    for p in range(2):
                        a.dve_probs(dve, i, p)
                    for p in range(2):
                        a.dve_add(dve, i, p)
                k.dve.end(T // 2)

            @block.scalar
            def _(act):
                with act.Fori(0, T // 2) as i:
                    for p in range(2):
                        act.wait_ge(a.probs_ready.sem, 2 * i + a.probs_ready.room(p + 1))
                        act.activation(a.SC[:, p, :, :], Z[:, bass.ds(2 * i + p, 1), :, :], ACT.Exp,
                                       scale=0.25).then_inc(a.exped.sem, 1)
                    for p in range(2):
                        a.act_out(act, i, p)

            @block.gpsimd
            def _(pool):
                with pool.Fori(0, T // 2) as i:
                    for p in range(2):
                        a.pool_values(pool, i, p)
        a.finished(scores=False)


def transport_kernel(k, mem, Q, K, off):
    nc, ps = k.nc, k.ps
    norm = mem.enter_context(nc.sbuf_tensor("a3_norm", [P, T, HEADS], F32))
    QN = mem.enter_context(nc.sbuf_tensor("a3_qn", [P, 2, HW], F32))
    QT = mem.enter_context(nc.sbuf_tensor("a3_qt", [P, 2, HW], F32))
    ten = mem.enter_context(nc.sbuf_tensor("a3_minus_ten", [P, 1], F32))
    squares_ready = k.count("squares_ready")
    norm2_ready = k.count("norm2_ready")
    norm_ready = k.count("norm_ready")
    qn_ready = k.count("qn_ready")
    qn_turned = k.count("qn_turned", 2)
    qt_ready = k.count("qt_ready", 2)
    scores_in = k.count("scores_in")
    scores_out = k.count("scores_out", 2)
    kernel_ready = k.count("kernel_ready")
    with nc.Block() as block:
        @block.scalar
        def _(act):
            act.activation(K[:, :, :, :], Q[:, :, :], ACT.Square).then_inc(squares_ready.sem, 1)
            act.wait_ge(norm2_ready.sem, norm2_ready.after(1))
            act.activation(norm[:, :, :], norm[:, :, :], ACT.Sqrt).then_inc(norm_ready.sem, 1)
            with act.Fori(0, T // 2) as i:
                for p in range(2):
                    act.wait_ge(qn_turned.sem, 2 * i + qn_turned.after(p + 1))
                    act.copy(QT[:, p, :], ps[:, p, 0:HW]).then_inc(qt_ready.sem, 1)
                    act.wait_ge(scores_in.sem, 2 * i + scores_in.after(p + 1))
                    dst = lambda rows: K[rows, bass.ds(2 * i + p, 1), :, :].rearrange("p t s m -> p (t s) m")
                    diagonal_blocks(ps, 4, 4, 32, act.copy, dst, (0, 1)).then_inc(scores_out.sem, 1)
            act.wait_ge(scores_out.sem, scores_out.after(2 * T))
            act.activation(K[:, :, :, :], K[:, :, :, :], ACT.Exp, bias=ten[:, :], scale=10.0).then_inc(kernel_ready.sem, 1)

        @block.vector
        def _(dve):
            k.dve.start()
            dve.memset(ten[:, :], -10.0)
            dve.wait_ge(squares_ready.sem, squares_ready.after(1))
            dve.tensor_reduce(norm[:, :, :], K[:, :, :, :], AX.X, ALU.add).then_inc(norm2_ready.sem, 1)
            dve.wait_ge(norm_ready.sem, norm_ready.after(1))
            k.dve(dve, dve.tensor_scalar(norm[:, :, :], norm[:, :, :], 1e-8, None, ALU.add))
            k.dve(dve, dve.reciprocal(norm[:, :, :], norm[:, :, :]))
            k.dve.end()
            with dve.Fori(0, T // 2) as i:
                for p in range(2):
                    dve.wait_ge(qn_turned.sem, 2 * i + qn_turned.room(p + 1))
                    n = 2 * i + p
                    as3 = lambda x: x.rearrange("p (h d) -> p h d", d=HP)
                    dve.tensor_tensor(as3(QN[:, p, :]), Q[:, bass.ds(n, 1), :].rearrange("p t (h d) -> p (t h) d", d=HP),
                                      norm[:, bass.ds(n, 1), :].rearrange("p t h -> p (t h)").unsqueeze(2).broadcast_to([P, HEADS, HP]),
                                      ALU.mult).then_inc(qn_ready.sem, 1)
                for p in range(2):
                    dve.wait_ge(scores_in.sem, 2 * i + scores_in.after(p + 1))
                    dst = lambda rows: K[rows, bass.ds(2 * i + p, 1), :, :].rearrange("p t s m -> p (t s) m")
                    diagonal_blocks(ps, 4, 4, 32, dve.tensor_copy, dst, (2, 3)).then_inc(scores_out.sem, 1)
            dve.wait_ge(kernel_ready.sem, kernel_ready.after(1))
            dve.tensor_tensor(K[:, :, :, :], K[:, :, :, :],
                              off[:, :].unsqueeze(1).unsqueeze(1).broadcast_to([P, T, HEADS, 32]), ALU.mult)

        @block.tensor
        def _(pe):
            with pe.Fori(0, T // 2) as i:
                for p in range(2):
                    pe.wait_ge(qn_ready.sem, 2 * i + qn_ready.after(p + 1))
                    pe.wait_ge(qt_ready.sem, 2 * i + qt_ready.room(p + 1))
                    for g in range(3):
                        last = pe.transpose(ps[:, p, g * P:(g + 1) * P], QN[:, p, g * P:(g + 1) * P], k.ident[:, :])
                    last.then_inc(qn_turned.sem, 1)
                for p in range(2):
                    pe.wait_ge(qt_ready.sem, 2 * i + qt_ready.after(p + 1))
                    pe.wait_ge(scores_out.sem, 4 * i + scores_out.room(2 * p + 2))
                    head_scores(pe, ps, QT[:, p, :], QT[:, p, :]).then_inc(scores_in.sem, 1)
    for s in (squares_ready, norm2_ready, norm_ready, kernel_ready):
        s.passed(1)
    for s in (qn_ready, qn_turned, qt_ready, scores_in):
        s.passed(T)
    scores_out.passed(2 * T)


def scale_kernel(k, mem, K, Z, blocks, eye):
    nc, ps = k.nc, k.ps
    NG = T // GT
    KV = mem.enter_context(nc.sbuf_tensor("a3_kv", [P, 2, GW], F32))
    KU = mem.enter_context(nc.sbuf_tensor("a3_ku", [P, 2, GW], F32))
    u = mem.enter_context(nc.sbuf_tensor("a3_u", [P, T * HEADS], F32))
    top = mem.enter_context(nc.sbuf_tensor("a3_top", [P, T * HEADS], F32))
    top_t = mem.enter_context(nc.sbuf_tensor("a3_top_t", [P, T * HEADS], F32))
    seq_top = mem.enter_context(nc.sbuf_tensor("a3_seq_top", [P, T * HEADS // 32], F32))
    u_ready = k.count("u_ready")
    ku_ready = k.count("ku_ready")
    ku_summed = k.count("ku_summed")
    n_pairs = GT * HEADS
    group = lambda X, g: X[:, g * GT:(g + 1) * GT, :, :].rearrange("p t h m -> p (t h) m")
    flat = lambda X, g: X[:, g * GT:(g + 1) * GT, :, :].rearrange("p t h m -> p (t h m)")
    part = lambda X, n: X[:, n, :].rearrange("p (q m) -> p q m", m=32)
    spread = lambda x: x.unsqueeze(2).broadcast_to([P, n_pairs, 32])
    with nc.Block() as block:
        @block.vector
        def _(dve):
            k.dve.start()
            k.dve(dve, dve.memset(Z[:, :, :, :], 1.0))
            k.dve.end()
            with dve.Fori(0, SINKHORN) as r:
                k.dve.start(r, 3 * NG)

                def row_scale(g):
                    k.dve(dve, dve.tensor_tensor(part(KV, g % 2), group(K, g), group(Z, g), ALU.mult))
                    ug = u[:, g * n_pairs:(g + 1) * n_pairs]
                    k.dve(dve, dve.tensor_reduce(ug, part(KV, g % 2), AX.X, ALU.add))
                    dve.reciprocal(ug, ug).then_inc(u_ready.sem, 1)

                def column_scale(g):
                    dve.wait_ge(ku_summed.sem, r * NG + ku_summed.after(g + 1))
                    n = 3 * (g % 2)
                    k.dve(dve, dve.reciprocal(flat(Z, g), ps[:, n:n + 3, :].rearrange("p a b -> p (a b)")))

                for g in range(NG):
                    row_scale(g)
                    if g:
                        column_scale(g - 1)
                column_scale(NG - 1)
            k.dve.end(SINKHORN)

            k.dve.start()
            link = lambda ins: k.dve(dve, ins)
            rows3 = lambda X: X[:, :, :, :].rearrange("p t h m -> p (t h) m")
            all_pairs = [P, T * HEADS, 32]
            link(dve.tensor_tensor(rows3(Z), rows3(Z), rows3(K), ALU.mult))
            link(dve.tensor_tensor(rows3(Z), rows3(Z), u[:, :].unsqueeze(2).broadcast_to(all_pairs), ALU.mult))
            link(dve.tensor_reduce(top[:, :], rows3(Z), AX.X, ALU.max))
            link(dve.transpose(top_t[:, :], top[:, :]))
            blocks3 = top_t[:, :].rearrange("p (q n) -> p q n", n=32)
            link(dve.tensor_reduce(seq_top[:, :], blocks3, AX.X, ALU.max))
            link(dve.reciprocal(seq_top[:, :], seq_top[:, :]))
            link(dve.tensor_copy(blocks3, seq_top[:, :].unsqueeze(2).broadcast_to([P, T * HEADS // 32, 32])))
            link(dve.transpose(top[:, :], top_t[:, :]))
            link(dve.tensor_tensor(rows3(Z), rows3(Z), top[:, :].unsqueeze(2).broadcast_to(all_pairs), ALU.mult))
            link(dve.tensor_tensor(rows3(Z), rows3(Z), eye[:, :].unsqueeze(1).broadcast_to(all_pairs), ALU.add))
            k.dve.end()

        @block.gpsimd
        def _(pool):
            with pool.Fori(0, SINKHORN) as r:
                for g in range(NG):
                    pool.wait_ge(u_ready.sem, r * NG + u_ready.after(g + 1))
                    ug = u[:, g * n_pairs:(g + 1) * n_pairs]
                    pool.tensor_tensor(part(KU, g % 2), group(K, g), spread(ug), ALU.mult).then_inc(ku_ready.sem, 1)

        @block.tensor
        def _(pe):
            with pe.Fori(0, SINKHORN) as r:
                for g in range(NG):
                    pe.wait_ge(ku_ready.sem, r * NG + ku_ready.after(g + 1))
                    for b in range(3):
                        last = pe.matmul(ps[:, 3 * (g % 2) + b, :], blocks[:, :], KU[:, g % 2, b * BANK:(b + 1) * BANK],
                                         start=True, stop=True)
                    last.then_inc(ku_summed.sem, 1)
    for s in (u_ready, ku_ready, ku_summed):
        s.passed(SINKHORN * NG)


def cosine_attention(k):
    nc, ps = k.nc, k.ps
    L = 64
    with ExitStack() as mem:
        sb = lambda name, shape: mem.enter_context(nc.sbuf_tensor(f"a0_{name}", shape, F32))
        w = sb("w", [C + 1, NC, 3, HW])
        wo, bo = sb("wo", [P, 3, D]), sb("bo", [1, D])
        log_scale, head_scale = sb("log_scale", [P, HEADS]), sb("head_scale", [P, HEADS])
        xt = sb("xt", [C + 1, NC, TOK])
        OT = sb("ot", [P, 3, TOK])
        load(k, [(w[:, :, :, :], "a0_w"), (wo[:, :, :], "a0_wo"), (bo[:, :], "a0_bo"),
                 (log_scale[:, :], "a0_log_scale"), (head_scale[:, :], "a0_head_scale")])
        front(k, [], xt_big=xt)
        with ExitStack() as inner:
            sb2 = lambda name, shape: inner.enter_context(nc.sbuf_tensor(f"a0_{name}", shape, F32))
            a = Attention(k, inner, "a0", 4, HP, L, 1.0, None, ot_big=OT)
            XT = sb2("xt_tile", [C + 1, 2, NC, P])
            SQ = sb2("squares", [P, 2, 2 * HW])
            norm = sb2("norm", [P, 2, 2, HEADS])
            QN, QT = sb2("qn", [P, 2, 2, HW]), sb2("qt", [P, 2, 2, HW])
            xt_staged = k.count("xt_staged")
            qkv_in = k.count("qkv_in", 2)
            squares_ready = k.count("squares_ready")
            norm2_ready = k.count("norm2_ready")
            norm_ready = k.count("norm_ready")
            qn_ready = k.count("qn_ready")
            qn_turned = k.count("qn_turned", 2)
            qt_ready = k.count("qt_ready", 2)
            with nc.Block() as block:
                @block.gpsimd
                def _(pool):
                    with pool.Fori(0, T // 2) as i:
                        for p in range(2):
                            pool.wait_ge(qkv_in.sem, 2 * i + qkv_in.room(p + 1))
                            for c in range(NC):
                                src = xt[:, c, :].rearrange("p (l n) -> p n l", l=L)[:, bass.ds((2 * i + p) * 2, 2), :]
                                last = pool.tensor_copy(XT[:, p, c, :].rearrange("p (n l) -> p n l", l=L), src)
                            last.then_inc(xt_staged.sem, 1)

                @block.tensor
                def _(pe):
                    with pe.Fori(0, T // 2) as i:
                        for p in range(2):
                            pe.wait_ge(xt_staged.sem, 2 * i + xt_staged.after(p + 1))
                            pe.wait_ge(a.ot_ready.sem, 2 * i + a.ot_ready.room(1))
                            pe.wait_ge(qt_ready.sem, 2 * i + (qt_ready.room(p + 1) + 1))
                            for m in range(3):
                                for c in range(NC):
                                    r = C + 1 - c
                                    last = pe.matmul(ps[:, m, 0:HW], XT[0:r, p, c, :], w[0:r, c, m, :], start=(c == 0), stop=(c == NC - 1))
                            last.then_inc(qkv_in.sem, 1)
                            pe.wait_ge(qn_ready.sem, 2 * i + qn_ready.after(p + 1))
                            for m in range(2):
                                for g in range(3):
                                    cols = slice(g * P, (g + 1) * P)
                                    last = pe.transpose(ps[:, m, cols], QN[:, p, m, cols], k.ident[:, :])
                            last.then_inc(qn_turned.sem, 1)
                            pe.wait_ge(qt_ready.sem, 2 * i + qt_ready.after(p + 1))
                            pe.wait_ge(a.scores_out.sem, 4 * i + a.scores_out.room(2 * p + 2))
                            head_scores(pe, ps, QT[:, p, 0, :], QT[:, p, 1, :]).then_inc(a.scores_in.sem, 1)
                        for p in range(2):
                            a.pe_values(pe, i, p)

                @block.scalar
                def _(act):
                    act.wait_ge(norm2_ready.sem, norm2_ready.after(1))
                    act.activation(log_scale[:, :], log_scale[:, :], ACT.Exp).then_inc(norm_ready.sem, 1)
                    with act.Fori(0, T // 2) as i:
                        for p in range(2):
                            act.wait_ge(qkv_in.sem, 2 * i + qkv_in.after(p + 1))
                            act.activation(SQ[:, p, :].rearrange("p (m d) -> p m d", m=2), ps[:, 0:2, 0:HW],
                                           ACT.Square).then_inc(squares_ready.sem, 1)
                            act.wait_ge(norm2_ready.sem, 2 * i + norm2_ready.after(p + 2))
                            act.activation(norm[:, p, :, :], norm[:, p, :, :], ACT.Sqrt).then_inc(norm_ready.sem, 1)
                            act.wait_ge(qn_turned.sem, 2 * i + qn_turned.after(p + 1))
                            act.copy(QT[:, p, :, :], ps[:, 0:2, 0:HW]).then_inc(qt_ready.sem, 1)
                            a.act_extract(act, i, p)
                        for p in range(2):
                            a.act_exp(act, i, p)
                        for p in range(2):
                            a.act_out(act, i, p)

                @block.vector
                def _(dve):
                    a.zero(dve)
                    dve.tensor_scalar(log_scale[:, :], log_scale[:, :], float(np.log(1.0 / 0.01)), None,
                                      ALU.min).then_inc(norm2_ready.sem, 1)
                    dve.wait_ge(norm_ready.sem, norm_ready.after(1))
                    with dve.Fori(0, T // 2) as i:
                        k.dve.start(i, 2 * (3 + 1 + 3))
                        for p in range(2):
                            dve.wait_ge(squares_ready.sem, 2 * i + squares_ready.after(p + 1))
                            nm = norm[:, p, :, :].rearrange("p m h -> p (m h)")
                            dve.tensor_reduce(nm, SQ[:, p, :].rearrange("p (h d) -> p h d", d=HP), AX.X,
                                              ALU.add).then_inc(norm2_ready.sem, 1)
                            dve.wait_ge(norm_ready.sem, 2 * i + norm_ready.after(p + 2))
                            k.dve(dve, dve.tensor_scalar(nm, nm, 1e-12, None, ALU.max))
                            k.dve(dve, dve.reciprocal(nm, nm))
                            k.dve(dve, dve.tensor_tensor(norm[:, p, 0, :], norm[:, p, 0, :], log_scale[:, :], ALU.mult))
                            as4 = lambda x: x.rearrange("p m (h d) -> p m h d", d=HP)
                            dve.tensor_tensor(as4(QN[:, p, :, :]), as4(ps[:, 0:2, 0:HW]),
                                              norm[:, p, :, :].unsqueeze(3).broadcast_to([P, 2, HEADS, HP]), ALU.mult)
                            dve.wait_ge(a.pv_done.sem, 2 * i + a.pv_done.room(p + 1))
                            as3 = lambda x: x.rearrange("p (h d) -> p h d", d=HP)
                            dve.tensor_tensor(as3(a.V[:, p, :]), as3(ps[:, 2, 0:HW]),
                                              head_scale[:, :].unsqueeze(2).broadcast_to([P, HEADS, HP]), ALU.mult).then_inc(qn_ready.sem, 1)
                            a.dve_extract(dve, i, p)
                            a.dve_shift(dve, i, p)
                        for p in range(2):
                            a.dve_probs(dve, i, p)
                    k.dve.end(T // 2)
            a.finished(staged=False)
            for s in (xt_staged, qkv_in, squares_ready, qn_ready, qn_turned, qt_ready):
                s.passed(T)
            norm2_ready.passed(T + 1)
            norm_ready.passed(T + 1)
        project_tiles(k, mem, OT, wo, bo)


def project_tiles(k, mem, OT, wo, bo):
    nc, ps = k.nc, k.ps
    tile = k.buffer(mem, "ot_tile", [P, 2, 3, P])
    ot_staged = k.count("ot_staged")
    out_ready = k.count("tile_projected", 2)
    out_added = k.count("tile_added", 2)
    with nc.Block() as block:
        @block.gpsimd
        def _(pool):
            with pool.Fori(0, T // 2) as i:
                for p in range(2):
                    pool.wait_ge(out_ready.sem, 2 * i + out_ready.room(p + 1))
                    pool.tensor_copy(tile[:, p, :, :], OT[:, :, bass.ds((2 * i + p) * P, P)]).then_inc(ot_staged.sem, 1)

        @block.tensor
        def _(pe):
            with pe.Fori(0, T // 2) as i:
                for p in range(2):
                    pe.wait_ge(ot_staged.sem, 2 * i + ot_staged.after(p + 1))
                    pe.wait_ge(out_added.sem, 2 * i + out_added.room(p + 1))
                    pe.matmul(ps[:, p, 0:D], k.ones[0:1, :], bo[0:1, :], start=True, stop=False)
                    for g in range(3):
                        last = pe.matmul(ps[:, p, 0:D], tile[:, p, g, :], wo[:, g, :], start=False, stop=(g == 2))
                    last.then_inc(out_ready.sem, 1)

        @block.vector
        def _(dve):
            with dve.Fori(0, T // 2) as i:
                for p in range(2):
                    h = k.H[:, bass.ds(2 * i + p, 1), :]
                    dve.wait_ge(out_ready.sem, 2 * i + out_ready.after(p + 1))
                    dve.tensor_tensor(h, h, ps[:, p, 0:D], ALU.add).then_inc(out_added.sem, 1)
    for s in (ot_staged, out_ready, out_added):
        s.passed(T)


def temporal_tokens(k):
    nc, ps = k.nc, k.ps
    FR, B, N = 16, 4, 64
    SPAN = FR * B * N
    with ExitStack() as mem:
        sb = lambda name, shape: mem.enter_context(nc.sbuf_tensor(f"tok_{name}", shape, F32))
        xf = sb("x", [C + 1, NC, SPAN])
        wd, wu, bu = sb("down", [C + 1, NC, C]), sb("up", [C, D]), sb("up_bias", [P, D])
        conv = sb("conv", [C, 5])
        hd, y, sg = sb("down_out", [C, SPAN]), sb("y", [C, B, FR // 2, N]), sb("sigmoid", [C, TOK])
        z = sb("z", [P, T, C])
        zs, zt = sb("z_tile", [P, 2, C]), sb("z_tile_t", [C, 2, P])
        scratch = k.dram["scratch"]
        loaded = k.count("weights_loaded")
        chunk_loaded = [k.count(f"x_chunk_loaded{n}") for n in range(4)]
        down_in = k.count("down_in")
        down_ready = k.count("down_ready", 4)
        conv_ready = k.count("conv_ready")
        sigmoid_ready = k.count("sigmoid_ready")
        z_ready = k.count("z_ready")
        z_stored = k.count("z_stored")
        z_loaded = k.count("z_loaded")
        NB = SPAN // BANK
        with nc.Block() as block:
            @block.sync
            def _(sp):
                for dst, name in ((wd[:, :, :], "tok_down"), (conv[:, :], "tok_conv"), (wu[:, :], "tok_up"), (bu[:, :], "tok_up_bias")):
                    sp.dma_start(dst, k.dram[name]).then_inc(loaded.sem, 16)
                q = SPAN // 4
                for n in range(4):
                    sp.dma_start(xf[:, :, n * q:(n + 1) * q], k.dram["tok_x"][:, :, n * q:(n + 1) * q]).then_inc(chunk_loaded[n].sem, 16)
                sp.wait_ge(z_ready.sem, z_ready.after(1))
                sp.dma_start(scratch.rearrange("(p n) -> p n", p=C), sg[:, :]).then_inc(z_stored.sem, 16)
                sp.wait_ge(z_stored.sem, z_stored.after(16))
                sp.dma_start(z[:, :, :], scratch.rearrange("(t p f) -> p t f", p=P, f=C)).then_inc(z_loaded.sem, 16)
                sp.wait_ge(z_loaded.sem, z_loaded.after(16))

            @block.tensor
            def _(pe):
                pe.wait_ge(loaded.sem, loaded.after(64))
                for n in range(4):
                    pe.wait_ge(chunk_loaded[n].sem, chunk_loaded[n].after(16))
                    for b in range(NB // 4 * n, NB // 4 * (n + 1)):
                        pe.wait_ge(down_ready.sem, down_ready.room(b + 1))
                        for c in range(NC):
                            r = C + 1 - c
                            last = pe.matmul(ps[0:C, b % 4, :], wd[0:r, c, :], xf[0:r, c, b * BANK:(b + 1) * BANK],
                                             start=(c == 0), stop=(c == NC - 1))
                        last.then_inc(down_in.sem, 1)

            @block.scalar
            def _(act):
                for b in range(NB):
                    act.wait_ge(down_in.sem, down_in.after(b + 1))
                    act.copy(hd[:, b * BANK:(b + 1) * BANK], ps[0:C, b % 4, :]).then_inc(down_ready.sem, 1)
                act.wait_ge(conv_ready.sem, conv_ready.after(1))
                act.activation(sg[:, :], y[:, :, :, :], ACT.Sigmoid, scale=1.702).then_inc(sigmoid_ready.sem, 1)

            @block.vector
            def _(dve):
                link = lambda ins: k.dve(dve, ins)
                k.dve.start()
                dve.wait_ge(down_ready.sem, down_ready.after(NB))
                frames = hd[:, :].rearrange("p (n b t) -> p b t n", n=N, b=B)
                for b in range(B):
                    link(dve.tensor_scalar(y[:, b, :, :], frames[:, b, 0:FR:2, :], conv[:, 1:2], conv[:, 4:5], ALU.mult, ALU.add))
                    link(dve.scalar_tensor_tensor(y[:, b, :, :], frames[:, b, 1:FR:2, :], conv[:, 2:3], y[:, b, :, :], ALU.mult, ALU.add))
                    link(dve.scalar_tensor_tensor(y[:, b, 1:, :], frames[:, b, 1:FR - 2:2, :], conv[:, 0:1], y[:, b, 1:, :], ALU.mult, ALU.add))
                    link(dve.scalar_tensor_tensor(y[:, b, :-1, :], frames[:, b, 2:FR:2, :], conv[:, 3:4], y[:, b, :-1, :], ALU.mult, ALU.add))
                dve.sem_inc(conv_ready.sem, 1)
                dve.wait_ge(sigmoid_ready.sem, sigmoid_ready.after(1))
                dve.tensor_tensor(sg[:, :], sg[:, :], y[:, :, :, :].rearrange("p b f n -> p (b f n)"), ALU.mult).then_inc(z_ready.sem, 1)
                k.dve.end()
        loaded.passed(64)
        for s in chunk_loaded + [z_stored, z_loaded]:
            s.passed(16)
        for s in (conv_ready, sigmoid_ready, z_ready):
            s.passed(1)
        down_in.passed(NB)
        down_ready.passed(NB)

        z_staged = k.count("z_staged")
        z_turned = k.count("z_turned", 2)
        zt_ready = k.count("zt_ready", 2)
        up_in = k.count("up_in", 2)
        up_added = k.count("up_added", 2)
        with nc.Block() as block:
            @block.gpsimd
            def _(pool):
                with pool.Fori(0, T // 2) as i:
                    for p in range(2):
                        pool.wait_ge(z_turned.sem, 2 * i + z_turned.room(p + 1))
                        pool.tensor_copy(zs[:, p, :], z[:, bass.ds(2 * i + p, 1), :]).then_inc(z_staged.sem, 1)

            @block.tensor
            def _(pe):
                with pe.Fori(0, T // 2) as i:
                    for p in range(2):
                        pe.wait_ge(z_staged.sem, 2 * i + z_staged.after(p + 1))
                        pe.wait_ge(zt_ready.sem, 2 * i + zt_ready.room(p + 1))
                        pe.transpose(ps[0:C, p, 0:P], zs[:, p, :], k.ident[:, :]).then_inc(z_turned.sem, 1)
                    for p in range(2):
                        pe.wait_ge(zt_ready.sem, 2 * i + zt_ready.after(p + 1))
                        pe.wait_ge(up_added.sem, 2 * i + up_added.room(p + 1))
                        pe.matmul(ps[:, 2 + p, 0:D], zt[:, p, :], wu[:, :], start=True, stop=True).then_inc(up_in.sem, 1)

            @block.scalar
            def _(act):
                with act.Fori(0, T // 2) as i:
                    for p in range(2):
                        act.wait_ge(z_turned.sem, 2 * i + z_turned.after(p + 1))
                        act.wait_ge(up_in.sem, 2 * i + up_in.room(p + 1))
                        act.copy(zt[:, p, :], ps[0:C, p, 0:P]).then_inc(zt_ready.sem, 1)

            @block.vector
            def _(dve):
                with dve.Fori(0, T // 2) as i:
                    for p in range(2):
                        dve.wait_ge(up_in.sem, 2 * i + up_in.after(p + 1))
                        dve.tensor_tensor(k.H[:, bass.ds(2 * i + p, 1), :], ps[:, 2 + p, 0:D], bu[:, :], ALU.add).then_inc(up_added.sem, 1)
        for s in (z_staged, z_turned, zt_ready, up_in, up_added):
            s.passed(T)


QH, QS, QD = 8, 64, 32
KE = 3


def complex_memory(k):
    nc = k.nc
    with ExitStack() as mem:
        sb = lambda name, shape: mem.enter_context(nc.sbuf_tensor(f"a2_{name}", shape, F32))
        H1 = sb("h1", [P, T, D])
        p_tok = sb("p_tok", [P, T])
        with ExitStack() as inner:
            memory_read(k, inner, H1, p_tok)
        H2 = sb("h2", [P, T, D])
        with ExitStack() as inner:
            reasoning(k, inner, H1, H2, p_tok)
        with ExitStack() as inner:
            routed_experts(k, inner, H2)


def memory_read(k, mem, H1, p_tok):
    nc, ps = k.nc, k.ps
    sb = lambda name, shape: mem.enter_context(nc.sbuf_tensor(f"a2_{name}", shape, F32))
    NG = QH // 2
    wpz = sb("wpz", [C + 1, NC, QH * 16])
    wri = sb("wri", [C + 1, NC, NG, P])
    pw2, pb2 = sb("pw2", [P, QH, 16]), sb("pb2", [P, QH])
    m1, m2 = sb("m1", [P, NG, 2, 64]), sb("m2", [P, NG, 2, 64])
    vt, wout, wgate = sb("vt", [C, NC, 4, P]), sb("wout", [C, NC, D]), sb("wgate", [C, NC, 4, 16])
    ob, gb, pair = sb("ob", [1, D]), sb("gb", [1, QH]), sb("pair", [P, 2])
    xt, PZ = sb("xt", [C + 1, NC, TOK]), sb("pz", [P, T, QH, 16])
    load(k, [(wpz[:, :, :], "a2_wpz"), (wri[:, :, :, :], "a2_wri"), (pw2[:, :, :], "a2_pw2"), (pb2[:, :], "a2_pb2"),
             (m1[:, :, :, :], "a2_m1"), (m2[:, :, :, :], "a2_m2"), (vt[:, :, :, :], "a2_vt"), (wout[:, :, :], "a2_wout"),
             (wgate[:, :, :, :], "a2_wgate"), (ob[:, :], "a2_ob"), (gb[:, :], "a2_gb"), (pair[:, :], "a2_pair")])
    front(k, [(wpz, PZ[:, :, :, :].rearrange("p t h c -> p t (h c)"))], xt_big=xt, xn_big=H1)

    one_minus_p, p_share = sb("one_minus_p", [P, T, QH]), sb("p_share", [P, T, QH])
    mnorm, msq = sb("mnorm", [P, NG]), sb("msq", [P, NG, 64])
    MRI = sb("mri", [P, NG, P])
    VO, VG = sb("vo", [P, 4, D]), sb("vg", [P, 4, QH])
    silu_ready = k.count("silu_ready")
    p_in = k.count("p_in")
    p_ready = k.count("p_ready")
    slots_squared = k.count("slots_squared")
    norm2_ready = k.count("norm2_ready")
    norm_ready = k.count("norm_ready")
    slots_ready = k.count("slots_ready")
    slots_turned = k.count("slots_turned")
    folded = k.count("folded")
    with nc.Block() as block:
        @block.scalar
        def _(act):
            act.activation(PZ[:, :, :, :], PZ[:, :, :, :], ACT.Silu).then_inc(silu_ready.sem, 1)
            act.activation(msq[:, :, :], m1[:, :, 0, :], ACT.Square).then_inc(slots_squared.sem, 1)
            act.wait_ge(p_in.sem, p_in.after(1))
            act.activation(p_share[:, :, :], p_share[:, :, :], ACT.Sigmoid).then_inc(p_ready.sem, 1)
            act.wait_ge(norm2_ready.sem, norm2_ready.after(1))
            act.activation(mnorm[:, :], mnorm[:, :], ACT.Sqrt).then_inc(norm_ready.sem, 1)
            act.wait_ge(folded.sem, folded.after(1))
            for n in range(4):
                act.copy(VO[:, n, :], ps[:, 2 + n // 2, (n % 2) * D:(n % 2 + 1) * D])
            gates = ps[:, 4, 0:64].rearrange("p (n j g) -> p n j g", n=4, j=2)
            for j in range(2):
                act.copy(VG[64 * j:64 * j + 64, :, :], gates[64 * j:64 * j + 64, :, j, :])

        @block.vector
        def _(dve):
            link = lambda ins: k.dve(dve, ins)
            k.dve.start()
            dve.wait_ge(silu_ready.sem, silu_ready.after(1))
            link(dve.tensor_tensor(PZ[:, :, :, :], PZ[:, :, :, :], pw2[:, :, :].unsqueeze(1).broadcast_to([P, T, QH, 16]), ALU.mult))
            link(dve.tensor_reduce(p_share[:, :, :], PZ[:, :, :, :], AX.X, ALU.add))
            dve.tensor_tensor(p_share[:, :, :], p_share[:, :, :], pb2[:, :].unsqueeze(1).broadcast_to([P, T, QH]), ALU.add).then_inc(p_in.sem, 1)
            dve.wait_ge(slots_squared.sem, slots_squared.after(1))
            dve.tensor_reduce(mnorm[:, :], msq[:, :, :], AX.X, ALU.add).then_inc(norm2_ready.sem, 1)
            dve.wait_ge(p_ready.sem, p_ready.after(1))
            link(dve.tensor_scalar(p_share[:, :, :], p_share[:, :, :], 0.95, None, ALU.mult))
            link(dve.tensor_scalar(one_minus_p[:, :, :], p_share[:, :, :], -1.0, 1.0, ALU.mult, ALU.add))
            link(dve.tensor_reduce(p_tok[:, :], p_share[:, :, :], AX.X, ALU.add))
            link(dve.tensor_scalar(p_tok[:, :], p_tok[:, :], 1.0 / QH, None, ALU.mult))
            link(dve.tensor_scalar(p_share[:, :, :], p_share[:, :, :], 1.0 / QD, None, ALU.mult))
            dve.wait_ge(norm_ready.sem, norm_ready.after(1))
            link(dve.tensor_scalar(mnorm[:, :], mnorm[:, :], 1e-12, None, ALU.max))
            link(dve.reciprocal(mnorm[:, :], mnorm[:, :]))
            for m in (m1, m2):
                flat = m[:, :, :, :].rearrange("p g a d -> p g (a d)")
                link(dve.tensor_tensor(flat, flat, mnorm[:, :].unsqueeze(2).broadcast_to([P, NG, P]), ALU.mult))
            neg = m2[:, :, :, 0:QD]
            dve.tensor_scalar(neg, neg, -1.0, None, ALU.mult).then_inc(slots_ready.sem, 1)
            dve.wait_ge(slots_turned.sem, slots_turned.after(1))
            for n in range(2):
                for j in range(2):
                    rows = slice(64 * j, 64 * j + 64)
                    src = ps[rows, n, :].rearrange("p (g s) -> p g s", g=NG)[:, :, rows]
                    dve.tensor_copy(MRI[rows, :, 64 * n:64 * n + 64], src)
            k.dve.end()

        @block.tensor
        def _(pe):
            for n in range(4):
                for c in range(NC):
                    pe.matmul(ps[:, 2 + n // 2, (n % 2) * D:(n % 2 + 1) * D], vt[:, c, n, :], wout[:, c, :], start=(c == 0), stop=(c == NC - 1))
                for c in range(NC):
                    last = pe.matmul(ps[:, 4, 16 * n:16 * n + 16], vt[:, c, n, :], wgate[:, c, n, :], start=(c == 0), stop=(c == NC - 1))
            last.then_inc(folded.sem, 1)
            pe.wait_ge(slots_ready.sem, slots_ready.after(1))
            for n, m in enumerate((m1, m2)):
                for g in range(NG):
                    last = pe.transpose(ps[:, n, g * P:(g + 1) * P], m[:, g, :, :].rearrange("p a d -> p (a d)"), k.ident[:, :])
            last.then_inc(slots_turned.sem, 1)
    for s in (silu_ready, p_in, p_ready, slots_squared, norm2_ready, norm_ready, slots_ready, slots_turned, folded):
        s.passed(1)

    PP, SQ = sb("pp", [P, 2, NG, P]), sb("pp_squares", [P, 2, NG, P])
    OV = sb("overlap", [P, 2, QH, 2, QS])
    AT, ATT = sb("attn", [P, 2, QH, QS]), sb("attn_t", [P, 2, 4, P])
    al, rs, gt = sb("alpha", [P, 2, QH]), sb("row_sum", [P, 2, QH]), sb("gates", [P, 2, QH])
    st = sb("gate_stat", [P, 2])
    proj_in = k.count("proj_in")
    proj_ready = k.count("proj_ready")
    overlap_in = k.count("overlap_in")
    overlap_ready = k.count("overlap_ready")
    attn_ready = k.count("attn_ready")
    attn_turned = k.count("attn_turned")
    attn_t_ready = k.count("attn_t_ready")
    logits_in = k.count("logits_in")
    logits_shifted = k.count("logits_shifted")
    gates_exped = k.count("gates_exped")
    mix_in = k.count("mix_in")
    mix_added = k.count("mix_added", 2)
    with nc.Block() as block:
        @block.tensor
        def _(pe):
            with pe.Fori(0, T // 2) as i:
                def turn(p, which):
                    pe.wait_ge(attn_ready.sem, 4 * i + attn_ready.after(2 * which + p + 1))
                    flat = AT[:, p, :, :].rearrange("p h s -> p (h s)")
                    for n in range(4):
                        last = pe.transpose(ps[:, p, n * P:(n + 1) * P], flat[:, n * P:(n + 1) * P], k.ident[:, :])
                    last.then_inc(attn_turned.sem, 1)

                for p in range(2):
                    for g in range(NG):
                        for c in range(NC):
                            last = pe.matmul(ps[:, p, g * P:(g + 1) * P], wri[0:C, c, g, :], xt[0:C, c, bass.ds((2 * i + p) * P, P)],
                                             start=(c == 0), stop=(c == NC - 1))
                    last.then_inc(proj_in.sem, 1)
                for p in range(2):
                    pe.wait_ge(proj_ready.sem, 2 * i + proj_ready.after(p + 1))
                    pe.wait_ge(mix_added.sem, 2 * i + mix_added.room(p + 1))
                    for g in range(NG):
                        for j in range(2):
                            rows = slice(64 * j, 64 * j + 64)
                            pe.matmul(ps[:, 2 + 2 * p + j, g * P:(g + 1) * P], PP[rows, p, g, :], MRI[rows, g, :], start=True, stop=True)
                    for g in range(NG):
                        last = pe.matmul(ps[:, 6 + p, 2 * g:2 * g + 2], SQ[:, p, g, :], pair[:, :], start=True, stop=True)
                    last.then_inc(overlap_in.sem, 1)
                for p in range(2):
                    turn(p, 0)
                for p in range(2):
                    pe.wait_ge(attn_t_ready.sem, 4 * i + attn_t_ready.after(p + 1))
                    pe.matmul(ps[:, 6 + p, 8:16], k.ones[0:1, :], gb[0:1, :], start=True, stop=False)
                    for n in range(4):
                        last = pe.matmul(ps[:, 6 + p, 8:16], ATT[:, p, n, :], VG[:, n, :], start=False, stop=(n == 3))
                    last.then_inc(logits_in.sem, 1)
                for p in range(2):
                    turn(p, 1)
                for p in range(2):
                    pe.wait_ge(attn_t_ready.sem, 4 * i + attn_t_ready.after(2 + p + 1))
                    pe.matmul(ps[:, 6 + p, 16:16 + D], k.ones[0:1, :], ob[0:1, :], start=True, stop=False)
                    for n in range(4):
                        last = pe.matmul(ps[:, 6 + p, 16:16 + D], ATT[:, p, n, :], VO[:, n, :], start=False, stop=(n == 3))
                    last.then_inc(mix_in.sem, 1)

        @block.scalar
        def _(act):
            with act.Fori(0, T // 2) as i:
                def turned(p, which):
                    act.wait_ge(attn_turned.sem, 4 * i + attn_turned.after(2 * which + p + 1))
                    act.copy(ATT[:, p, :, :], ps[:, p, :]).then_inc(attn_t_ready.sem, 1)

                for p in range(2):
                    act.wait_ge(proj_in.sem, 2 * i + proj_in.after(p + 1))
                    act.copy(PP[:, p, :, :], ps[:, p, :])
                    act.activation(SQ[:, p, :, :], ps[:, p, :], ACT.Square).then_inc(proj_ready.sem, 1)
                for p in range(2):
                    act.wait_ge(overlap_in.sem, 2 * i + overlap_in.after(p + 1))
                    act.activation(OV[:, p, :, :, :].rearrange("p (j g) a s -> p j (g a s)", j=2), ps[:, 2 + 2 * p:4 + 2 * p, :],
                                   ACT.Square).then_inc(overlap_ready.sem, 1)
                for p in range(2):
                    turned(p, 0)
                for p in range(2):
                    act.wait_ge(logits_shifted.sem, 2 * i + logits_shifted.after(p + 1))
                    act.activation(gt[:, p, :], gt[:, p, :], ACT.Exp).then_inc(gates_exped.sem, 1)
                for p in range(2):
                    turned(p, 1)

        @block.vector
        def _(dve):
            link = lambda ins: k.dve(dve, ins)
            with dve.Fori(0, T // 2) as i:
                k.dve.start(i, 2 * (3 + 6 + 1 + 3))
                tile = lambda X, p: X[:, bass.ds(2 * i + p, 1), :].rearrange("p t h -> p (t h)")
                wide = lambda x: x.unsqueeze(2).broadcast_to([P, QH, QS])
                for p in range(2):
                    dve.wait_ge(overlap_in.sem, 2 * i + overlap_in.after(p + 1))
                    a, at = al[:, p, :], AT[:, p, :, :]
                    n2 = ps[:, 6 + p, 0:8].rearrange("p (g j) -> p j g", j=2)
                    link(dve.tensor_scalar(a.rearrange("p (j g) -> p j g", j=2), n2, 1e-24, None, ALU.max))
                    link(dve.reciprocal(a, a))
                    link(dve.tensor_tensor(a, a, tile(one_minus_p, p), ALU.mult))
                    dve.wait_ge(overlap_ready.sem, 2 * i + overlap_ready.after(p + 1))
                    link(dve.tensor_tensor(at, OV[:, p, :, 0, :], OV[:, p, :, 1, :], ALU.add))
                    link(dve.tensor_tensor(at, at, wide(a), ALU.mult))
                    link(dve.tensor_tensor(at, at, wide(tile(p_share, p)), ALU.add))
                    r = rs[:, p, :]
                    link(dve.tensor_reduce(r, at, AX.X, ALU.add))
                    link(dve.tensor_scalar(r, r, 1e-8, None, ALU.add))
                    link(dve.reciprocal(r, r))
                    dve.tensor_tensor(at, at, wide(r), ALU.mult).then_inc(attn_ready.sem, 1)
                for p in range(2):
                    dve.wait_ge(logits_in.sem, 2 * i + logits_in.after(p + 1))
                    link(dve.tensor_reduce(st[:, p:p + 1], ps[:, 6 + p, 8:16], AX.X, ALU.max))
                    dve.tensor_scalar(gt[:, p, :], ps[:, 6 + p, 8:16], st[:, p:p + 1], None, ALU.subtract).then_inc(logits_shifted.sem, 1)
                for p in range(2):
                    dve.wait_ge(gates_exped.sem, 2 * i + gates_exped.after(p + 1))
                    link(dve.tensor_reduce(st[:, p:p + 1], gt[:, p, :], AX.X, ALU.add))
                    link(dve.reciprocal(st[:, p:p + 1], st[:, p:p + 1]))
                    link(dve.tensor_scalar(gt[:, p, :], gt[:, p, :], st[:, p:p + 1], None, ALU.mult))
                    at = AT[:, p, :, :]
                    dve.tensor_tensor(at, at, wide(gt[:, p, :]), ALU.mult).then_inc(attn_ready.sem, 1)
                for p in range(2):
                    h = H1[:, bass.ds(2 * i + p, 1), :]
                    dve.wait_ge(mix_in.sem, 2 * i + mix_in.after(p + 1))
                    dve.tensor_tensor(h, h, ps[:, 6 + p, 16:16 + D], ALU.add).then_inc(mix_added.sem, 1)
            k.dve.end(T // 2)
    for s in (proj_in, proj_ready, overlap_in, overlap_ready, logits_in, logits_shifted, gates_exped, mix_in, mix_added):
        s.passed(T)
    for s in (attn_ready, attn_turned, attn_t_ready):
        s.passed(2 * T)


def reasoning(k, mem, H1, H2, p_tok):
    nc, ps = k.nc, k.ps
    sb = lambda name, shape: mem.enter_context(nc.sbuf_tensor(f"a2_{name}", shape, F32))
    wenc, wr, rb = sb("wenc", [C, NC, 64]), sb("wr", [64, D]), sb("rb", [P, D])
    PC, beta = sb("pc", [32, 4, 32]), sb("beta", [P, 1])
    sq, nrm, prod = sb("pc_sq", [32, 4, 32]), sb("pc_norm", [32, 2]), sb("pc_prod", [32, 4, 32])
    g_ = sb("g", [32, 4])
    A4, AB = sb("a4", [32, 4, 2, 32]), sb("ab", [64, P])
    q_tok = sb("q_tok", [P, T])
    load(k, [(wenc[:, :, :], "a2_wenc"), (wr[:, :], "a2_wr"), (rb[:, :], "a2_rb"), (PC[:, :, :], "a2_pc"), (beta[:, :], "a2_beta")])
    sigmoid_ready = k.count("sigmoid_ready")
    norm2_ready, norm_ready = k.count("norm2_ready"), k.count("norm_ready")
    with nc.Block() as block:
        @block.scalar
        def _(act):
            act.activation(beta[:, :], beta[:, :], ACT.Sigmoid).then_inc(sigmoid_ready.sem, 1)
            act.wait_ge(norm2_ready.sem, norm2_ready.after(1))
            act.activation(nrm[:, :], nrm[:, :], ACT.Sqrt).then_inc(norm_ready.sem, 1)

        @block.vector
        def _(dve):
            link = lambda ins: k.dve(dve, ins)
            k.dve.start()
            dve.tensor_scalar(q_tok[:, :], p_tok[:, :], -1.0, 1.0, ALU.mult, ALU.add)
            link(dve.tensor_tensor(sq[:, :, :], PC[:, :, :], PC[:, :, :], ALU.mult))
            dve.tensor_reduce(nrm[:, :], sq[:, :, :].rearrange("p (x a) d -> p x (a d)", x=2), AX.X, ALU.add).then_inc(norm2_ready.sem, 1)
            dve.wait_ge(norm_ready.sem, norm_ready.after(1))
            link(dve.tensor_scalar(nrm[:, :], nrm[:, :], 1e-12, None, ALU.max))
            link(dve.reciprocal(nrm[:, :], nrm[:, :]))
            both = PC[:, :, :].rearrange("p (x a) d -> p x (a d)", x=2)
            link(dve.tensor_tensor(both, both, nrm[:, :].unsqueeze(2).broadcast_to([32, 2, 64]), ALU.mult))
            Pr, Pi, Cr, Ci = (PC[:, n, :] for n in range(4))
            for n, (a, b) in enumerate(((Pr, Cr), (Pi, Ci), (Pr, Ci), (Pi, Cr))):
                link(dve.tensor_tensor(prod[:, n, :], a, b, ALU.mult))
            link(dve.tensor_reduce(g_[:, :], prod[:, :, :], AX.X, ALU.add))
            link(dve.tensor_tensor(g_[:, 0:1], g_[:, 0:1], g_[:, 1:2], ALU.add))
            link(dve.tensor_tensor(g_[:, 1:2], g_[:, 2:3], g_[:, 3:4], ALU.subtract))
            g_re, g_im = g_[:, 0:1], g_[:, 1:2]
            X, Y = A4[:, 0, 0, :], A4[:, 0, 1, :]
            link(dve.tensor_scalar(prod[:, 0, :], Pi, g_im, None, ALU.mult))
            link(dve.tensor_scalar(prod[:, 1, :], Pr, g_im, None, ALU.mult))
            link(dve.scalar_tensor_tensor(X, Pr, g_re, prod[:, 0, :], ALU.mult, ALU.subtract))
            link(dve.scalar_tensor_tensor(Y, Pi, g_re, prod[:, 1, :], ALU.mult, ALU.add))
            link(dve.tensor_copy(A4[:, 1, 0, :], Y))
            link(dve.tensor_scalar(A4[:, 1, 1, :], X, -1.0, None, ALU.mult))
            link(dve.tensor_copy(A4[:, 2, 0, :], Cr))
            link(dve.tensor_copy(A4[:, 2, 1, :], Ci))
            link(dve.tensor_copy(A4[:, 3, 0, :], Ci))
            link(dve.tensor_scalar(A4[:, 3, 1, :], Cr, -1.0, None, ALU.mult))
            for half in range(2):
                link(dve.transpose(AB[32 * half:32 * half + 32, :].rearrange("p (v s) -> p v s", v=4), A4[:, :, half, :]))
            k.dve.end()
            dve.wait_ge(sigmoid_ready.sem, sigmoid_ready.after(1))
    for s in (sigmoid_ready, norm2_ready, norm_ready):
        s.passed(1)

    Hs, HT = sb("h_tile", [P, 2, D]), sb("h_tile_t", [C, 2, NC, P])
    E, ES = sb("enc", [64, 2, P]), sb("enc_sq", [64, 2, P])
    CP, CT, cs = sb("coupling", [P, 2, 32]), sb("coupling_t", [P, 2, P]), sb("coupling_stat", [P, 2, 8])
    R, F, M, FT = sb("r", [P, 2, P]), sb("feats", [P, 2, P]), sb("feat_products", [P, 2, P]), sb("feats_t", [64, 2, P])
    RE = sb("reason", [P, 2, D])
    h_staged = k.count("h_staged")
    h_turned = k.count("h_turned", 2)
    ht_ready = k.count("ht_ready")
    coupled = k.count("coupled")
    enc_ready = k.count("enc_ready")
    shifted = k.count("coupling_shifted")
    exped = k.count("coupling_exped")
    ct_ready = k.count("coupling_t_ready")
    sums_in = k.count("sums_in")
    r_ready = k.count("r_ready")
    feats_ready = k.count("feats_ready")
    feats_turned = k.count("feats_turned")
    ft_ready = k.count("ft_ready")
    reason_in = k.count("reason_in")
    h2_ready = k.count("h2_ready", 2)
    with nc.Block() as block:
        @block.gpsimd
        def _(pool):
            with pool.Fori(0, T // 2) as i:
                for p in range(2):
                    pool.wait_ge(h2_ready.sem, 2 * i + h2_ready.room(p + 1))
                    pool.tensor_copy(Hs[:, p, :], H1[:, bass.ds(2 * i + p, 1), :]).then_inc(h_staged.sem, 1)

        @block.tensor
        def _(pe):
            with pe.Fori(0, T // 2) as i:
                for p in range(2):
                    pe.wait_ge(h_staged.sem, 2 * i + h_staged.after(p + 1))
                    for c in range(NC):
                        last = pe.transpose(ps[0:C, p, c * P:(c + 1) * P], Hs[:, p, c * C:(c + 1) * C], k.ident[:, :])
                    last.then_inc(h_turned.sem, 1)
                for p in range(2):
                    pe.wait_ge(ht_ready.sem, 2 * i + ht_ready.after(p + 1))
                    for c in range(NC):
                        pe.matmul(ps[:, 2 + p, 0:P], HT[:, p, c, :], HT[:, p, c, :], start=(c == 0), stop=(c == NC - 1))
                    for c in range(NC):
                        last = pe.matmul(ps[0:64, 4 + p, 0:P], wenc[:, c, :], HT[:, p, c, :], start=(c == 0), stop=(c == NC - 1))
                    last.then_inc(coupled.sem, 1)
                for p in range(2):
                    pe.wait_ge(enc_ready.sem, 2 * i + enc_ready.after(p + 1))
                    pe.wait_ge(ct_ready.sem, 2 * i + ct_ready.after(p + 1))
                    pe.matmul(ps[:, 4 + p, P:2 * P], E[:, p, :], AB[:, :], start=True, stop=True)
                    pe.matmul(ps[:, 4 + p, 2 * P:2 * P + 1], ES[:, p, :], k.ones[0:64, 0:1], start=True, stop=True)
                    pe.matmul(ps[:, 4 + p, 2 * P + 1:2 * P + 2], CT[:, p, :], q_tok[:, bass.ds(2 * i + p, 1)],
                              start=True, stop=True).then_inc(sums_in.sem, 1)
                for p in range(2):
                    pe.wait_ge(feats_ready.sem, 2 * i + feats_ready.after(p + 1))
                    pe.transpose(ps[:, 6 + p, 0:P], F[:, p, :], k.ident[:, :]).then_inc(feats_turned.sem, 1)
                for p in range(2):
                    pe.wait_ge(ft_ready.sem, 2 * i + ft_ready.after(p + 1))
                    pe.matmul(ps[:, 6 + p, P:P + D], FT[:, p, :], wr[:, :], start=True, stop=True).then_inc(reason_in.sem, 1)

        @block.scalar
        def _(act):
            with act.Fori(0, T // 2) as i:
                for p in range(2):
                    act.wait_ge(h_turned.sem, 2 * i + h_turned.after(p + 1))
                    act.copy(HT[:, p, :, :], ps[0:C, p, 0:2 * P]).then_inc(ht_ready.sem, 1)
                for p in range(2):
                    act.wait_ge(coupled.sem, 2 * i + coupled.after(p + 1))
                    act.copy(E[:, p, :], ps[0:64, 4 + p, 0:P])
                    act.activation(ES[:, p, :], ps[0:64, 4 + p, 0:P], ACT.Square).then_inc(enc_ready.sem, 1)
                for p in range(2):
                    act.wait_ge(shifted.sem, 2 * i + shifted.after(p + 1))
                    act.activation(CP[:, p, :], CP[:, p, :], ACT.Exp, scale=float(D) ** -0.5).then_inc(exped.sem, 1)
                for p in range(2):
                    act.wait_ge(sums_in.sem, 2 * i + sums_in.after(p + 1))
                    act.copy(R[:, p, :], ps[:, 4 + p, P:2 * P])
                    act.copy(cs[:, p, 4:6], ps[:, 4 + p, 2 * P:2 * P + 2]).then_inc(r_ready.sem, 1)
                for p in range(2):
                    act.wait_ge(feats_turned.sem, 2 * i + feats_turned.after(p + 1))
                    act.copy(FT[:, p, :], ps[0:64, 6 + p, 0:P]).then_inc(ft_ready.sem, 1)

        @block.vector
        def _(dve):
            link = lambda ins: k.dve(dve, ins)
            k.dve.start()
            dve.memset(F[:, :, 64:P], 0.0)
            link(dve.memset(CT[:, :, :], 0.0))
            k.dve.end()
            with dve.Fori(0, T // 2) as i:
                k.dve.start(i, 2 * (2 + 1 + 9 + 2))
                for p in range(2):
                    dve.wait_ge(coupled.sem, 2 * i + coupled.after(p + 1))
                    cp = CP[:, p, :]
                    for b in range(4):
                        rows = slice(32 * b, 32 * b + 32)
                        last = dve.tensor_copy(CP[rows, p, :], ps[rows, 2 + p, rows])
                    link(last)
                    link(dve.tensor_reduce(cs[:, p, 0:1], cp, AX.X, ALU.max))
                    dve.tensor_scalar(cp, cp, cs[:, p, 0:1], None, ALU.subtract).then_inc(shifted.sem, 1)
                for p in range(2):
                    dve.wait_ge(exped.sem, 2 * i + exped.after(p + 1))
                    link(dve.tensor_reduce(cs[:, p, 1:2], CP[:, p, :], AX.X, ALU.add))
                    for b in range(4):
                        rows = slice(32 * b, 32 * b + 32)
                        last = dve.transpose(CT[rows, p, rows], CP[rows, p, :])
                    last.then_inc(ct_ready.sem, 1)
                for p in range(2):
                    dve.wait_ge(r_ready.sem, 2 * i + r_ready.after(p + 1))
                    c_ = lambda n: cs[:, p, n:n + 1]
                    link(dve.reciprocal(c_(1), c_(1)))
                    link(dve.tensor_scalar(c_(2), c_(5), c_(1), beta[:, :], ALU.mult, ALU.mult))
                    link(dve.tensor_scalar(c_(2), c_(2), -1.0, 1.0, ALU.mult, ALU.add))
                    link(dve.tensor_tensor(c_(2), c_(2), p_tok[:, bass.ds(2 * i + p, 1)], ALU.mult))
                    link(dve.tensor_scalar(c_(2), c_(2), 0.0, 0.95, ALU.max, ALU.min))
                    link(dve.tensor_scalar(c_(2), c_(2), -1.0, 1.0, ALU.mult, ALU.add))
                    link(dve.tensor_scalar(c_(3), c_(4), 1e-24, None, ALU.max))
                    link(dve.reciprocal(c_(3), c_(3)))
                    t = R[:, p, 0:64].rearrange("p (v s) -> p v s", v=2)
                    by = lambda n: R[:, p, 32 * n:32 * n + 32].unsqueeze(1).broadcast_to([P, 2, 32])
                    mm = lambda n: M[:, p, 64 * n:64 * n + 64].rearrange("p (v s) -> p v s", v=2)
                    dve.tensor_tensor(mm(0), t, by(2), ALU.mult)
                    link(dve.tensor_tensor(mm(1), t, by(3), ALU.mult))
                    dve.tensor_tensor(F[:, p, 0:32], M[:, p, 0:32], M[:, p, 96:128], ALU.add)
                    dve.tensor_tensor(F[:, p, 32:64], M[:, p, 32:64], M[:, p, 64:96], ALU.subtract).then_inc(feats_ready.sem, 1)
                for p in range(2):
                    dve.wait_ge(reason_in.sem, 2 * i + reason_in.after(p + 1))
                    re = RE[:, p, :]
                    link(dve.scalar_tensor_tensor(re, ps[:, 6 + p, P:P + D], cs[:, p, 3:4], rb[:, :], ALU.mult, ALU.add))
                    link(dve.tensor_scalar(re, re, cs[:, p, 2:3], None, ALU.mult))
                    dve.tensor_tensor(H2[:, bass.ds(2 * i + p, 1), :], re, Hs[:, p, :], ALU.add).then_inc(h2_ready.sem, 1)
            k.dve.end(T // 2)
    for s in (h_staged, h_turned, ht_ready, coupled, enc_ready, shifted, exped, ct_ready, sums_in, r_ready, feats_ready,
              feats_turned, ft_ready, reason_in, h2_ready):
        s.passed(T)


def routed_experts(k, mem, H2):
    nc, ps = k.nc, k.ps
    sb = lambda name, shape: mem.enter_context(nc.sbuf_tensor(f"a2_{name}", shape, F32))
    W1 = KE * D
    NR = 16
    cut = 2 * D
    w1a, w1b = sb("w1a", [C + 1, NC, cut]), sb("w1b", [C + 1, NC, D + NR])
    eg, ebt = sb("eg", [P, KE, D]), sb("ebt", [P, KE, D])
    w2, b2 = sb("ew2", [C, 2 * KE, D]), sb("eb2", [KE, D])
    rw2, rb2 = sb("rw2", [P, KE, NR]), sb("rb2", [P, KE])
    X, R = sb("x", [P, T, W1]), sb("router_in", [P, T, D + NR])
    load(k, [(w1a[:, :, :], "a2_w1a"), (w1b[:, :, :], "a2_w1b"), (eg[:, :, :], "a2_eg"), (ebt[:, :, :], "a2_ebt"),
             (w2[:, :, :], "a2_w2"), (b2[:, :], "a2_b2"), (rw2[:, :, :], "a2_rw2"), (rb2[:, :], "a2_rb2")])
    front(k, [(w1a, X[:, :, 0:cut]), (w1b, R[:, :, :])], src=H2)
    Y = sb("y", [P, 4, KE, D])
    stat, rg, rstat = sb("estat", [P, T, KE]), sb("rg", [P, T, KE]), sb("rstat", [P, T])
    prod = sb("rprod", [P, T, KE, NR])
    squared = k.count("x_squared")
    var_ready, std_ready = k.count("var_ready"), k.count("std_ready")
    centred = k.count("x_centred")
    normed = k.count("x_normed")
    gelu_ready = k.count("gelu_ready")
    router_in = k.count("router_ready")
    scores_ready, exps_ready = k.count("scores_ready"), k.count("exps_ready")
    NQ = T // 4
    with nc.Block() as block:
        @block.scalar
        def _(act):
            act.activation(R[:, :, D:D + NR], R[:, :, D:D + NR], ACT.Gelu).then_inc(router_in.sem, 1)
            for n in range(NQ):
                act.wait_ge(centred.sem, centred.after(n + 1))
                act.activation(Y[:, :, :, :], X[:, 4 * n:4 * n + 4, :], ACT.Square).then_inc(squared.sem, 1)
            act.wait_ge(scores_ready.sem, scores_ready.after(1))
            act.activation(rg[:, :, :], rg[:, :, :], ACT.Exp).then_inc(exps_ready.sem, 1)
            act.wait_ge(var_ready.sem, var_ready.after(1))
            act.activation(stat[:, :, :], stat[:, :, :], ACT.Sqrt).then_inc(std_ready.sem, 1)
            for n in range(NQ):
                act.wait_ge(normed.sem, normed.after(n + 1))
                x = X[:, 4 * n:4 * n + 4, :]
                act.activation(x, x, ACT.Gelu).then_inc(gelu_ready.sem, 1)

        @block.vector
        def _(dve):
            link = lambda ins: k.dve(dve, ins)
            k.dve.start()
            link(dve.tensor_copy(X[:, :, cut:W1], R[:, :, 0:D]))
            as4 = lambda n: X[:, 4 * n:4 * n + 4, :].rearrange("p t (e d) -> p (t e) d", e=KE)
            st = lambda n: stat[:, 4 * n:4 * n + 4, :].rearrange("p t e -> p (t e)")
            wide = lambda x: x.unsqueeze(2).broadcast_to([P, 4 * KE, D])
            for n in range(NQ):
                link(dve.tensor_reduce(st(n), as4(n), AX.X, ALU.add))
                link(dve.tensor_scalar(st(n), st(n), 1.0 / D, None, ALU.mult))
                dve.tensor_tensor(as4(n), as4(n), wide(st(n)), ALU.subtract).then_inc(centred.sem, 1)
                dve.wait_ge(squared.sem, squared.after(n + 1))
                link(dve.tensor_reduce(st(n), Y[:, :, :, :].rearrange("p t e d -> p (t e) d"), AX.X, ALU.add))
            dve.wait_ge(router_in.sem, router_in.after(1))
            full = [P, T, KE, NR]
            link(dve.tensor_tensor(prod[:, :, :, :], R[:, :, D:D + NR].unsqueeze(2).broadcast_to(full),
                                   rw2[:, :, :].unsqueeze(1).broadcast_to(full), ALU.mult))
            link(dve.tensor_reduce(rg[:, :, :], prod[:, :, :, :], AX.X, ALU.add))
            link(dve.tensor_tensor(rg[:, :, :], rg[:, :, :], rb2[:, :].unsqueeze(1).broadcast_to([P, T, KE]), ALU.add))
            link(dve.tensor_reduce(rstat[:, :], rg[:, :, :], AX.X, ALU.max))
            rw = rstat[:, :].unsqueeze(2).broadcast_to([P, T, KE])
            dve.tensor_tensor(rg[:, :, :], rg[:, :, :], rw, ALU.subtract).then_inc(scores_ready.sem, 1)
            dve.tensor_scalar(stat[:, :, :], stat[:, :, :], 1.0 / D, EPS, ALU.mult, ALU.add).then_inc(var_ready.sem, 1)
            dve.wait_ge(exps_ready.sem, exps_ready.after(1))
            link(dve.tensor_reduce(rstat[:, :], rg[:, :, :], AX.X, ALU.add))
            link(dve.reciprocal(rstat[:, :], rstat[:, :]))
            link(dve.tensor_tensor(rg[:, :, :], rg[:, :, :], rw, ALU.mult))
            dve.wait_ge(std_ready.sem, std_ready.after(1))
            link(dve.reciprocal(stat[:, :, :], stat[:, :, :]))
            for n in range(NQ):
                x4 = X[:, 4 * n:4 * n + 4, :]
                link(dve.tensor_tensor(as4(n), as4(n), wide(st(n)), ALU.mult))
                by = lambda w: w[:, :, :].rearrange("p e d -> p (e d)").unsqueeze(1).broadcast_to([P, 4, W1])
                link(dve.tensor_tensor(x4, x4, by(eg), ALU.mult))
                dve.tensor_tensor(x4, x4, by(ebt), ALU.add).then_inc(normed.sem, 1)
            for n in range(NQ):
                dve.wait_ge(gelu_ready.sem, gelu_ready.after(n + 1))
                rgn = rg[:, 4 * n:4 * n + 4, :].rearrange("p t e -> p (t e)")
                dve.tensor_tensor(as4(n), as4(n), wide(rgn), ALU.mult)
            k.dve.end()
    for s in (var_ready, std_ready, router_in, scores_ready, exps_ready):
        s.passed(1)
    for s in (squared, centred, normed, gelu_ready):
        s.passed(NQ)

    G, RG = sb("g_tile", [P, 2, W1]), sb("rg_tile", [P, 2, KE])
    GT, RT = sb("g_tile_t", [C, 2, 2 * KE, P]), sb("rg_tile_t", [KE, 2, P])
    staged = k.count("g_staged")
    turned = k.count("g_turned", 2)
    gt_ready = k.count("gt_ready")
    y_in = k.count("y_in")
    y_added = k.count("y_added", 2)
    with nc.Block() as block:
        @block.gpsimd
        def _(pool):
            with pool.Fori(0, T // 2) as i:
                for p in range(2):
                    pool.wait_ge(turned.sem, 2 * i + turned.room(p + 1))
                    pool.tensor_copy(G[:, p, :], X[:, bass.ds(2 * i + p, 1), :])
                    pool.tensor_copy(RG[:, p, :], rg[:, bass.ds(2 * i + p, 1), :]).then_inc(staged.sem, 1)

        @block.tensor
        def _(pe):
            with pe.Fori(0, T // 2) as i:
                for p in range(2):
                    pe.wait_ge(staged.sem, 2 * i + staged.after(p + 1))
                    for c in range(2 * KE):
                        pe.transpose(ps[0:C, 2 * p + c // 4, (c % 4) * P:(c % 4 + 1) * P], G[:, p, c * C:(c + 1) * C], k.ident[:, :])
                    pe.transpose(ps[0:KE, 2 * p + 1, 3 * P:4 * P], RG[:, p, :], k.ident[:, :]).then_inc(turned.sem, 1)
                for p in range(2):
                    pe.wait_ge(gt_ready.sem, 2 * i + gt_ready.after(p + 1))
                    pe.wait_ge(y_added.sem, 2 * i + y_added.room(p + 1))
                    pe.matmul(ps[:, 4 + p, 0:D], RT[:, p, :], b2[:, :], start=True, stop=False)
                    for c in range(2 * KE):
                        last = pe.matmul(ps[:, 4 + p, 0:D], GT[:, p, c, :], w2[:, c, :], start=False, stop=(c == 2 * KE - 1))
                    last.then_inc(y_in.sem, 1)

        @block.scalar
        def _(act):
            with act.Fori(0, T // 2) as i:
                for p in range(2):
                    act.wait_ge(turned.sem, 2 * i + turned.after(p + 1))
                    act.copy(GT[:, p, 0:4, :], ps[0:C, 2 * p, :])
                    act.copy(GT[:, p, 4:6, :], ps[0:C, 2 * p + 1, 0:2 * P])
                    act.copy(RT[:, p, :], ps[0:KE, 2 * p + 1, 3 * P:4 * P]).then_inc(gt_ready.sem, 1)

        @block.vector
        def _(dve):
            with dve.Fori(0, T // 2) as i:
                k.dve.start(i, 2)
                for p in range(2):
                    h = k.H[:, bass.ds(2 * i + p, 1), :]
                    k.dve(dve, dve.tensor_tensor(h, h, H2[:, bass.ds(2 * i + p, 1), :], ALU.add))
                    dve.wait_ge(y_in.sem, 2 * i + y_in.after(p + 1))
                    dve.tensor_tensor(h, h, ps[:, 4 + p, 0:D], ALU.add).then_inc(y_added.sem, 1)
            k.dve.end(T // 2)
    for s in (staged, turned, gt_ready, y_in, y_added):
        s.passed(T)


def finish(k, out):
    stored = k.count("output_stored")
    with k.nc.Block() as block:
        @block.sync
        def _(sp):
            sp.dma_start(out, k.H[:, :, :]).then_inc(stored.sem, 16)
            sp.wait_ge(stored.sem, stored.after(16))


def build(nc, dram, out):
    with ExitStack() as ctx:
        k = Core(nc, ctx, dram)
        k.all_primed = [k.count(n, c) for n, c in PRIMED.items()]
        begin(k)
        temporal_tokens(k)
        cosine_attention(k)
        moe(k, "f0", 8, 768, "argmax", 1, ACT.Gelu, bias2=True)
        rotary_attention(k)
        causal_mixture(k)
        complex_memory(k)
        moe(k, "f2", 8, 512, "balanced", 2, ACT.Silu)
        transport_attention(k)
        moe(k, "f3", 5, 256, "top", 2, ACT.Silu, gated=True)
        finish(k, out)


def by_chunk(w, bias=None):
    n = w.shape[1]
    a = np.zeros((C + 1, NC, n), np.float32)
    a[:C] = w.reshape(NC, C, n).transpose(1, 0, 2)
    if bias is not None:
        a[C, 0] = bias
    return a


def rows(a):
    a = np.asarray(a)
    return np.ascontiguousarray(np.broadcast_to(a[None], (P,) + a.shape))


def pad_heads(w):
    a = np.zeros(w.shape[:-1] + (HEADS, HP), np.float32)
    a[..., :16] = w.reshape(w.shape[:-1] + (HEADS, 16))
    return a.reshape(w.shape[:-1] + (HW,))


def expert_rows(w):
    E, F, _ = w.shape
    return w.reshape(E, F // P, P, D).transpose(2, 0, 1, 3)


def expert_chunks(w, bias=None):
    return np.stack([by_chunk(w[e], None if bias is None else bias[e]) for e in range(w.shape[0])], 1)


def head_rows(w):
    n = w.shape[1]
    return pad_heads(w.T).T.reshape(3, P, n).transpose(1, 0, 2)


def layouts(i):
    a = {"identity": np.eye(P, dtype=np.float32)}
    for E in (3, 5, 8):
        a[f"lower{E}"] = rows(np.tril(np.ones((E, E), np.float32), -1).reshape(E * E))
    a["f0_router"] = by_chunk(i["L0_ffn_gate_w"], i["L0_ffn_gate_b"])
    a["f0_w1"] = expert_chunks(i["L0_ffn_w1"], i["L0_ffn_b1"])
    a["f0_w2"] = expert_rows(i["L0_ffn_w2"])
    a["f0_b2"] = rows(i["L0_ffn_b2"])
    a["f2_router"] = by_chunk(i["L2_ffn_router_w"].T)
    a["f2_w1"] = expert_chunks(i["L2_ffn_w1"].transpose(0, 2, 1))
    a["f2_w2"] = expert_rows(i["L2_ffn_w2"].transpose(0, 2, 1))
    a["f3_router"] = by_chunk(i["L3_ffn_router_w"].T, i["L3_ffn_router_b"])
    a["f3_w1"] = expert_chunks(i["L3_ffn_gate_w"])
    a["f3_up"] = expert_chunks(i["L3_ffn_up_w"])
    a["f3_w2"] = expert_rows(i["L3_ffn_down_w"])
    w, b = i["L1_attn_qkv_w"].T, i["L1_attn_qkv_b"]
    swap = np.arange(D) ^ 1
    parts = [(0, slice(None)), (0, swap), (1, slice(None)), (1, swap)]
    a["a1_wqk"] = np.stack([by_chunk(pad_heads(w[:, m * D:(m + 1) * D][:, s]), pad_heads(b[m * D:(m + 1) * D][s])) for m, s in parts], 2)
    a["a1_wv"] = by_chunk(pad_heads(w[:, 2 * D:]), pad_heads(b[2 * D:]))
    a["a1_wo"] = head_rows(i["L1_attn_proj_w"].T)
    a["a1_bo"] = i["L1_attn_proj_b"][None]
    freq = (1.0 / np.float32(10000.0) ** (np.arange(0, 16, 2, dtype=np.float32) / 16)).astype(np.float32)
    angle = freq[:, None] * np.arange(32, dtype=np.float32)[None]
    cos, sin = np.zeros((4, 32, 32), np.float32), np.zeros((4, 32, 32), np.float32)
    cos[:, 0:16:2] = cos[:, 1:16:2] = np.cos(angle)
    sin[:, 0:16:2], sin[:, 1:16:2] = -np.sin(angle), np.sin(angle)
    a["a1_turn"] = np.stack([cos.reshape(P, 32), sin.reshape(P, 32)], 1)
    a["f1_wqk"] = by_chunk(i["L1_ffn_Wqk"], i["L1_ffn_bqk"])
    wv = i["L1_ffn_Wv"].transpose(1, 0, 2).reshape(D, D)
    a["f1_wvg"] = by_chunk(np.concatenate([wv, i["L1_ffn_Wg1"]], 1), np.concatenate([i["L1_ffn_bv"].reshape(D), i["L1_ffn_bg1"]]))
    a["f1_wo"] = i["L1_ffn_Wp"].reshape(3, 64, D).transpose(1, 0, 2)
    a["f1_bo"] = i["L1_ffn_bp"][None]
    a["f1_conv"] = np.concatenate([i["L1_ffn_conv_w"][:, 0, :], i["L1_ffn_conv_b"][:, None]], 1)
    query = np.arange(P)[:, None] % 32
    key = np.arange(32)[None]
    a["f1_mask"] = np.repeat(np.where(key > query, np.float32(-1e30), np.float32(0))[:, None], 3, 1)
    pos = np.zeros((P, 3, 32), np.float32)
    pos[:, 2] = np.tile(i["L1_ffn_pos_bias"][:32, :32], (4, 1))
    a["f1_pos"] = pos
    a["f1_wg2"] = rows(i["L1_ffn_Wg2"].T)
    a["f1_bg2"] = rows(i["L1_ffn_bg2"])
    order = np.arange(8).reshape(4, 2).T.reshape(8)
    chunk4 = lambda x: x.reshape((NC, C) + x.shape[1:]).swapaxes(0, 1)
    a["a2_wpz"] = by_chunk(i["L2_attn_pw1"][order].reshape(128, D).T, i["L2_attn_pb1"][order].reshape(128))
    ri = np.concatenate([i["L2_attn_W_real"], i["L2_attn_W_imag"]], 2).transpose(1, 0, 2).reshape(D, 512)
    a["a2_wri"] = by_chunk(ri).reshape(C + 1, NC, 4, P)
    a["a2_pw2"], a["a2_pb2"] = rows(i["L2_attn_pw2"][order]), rows(i["L2_attn_pb2"][order])
    for n, parts in (("a2_m1", ("m_real", "m_imag")), ("a2_m2", ("m_imag", "m_real"))):
        mm = np.concatenate([i[f"L2_attn_{x}"] for x in parts], 2)
        mm = mm.reshape(4, 2 * 64, 64).transpose(1, 0, 2)
        a[n] = np.repeat(mm[:, :, None], 2, 2)
    vals = i["L2_attn_values"][order].reshape(512, D).T
    a["a2_vt"] = chunk4(vals.reshape(D, 4, P))
    a["a2_wout"], a["a2_ob"] = chunk4(i["L2_attn_out_w"].T), i["L2_attn_out_b"][None]
    gw = i["L2_attn_gate_w"].reshape(8, 8, D)[order][:, order]
    a["a2_wgate"] = chunk4(gw.transpose(2, 1, 0).reshape(D, 4, 16))
    a["a2_gb"] = i["L2_attn_gate_b"][order][None]
    a["a2_pair"] = (np.arange(P)[:, None] // 64 == np.arange(2)[None]).astype(np.float32)
    a["a2_wenc"] = chunk4(np.concatenate([i["L2_attn_enc_r_w"], i["L2_attn_enc_i_w"]], 0).T)
    a["a2_wr"], a["a2_rb"] = i["L2_attn_r_out_w"].T, rows(i["L2_attn_r_out_b"])
    a["a2_pc"] = np.stack([i[f"L2_attn_{x}"] for x in ("P_real", "P_imag", "C_real", "C_imag")], 1)
    a["a2_beta"] = np.broadcast_to(i["L2_attn_beta"].reshape(1, 1), (P, 1))
    w1 = i["L2_attn_ew1"].transpose(2, 0, 1).reshape(D, 3 * D)
    b1 = i["L2_attn_eb1"].reshape(3 * D)
    a["a2_w1a"] = by_chunk(w1[:, :2 * D], b1[:2 * D])
    a["a2_w1b"] = by_chunk(np.concatenate([w1[:, 2 * D:], i["L2_attn_rw1"].T], 1), np.concatenate([b1[2 * D:], i["L2_attn_rb1"]]))
    a["a2_eg"], a["a2_ebt"] = rows(i["L2_attn_eg"]), rows(i["L2_attn_ebt"])
    a["a2_w2"] = i["L2_attn_ew2"].transpose(0, 2, 1).reshape(6, C, D).transpose(1, 0, 2)
    a["a2_b2"] = i["L2_attn_eb2"]
    a["a2_rw2"], a["a2_rb2"] = rows(i["L2_attn_rw2"]), rows(i["L2_attn_rb2"])
    a["tok_x"] = by_chunk(i["x"].reshape(4096, D).T)
    a["tok_x"][C, 0] = 1.0
    a["tok_down"] = by_chunk(i["L0_tok_w_down"], i["L0_tok_b_down"])
    a["tok_up"] = i["L0_tok_w_up"]
    a["tok_up_bias"] = rows(i["L0_tok_b_up"])
    a["tok_conv"] = np.concatenate([i["L0_tok_w_conv"][:, 0, :], i["L0_tok_b_conv"][:, None]], 1)
    w, b = i["L0_attn_in_proj_weight"].T, i["L0_attn_in_proj_bias"]
    a["a0_w"] = np.stack([by_chunk(pad_heads(w[:, m * D:(m + 1) * D]), pad_heads(b[m * D:(m + 1) * D])) for m in range(3)], 2)
    a["a0_wo"], a["a0_bo"] = head_rows(i["L0_attn_out_w"].T), i["L0_attn_out_b"][None]
    a["a0_log_scale"] = rows(i["L0_attn_logit_scale"][:, 0, 0])
    a["a0_head_scale"] = rows(i["L0_attn_head_scale"][:, 0, 0])
    w = i["L3_attn_w_qkv"].T
    a["a3_wq"], a["a3_wv"] = by_chunk(pad_heads(w[:, 0:D])), by_chunk(pad_heads(w[:, 2 * D:]))
    a["a3_wo"], a["a3_bo"] = head_rows(i["L3_attn_w_proj"].T), i["L3_attn_b_proj"][None]
    a["eye32"] = (key == query).astype(np.float32)
    a["off32"] = (key != query).astype(np.float32)
    a["blocks32"] = (np.arange(P)[:, None] // 32 == np.arange(P)[None] // 32).astype(np.float32)
    return {n: np.ascontiguousarray(v) for n, v in a.items()}


PRIMED = {"xn_transposed": U, "xt_spread": U, "projection_read": 2, "hidden_ready": 4, "expert_out": 8,
          "expert_added": 4, "gate_ready": 2,
          "scores_out": 2, "probs_ready": 2, "pv_done": 2, "ot_ready": 1, "out_added": 1, "qk_ready": 1,
          "keys_ready": 1, "qn_turned": 2, "qt_ready": 2, "qkv_in": 2, "tile_projected": 2,
          "tile_added": 2, "down_ready": 4, "z_turned": 2, "zt_ready": 2, "up_in": 2, "up_added": 2, "mix_added": 2,
          "h_turned": 2, "h2_ready": 2, "g_turned": 2, "y_added": 2}


def kernel(**inputs):
    from concourse import bacc
    from concourse.bass_utils import run_bass_kernel_spmd

    nc = bacc.Bacc("TRN2", target_bir_lowering=False, num_devices=1)
    arrays = {f"in_{n}": a for n, a in layouts({n: np.asarray(v) for n, v in inputs.items()}).items()}
    dram = {n[3:]: nc.dram_tensor(n, a.shape, F32, kind="ExternalInput").ap() for n, a in arrays.items()}
    dram["scratch"] = nc.dram_tensor("scratch", (C * TOK,), F32, kind="Internal").ap()
    out = nc.dram_tensor("out", (P, T, D), F32, kind="ExternalOutput").ap()
    build(nc, dram, out)
    r = run_bass_kernel_spmd(nc, [arrays], core_ids=[0])
    return np.ascontiguousarray(r.results[0]["out"].transpose(1, 0, 2).reshape(64, 32, D))
```

```python
from contextlib import ExitStack

import numpy as np

import concourse.bass as bass
from concourse import mybir
from concourse.alu_op_type import AluOpType as ALU

F32 = mybir.dt.float32
ACT = mybir.ActivationFunctionType
AX = mybir.AxisListType

P = 128
D = 192
C = 96
NC = D // C
TOK = 2048
T = TOK // P
U = 4
BANK = 512
HEADS = 12
HP = 32
HW = HEADS * HP
EPS = 1e-5


class Count:

    def __init__(self, nc, ctx, name, primed=0):
        self.sem = ctx.enter_context(nc.semaphore(name))
        self.primed, self.base = primed, 0

    def after(self, n):
        return self.base + self.primed + n

    def room(self, n):
        return self.base + n

    def passed(self, n):
        self.base += n


class Chain:

    def __init__(self, nc, ctx, name):
        self.sem = ctx.enter_context(nc.semaphore(name))
        self.base, self.turn, self.per, self.steps = 0, 0, 0, 0

    def start(self, turn=0, per=0):
        self.turn, self.per, self.steps = turn, per, 0

    def __call__(self, eng, ins):
        self.steps += 1
        ins.then_inc(self.sem, 1)
        eng.wait_ge(self.sem, self.turn * self.per + (self.base + self.steps))

    def apart(self, eng, ins):
        self(eng, ins)
        self.steps += 1
        eng.sem_inc(self.sem, 1)

    def end(self, turns=1):
        if turns > 1:
            assert self.steps == self.per, (self.steps, self.per)
        self.base += turns * self.steps


class Core:

    def __init__(self, nc, ctx, dram):
        self.nc, self.ctx, self.dram = nc, ctx, dram
        self.counts = {}
        self.buffers = 0
        self.H = self.keep("residual", [P, T, D])
        self.ident = self.keep("identity", [P, P])
        self.ones = self.keep("ones", [P, P])
        self.ps = ctx.enter_context(nc.psum_tensor("psum", [P, 8, BANK], F32))
        self.dve, self.act, self.pool = (Chain(nc, ctx, f"{e}_step_done") for e in ("vector", "scalar", "gpsimd"))

    def keep(self, name, shape):
        return self.ctx.enter_context(self.nc.sbuf_tensor(name, shape, F32))

    def buffer(self, mem, name, shape):
        self.buffers += 1
        return mem.enter_context(self.nc.sbuf_tensor(f"{name}_{self.buffers}", shape, F32))

    def count(self, name, primed=0):
        if name not in self.counts:
            self.counts[name] = Count(self.nc, self.ctx, name, primed)
        assert self.counts[name].primed == primed
        return self.counts[name]


def bcast(ap, shape):
    return ap.broadcast_to(shape)


def load(k, pairs):
    loaded = k.count("weights_loaded")
    with k.nc.Block() as block:
        @block.sync
        def _(sp):
            for n, (dst, name) in enumerate(pairs):
                sp.dma_start(dst, k.dram[name]).then_inc(loaded.sem, 16)
            sp.wait_ge(loaded.sem, loaded.after(16 * len(pairs)))
    loaded.passed(16 * len(pairs))


def begin(k):
    nc = k.nc
    loaded = k.count("weights_loaded")
    with nc.Block() as block:
        @block.sync
        def _(sp):
            sp.dma_start(k.ident[:, :], k.dram["identity"]).then_inc(loaded.sem, 16)
            for s in k.all_primed:
                sp.sem_inc(s.sem, s.primed)
            sp.wait_ge(loaded.sem, loaded.after(16))

        @block.gpsimd
        def _(pool):
            pool.memset(k.ones[:, :], 1.0)
    loaded.passed(16)


def front(k, outs, xt_big=None, xn_big=None, src=None):
    nc, ps = k.nc, k.ps
    norm = src is None
    xn_ready = k.count("xn_ready")
    var_ready = k.count("var_ready")
    std_ready = k.count("std_ready")
    xn_transposed = k.count("xn_transposed", U)
    xt_ready = k.count("xt_ready")
    xt_spread = k.count("xt_spread", U)
    projected = k.count("projected")
    projection_read = k.count("projection_read", 2)
    with ExitStack() as mem:
        XN = k.buffer(mem, "xn_tiles", [P, U, D])
        XT = k.buffer(mem, "xt_tiles", [C + 1, U, NC, P])
        stats = k.buffer(mem, "bn_stats", [P, T, 6])
        mv = k.buffer(mem, "mean_var", [P, T, 2])
        rstd = k.buffer(mem, "rstd", [P, T])
        spreads = xt_big is not None or xn_big is not None
        with nc.Block() as block:
            @block.vector
            def _(dve):
                dve.memset(XT[C:C + 1, :, :, :], 1.0).then_inc(k.dve.sem, 1)
                dve.wait_ge(k.dve.sem, k.dve.base + 1)
                k.dve.base += 1
                if norm:
                    k.dve.start()
                    for t in range(T):
                        last = dve.bn_stats(stats[:, t, :], k.H[:, t, :])
                    k.dve(dve, last)
                    for t in range(T):
                        last = dve.bn_aggr(mv[:, t, :], stats[:, t, :])
                    k.dve(dve, last)
                    dve.tensor_scalar(rstd[:, :], mv[:, :, 1], EPS, None, ALU.add).then_inc(var_ready.sem, 1)
                    dve.wait_ge(std_ready.sem, std_ready.after(1))
                    k.dve(dve, dve.reciprocal(rstd[:, :], rstd[:, :]))
                    k.dve.end()
                with dve.Fori(0, T // U) as i:
                    for u in range(U):
                        dve.wait_ge(xn_transposed.sem, i * U + xn_transposed.room(u + 1))
                        if xn_big is not None:
                            dve.wait_ge(xt_spread.sem, i * U + xt_spread.room(u + 1))
                        x = (k.H if norm else src)[:, bass.ds(i * U + u, 1), :]
                        if norm:
                            last = dve.tensor_scalar(XN[:, u, :], x, mv[:, bass.ds(i * U + u, 1), 0], rstd[:, bass.ds(i * U + u, 1)],
                                                     ALU.subtract, ALU.mult)
                        else:
                            last = dve.tensor_copy(XN[:, u, :], x)
                        last.then_inc(xn_ready.sem, 1)

            @block.tensor
            def _(pe):
                with pe.Fori(0, T // U) as i:
                    for u in range(U):
                        pe.wait_ge(xn_ready.sem, i * U + xn_ready.after(u + 1))
                        for c in range(NC):
                            last = pe.transpose(ps[0:C, u // 2, (2 * (u % 2) + c) * P:(2 * (u % 2) + c + 1) * P],
                                                XN[:, u, c * C:(c + 1) * C], k.ident[:, :])
                        last.then_inc(xn_transposed.sem, 1)
                    if not outs:
                        pe.wait_ge(xt_ready.sem, i * (U // 2) + xt_ready.after(U // 2))
                    for u in range(U):
                        if not outs:
                            break
                        if u % 2 == 0:
                            pe.wait_ge(xt_ready.sem, i * (U // 2) + xt_ready.after(u // 2 + 1))
                        pe.wait_ge(projection_read.sem, i * U + projection_read.room(u + 1))
                        for n, (w, dst) in enumerate(outs):
                            width = dst.shape[2]
                            for c in range(NC):
                                r = C + 1 - c
                                last = pe.matmul(ps[:, 2 + 2 * (u % 2) + n, 0:width], XT[0:r, u, c, :],
                                                 w[0:r, c, :], start=(c == 0), stop=(c == NC - 1))
                        last.then_inc(projected.sem, 1)

            @block.scalar
            def _(act):
                if norm:
                    act.wait_ge(var_ready.sem, var_ready.after(1))
                    act.activation(rstd[:, :], rstd[:, :], ACT.Sqrt).then_inc(std_ready.sem, 1)
                with act.Fori(0, T // U) as i:
                    for h in range(U // 2):
                        act.wait_ge(xn_transposed.sem, i * U + xn_transposed.after(2 * h + 2))
                        if spreads:
                            act.wait_ge(xt_spread.sem, i * U + xt_spread.room(2 * h + 2))
                        act.copy(XT[0:C, 2 * h:2 * h + 2, :, :], ps[0:C, h, :]).then_inc(xt_ready.sem, 1)
                    for u in range(U):
                        if not outs:
                            break
                        act.wait_ge(projected.sem, i * U + projected.after(u + 1))
                        for n, (w, dst) in enumerate(outs):
                            width = dst.shape[2]
                            last = act.copy(dst[:, bass.ds(i * U + u, 1), :], ps[:, 2 + 2 * (u % 2) + n, 0:width])
                        last.then_inc(projection_read.sem, 1)

            @block.gpsimd
            def _(pool):
                if not spreads:
                    return
                if xt_big is not None:
                    k.pool.start()
                    k.pool(pool, pool.memset(xt_big[C:C + 1, :, :], 1.0))
                    k.pool.end()
                with pool.Fori(0, T // U) as i:
                    for u in range(U):
                        if xn_big is not None:
                            pool.wait_ge(xn_ready.sem, i * U + xn_ready.after(u + 1))
                            last = pool.tensor_copy(xn_big[:, bass.ds(i * U + u, 1), :], XN[:, u, :])
                        if xt_big is not None:
                            pool.wait_ge(xt_ready.sem, i * (U // 2) + xt_ready.after(u // 2 + 1))
                            last = pool.tensor_copy(xt_big[0:C, :, bass.ds((i * U + u) * P, P)], XT[0:C, u, :, :])
                        last.then_inc(xt_spread.sem, 1)
    if norm:
        var_ready.passed(1)
        std_ready.passed(1)
    xn_ready.passed(T)
    xn_transposed.passed(T)
    xt_ready.passed(T // 2)
    if spreads:
        xt_spread.passed(T)
    if outs:
        projected.passed(T)
        projection_read.passed(T)


def route(k, L, E, kind, mem, lower=None, top=1, gates=None):
    nc, ps = k.nc, k.ps
    scores_ready = k.count("scores_ready")
    exps_ready = k.count("exps_ready")
    load_ready = k.count("load_ready")
    load_summed = k.count("load_summed")
    st = k.buffer(mem, "route_stat", [P, T])
    beats = k.buffer(mem, "route_beats", [P, T, E, E])
    ties = k.buffer(mem, "route_ties", [P, T, E, E])
    sel = k.buffer(mem, "route_selected", [P, T, E])
    load_e = k.buffer(mem, "route_load", [P, E])
    per_token = [P, T, E]
    pair = [P, T, E, E]
    row = lambda a: a[:, :].unsqueeze(2).broadcast_to(per_token)
    passes = 2 if kind == "softmax_top" else 1
    with nc.Block() as block:
        @block.vector
        def _(dve):
            link = lambda ins: k.dve(dve, ins)
            k.dve.start()

            def normalise(W):
                link(dve.tensor_reduce(st[:, :], W, AX.X, ALU.add))
                link(dve.reciprocal(st[:, :], st[:, :]))
                link(dve.tensor_tensor(W, W, row(st), ALU.mult))

            link(dve.tensor_reduce(st[:, :], L, AX.X, ALU.max))
            dve.tensor_tensor(L, L, row(st), ALU.subtract).then_inc(scores_ready.sem, 1)
            dve.wait_ge(exps_ready.sem, exps_ready.after(1))
            normalise(L)
            link(dve.tensor_tensor(beats[:, :, :, :], L.unsqueeze(2).broadcast_to(pair),
                                   L.unsqueeze(3).broadcast_to(pair), ALU.is_gt))
            link(dve.tensor_tensor(ties[:, :, :, :], L.unsqueeze(2).broadcast_to(pair),
                                   L.unsqueeze(3).broadcast_to(pair), ALU.is_equal))
            tri = lower[:, 0:E * E].rearrange("p (e j) -> p e j", e=E).unsqueeze(1).broadcast_to(pair)
            link(dve.tensor_tensor(ties[:, :, :, :], ties[:, :, :, :], tri, ALU.mult))
            link(dve.tensor_tensor(beats[:, :, :, :], beats[:, :, :, :], ties[:, :, :, :], ALU.add))
            link(dve.tensor_reduce(sel[:, :, :], beats[:, :, :, :], AX.X, ALU.add))
            if kind == "argmax":
                link(dve.tensor_scalar(L, sel[:, :, :], float(top), None, ALU.is_lt))
                return k.dve.end()
            link(dve.tensor_scalar(sel[:, :, :], sel[:, :, :], float(top), None, ALU.is_lt))
            if kind == "balanced":
                dve.tensor_reduce(load_e[:, :], L.rearrange("p t e -> p e t"), AX.X,
                                  ALU.add).then_inc(load_ready.sem, 1)
                dve.wait_ge(load_summed.sem, load_summed.after(1))
                link(dve.tensor_scalar(load_e[:, :], ps[:, 0, 0:E], -1.0, 1.0 - 0.9, ALU.add, ALU.mult))
                link(dve.tensor_scalar(load_e[:, :], load_e[:, :], 1.0, 0.01, ALU.add, ALU.add))
                link(dve.reciprocal(load_e[:, :], load_e[:, :]))
                link(dve.tensor_tensor(L, L, load_e[:, :].unsqueeze(1).broadcast_to(per_token), ALU.mult))
            if kind == "softmax_top":
                link(dve.tensor_reduce(st[:, :], L, AX.X, ALU.max))
                dve.tensor_tensor(L, L, row(st), ALU.subtract).then_inc(scores_ready.sem, 1)
                dve.wait_ge(exps_ready.sem, exps_ready.after(2))
            link(dve.tensor_tensor(L, L, sel[:, :, :], ALU.mult))
            normalise(L)
            k.dve.end()

        @block.scalar
        def _(act):
            for n in range(passes):
                act.wait_ge(scores_ready.sem, scores_ready.after(n + 1))
                act.activation(L, L, ACT.Exp).then_inc(exps_ready.sem, 1)

        @block.tensor
        def _(pe):
            if kind == "balanced":
                pe.wait_ge(load_ready.sem, load_ready.after(1))
                pe.matmul(ps[:, 0, 0:E], k.ones[:, :], load_e[:, :], start=True,
                          stop=True).then_inc(load_summed.sem, 1)
    scores_ready.passed(passes)
    exps_ready.passed(passes)
    if kind == "balanced":
        load_ready.passed(1)
        load_summed.passed(1)


def experts(k, E, F, xt, w1, w2, W, func, w1_up=None, b2=None):
    nc, ps = k.nc, k.ps
    NF = F // P
    G = TOK // BANK
    J = BANK // P
    hidden_in = k.count("hidden_in")
    hidden_ready = k.count("hidden_ready", 4)
    expert_out = k.count("expert_out", 2 * J)
    expert_added = k.count("expert_added", J)
    gate_ready = k.count("gate_ready", 2)
    per_chunk = 1 if w1_up is None else 2
    ring = 4 // per_chunk
    with ExitStack() as mem:
        hid = k.buffer(mem, "hidden", [P, 2, NF, BANK])
        gate = k.buffer(mem, "gate", [P, 2, BANK]) if w1_up is not None else None
        with nc.Block() as block:
            @block.tensor
            def _(pe):
                with pe.Fori(0, G) as g:
                    def first(e):
                        for f in range(NF):
                            n = e * NF + f
                            pe.wait_ge(hidden_ready.sem, g * (E * NF) + (hidden_ready.base + hidden_ready.primed - ring + n + 1))
                            for m, w in enumerate((w1,) if w1_up is None else (w1, w1_up)):
                                for c in range(NC):
                                    r = C + 1 - c
                                    last = pe.matmul(ps[:, (n % ring) * per_chunk + m, :], w[0:r, e, c, f * P:(f + 1) * P],
                                                     xt[0:r, c, bass.ds(g * BANK, BANK)], start=(c == 0), stop=(c == NC - 1))
                            last.then_inc(hidden_in.sem, 1)

                    def second(e):
                        pe.wait_ge(hidden_ready.sem, g * (E * NF) + hidden_ready.after((e + 1) * NF))
                        for j in range(J):
                            pe.wait_ge(expert_added.sem, g * (E * J) + expert_added.room(e * J + j + 1))
                            for f in range(NF):
                                last = pe.matmul(ps[:, 4 + j, 0:D], hid[:, e % 2, f, j * P:(j + 1) * P], w2[:, e, f, :],
                                                 start=(f == 0), stop=(f == NF - 1))
                            last.then_inc(expert_out.sem, 1)

                    first(0)
                    for e in range(E):
                        if e + 1 < E:
                            first(e + 1)
                        second(e)

            @block.scalar
            def _(act):
                with act.Fori(0, G) as g:
                    for e in range(E):
                        if w1_up is None:
                            act.wait_ge(expert_out.sem, g * (E * J) + expert_out.room((e + 1) * J))
                        for f in range(NF):
                            n = e * NF + f
                            act.wait_ge(hidden_in.sem, g * (E * NF) + hidden_in.after(n + 1))
                            if w1_up is None:
                                act.activation(hid[:, e % 2, f, :], ps[:, n % ring, :], func).then_inc(hidden_ready.sem, 1)
                            else:
                                act.wait_ge(hidden_ready.sem, g * (E * NF) + (hidden_ready.base + hidden_ready.primed - 2 + n + 1))
                                act.activation(gate[:, n % 2, :], ps[:, (n % ring) * 2, :], func).then_inc(gate_ready.sem, 1)

            @block.vector
            def _(dve):
                with dve.Fori(0, G) as g:
                    def up(e):
                        dve.wait_ge(expert_out.sem, g * (E * J) + expert_out.room((e + 1) * J))
                        for f in range(NF):
                            n = e * NF + f
                            dve.wait_ge(gate_ready.sem, g * (E * NF) + gate_ready.after(n + 1))
                            dve.tensor_tensor(hid[:, e % 2, f, :], gate[:, n % 2, :], ps[:, (n % ring) * 2 + 1, :],
                                              ALU.mult).then_inc(hidden_ready.sem, 1)

                    def add(e):
                        for j in range(J):
                            t = g * J + j
                            h = k.H[:, bass.ds(t, 1), :]
                            dve.wait_ge(expert_added.sem, g * (E * J) + expert_added.room(e * J + j + 1))
                            if b2 is not None:
                                k.dve(dve, dve.scalar_tensor_tensor(h, b2[:, e, :], W[:, bass.ds(t, 1), e:e + 1], h, ALU.mult, ALU.add))
                            dve.wait_ge(expert_out.sem, g * (E * J) + expert_out.after(e * J + j + 1))
                            dve.scalar_tensor_tensor(h, ps[:, 4 + j, 0:D], W[:, bass.ds(t, 1), e:e + 1], h, ALU.mult,
                                                     ALU.add).then_inc(expert_added.sem, 1)
                    k.dve.start(g, E * J if b2 is not None else 0)
                    if w1_up is not None:
                        up(0)
                    for e in range(E):
                        if w1_up is not None and e + 1 < E:
                            up(e + 1)
                        add(e)
                k.dve.end(G)
    hidden_in.passed(G * E * NF)
    hidden_ready.passed(G * E * NF)
    expert_out.passed(G * E * J)
    expert_added.passed(G * E * J)
    if w1_up is not None:
        gate_ready.passed(G * E * NF)


def moe(k, tag, E, F, kind, top, func, gated=False, bias2=False):
    nc = k.nc
    with ExitStack() as mem:
        sb = lambda name, shape: mem.enter_context(nc.sbuf_tensor(f"{tag}_{name}", shape, F32))
        router, w1, w2 = sb("router", [C + 1, NC, E]), sb("w1", [C + 1, E, NC, F]), sb("w2", [P, E, F // P, D])
        up = sb("up", [C + 1, E, NC, F]) if gated else None
        b2 = sb("b2", [P, E, D]) if bias2 else None
        lower = sb("lower", [P, E * E])
        pairs = [(router[:, :, :], f"{tag}_router"), (w1[:, :, :, :], f"{tag}_w1"), (w2[:, :, :, :], f"{tag}_w2"), (lower[:, :], f"lower{E}")]
        if gated:
            pairs.append((up[:, :, :, :], f"{tag}_up"))
        if bias2:
            pairs.append((b2[:, :, :], f"{tag}_b2"))
        xt = sb("xt", [C + 1, NC, TOK])
        W = sb("weights", [P, T, E])
        load(k, pairs)
        front(k, [(router, W)], xt_big=xt)
        with ExitStack() as inner:
            route(k, W[:, :, :], E, kind, inner, lower, top)
        experts(k, E, F, xt, w1, w2, W, func, w1_up=up, b2=b2)


def diagonal_blocks(ps, bank, NJ, L, eng_copy, dst_of, blocks):
    for b in blocks:
        rows = slice(b * L, (b + 1) * L)
        src = ps[rows, bank:bank + NJ, 0:3 * P].rearrange("p j (g m) -> p j g m", m=P)[:, :, :, b * L:(b + 1) * L]
        dst = dst_of(rows)
        if NJ == 1:
            src = src[:, 0, :, :]
        else:
            dst = dst.rearrange("p (j g) m -> p j g m", j=NJ)
        last = eng_copy(dst, src)
    return last


def in_turns(eng, depth, step, link=None, steps=0):
    late = depth - 1

    def call(i, newest, first=False, last=False):
        tiles = [newest - n for n in range(depth)]
        step(i, *(None if (first and n < 0) or (last and n > 1) else n for n in tiles))

    if link:
        link.start()
    for n in range(late):
        call(0, n, first=True)
    if link:
        link.end()
    turns = (T - late) // 2
    with eng.Fori(0, turns) as i:
        if link:
            link.start(i, 2 * steps)
        for n in range(2):
            call(i, late + n)
    if link:
        link.end(turns)
        link.start()
    end = T // 2 - 1
    for n in range(2 * turns + late - 2 * end, 2 + late):
        call(end, n, last=True)
    if link:
        link.end()


class Attention:

    G = 3

    def __init__(self, k, mem, tag, NJ, M, L, scale, values, wo=None, bo=None, ot_big=None, mask=None, head_w=None,
                 score_bank=4, out_bank=0):
        self.k, self.NJ, self.M, self.L, self.scale, self.values = k, NJ, M, L, scale, values
        self.S, self.mask, self.head_w = NJ * self.G, mask, head_w
        self.wo, self.bo, self.ot_big, self.score_bank, self.out_bank = wo, bo, ot_big, score_bank, out_bank
        sb = lambda name, shape: mem.enter_context(k.nc.sbuf_tensor(f"{tag}_{name}", shape, F32))
        S = self.S
        self.SC = sb("scores", [P, 2, S, L])
        self.PT = sb("probs_t", [P, 2, S, P])
        self.V = sb("values", [P, 2, S * M])
        self.OT = sb("out_t", [NJ * M, 2, self.G, P])
        self.stat = sb("row_stat", [P, 2, S])
        self.scores_in = k.count("scores_in")
        self.scores_out = k.count("scores_out", 2)
        self.shifted = k.count("shifted")
        self.exped = k.count("exped")
        self.probs_ready = k.count("probs_ready", 2)
        self.v_staged = k.count("v_staged")
        self.pv_done = k.count("pv_done", 2)
        self.ot_ready = k.count("ot_ready", 1)
        self.out_ready = k.count("out_ready")
        self.out_added = k.count("out_added", 1)

    def finished(self, n=T, scores=True, staged=True):
        for s in (self.exped, self.probs_ready, self.pv_done, self.ot_ready):
            s.passed(n)
        if staged:
            self.v_staged.passed(n)
        if scores:
            self.scores_in.passed(n)
            self.shifted.passed(n)
            self.scores_out.passed(2 * n)
        if self.wo is not None:
            self.out_ready.passed(n)
            self.out_added.passed(n)

    def zero(self, dve):
        self.k.dve.start()
        self.k.dve(dve, dve.memset(self.PT[:, :, :, :], 0.0))
        self.k.dve.end()

    def _blocks(self, eng_copy, p, blocks):
        dst = lambda rows: self.SC[rows, p % 2, :, :]
        diagonal_blocks(self.k.ps, self.score_bank, self.NJ, self.L, eng_copy, dst, blocks).then_inc(self.scores_out.sem, 1)

    def act_extract(self, act, i, p):
        half = range(0, P // self.L // 2)
        act.wait_ge(self.scores_in.sem, 2 * i + self.scores_in.after(p + 1))
        act.wait_ge(self.probs_ready.sem, 2 * i + self.probs_ready.room(p + 1))
        self._blocks(act.copy, p, half)

    def dve_extract(self, dve, i, p):
        half = range(P // self.L // 2, P // self.L)
        dve.wait_ge(self.scores_in.sem, 2 * i + self.scores_in.after(p + 1))
        self._blocks(dve.tensor_copy, p, half)

    SHIFT_STEPS, PROB_STEPS = 1, 3

    def dve_shift(self, dve, i, p):
        k, sc = self.k, self.SC[:, p % 2, :, :]
        dve.wait_ge(self.scores_out.sem, 4 * i + self.scores_out.after(2 * p + 2))
        if self.mask is not None:
            k.dve(dve, dve.scalar_tensor_tensor(sc, sc, self.scale, self.mask[:, :, :], ALU.mult, ALU.add))
        st = self.stat[:, p % 2, :]
        k.dve(dve, dve.tensor_reduce(st, sc, AX.X, ALU.max))
        dve.tensor_tensor(sc, sc, st.unsqueeze(2).broadcast_to([P, self.S, self.L]), ALU.subtract).then_inc(self.shifted.sem, 1)

    def act_exp(self, act, i, p):
        act.wait_ge(self.shifted.sem, 2 * i + self.shifted.after(p + 1))
        sc = self.SC[:, p % 2, :, :]
        act.activation(sc, sc, ACT.Exp, scale=1.0 if self.mask is not None else self.scale).then_inc(self.exped.sem, 1)

    def dve_probs(self, dve, i, p):
        k, L, sc, st = self.k, self.L, self.SC[:, p % 2, :, :], self.stat[:, p % 2, :]
        dve.wait_ge(self.exped.sem, 2 * i + self.exped.after(p + 1))
        k.dve(dve, dve.tensor_reduce(st, sc, AX.X, ALU.add))
        k.dve(dve, dve.reciprocal(st, st))
        if self.head_w is not None:
            k.dve(dve, dve.tensor_tensor(st, st, self.head_w[:, bass.ds(2 * i + p, 1), :], ALU.mult))
        k.dve(dve, dve.tensor_tensor(sc, sc, st.unsqueeze(2).broadcast_to([P, self.S, L]), ALU.mult))
        dve.wait_ge(self.pv_done.sem, 2 * i + self.pv_done.room(p + 1))
        n = L // 32
        for b in range(P // L):
            for r in range(n):
                for c in range(n):
                    rows = slice(b * L + 32 * r, b * L + 32 * r + 32)
                    out_rows = slice(b * L + 32 * c, b * L + 32 * c + 32)
                    last = dve.transpose(self.PT[out_rows, p % 2, :, b * L + 32 * r:b * L + 32 * r + 32],
                                         self.SC[rows, p % 2, :, 32 * c:32 * c + 32])
        last.then_inc(self.probs_ready.sem, 1)

    def pool_values(self, pool, i, p):
        pool.wait_ge(self.pv_done.sem, 2 * i + self.pv_done.room(p + 1))
        pool.tensor_copy(self.V[:, p % 2, :], self.values[:, bass.ds(2 * i + p, 1), :]).then_inc(self.v_staged.sem, 1)

    def pe_values(self, pe, i, p):
        k, M = self.k, self.M
        if self.values is not None:
            pe.wait_ge(self.v_staged.sem, 2 * i + self.v_staged.after(p + 1))
        pe.wait_ge(self.probs_ready.sem, 2 * i + self.probs_ready.after(p + 1))
        pe.wait_ge(self.ot_ready.sem, 2 * i + self.ot_ready.room(p + 1))
        for g in range(self.G):
            for j in range(self.NJ):
                h = self.NJ * g + j
                last = pe.matmul(k.ps[j * M:(j + 1) * M, self.out_bank, g * P:(g + 1) * P], self.V[:, p % 2, h * M:(h + 1) * M],
                                 self.PT[:, p % 2, j * self.G + g, :], start=True, stop=True)
        last.then_inc(self.pv_done.sem, 1)

    def act_out(self, act, i, p):
        act.wait_ge(self.pv_done.sem, 2 * i + self.pv_done.after(p + 1))
        src = self.k.ps[0:self.NJ * self.M, self.out_bank, 0:self.G * P]
        if self.ot_big is not None:
            src = src.rearrange("p (g n l) -> p g n l", g=self.G, l=self.L)
            dst = self.ot_big[:, :, :].rearrange("p g (l n) -> p g n l", l=self.L)
            n = P // self.L
            for g in range(self.G):
                last = act.copy(dst[:, g, bass.ds((2 * i + p) * n, n), :], src[:, g, :, :])
            last.then_inc(self.ot_ready.sem, 1)
            return
        act.copy(self.OT[:, p % 2, :, :], src).then_inc(self.ot_ready.sem, 1)

    def pe_project(self, pe, i, p):
        k = self.k
        pe.wait_ge(self.ot_ready.sem, 2 * i + self.ot_ready.after(p + 1))
        pe.wait_ge(self.out_added.sem, 2 * i + self.out_added.room(p + 1))
        dst = k.ps[:, self.out_bank + 1, 0:D]
        pe.matmul(dst, k.ones[0:1, :], self.bo[0:1, :], start=True, stop=False)
        for g in range(self.G):
            last = pe.matmul(dst, self.OT[:, p % 2, g, :], self.wo[:, g, :], start=False, stop=(g == self.G - 1))
        last.then_inc(self.out_ready.sem, 1)

    def dve_add(self, dve, i, p):
        k = self.k
        h = k.H[:, bass.ds(2 * i + p, 1), :]
        dve.wait_ge(self.out_ready.sem, 2 * i + self.out_ready.after(p + 1))
        dve.tensor_tensor(h, h, k.ps[:, self.out_bank + 1, 0:D], ALU.add).then_inc(self.out_added.sem, 1)


def head_scores(pe, ps, q, kk):
    for g in range(3):
        for j in range(4):
            rows = slice(32 * j, 32 * j + 32)
            cols = slice(g * P, (g + 1) * P)
            last = pe.matmul(ps[:, 4 + j, cols], q[rows, cols], kk[rows, cols], start=True, stop=True)
    return last


def rotary_attention(k):
    nc, ps = k.nc, k.ps
    with ExitStack() as mem:
        sb = lambda name, shape: mem.enter_context(nc.sbuf_tensor(f"a1_{name}", shape, F32))
        wqk, wv = sb("wqk", [C + 1, NC, 4, HW]), sb("wv", [C + 1, NC, HW])
        wo, bo = sb("wo", [P, 3, D]), sb("bo", [1, D])
        turn = sb("turn", [P, 2, 32])
        xt, V = sb("xt", [C + 1, NC, TOK]), sb("v", [P, T, HW])
        load(k, [(wqk[:, :, :, :], "a1_wqk"), (wv[:, :, :], "a1_wv"), (wo[:, :, :], "a1_wo"), (bo[:, :], "a1_bo"), (turn[:, :, :], "a1_turn")])
        front(k, [(wv, V)], xt_big=xt)
        a = Attention(k, mem, "a1", 4, HP, 32, 0.25, V, wo, bo)
        QK = sb("qk", [P, 2, 2, HW])
        by_cos, by_sin = sb("by_cos", [P, 2, HW]), sb("by_sin", [P, 2, HW])
        qk_in = k.count("qk_in")
        qk_ready = k.count("qk_ready", 1)
        with nc.Block() as block:
            @block.tensor
            def _(pe):
                def step(i, new, old):
                    if new is not None:
                        for half in range(2):
                            if old is not None:
                                pe.wait_ge(qk_ready.sem, 4 * i + qk_ready.after(2 * new - 1 + half))
                            for m in range(2 * half, 2 * half + 2):
                                if old is not None and m == 0:
                                    pe.wait_ge(a.ot_ready.sem, 2 * i + a.ot_ready.room(new))
                                if old is not None and m == 1:
                                    pe.wait_ge(a.out_added.sem, 2 * i + a.out_added.room(new))
                                for g in range(3):
                                    for c in range(NC):
                                        r = C + 1 - c
                                        last = pe.matmul(ps[:, m, g * P:(g + 1) * P], wqk[0:r, c, m, g * P:(g + 1) * P],
                                                         xt[0:r, c, bass.ds((2 * i + new) * P, P)], start=(c == 0), stop=(c == NC - 1))
                            last.then_inc(qk_in.sem, 1)
                        pe.wait_ge(qk_ready.sem, 4 * i + qk_ready.after(2 * new + 1))
                    if old is not None:
                        a.pe_values(pe, i, old)
                    if new is not None:
                        pe.wait_ge(qk_ready.sem, 4 * i + qk_ready.after(2 * new + 2))
                        pe.wait_ge(a.scores_out.sem, 4 * i + a.scores_out.room(2 * new + 2))
                        head_scores(pe, ps, QK[:, new % 2, 0, :], QK[:, new % 2, 1, :]).then_inc(a.scores_in.sem, 1)
                    if old is not None:
                        a.pe_project(pe, i, old)

                in_turns(pe, 2, step)

            @block.vector
            def _(dve):
                a.zero(dve)

                def step(i, new, old):
                    if old is not None:
                        a.dve_probs(dve, i, old)
                    if new is not None:
                        for m in range(2):
                            dve.wait_ge(qk_in.sem, 4 * i + qk_in.after(2 * new + m + 1))
                            rep = lambda n: turn[:, n, :].unsqueeze(1).broadcast_to([P, HEADS, 32])
                            part = lambda n: ps[:, 2 * m + n, 0:HW].rearrange("p (h d) -> p h d", d=32)
                            as3 = lambda b: b[:, m, :].rearrange("p (h d) -> p h d", d=32)
                            dve.tensor_tensor(as3(by_cos), part(0), rep(0), ALU.mult)
                            k.dve(dve, dve.tensor_tensor(as3(by_sin), part(1), rep(1), ALU.mult))
                            dve.tensor_tensor(QK[:, new % 2, m, :], by_cos[:, m, :], by_sin[:, m, :], ALU.add).then_inc(qk_ready.sem, 1)
                        a.dve_extract(dve, i, new)
                    if old is not None:
                        a.dve_add(dve, i, old)
                    if new is not None:
                        a.dve_shift(dve, i, new)

                in_turns(dve, 2, step, k.dve, 2 + 1 + 3)

            @block.scalar
            def _(act):
                def step(i, new, old):
                    if old is not None:
                        a.act_out(act, i, old)
                    if new is not None:
                        a.act_extract(act, i, new)
                        a.act_exp(act, i, new)

                in_turns(act, 2, step)

            @block.gpsimd
            def _(pool):
                with pool.Fori(0, T // 2) as i:
                    for p in range(2):
                        a.pool_values(pool, i, p)
        a.finished()
        qk_in.passed(2 * T)
        qk_ready.passed(2 * T)


def causal_mixture(k):
    nc, ps = k.nc, k.ps
    E, HD = 3, 64
    with ExitStack() as mem:
        sb = lambda name, shape: mem.enter_context(nc.sbuf_tensor(f"f1_{name}", shape, F32))
        wqk, wvg = sb("wqk", [C + 1, NC, 2 * D]), sb("wvg", [C + 1, NC, D + 32])
        wo, bo = sb("wo", [HD, E, D]), sb("bo", [1, D])
        conv = sb("conv", [HD, 4])
        mask, pos = sb("mask", [P, E, 32]), sb("pos", [P, E, 32])
        wg2, bg2, lower = sb("wg2", [P, E, 32]), sb("bg2", [P, E]), sb("lower", [P, E * E])
        xt, VG = sb("xt", [C + 1, NC, TOK]), sb("vg", [P, T, D + 32])
        W = sb("w", [P, T, E])
        load(k, [(wqk[:, :, :], "f1_wqk"), (wvg[:, :, :], "f1_wvg"), (wo[:, :, :], "f1_wo"), (bo[:, :], "f1_bo"),
                 (conv[:, :], "f1_conv"), (mask[:, :, :], "f1_mask"), (pos[:, :, :], "f1_pos"),
                 (wg2[:, :, :], "f1_wg2"), (bg2[:, :], "f1_bg2"), (lower[:, :], "lower3")])
        front(k, [(wvg, VG)], xt_big=xt)
        with ExitStack() as inner:
            prod = inner.enter_context(nc.sbuf_tensor("f1_prod", [P, T, E, 32], F32))
            with nc.Block() as block:
                @block.vector
                def _(dve):
                    link = lambda ins: k.dve(dve, ins)
                    k.dve.start()
                    g1 = VG[:, :, D:D + 32]
                    link(dve.tensor_scalar(g1, g1, 0.0, None, ALU.max))
                    link(dve.tensor_tensor(prod[:, :, :, :], g1.unsqueeze(2).broadcast_to([P, T, E, 32]),
                                           wg2[:, :, :].unsqueeze(1).broadcast_to([P, T, E, 32]), ALU.mult))
                    link(dve.tensor_reduce(W[:, :, :], prod[:, :, :, :], AX.X, ALU.add))
                    link(dve.tensor_tensor(W[:, :, :], W[:, :, :], bg2[:, :].unsqueeze(1).broadcast_to([P, T, E]), ALU.add))
                    link(dve.tensor_tensor(mask[:, :, :], mask[:, :, :], pos[:, :, :], ALU.add))
                    k.dve.end()
            route(k, W[:, :, :], E, "softmax_top", inner, lower, 2)
        a = Attention(k, mem, "f1", 1, HD, 32, 0.125, VG[:, :, 0:D], wo, bo, mask=mask, head_w=W, out_bank=2)
        Q, K = sb("q", [HD, 2, E, P]), sb("k", [HD, 2, E, P])
        qk_in = k.count("qk_in")
        qk_ready = k.count("qk_ready", 1)
        keys_ready = k.count("keys_ready", 1)
        with nc.Block() as block:
            @block.tensor
            def _(pe):
                def step(i, new, old):
                    if new is not None:
                        pe.wait_ge(qk_ready.sem, 2 * i + qk_ready.room(new + 1))
                        pe.wait_ge(keys_ready.sem, 2 * i + keys_ready.room(new + 1))
                        for m in range(2):
                            for e in range(E):
                                cols = slice(m * D + e * HD, m * D + (e + 1) * HD)
                                for c in range(NC):
                                    r = C + 1 - c
                                    last = pe.matmul(ps[0:HD, m, e * P:(e + 1) * P], wqk[0:r, c, cols],
                                                     xt[0:r, c, bass.ds((2 * i + new) * P, P)], start=(c == 0), stop=(c == NC - 1))
                        last.then_inc(qk_in.sem, 1)
                    if old is not None:
                        a.pe_values(pe, i, old)
                    if new is not None:
                        pe.wait_ge(qk_ready.sem, 2 * i + qk_ready.after(new + 1))
                        pe.wait_ge(keys_ready.sem, 2 * i + keys_ready.after(new + 1))
                        pe.wait_ge(a.scores_out.sem, 4 * i + a.scores_out.room(2 * new + 2))
                        for e in range(E):
                            last = pe.matmul(ps[:, 4, e * P:(e + 1) * P], Q[:, new % 2, e, :], K[:, new % 2, e, :], start=True, stop=True)
                        last.then_inc(a.scores_in.sem, 1)
                    if old is not None:
                        a.pe_project(pe, i, old)

                in_turns(pe, 2, step)

            @block.vector
            def _(dve):
                a.zero(dve)

                def step(i, new, old):
                    if old is not None:
                        a.dve_probs(dve, i, old)
                    if new is not None:
                        dve.wait_ge(qk_in.sem, 2 * i + qk_in.after(new + 1))
                        q, src = Q[:, new % 2, 0, :], ps[0:HD, 0, 0:P]
                        k.dve(dve, dve.tensor_scalar(q, src, conv[:, 1:2], conv[:, 3:4], ALU.mult, ALU.add))
                        seq = lambda x, a0, a1: x.rearrange("p (b s) -> p b s", s=32)[:, :, a0:a1]
                        k.dve(dve, dve.scalar_tensor_tensor(seq(q, 1, 32), seq(src, 0, 31), conv[:, 0:1], seq(q, 1, 32), ALU.mult, ALU.add))
                        dve.scalar_tensor_tensor(seq(q, 0, 31), seq(src, 1, 32), conv[:, 2:3], seq(q, 0, 31), ALU.mult,
                                                 ALU.add).then_inc(qk_ready.sem, 1)
                        a.dve_extract(dve, i, new)
                    if old is not None:
                        a.dve_add(dve, i, old)
                    if new is not None:
                        a.dve_shift(dve, i, new)

                in_turns(dve, 2, step, k.dve, 2 + 2 + 4)

            @block.scalar
            def _(act):
                def step(i, new, old):
                    if new is not None:
                        act.wait_ge(qk_in.sem, 2 * i + qk_in.after(new + 1))
                        act.copy(K[:, new % 2, :, :], ps[0:HD, 1, 0:E * P])
                        act.wait_ge(qk_ready.sem, 2 * i + qk_ready.after(new + 1))
                        act.copy(Q[:, new % 2, 1:E, :], ps[0:HD, 0, P:E * P]).then_inc(keys_ready.sem, 1)
                    if old is not None:
                        a.act_out(act, i, old)
                    if new is not None:
                        a.act_extract(act, i, new)
                        a.act_exp(act, i, new)

                in_turns(act, 2, step)

            @block.gpsimd
            def _(pool):
                with pool.Fori(0, T // 2) as i:
                    for p in range(2):
                        a.pool_values(pool, i, p)
        a.finished()
        for s in (qk_in, qk_ready, keys_ready):
            s.passed(T)


SINKHORN = 10
GT = 4
GW = GT * HW


def transport_attention(k):
    nc, ps = k.nc, k.ps
    with ExitStack() as mem:
        sb = lambda name, shape: mem.enter_context(nc.sbuf_tensor(f"a3_{name}", shape, F32))
        wq, wv = sb("wq", [C + 1, NC, HW]), sb("wv", [C + 1, NC, HW])
        wo, bo = sb("wo", [P, 3, D]), sb("bo", [1, D])
        eye, off, blocks = sb("eye", [P, 32]), sb("off", [P, 32]), sb("blocks", [P, P])
        V, K = sb("v", [P, T, HW]), sb("kernel", [P, T, HEADS, 32])
        load(k, [(wq[:, :, :], "a3_wq"), (wv[:, :, :], "a3_wv"), (wo[:, :, :], "a3_wo"), (bo[:, :], "a3_bo"),
                 (eye[:, :], "eye32"), (off[:, :], "off32"), (blocks[:, :], "blocks32")])
        with ExitStack() as inner:
            Q = inner.enter_context(nc.sbuf_tensor("a3_q", [P, T, HW], F32))
            front(k, [(wq, Q), (wv, V)])
            transport_kernel(k, inner, Q, K, off)
        Z = sb("z", [P, T, HEADS, 32])
        with ExitStack() as inner:
            scale_kernel(k, inner, K, Z, blocks, eye)
        a = Attention(k, mem, "a3", 4, HP, 32, 0.25, V, wo, bo)
        with nc.Block() as block:
            @block.tensor
            def _(pe):
                def step(i, new, old):
                    if old is not None:
                        a.pe_project(pe, i, old)
                    if new is not None:
                        a.pe_values(pe, i, new)

                in_turns(pe, 2, step)

            @block.vector
            def _(dve):
                a.zero(dve)

                def step(i, new, old):
                    if new is not None:
                        a.dve_probs(dve, i, new)
                    if old is not None:
                        a.dve_add(dve, i, old)

                in_turns(dve, 2, step, k.dve, 3)

            @block.scalar
            def _(act):
                def step(i, new, old):
                    if new is not None:
                        act.wait_ge(a.probs_ready.sem, 2 * i + a.probs_ready.room(new + 1))
                        act.activation(a.SC[:, new % 2, :, :], Z[:, bass.ds(2 * i + new, 1), :, :], ACT.Exp,
                                       scale=0.25).then_inc(a.exped.sem, 1)
                    if old is not None:
                        a.act_out(act, i, old)

                in_turns(act, 2, step)

            @block.gpsimd
            def _(pool):
                with pool.Fori(0, T // 2) as i:
                    for p in range(2):
                        a.pool_values(pool, i, p)
        a.finished(scores=False)


def transport_kernel(k, mem, Q, K, off):
    nc, ps = k.nc, k.ps
    norm = mem.enter_context(nc.sbuf_tensor("a3_norm", [P, T, HEADS], F32))
    QN = mem.enter_context(nc.sbuf_tensor("a3_qn", [P, 2, HW], F32))
    QT = mem.enter_context(nc.sbuf_tensor("a3_qt", [P, 2, HW], F32))
    ten = mem.enter_context(nc.sbuf_tensor("a3_minus_ten", [P, 1], F32))
    squares_ready = k.count("squares_ready")
    norm2_ready = k.count("norm2_ready")
    norm_ready = k.count("norm_ready")
    qn_ready = k.count("qn_ready")
    qn_turned = k.count("qn_turned", 2)
    qt_ready = k.count("qt_ready", 2)
    scores_in = k.count("scores_in")
    scores_out = k.count("scores_out", 2)
    kernel_ready = k.count("kernel_ready")
    with nc.Block() as block:
        @block.scalar
        def _(act):
            act.activation(K[:, :, :, :], Q[:, :, :], ACT.Square).then_inc(squares_ready.sem, 1)
            act.wait_ge(norm2_ready.sem, norm2_ready.after(1))
            act.activation(norm[:, :, :], norm[:, :, :], ACT.Sqrt).then_inc(norm_ready.sem, 1)
            with act.Fori(0, T // 2) as i:
                for p in range(2):
                    act.wait_ge(qn_turned.sem, 2 * i + qn_turned.after(p + 1))
                    act.copy(QT[:, p, :], ps[:, p, 0:HW]).then_inc(qt_ready.sem, 1)
                    act.wait_ge(scores_in.sem, 2 * i + scores_in.after(p + 1))
                    dst = lambda rows: K[rows, bass.ds(2 * i + p, 1), :, :].rearrange("p t s m -> p (t s) m")
                    diagonal_blocks(ps, 4, 4, 32, act.copy, dst, (0, 1)).then_inc(scores_out.sem, 1)
            act.wait_ge(scores_out.sem, scores_out.after(2 * T))
            act.activation(K[:, :, :, :], K[:, :, :, :], ACT.Exp, bias=ten[:, :], scale=10.0).then_inc(kernel_ready.sem, 1)

        @block.vector
        def _(dve):
            k.dve.start()
            dve.memset(ten[:, :], -10.0)
            dve.wait_ge(squares_ready.sem, squares_ready.after(1))
            dve.tensor_reduce(norm[:, :, :], K[:, :, :, :], AX.X, ALU.add).then_inc(norm2_ready.sem, 1)
            dve.wait_ge(norm_ready.sem, norm_ready.after(1))
            k.dve(dve, dve.tensor_scalar(norm[:, :, :], norm[:, :, :], 1e-8, None, ALU.add))
            k.dve(dve, dve.reciprocal(norm[:, :, :], norm[:, :, :]))
            k.dve.end()
            with dve.Fori(0, T // 2) as i:
                for p in range(2):
                    dve.wait_ge(qn_turned.sem, 2 * i + qn_turned.room(p + 1))
                    n = 2 * i + p
                    as3 = lambda x: x.rearrange("p (h d) -> p h d", d=HP)
                    dve.tensor_tensor(as3(QN[:, p, :]), Q[:, bass.ds(n, 1), :].rearrange("p t (h d) -> p (t h) d", d=HP),
                                      norm[:, bass.ds(n, 1), :].rearrange("p t h -> p (t h)").unsqueeze(2).broadcast_to([P, HEADS, HP]),
                                      ALU.mult).then_inc(qn_ready.sem, 1)
                for p in range(2):
                    dve.wait_ge(scores_in.sem, 2 * i + scores_in.after(p + 1))
                    dst = lambda rows: K[rows, bass.ds(2 * i + p, 1), :, :].rearrange("p t s m -> p (t s) m")
                    diagonal_blocks(ps, 4, 4, 32, dve.tensor_copy, dst, (2, 3)).then_inc(scores_out.sem, 1)
            dve.wait_ge(kernel_ready.sem, kernel_ready.after(1))
            dve.tensor_tensor(K[:, :, :, :], K[:, :, :, :],
                              off[:, :].unsqueeze(1).unsqueeze(1).broadcast_to([P, T, HEADS, 32]), ALU.mult)

        @block.tensor
        def _(pe):
            with pe.Fori(0, T // 2) as i:
                for p in range(2):
                    pe.wait_ge(qn_ready.sem, 2 * i + qn_ready.after(p + 1))
                    pe.wait_ge(qt_ready.sem, 2 * i + qt_ready.room(p + 1))
                    for g in range(3):
                        last = pe.transpose(ps[:, p, g * P:(g + 1) * P], QN[:, p, g * P:(g + 1) * P], k.ident[:, :])
                    last.then_inc(qn_turned.sem, 1)
                for p in range(2):
                    pe.wait_ge(qt_ready.sem, 2 * i + qt_ready.after(p + 1))
                    pe.wait_ge(scores_out.sem, 4 * i + scores_out.room(2 * p + 2))
                    head_scores(pe, ps, QT[:, p, :], QT[:, p, :]).then_inc(scores_in.sem, 1)
    for s in (squares_ready, norm2_ready, norm_ready, kernel_ready):
        s.passed(1)
    for s in (qn_ready, qn_turned, qt_ready, scores_in):
        s.passed(T)
    scores_out.passed(2 * T)


def scale_kernel(k, mem, K, Z, blocks, eye):
    nc, ps = k.nc, k.ps
    NG = T // GT
    STEPS = 2 * SINKHORN - 1
    KV = mem.enter_context(nc.sbuf_tensor("a3_kv", [P, GW], F32))
    KU = mem.enter_context(nc.sbuf_tensor("a3_ku", [P, T, HEADS, 32], F32))
    u = mem.enter_context(nc.sbuf_tensor("a3_u", [P, T * HEADS], F32))
    v = mem.enter_context(nc.sbuf_tensor("a3_v_scale", [P, T * HEADS], F32))
    top = mem.enter_context(nc.sbuf_tensor("a3_top", [P, T * HEADS], F32))
    top_t = mem.enter_context(nc.sbuf_tensor("a3_top_t", [P, T * HEADS], F32))
    seq_top = mem.enter_context(nc.sbuf_tensor("a3_seq_top", [P, T * HEADS // 32], F32))
    scaled = k.count("scaled")
    diagonal_ready = k.count("diagonal_ready")
    vector_spread = k.count("vector_spread")
    ku_ready = k.count("ku_ready")
    n_pairs = GT * HEADS
    pairs = lambda x, g: x[:, g * n_pairs:(g + 1) * n_pairs]
    group = lambda X, g: X[:, g * GT:(g + 1) * GT, :, :].rearrange("p t h m -> p (t h) m")
    flat = lambda X, g: X[:, g * GT:(g + 1) * GT, :, :].rearrange("p t h m -> p (t h m)")
    kv3 = KV[:, :].rearrange("p (q m) -> p q m", m=32)
    slot = lambda g: ps[:, 3 * (g % 2):3 * (g % 2) + 3, :].rearrange("p a b -> p (a b)")
    slot3 = lambda g: slot(g).rearrange("p (q m) -> p q m", m=32)
    with nc.Block() as block:
        @block.vector
        def _(dve):
            link = lambda ins: k.dve(dve, ins)

            def step(n, g, dst):
                dve.wait_ge(vector_spread.sem, n * NG + vector_spread.after(g + 1))
                link(dve.tensor_tensor(kv3, group(K, g), slot3(g), ALU.mult))
                link(dve.tensor_reduce(pairs(dst, g), kv3, AX.X, ALU.add))
                dve.reciprocal(pairs(dst, g), pairs(dst, g)).then_inc(scaled.sem, 1)

            k.dve.start()
            for g in range(NG):
                link(dve.tensor_reduce(pairs(u, g), group(K, g), AX.X, ALU.add))
                dve.reciprocal(pairs(u, g), pairs(u, g)).then_inc(scaled.sem, 1)
            k.dve.end()
            with dve.Fori(0, SINKHORN - 1) as r:
                k.dve.start(r, 2 * 2 * NG)
                for g in range(NG):
                    step(2 * r, g, v)
                for g in range(NG):
                    step(2 * r + 1, g, u)
            k.dve.end(SINKHORN - 1)
            k.dve.start()
            for g in range(NG):
                step(STEPS - 1, g, v)
            for g in range(NG):
                dve.wait_ge(vector_spread.sem, STEPS * NG + vector_spread.after(g + 1))
                dve.wait_ge(ku_ready.sem, ku_ready.after(g + 1))
                dve.tensor_tensor(group(Z, g), group(KU, g), slot3(g), ALU.mult).then_inc(scaled.sem, 1)
            dve.wait_ge(scaled.sem, scaled.after((STEPS + 2) * NG))
            rows3 = lambda X: X[:, :, :, :].rearrange("p t h m -> p (t h) m")
            all_pairs = [P, T * HEADS, 32]
            link(dve.tensor_reduce(top[:, :], rows3(Z), AX.X, ALU.max))
            link(dve.transpose(top_t[:, :], top[:, :]))
            blocks3 = top_t[:, :].rearrange("p (q n) -> p q n", n=32)
            link(dve.tensor_reduce(seq_top[:, :], blocks3, AX.X, ALU.max))
            link(dve.reciprocal(seq_top[:, :], seq_top[:, :]))
            link(dve.tensor_copy(blocks3, seq_top[:, :].unsqueeze(2).broadcast_to([P, T * HEADS // 32, 32])))
            link(dve.transpose(top[:, :], top_t[:, :]))
            link(dve.tensor_tensor(rows3(Z), rows3(Z), top[:, :].unsqueeze(2).broadcast_to(all_pairs), ALU.mult))
            link(dve.tensor_tensor(rows3(Z), rows3(Z), eye[:, :].unsqueeze(1).broadcast_to(all_pairs), ALU.add))
            k.dve.end()

        @block.gpsimd
        def _(pool):
            def diagonals(n, src):
                for g in range(NG):
                    pool.wait_ge(scaled.sem, n * NG + scaled.after(g + 1))
                    pool.tensor_tensor(group(Z, g), eye[:, :].unsqueeze(1).broadcast_to([P, n_pairs, 32]),
                                       pairs(src, g).unsqueeze(2).broadcast_to([P, n_pairs, 32]),
                                       ALU.mult).then_inc(diagonal_ready.sem, 1)

            with pool.Fori(0, SINKHORN - 1) as r:
                diagonals(2 * r, u)
                diagonals(2 * r + 1, v)
            diagonals(STEPS - 1, u)
            diagonals(STEPS, v)
            for g in range(NG):
                pool.tensor_tensor(group(KU, g), group(K, g), pairs(u, g).unsqueeze(2).broadcast_to([P, n_pairs, 32]),
                                   ALU.mult).then_inc(ku_ready.sem, 1)

        @block.tensor
        def _(pe):
            def spread(n):
                for g in range(NG):
                    pe.wait_ge(diagonal_ready.sem, n * NG + diagonal_ready.after(g + 1))
                    pe.wait_ge(scaled.sem, n * NG + scaled.after(NG + g - 1))
                    for b in range(3):
                        last = pe.matmul(ps[:, 3 * (g % 2) + b, :], blocks[:, :], flat(Z, g)[:, b * BANK:(b + 1) * BANK],
                                         start=True, stop=True)
                    last.then_inc(vector_spread.sem, 1)

            with pe.Fori(0, SINKHORN - 1) as r:
                spread(2 * r)
                spread(2 * r + 1)
            spread(STEPS - 1)
            spread(STEPS)
    scaled.passed((STEPS + 2) * NG)
    diagonal_ready.passed((STEPS + 1) * NG)
    vector_spread.passed((STEPS + 1) * NG)
    ku_ready.passed(NG)


def cosine_attention(k):
    nc, ps = k.nc, k.ps
    L = 64
    with ExitStack() as mem:
        sb = lambda name, shape: mem.enter_context(nc.sbuf_tensor(f"a0_{name}", shape, F32))
        w = sb("w", [C + 1, NC, 3, HW])
        wo, bo = sb("wo", [P, 3, D]), sb("bo", [1, D])
        log_scale, head_scale = sb("log_scale", [P, HEADS]), sb("head_scale", [P, HEADS])
        xt = sb("xt", [C + 1, NC, TOK])
        OT = sb("ot", [P, 3, TOK])
        load(k, [(w[:, :, :, :], "a0_w"), (wo[:, :, :], "a0_wo"), (bo[:, :], "a0_bo"),
                 (log_scale[:, :], "a0_log_scale"), (head_scale[:, :], "a0_head_scale")])
        front(k, [], xt_big=xt)
        with ExitStack() as inner:
            sb2 = lambda name, shape: inner.enter_context(nc.sbuf_tensor(f"a0_{name}", shape, F32))
            a = Attention(k, inner, "a0", 4, HP, L, 1.0, None, ot_big=OT, out_bank=3)
            XT = sb2("xt_tile", [C + 1, 2, NC, P])
            SQ = sb2("squares", [P, 2, 2 * HW])
            norm = sb2("norm", [P, 2, 2, HEADS])
            QN, QT = sb2("qn", [P, 2, 2, HW]), sb2("qt", [P, 2, 2, HW])
            xt_staged = k.count("xt_staged")
            qk_in = k.count("qk_in")
            qkv_in = k.count("qkv_in", 2)
            v_ready = k.count("v_ready")
            squares_ready = k.count("squares_ready")
            norm2_ready = k.count("norm2_ready")
            norm_ready = k.count("norm_ready")
            qn_ready = k.count("qn_ready")
            qn_turned = k.count("qn_turned", 2)
            qt_ready = k.count("qt_ready", 2)
            with nc.Block() as block:
                @block.gpsimd
                def _(pool):
                    with pool.Fori(0, T // 2) as i:
                        for p in range(2):
                            pool.wait_ge(qkv_in.sem, 2 * i + qkv_in.room(p + 1))
                            for c in range(NC):
                                src = xt[:, c, :].rearrange("p (l n) -> p n l", l=L)[:, bass.ds((2 * i + p) * 2, 2), :]
                                last = pool.tensor_copy(XT[:, p, c, :].rearrange("p (n l) -> p n l", l=L), src)
                            last.then_inc(xt_staged.sem, 1)

                @block.tensor
                def _(pe):
                    def step(i, new, mid, old):
                        if mid is not None:
                            pe.wait_ge(qn_ready.sem, 2 * i + qn_ready.after(mid + 1))
                            pe.wait_ge(a.scores_out.sem, 4 * i + a.scores_out.room(2 * mid + 2))
                            for m in range(2):
                                for g in range(3):
                                    cols = slice(g * P, (g + 1) * P)
                                    last = pe.transpose(ps[:, 4 + m, cols], QN[:, mid % 2, m, cols], k.ident[:, :])
                            last.then_inc(qn_turned.sem, 1)
                        if new is not None:
                            pe.wait_ge(xt_staged.sem, 2 * i + xt_staged.after(new + 1))
                            for m in range(3):
                                if m == 2 and mid is not None:
                                    pe.wait_ge(v_ready.sem, 2 * i + v_ready.after(new))
                                for c in range(NC):
                                    r = C + 1 - c
                                    last = pe.matmul(ps[:, m, 0:HW], XT[0:r, new % 2, c, :], w[0:r, c, m, :], start=(c == 0), stop=(c == NC - 1))
                                if m == 1:
                                    last.then_inc(qk_in.sem, 1)
                            last.then_inc(qkv_in.sem, 1)
                        if mid is not None:
                            pe.wait_ge(qt_ready.sem, 2 * i + qt_ready.after(mid + 1))
                            head_scores(pe, ps, QT[:, mid % 2, 0, :], QT[:, mid % 2, 1, :]).then_inc(a.scores_in.sem, 1)
                        if old is not None:
                            a.pe_values(pe, i, old)

                    in_turns(pe, 3, step)

                @block.scalar
                def _(act):
                    act.wait_ge(norm2_ready.sem, norm2_ready.after(1))
                    act.activation(log_scale[:, :], log_scale[:, :], ACT.Exp).then_inc(norm_ready.sem, 1)

                    def step(i, new, mid, old):
                        if mid is not None:
                            act.wait_ge(qn_turned.sem, 2 * i + qn_turned.after(mid + 1))
                            act.copy(QT[:, mid % 2, :, :], ps[:, 4:6, 0:HW]).then_inc(qt_ready.sem, 1)
                        if new is not None:
                            act.wait_ge(qk_in.sem, 2 * i + qk_in.after(new + 1))
                            act.activation(SQ[:, new % 2, :].rearrange("p (m d) -> p m d", m=2), ps[:, 0:2, 0:HW],
                                           ACT.Square).then_inc(squares_ready.sem, 1)
                            act.wait_ge(norm2_ready.sem, 2 * i + norm2_ready.after(new + 2))
                            act.activation(norm[:, new % 2, :, :], norm[:, new % 2, :, :], ACT.Sqrt).then_inc(norm_ready.sem, 1)
                        if mid is not None:
                            a.act_extract(act, i, mid)
                            a.act_exp(act, i, mid)
                        if old is not None:
                            a.act_out(act, i, old)

                    in_turns(act, 3, step)

                @block.vector
                def _(dve):
                    a.zero(dve)
                    dve.tensor_scalar(log_scale[:, :], log_scale[:, :], float(np.log(1.0 / 0.01)), None,
                                      ALU.min).then_inc(norm2_ready.sem, 1)
                    dve.wait_ge(norm_ready.sem, norm_ready.after(1))

                    def step(i, new, mid, old):
                        if old is not None:
                            a.dve_probs(dve, i, old)
                        if new is not None:
                            p = new % 2
                            dve.wait_ge(squares_ready.sem, 2 * i + squares_ready.after(new + 1))
                            nm = norm[:, p, :, :].rearrange("p m h -> p (m h)")
                            dve.tensor_reduce(nm, SQ[:, p, :].rearrange("p (h d) -> p h d", d=HP), AX.X,
                                              ALU.add).then_inc(norm2_ready.sem, 1)
                            dve.wait_ge(norm_ready.sem, 2 * i + norm_ready.after(new + 2))
                            k.dve(dve, dve.tensor_scalar(nm, nm, 1e-12, None, ALU.max))
                            k.dve(dve, dve.reciprocal(nm, nm))
                            k.dve(dve, dve.tensor_tensor(norm[:, p, 0, :], norm[:, p, 0, :], log_scale[:, :], ALU.mult))
                            as4 = lambda x: x.rearrange("p m (h d) -> p m h d", d=HP)
                            dve.tensor_tensor(as4(QN[:, p, :, :]), as4(ps[:, 0:2, 0:HW]),
                                              norm[:, p, :, :].unsqueeze(3).broadcast_to([P, 2, HEADS, HP]), ALU.mult).then_inc(qn_ready.sem, 1)
                        if mid is not None:
                            a.dve_extract(dve, i, mid)
                            a.dve_shift(dve, i, mid)
                        if new is not None:
                            dve.wait_ge(qkv_in.sem, 2 * i + qkv_in.after(new + 1))
                            dve.wait_ge(a.pv_done.sem, 2 * i + a.pv_done.room(new + 1))
                            as3 = lambda x: x.rearrange("p (h d) -> p h d", d=HP)
                            dve.tensor_tensor(as3(a.V[:, p, :]), as3(ps[:, 2, 0:HW]),
                                              head_scale[:, :].unsqueeze(2).broadcast_to([P, HEADS, HP]), ALU.mult).then_inc(v_ready.sem, 1)

                    in_turns(dve, 3, step, k.dve, 3 + 1 + 3)
            a.finished(staged=False)
            for s in (xt_staged, qk_in, qkv_in, squares_ready, qn_ready, qn_turned, qt_ready, v_ready):
                s.passed(T)
            norm2_ready.passed(T + 1)
            norm_ready.passed(T + 1)
        project_tiles(k, mem, OT, wo, bo)


def project_tiles(k, mem, OT, wo, bo):
    nc, ps = k.nc, k.ps
    tile = k.buffer(mem, "ot_tile", [P, 2, 3, P])
    ot_staged = k.count("ot_staged")
    out_ready = k.count("tile_projected", 2)
    out_added = k.count("tile_added", 2)
    with nc.Block() as block:
        @block.gpsimd
        def _(pool):
            with pool.Fori(0, T // 2) as i:
                for p in range(2):
                    pool.wait_ge(out_ready.sem, 2 * i + out_ready.room(p + 1))
                    pool.tensor_copy(tile[:, p, :, :], OT[:, :, bass.ds((2 * i + p) * P, P)]).then_inc(ot_staged.sem, 1)

        @block.tensor
        def _(pe):
            with pe.Fori(0, T // 2) as i:
                for p in range(2):
                    pe.wait_ge(ot_staged.sem, 2 * i + ot_staged.after(p + 1))
                    pe.wait_ge(out_added.sem, 2 * i + out_added.room(p + 1))
                    pe.matmul(ps[:, p, 0:D], k.ones[0:1, :], bo[0:1, :], start=True, stop=False)
                    for g in range(3):
                        last = pe.matmul(ps[:, p, 0:D], tile[:, p, g, :], wo[:, g, :], start=False, stop=(g == 2))
                    last.then_inc(out_ready.sem, 1)

        @block.vector
        def _(dve):
            with dve.Fori(0, T // 2) as i:
                for p in range(2):
                    h = k.H[:, bass.ds(2 * i + p, 1), :]
                    dve.wait_ge(out_ready.sem, 2 * i + out_ready.after(p + 1))
                    dve.tensor_tensor(h, h, ps[:, p, 0:D], ALU.add).then_inc(out_added.sem, 1)
    for s in (ot_staged, out_ready, out_added):
        s.passed(T)


def temporal_tokens(k):
    nc, ps = k.nc, k.ps
    FR, B, N = 16, 4, 64
    SPAN = FR * B * N
    with ExitStack() as mem:
        sb = lambda name, shape: mem.enter_context(nc.sbuf_tensor(f"tok_{name}", shape, F32))
        xf = sb("x", [C + 1, NC, SPAN])
        wd, wu, bu = sb("down", [C + 1, NC, C]), sb("up", [C, D]), sb("up_bias", [P, D])
        conv = sb("conv", [C, 5])
        hd, y, sg = sb("down_out", [C, SPAN]), sb("y", [C, B, FR // 2, N]), sb("sigmoid", [C, TOK])
        z = sb("z", [P, T, C])
        zs, zt = sb("z_tile", [P, 2, C]), sb("z_tile_t", [C, 2, P])
        scratch = k.dram["scratch"]
        loaded = k.count("weights_loaded")
        chunk_loaded = [k.count(f"x_chunk_loaded{n}") for n in range(4)]
        down_in = k.count("down_in")
        down_ready = k.count("down_ready", 4)
        conv_ready = k.count("conv_ready")
        sigmoid_ready = k.count("sigmoid_ready")
        z_ready = k.count("z_ready")
        z_stored = k.count("z_stored")
        z_loaded = k.count("z_loaded")
        NB = SPAN // BANK
        with nc.Block() as block:
            @block.sync
            def _(sp):
                for dst, name in ((wd[:, :, :], "tok_down"), (conv[:, :], "tok_conv"), (wu[:, :], "tok_up"), (bu[:, :], "tok_up_bias")):
                    sp.dma_start(dst, k.dram[name]).then_inc(loaded.sem, 16)
                q = SPAN // 4
                for n in range(4):
                    sp.dma_start(xf[:, :, n * q:(n + 1) * q], k.dram["tok_x"][:, :, n * q:(n + 1) * q]).then_inc(chunk_loaded[n].sem, 16)
                sp.wait_ge(z_ready.sem, z_ready.after(1))
                sp.dma_start(scratch.rearrange("(p n) -> p n", p=C), sg[:, :]).then_inc(z_stored.sem, 16)
                sp.wait_ge(z_stored.sem, z_stored.after(16))
                sp.dma_start(z[:, :, :], scratch.rearrange("(t p f) -> p t f", p=P, f=C)).then_inc(z_loaded.sem, 16)
                sp.wait_ge(z_loaded.sem, z_loaded.after(16))

            @block.tensor
            def _(pe):
                pe.wait_ge(loaded.sem, loaded.after(64))
                for n in range(4):
                    pe.wait_ge(chunk_loaded[n].sem, chunk_loaded[n].after(16))
                    for b in range(NB // 4 * n, NB // 4 * (n + 1)):
                        pe.wait_ge(down_ready.sem, down_ready.room(b + 1))
                        for c in range(NC):
                            r = C + 1 - c
                            last = pe.matmul(ps[0:C, b % 4, :], wd[0:r, c, :], xf[0:r, c, b * BANK:(b + 1) * BANK],
                                             start=(c == 0), stop=(c == NC - 1))
                        last.then_inc(down_in.sem, 1)

            @block.scalar
            def _(act):
                for b in range(NB):
                    act.wait_ge(down_in.sem, down_in.after(b + 1))
                    act.copy(hd[:, b * BANK:(b + 1) * BANK], ps[0:C, b % 4, :]).then_inc(down_ready.sem, 1)
                act.wait_ge(conv_ready.sem, conv_ready.after(1))
                act.activation(sg[:, :], y[:, :, :, :], ACT.Sigmoid, scale=1.702).then_inc(sigmoid_ready.sem, 1)

            @block.vector
            def _(dve):
                link = lambda ins: k.dve(dve, ins)
                k.dve.start()
                dve.wait_ge(down_ready.sem, down_ready.after(NB))
                frames = hd[:, :].rearrange("p (n b t) -> p b t n", n=N, b=B)
                for b in range(B):
                    link(dve.tensor_scalar(y[:, b, :, :], frames[:, b, 0:FR:2, :], conv[:, 1:2], conv[:, 4:5], ALU.mult, ALU.add))
                    link(dve.scalar_tensor_tensor(y[:, b, :, :], frames[:, b, 1:FR:2, :], conv[:, 2:3], y[:, b, :, :], ALU.mult, ALU.add))
                    link(dve.scalar_tensor_tensor(y[:, b, 1:, :], frames[:, b, 1:FR - 2:2, :], conv[:, 0:1], y[:, b, 1:, :], ALU.mult, ALU.add))
                    link(dve.scalar_tensor_tensor(y[:, b, :-1, :], frames[:, b, 2:FR:2, :], conv[:, 3:4], y[:, b, :-1, :], ALU.mult, ALU.add))
                dve.sem_inc(conv_ready.sem, 1)
                dve.wait_ge(sigmoid_ready.sem, sigmoid_ready.after(1))
                dve.tensor_tensor(sg[:, :], sg[:, :], y[:, :, :, :].rearrange("p b f n -> p (b f n)"), ALU.mult).then_inc(z_ready.sem, 1)
                k.dve.end()
        loaded.passed(64)
        for s in chunk_loaded + [z_stored, z_loaded]:
            s.passed(16)
        for s in (conv_ready, sigmoid_ready, z_ready):
            s.passed(1)
        down_in.passed(NB)
        down_ready.passed(NB)

        z_staged = k.count("z_staged")
        z_turned = k.count("z_turned", 2)
        zt_ready = k.count("zt_ready", 2)
        up_in = k.count("up_in", 2)
        up_added = k.count("up_added", 2)
        with nc.Block() as block:
            @block.gpsimd
            def _(pool):
                with pool.Fori(0, T // 2) as i:
                    for p in range(2):
                        pool.wait_ge(z_turned.sem, 2 * i + z_turned.room(p + 1))
                        pool.tensor_copy(zs[:, p, :], z[:, bass.ds(2 * i + p, 1), :]).then_inc(z_staged.sem, 1)

            @block.tensor
            def _(pe):
                with pe.Fori(0, T // 2) as i:
                    for p in range(2):
                        pe.wait_ge(z_staged.sem, 2 * i + z_staged.after(p + 1))
                        pe.wait_ge(zt_ready.sem, 2 * i + zt_ready.room(p + 1))
                        pe.transpose(ps[0:C, p, 0:P], zs[:, p, :], k.ident[:, :]).then_inc(z_turned.sem, 1)
                    for p in range(2):
                        pe.wait_ge(zt_ready.sem, 2 * i + zt_ready.after(p + 1))
                        pe.wait_ge(up_added.sem, 2 * i + up_added.room(p + 1))
                        pe.matmul(ps[:, 2 + p, 0:D], zt[:, p, :], wu[:, :], start=True, stop=True).then_inc(up_in.sem, 1)

            @block.scalar
            def _(act):
                with act.Fori(0, T // 2) as i:
                    for p in range(2):
                        act.wait_ge(z_turned.sem, 2 * i + z_turned.after(p + 1))
                        act.wait_ge(up_in.sem, 2 * i + up_in.room(p + 1))
                        act.copy(zt[:, p, :], ps[0:C, p, 0:P]).then_inc(zt_ready.sem, 1)

            @block.vector
            def _(dve):
                with dve.Fori(0, T // 2) as i:
                    for p in range(2):
                        dve.wait_ge(up_in.sem, 2 * i + up_in.after(p + 1))
                        dve.tensor_tensor(k.H[:, bass.ds(2 * i + p, 1), :], ps[:, 2 + p, 0:D], bu[:, :], ALU.add).then_inc(up_added.sem, 1)
        for s in (z_staged, z_turned, zt_ready, up_in, up_added):
            s.passed(T)


QH, QS, QD = 8, 64, 32
KE = 3


def complex_memory(k):
    nc = k.nc
    with ExitStack() as mem:
        sb = lambda name, shape: mem.enter_context(nc.sbuf_tensor(f"a2_{name}", shape, F32))
        H1 = sb("h1", [P, T, D])
        p_tok = sb("p_tok", [P, T])
        with ExitStack() as inner:
            memory_read(k, inner, H1, p_tok)
        H2 = sb("h2", [P, T, D])
        with ExitStack() as inner:
            reasoning(k, inner, H1, H2, p_tok)
        with ExitStack() as inner:
            routed_experts(k, inner, H2)


def memory_read(k, mem, H1, p_tok):
    nc, ps = k.nc, k.ps
    sb = lambda name, shape: mem.enter_context(nc.sbuf_tensor(f"a2_{name}", shape, F32))
    NG = QH // 2
    wpz = sb("wpz", [C + 1, NC, QH * 16])
    wri = sb("wri", [C + 1, NC, NG, P])
    pw2, pb2 = sb("pw2", [P, QH, 16]), sb("pb2", [P, QH])
    m1, m2 = sb("m1", [P, NG, 2, 64]), sb("m2", [P, NG, 2, 64])
    vt, wout, wgate = sb("vt", [C, NC, 4, P]), sb("wout", [C, NC, D]), sb("wgate", [C, NC, 4, 16])
    ob, gb, pair = sb("ob", [1, D]), sb("gb", [1, QH]), sb("pair", [P, 2])
    xt, PZ = sb("xt", [C + 1, NC, TOK]), sb("pz", [P, T, QH, 16])
    load(k, [(wpz[:, :, :], "a2_wpz"), (wri[:, :, :, :], "a2_wri"), (pw2[:, :, :], "a2_pw2"), (pb2[:, :], "a2_pb2"),
             (m1[:, :, :, :], "a2_m1"), (m2[:, :, :, :], "a2_m2"), (vt[:, :, :, :], "a2_vt"), (wout[:, :, :], "a2_wout"),
             (wgate[:, :, :, :], "a2_wgate"), (ob[:, :], "a2_ob"), (gb[:, :], "a2_gb"), (pair[:, :], "a2_pair")])
    front(k, [(wpz, PZ[:, :, :, :].rearrange("p t h c -> p t (h c)"))], xt_big=xt, xn_big=H1)

    one_minus_p, p_share = sb("one_minus_p", [P, T, QH]), sb("p_share", [P, T, QH])
    mnorm, msq = sb("mnorm", [P, NG]), sb("msq", [P, NG, 64])
    MRI = sb("mri", [P, NG, P])
    VO, VG = sb("vo", [P, 4, D]), sb("vg", [P, 4, QH])
    silu_ready = k.count("silu_ready")
    p_in = k.count("p_in")
    p_ready = k.count("p_ready")
    slots_squared = k.count("slots_squared")
    norm2_ready = k.count("norm2_ready")
    norm_ready = k.count("norm_ready")
    slots_ready = k.count("slots_ready")
    slots_turned = k.count("slots_turned")
    folded = k.count("folded")
    with nc.Block() as block:
        @block.scalar
        def _(act):
            act.activation(PZ[:, :, :, :], PZ[:, :, :, :], ACT.Silu).then_inc(silu_ready.sem, 1)
            act.activation(msq[:, :, :], m1[:, :, 0, :], ACT.Square).then_inc(slots_squared.sem, 1)
            act.wait_ge(p_in.sem, p_in.after(1))
            act.activation(p_share[:, :, :], p_share[:, :, :], ACT.Sigmoid).then_inc(p_ready.sem, 1)
            act.wait_ge(norm2_ready.sem, norm2_ready.after(1))
            act.activation(mnorm[:, :], mnorm[:, :], ACT.Sqrt).then_inc(norm_ready.sem, 1)
            act.wait_ge(folded.sem, folded.after(1))
            for n in range(4):
                act.copy(VO[:, n, :], ps[:, 2 + n // 2, (n % 2) * D:(n % 2 + 1) * D])
            gates = ps[:, 4, 0:64].rearrange("p (n j g) -> p n j g", n=4, j=2)
            for j in range(2):
                act.copy(VG[64 * j:64 * j + 64, :, :], gates[64 * j:64 * j + 64, :, j, :])

        @block.vector
        def _(dve):
            link = lambda ins: k.dve(dve, ins)
            k.dve.start()
            dve.wait_ge(silu_ready.sem, silu_ready.after(1))
            link(dve.tensor_tensor(PZ[:, :, :, :], PZ[:, :, :, :], pw2[:, :, :].unsqueeze(1).broadcast_to([P, T, QH, 16]), ALU.mult))
            link(dve.tensor_reduce(p_share[:, :, :], PZ[:, :, :, :], AX.X, ALU.add))
            dve.tensor_tensor(p_share[:, :, :], p_share[:, :, :], pb2[:, :].unsqueeze(1).broadcast_to([P, T, QH]), ALU.add).then_inc(p_in.sem, 1)
            dve.wait_ge(slots_squared.sem, slots_squared.after(1))
            dve.tensor_reduce(mnorm[:, :], msq[:, :, :], AX.X, ALU.add).then_inc(norm2_ready.sem, 1)
            dve.wait_ge(p_ready.sem, p_ready.after(1))
            link(dve.tensor_scalar(p_share[:, :, :], p_share[:, :, :], 0.95, None, ALU.mult))
            link(dve.tensor_scalar(one_minus_p[:, :, :], p_share[:, :, :], -1.0, 1.0, ALU.mult, ALU.add))
            link(dve.tensor_reduce(p_tok[:, :], p_share[:, :, :], AX.X, ALU.add))
            link(dve.tensor_scalar(p_tok[:, :], p_tok[:, :], 1.0 / QH, None, ALU.mult))
            link(dve.tensor_scalar(p_share[:, :, :], p_share[:, :, :], 1.0 / QD, None, ALU.mult))
            dve.wait_ge(norm_ready.sem, norm_ready.after(1))
            link(dve.tensor_scalar(mnorm[:, :], mnorm[:, :], 1e-12, None, ALU.max))
            link(dve.reciprocal(mnorm[:, :], mnorm[:, :]))
            for m in (m1, m2):
                flat = m[:, :, :, :].rearrange("p g a d -> p g (a d)")
                link(dve.tensor_tensor(flat, flat, mnorm[:, :].unsqueeze(2).broadcast_to([P, NG, P]), ALU.mult))
            neg = m2[:, :, :, 0:QD]
            dve.tensor_scalar(neg, neg, -1.0, None, ALU.mult).then_inc(slots_ready.sem, 1)
            dve.wait_ge(slots_turned.sem, slots_turned.after(1))
            for n in range(2):
                for j in range(2):
                    rows = slice(64 * j, 64 * j + 64)
                    src = ps[rows, n, :].rearrange("p (g s) -> p g s", g=NG)[:, :, rows]
                    dve.tensor_copy(MRI[rows, :, 64 * n:64 * n + 64], src)
            k.dve.end()

        @block.tensor
        def _(pe):
            for n in range(4):
                for c in range(NC):
                    pe.matmul(ps[:, 2 + n // 2, (n % 2) * D:(n % 2 + 1) * D], vt[:, c, n, :], wout[:, c, :], start=(c == 0), stop=(c == NC - 1))
                for c in range(NC):
                    last = pe.matmul(ps[:, 4, 16 * n:16 * n + 16], vt[:, c, n, :], wgate[:, c, n, :], start=(c == 0), stop=(c == NC - 1))
            last.then_inc(folded.sem, 1)
            pe.wait_ge(slots_ready.sem, slots_ready.after(1))
            for n, m in enumerate((m1, m2)):
                for g in range(NG):
                    last = pe.transpose(ps[:, n, g * P:(g + 1) * P], m[:, g, :, :].rearrange("p a d -> p (a d)"), k.ident[:, :])
            last.then_inc(slots_turned.sem, 1)
    for s in (silu_ready, p_in, p_ready, slots_squared, norm2_ready, norm_ready, slots_ready, slots_turned, folded):
        s.passed(1)

    PP, SQ = sb("pp", [P, 2, NG, P]), sb("pp_squares", [P, 2, NG, P])
    OV = sb("overlap", [P, 2, QH, 2, QS])
    AT, ATT = sb("attn", [P, 2, QH, QS]), sb("attn_t", [P, 2, 4, P])
    al, rs, gt = sb("alpha", [P, 2, QH]), sb("row_sum", [P, 2, QH]), sb("gates", [P, 2, QH])
    st = sb("gate_stat", [P, 2])
    proj_in = k.count("proj_in")
    proj_ready = k.count("proj_ready")
    overlap_in = k.count("overlap_in")
    overlap_ready = k.count("overlap_ready")
    attn_ready = k.count("attn_ready")
    attn_turned = k.count("attn_turned")
    attn_t_ready = k.count("attn_t_ready")
    logits_in = k.count("logits_in")
    logits_shifted = k.count("logits_shifted")
    gates_exped = k.count("gates_exped")
    mix_in = k.count("mix_in")
    mix_added = k.count("mix_added", 2)
    with nc.Block() as block:
        @block.tensor
        def _(pe):
            with pe.Fori(0, T // 2) as i:
                def turn(p, which):
                    pe.wait_ge(attn_ready.sem, 4 * i + attn_ready.after(2 * which + p + 1))
                    flat = AT[:, p, :, :].rearrange("p h s -> p (h s)")
                    for n in range(4):
                        last = pe.transpose(ps[:, p, n * P:(n + 1) * P], flat[:, n * P:(n + 1) * P], k.ident[:, :])
                    last.then_inc(attn_turned.sem, 1)

                for p in range(2):
                    for g in range(NG):
                        for c in range(NC):
                            last = pe.matmul(ps[:, p, g * P:(g + 1) * P], wri[0:C, c, g, :], xt[0:C, c, bass.ds((2 * i + p) * P, P)],
                                             start=(c == 0), stop=(c == NC - 1))
                    last.then_inc(proj_in.sem, 1)
                for p in range(2):
                    pe.wait_ge(proj_ready.sem, 2 * i + proj_ready.after(p + 1))
                    pe.wait_ge(mix_added.sem, 2 * i + mix_added.room(p + 1))
                    for g in range(NG):
                        for j in range(2):
                            rows = slice(64 * j, 64 * j + 64)
                            pe.matmul(ps[:, 2 + 2 * p + j, g * P:(g + 1) * P], PP[rows, p, g, :], MRI[rows, g, :], start=True, stop=True)
                    for g in range(NG):
                        last = pe.matmul(ps[:, 6 + p, 2 * g:2 * g + 2], SQ[:, p, g, :], pair[:, :], start=True, stop=True)
                    last.then_inc(overlap_in.sem, 1)
                for p in range(2):
                    turn(p, 0)
                for p in range(2):
                    pe.wait_ge(attn_t_ready.sem, 4 * i + attn_t_ready.after(p + 1))
                    pe.matmul(ps[:, 6 + p, 8:16], k.ones[0:1, :], gb[0:1, :], start=True, stop=False)
                    for n in range(4):
                        last = pe.matmul(ps[:, 6 + p, 8:16], ATT[:, p, n, :], VG[:, n, :], start=False, stop=(n == 3))
                    last.then_inc(logits_in.sem, 1)
                for p in range(2):
                    turn(p, 1)
                for p in range(2):
                    pe.wait_ge(attn_t_ready.sem, 4 * i + attn_t_ready.after(2 + p + 1))
                    pe.matmul(ps[:, 6 + p, 16:16 + D], k.ones[0:1, :], ob[0:1, :], start=True, stop=False)
                    for n in range(4):
                        last = pe.matmul(ps[:, 6 + p, 16:16 + D], ATT[:, p, n, :], VO[:, n, :], start=False, stop=(n == 3))
                    last.then_inc(mix_in.sem, 1)

        @block.scalar
        def _(act):
            with act.Fori(0, T // 2) as i:
                def turned(p, which):
                    act.wait_ge(attn_turned.sem, 4 * i + attn_turned.after(2 * which + p + 1))
                    act.copy(ATT[:, p, :, :], ps[:, p, :]).then_inc(attn_t_ready.sem, 1)

                for p in range(2):
                    act.wait_ge(proj_in.sem, 2 * i + proj_in.after(p + 1))
                    act.copy(PP[:, p, :, :], ps[:, p, :])
                    act.activation(SQ[:, p, :, :], ps[:, p, :], ACT.Square).then_inc(proj_ready.sem, 1)
                for p in range(2):
                    act.wait_ge(overlap_in.sem, 2 * i + overlap_in.after(p + 1))
                    act.activation(OV[:, p, :, :, :].rearrange("p (j g) a s -> p j (g a s)", j=2), ps[:, 2 + 2 * p:4 + 2 * p, :],
                                   ACT.Square).then_inc(overlap_ready.sem, 1)
                for p in range(2):
                    turned(p, 0)
                for p in range(2):
                    act.wait_ge(logits_shifted.sem, 2 * i + logits_shifted.after(p + 1))
                    act.activation(gt[:, p, :], gt[:, p, :], ACT.Exp).then_inc(gates_exped.sem, 1)
                for p in range(2):
                    turned(p, 1)

        @block.vector
        def _(dve):
            link = lambda ins: k.dve(dve, ins)
            with dve.Fori(0, T // 2) as i:
                k.dve.start(i, 2 * (3 + 6 + 1 + 3))
                tile = lambda X, p: X[:, bass.ds(2 * i + p, 1), :].rearrange("p t h -> p (t h)")
                wide = lambda x: x.unsqueeze(2).broadcast_to([P, QH, QS])
                for p in range(2):
                    dve.wait_ge(overlap_in.sem, 2 * i + overlap_in.after(p + 1))
                    a, at = al[:, p, :], AT[:, p, :, :]
                    n2 = ps[:, 6 + p, 0:8].rearrange("p (g j) -> p j g", j=2)
                    link(dve.tensor_scalar(a.rearrange("p (j g) -> p j g", j=2), n2, 1e-24, None, ALU.max))
                    link(dve.reciprocal(a, a))
                    link(dve.tensor_tensor(a, a, tile(one_minus_p, p), ALU.mult))
                    dve.wait_ge(overlap_ready.sem, 2 * i + overlap_ready.after(p + 1))
                    link(dve.tensor_tensor(at, OV[:, p, :, 0, :], OV[:, p, :, 1, :], ALU.add))
                    link(dve.tensor_tensor(at, at, wide(a), ALU.mult))
                    link(dve.tensor_tensor(at, at, wide(tile(p_share, p)), ALU.add))
                    r = rs[:, p, :]
                    link(dve.tensor_reduce(r, at, AX.X, ALU.add))
                    link(dve.tensor_scalar(r, r, 1e-8, None, ALU.add))
                    link(dve.reciprocal(r, r))
                    dve.tensor_tensor(at, at, wide(r), ALU.mult).then_inc(attn_ready.sem, 1)
                for p in range(2):
                    dve.wait_ge(logits_in.sem, 2 * i + logits_in.after(p + 1))
                    link(dve.tensor_reduce(st[:, p:p + 1], ps[:, 6 + p, 8:16], AX.X, ALU.max))
                    dve.tensor_scalar(gt[:, p, :], ps[:, 6 + p, 8:16], st[:, p:p + 1], None, ALU.subtract).then_inc(logits_shifted.sem, 1)
                for p in range(2):
                    dve.wait_ge(gates_exped.sem, 2 * i + gates_exped.after(p + 1))
                    link(dve.tensor_reduce(st[:, p:p + 1], gt[:, p, :], AX.X, ALU.add))
                    link(dve.reciprocal(st[:, p:p + 1], st[:, p:p + 1]))
                    link(dve.tensor_scalar(gt[:, p, :], gt[:, p, :], st[:, p:p + 1], None, ALU.mult))
                    at = AT[:, p, :, :]
                    dve.tensor_tensor(at, at, wide(gt[:, p, :]), ALU.mult).then_inc(attn_ready.sem, 1)
                for p in range(2):
                    h = H1[:, bass.ds(2 * i + p, 1), :]
                    dve.wait_ge(mix_in.sem, 2 * i + mix_in.after(p + 1))
                    dve.tensor_tensor(h, h, ps[:, 6 + p, 16:16 + D], ALU.add).then_inc(mix_added.sem, 1)
            k.dve.end(T // 2)
    for s in (proj_in, proj_ready, overlap_in, overlap_ready, logits_in, logits_shifted, gates_exped, mix_in, mix_added):
        s.passed(T)
    for s in (attn_ready, attn_turned, attn_t_ready):
        s.passed(2 * T)


def reasoning(k, mem, H1, H2, p_tok):
    nc, ps = k.nc, k.ps
    sb = lambda name, shape: mem.enter_context(nc.sbuf_tensor(f"a2_{name}", shape, F32))
    wenc, wr, rb = sb("wenc", [C, NC, 64]), sb("wr", [64, D]), sb("rb", [P, D])
    PC, beta = sb("pc", [32, 4, 32]), sb("beta", [P, 1])
    sq, nrm, prod = sb("pc_sq", [32, 4, 32]), sb("pc_norm", [32, 2]), sb("pc_prod", [32, 4, 32])
    g_ = sb("g", [32, 4])
    A4, AB = sb("a4", [32, 4, 2, 32]), sb("ab", [64, P])
    q_tok = sb("q_tok", [P, T])
    load(k, [(wenc[:, :, :], "a2_wenc"), (wr[:, :], "a2_wr"), (rb[:, :], "a2_rb"), (PC[:, :, :], "a2_pc"), (beta[:, :], "a2_beta")])
    sigmoid_ready = k.count("sigmoid_ready")
    norm2_ready, norm_ready = k.count("norm2_ready"), k.count("norm_ready")
    with nc.Block() as block:
        @block.scalar
        def _(act):
            act.activation(beta[:, :], beta[:, :], ACT.Sigmoid).then_inc(sigmoid_ready.sem, 1)
            act.wait_ge(norm2_ready.sem, norm2_ready.after(1))
            act.activation(nrm[:, :], nrm[:, :], ACT.Sqrt).then_inc(norm_ready.sem, 1)

        @block.vector
        def _(dve):
            link = lambda ins: k.dve(dve, ins)
            k.dve.start()
            dve.tensor_scalar(q_tok[:, :], p_tok[:, :], -1.0, 1.0, ALU.mult, ALU.add)
            link(dve.tensor_tensor(sq[:, :, :], PC[:, :, :], PC[:, :, :], ALU.mult))
            dve.tensor_reduce(nrm[:, :], sq[:, :, :].rearrange("p (x a) d -> p x (a d)", x=2), AX.X, ALU.add).then_inc(norm2_ready.sem, 1)
            dve.wait_ge(norm_ready.sem, norm_ready.after(1))
            link(dve.tensor_scalar(nrm[:, :], nrm[:, :], 1e-12, None, ALU.max))
            link(dve.reciprocal(nrm[:, :], nrm[:, :]))
            both = PC[:, :, :].rearrange("p (x a) d -> p x (a d)", x=2)
            link(dve.tensor_tensor(both, both, nrm[:, :].unsqueeze(2).broadcast_to([32, 2, 64]), ALU.mult))
            Pr, Pi, Cr, Ci = (PC[:, n, :] for n in range(4))
            for n, (a, b) in enumerate(((Pr, Cr), (Pi, Ci), (Pr, Ci), (Pi, Cr))):
                link(dve.tensor_tensor(prod[:, n, :], a, b, ALU.mult))
            link(dve.tensor_reduce(g_[:, :], prod[:, :, :], AX.X, ALU.add))
            link(dve.tensor_tensor(g_[:, 0:1], g_[:, 0:1], g_[:, 1:2], ALU.add))
            link(dve.tensor_tensor(g_[:, 1:2], g_[:, 2:3], g_[:, 3:4], ALU.subtract))
            g_re, g_im = g_[:, 0:1], g_[:, 1:2]
            X, Y = A4[:, 0, 0, :], A4[:, 0, 1, :]
            link(dve.tensor_scalar(prod[:, 0, :], Pi, g_im, None, ALU.mult))
            link(dve.tensor_scalar(prod[:, 1, :], Pr, g_im, None, ALU.mult))
            link(dve.scalar_tensor_tensor(X, Pr, g_re, prod[:, 0, :], ALU.mult, ALU.subtract))
            link(dve.scalar_tensor_tensor(Y, Pi, g_re, prod[:, 1, :], ALU.mult, ALU.add))
            link(dve.tensor_copy(A4[:, 1, 0, :], Y))
            link(dve.tensor_scalar(A4[:, 1, 1, :], X, -1.0, None, ALU.mult))
            link(dve.tensor_copy(A4[:, 2, 0, :], Cr))
            link(dve.tensor_copy(A4[:, 2, 1, :], Ci))
            link(dve.tensor_copy(A4[:, 3, 0, :], Ci))
            link(dve.tensor_scalar(A4[:, 3, 1, :], Cr, -1.0, None, ALU.mult))
            for half in range(2):
                link(dve.transpose(AB[32 * half:32 * half + 32, :].rearrange("p (v s) -> p v s", v=4), A4[:, :, half, :]))
            k.dve.end()
            dve.wait_ge(sigmoid_ready.sem, sigmoid_ready.after(1))
    for s in (sigmoid_ready, norm2_ready, norm_ready):
        s.passed(1)

    Hs, HT = sb("h_tile", [P, 2, D]), sb("h_tile_t", [C, 2, NC, P])
    E, ES = sb("enc", [64, 2, P]), sb("enc_sq", [64, 2, P])
    CP, CT, cs = sb("coupling", [P, 2, 32]), sb("coupling_t", [P, 2, P]), sb("coupling_stat", [P, 2, 8])
    R, F, M, FT = sb("r", [P, 2, P]), sb("feats", [P, 2, P]), sb("feat_products", [P, 2, P]), sb("feats_t", [64, 2, P])
    RE = sb("reason", [P, 2, D])
    h_staged = k.count("h_staged")
    h_turned = k.count("h_turned", 2)
    ht_ready = k.count("ht_ready")
    coupled = k.count("coupled")
    enc_ready = k.count("enc_ready")
    shifted = k.count("coupling_shifted")
    exped = k.count("coupling_exped")
    ct_ready = k.count("coupling_t_ready")
    sums_in = k.count("sums_in")
    r_ready = k.count("r_ready")
    feats_ready = k.count("feats_ready")
    feats_turned = k.count("feats_turned")
    ft_ready = k.count("ft_ready")
    reason_in = k.count("reason_in")
    h2_ready = k.count("h2_ready", 2)
    with nc.Block() as block:
        @block.gpsimd
        def _(pool):
            with pool.Fori(0, T // 2) as i:
                for p in range(2):
                    pool.wait_ge(h2_ready.sem, 2 * i + h2_ready.room(p + 1))
                    pool.tensor_copy(Hs[:, p, :], H1[:, bass.ds(2 * i + p, 1), :]).then_inc(h_staged.sem, 1)

        @block.tensor
        def _(pe):
            with pe.Fori(0, T // 2) as i:
                for p in range(2):
                    pe.wait_ge(h_staged.sem, 2 * i + h_staged.after(p + 1))
                    for c in range(NC):
                        last = pe.transpose(ps[0:C, p, c * P:(c + 1) * P], Hs[:, p, c * C:(c + 1) * C], k.ident[:, :])
                    last.then_inc(h_turned.sem, 1)
                for p in range(2):
                    pe.wait_ge(ht_ready.sem, 2 * i + ht_ready.after(p + 1))
                    for c in range(NC):
                        pe.matmul(ps[:, 2 + p, 0:P], HT[:, p, c, :], HT[:, p, c, :], start=(c == 0), stop=(c == NC - 1))
                    for c in range(NC):
                        last = pe.matmul(ps[0:64, 4 + p, 0:P], wenc[:, c, :], HT[:, p, c, :], start=(c == 0), stop=(c == NC - 1))
                    last.then_inc(coupled.sem, 1)
                for p in range(2):
                    pe.wait_ge(enc_ready.sem, 2 * i + enc_ready.after(p + 1))
                    pe.wait_ge(ct_ready.sem, 2 * i + ct_ready.after(p + 1))
                    pe.matmul(ps[:, 4 + p, P:2 * P], E[:, p, :], AB[:, :], start=True, stop=True)
                    pe.matmul(ps[:, 4 + p, 2 * P:2 * P + 1], ES[:, p, :], k.ones[0:64, 0:1], start=True, stop=True)
                    pe.matmul(ps[:, 4 + p, 2 * P + 1:2 * P + 2], CT[:, p, :], q_tok[:, bass.ds(2 * i + p, 1)],
                              start=True, stop=True).then_inc(sums_in.sem, 1)
                for p in range(2):
                    pe.wait_ge(feats_ready.sem, 2 * i + feats_ready.after(p + 1))
                    pe.transpose(ps[:, 6 + p, 0:P], F[:, p, :], k.ident[:, :]).then_inc(feats_turned.sem, 1)
                for p in range(2):
                    pe.wait_ge(ft_ready.sem, 2 * i + ft_ready.after(p + 1))
                    pe.matmul(ps[:, 6 + p, P:P + D], FT[:, p, :], wr[:, :], start=True, stop=True).then_inc(reason_in.sem, 1)

        @block.scalar
        def _(act):
            with act.Fori(0, T // 2) as i:
                for p in range(2):
                    act.wait_ge(h_turned.sem, 2 * i + h_turned.after(p + 1))
                    act.copy(HT[:, p, :, :], ps[0:C, p, 0:2 * P]).then_inc(ht_ready.sem, 1)
                for p in range(2):
                    act.wait_ge(coupled.sem, 2 * i + coupled.after(p + 1))
                    act.copy(E[:, p, :], ps[0:64, 4 + p, 0:P])
                    act.activation(ES[:, p, :], ps[0:64, 4 + p, 0:P], ACT.Square).then_inc(enc_ready.sem, 1)
                for p in range(2):
                    act.wait_ge(shifted.sem, 2 * i + shifted.after(p + 1))
                    act.activation(CP[:, p, :], CP[:, p, :], ACT.Exp, scale=float(D) ** -0.5).then_inc(exped.sem, 1)
                for p in range(2):
                    act.wait_ge(sums_in.sem, 2 * i + sums_in.after(p + 1))
                    act.copy(R[:, p, :], ps[:, 4 + p, P:2 * P])
                    act.copy(cs[:, p, 4:6], ps[:, 4 + p, 2 * P:2 * P + 2]).then_inc(r_ready.sem, 1)
                for p in range(2):
                    act.wait_ge(feats_turned.sem, 2 * i + feats_turned.after(p + 1))
                    act.copy(FT[:, p, :], ps[0:64, 6 + p, 0:P]).then_inc(ft_ready.sem, 1)

        @block.vector
        def _(dve):
            link = lambda ins: k.dve(dve, ins)
            k.dve.start()
            dve.memset(F[:, :, 64:P], 0.0)
            link(dve.memset(CT[:, :, :], 0.0))
            k.dve.end()
            with dve.Fori(0, T // 2) as i:
                k.dve.start(i, 2 * (2 + 1 + 9 + 2))
                for p in range(2):
                    dve.wait_ge(coupled.sem, 2 * i + coupled.after(p + 1))
                    cp = CP[:, p, :]
                    for b in range(4):
                        rows = slice(32 * b, 32 * b + 32)
                        last = dve.tensor_copy(CP[rows, p, :], ps[rows, 2 + p, rows])
                    link(last)
                    link(dve.tensor_reduce(cs[:, p, 0:1], cp, AX.X, ALU.max))
                    dve.tensor_scalar(cp, cp, cs[:, p, 0:1], None, ALU.subtract).then_inc(shifted.sem, 1)
                for p in range(2):
                    dve.wait_ge(exped.sem, 2 * i + exped.after(p + 1))
                    link(dve.tensor_reduce(cs[:, p, 1:2], CP[:, p, :], AX.X, ALU.add))
                    for b in range(4):
                        rows = slice(32 * b, 32 * b + 32)
                        last = dve.transpose(CT[rows, p, rows], CP[rows, p, :])
                    last.then_inc(ct_ready.sem, 1)
                for p in range(2):
                    dve.wait_ge(r_ready.sem, 2 * i + r_ready.after(p + 1))
                    c_ = lambda n: cs[:, p, n:n + 1]
                    link(dve.reciprocal(c_(1), c_(1)))
                    link(dve.tensor_scalar(c_(2), c_(5), c_(1), beta[:, :], ALU.mult, ALU.mult))
                    link(dve.tensor_scalar(c_(2), c_(2), -1.0, 1.0, ALU.mult, ALU.add))
                    link(dve.tensor_tensor(c_(2), c_(2), p_tok[:, bass.ds(2 * i + p, 1)], ALU.mult))
                    link(dve.tensor_scalar(c_(2), c_(2), 0.0, 0.95, ALU.max, ALU.min))
                    link(dve.tensor_scalar(c_(2), c_(2), -1.0, 1.0, ALU.mult, ALU.add))
                    link(dve.tensor_scalar(c_(3), c_(4), 1e-24, None, ALU.max))
                    link(dve.reciprocal(c_(3), c_(3)))
                    t = R[:, p, 0:64].rearrange("p (v s) -> p v s", v=2)
                    by = lambda n: R[:, p, 32 * n:32 * n + 32].unsqueeze(1).broadcast_to([P, 2, 32])
                    mm = lambda n: M[:, p, 64 * n:64 * n + 64].rearrange("p (v s) -> p v s", v=2)
                    dve.tensor_tensor(mm(0), t, by(2), ALU.mult)
                    link(dve.tensor_tensor(mm(1), t, by(3), ALU.mult))
                    dve.tensor_tensor(F[:, p, 0:32], M[:, p, 0:32], M[:, p, 96:128], ALU.add)
                    dve.tensor_tensor(F[:, p, 32:64], M[:, p, 32:64], M[:, p, 64:96], ALU.subtract).then_inc(feats_ready.sem, 1)
                for p in range(2):
                    dve.wait_ge(reason_in.sem, 2 * i + reason_in.after(p + 1))
                    re = RE[:, p, :]
                    link(dve.scalar_tensor_tensor(re, ps[:, 6 + p, P:P + D], cs[:, p, 3:4], rb[:, :], ALU.mult, ALU.add))
                    link(dve.tensor_scalar(re, re, cs[:, p, 2:3], None, ALU.mult))
                    dve.tensor_tensor(H2[:, bass.ds(2 * i + p, 1), :], re, Hs[:, p, :], ALU.add).then_inc(h2_ready.sem, 1)
            k.dve.end(T // 2)
    for s in (h_staged, h_turned, ht_ready, coupled, enc_ready, shifted, exped, ct_ready, sums_in, r_ready, feats_ready,
              feats_turned, ft_ready, reason_in, h2_ready):
        s.passed(T)


def routed_experts(k, mem, H2):
    nc, ps = k.nc, k.ps
    sb = lambda name, shape: mem.enter_context(nc.sbuf_tensor(f"a2_{name}", shape, F32))
    W1 = KE * D
    NR = 16
    cut = 2 * D
    w1a, w1b = sb("w1a", [C + 1, NC, cut]), sb("w1b", [C + 1, NC, D + NR])
    eg, ebt = sb("eg", [P, KE, D]), sb("ebt", [P, KE, D])
    w2, b2 = sb("ew2", [C, 2 * KE, D]), sb("eb2", [KE, D])
    rw2, rb2 = sb("rw2", [P, KE, NR]), sb("rb2", [P, KE])
    X, R = sb("x", [P, T, W1]), sb("router_in", [P, T, D + NR])
    load(k, [(w1a[:, :, :], "a2_w1a"), (w1b[:, :, :], "a2_w1b"), (eg[:, :, :], "a2_eg"), (ebt[:, :, :], "a2_ebt"),
             (w2[:, :, :], "a2_w2"), (b2[:, :], "a2_b2"), (rw2[:, :, :], "a2_rw2"), (rb2[:, :], "a2_rb2")])
    front(k, [(w1a, X[:, :, 0:cut]), (w1b, R[:, :, :])], src=H2)
    Y = sb("y", [P, 4, KE, D])
    stat, rg, rstat = sb("estat", [P, T, KE]), sb("rg", [P, T, KE]), sb("rstat", [P, T])
    prod = sb("rprod", [P, T, KE, NR])
    squared = k.count("x_squared")
    var_ready, std_ready = k.count("var_ready"), k.count("std_ready")
    centred = k.count("x_centred")
    normed = k.count("x_normed")
    gelu_ready = k.count("gelu_ready")
    router_in = k.count("router_ready")
    scores_ready, exps_ready = k.count("scores_ready"), k.count("exps_ready")
    NQ = T // 4
    with nc.Block() as block:
        @block.scalar
        def _(act):
            act.activation(R[:, :, D:D + NR], R[:, :, D:D + NR], ACT.Gelu).then_inc(router_in.sem, 1)
            for n in range(NQ):
                act.wait_ge(centred.sem, centred.after(n + 1))
                act.activation(Y[:, :, :, :], X[:, 4 * n:4 * n + 4, :], ACT.Square).then_inc(squared.sem, 1)
            act.wait_ge(scores_ready.sem, scores_ready.after(1))
            act.activation(rg[:, :, :], rg[:, :, :], ACT.Exp).then_inc(exps_ready.sem, 1)
            act.wait_ge(var_ready.sem, var_ready.after(1))
            act.activation(stat[:, :, :], stat[:, :, :], ACT.Sqrt).then_inc(std_ready.sem, 1)
            for n in range(NQ):
                act.wait_ge(normed.sem, normed.after(n + 1))
                x = X[:, 4 * n:4 * n + 4, :]
                act.activation(x, x, ACT.Gelu).then_inc(gelu_ready.sem, 1)

        @block.vector
        def _(dve):
            link = lambda ins: k.dve(dve, ins)
            k.dve.start()
            link(dve.tensor_copy(X[:, :, cut:W1], R[:, :, 0:D]))
            as4 = lambda n: X[:, 4 * n:4 * n + 4, :].rearrange("p t (e d) -> p (t e) d", e=KE)
            st = lambda n: stat[:, 4 * n:4 * n + 4, :].rearrange("p t e -> p (t e)")
            wide = lambda x: x.unsqueeze(2).broadcast_to([P, 4 * KE, D])
            for n in range(NQ):
                link(dve.tensor_reduce(st(n), as4(n), AX.X, ALU.add))
                link(dve.tensor_scalar(st(n), st(n), 1.0 / D, None, ALU.mult))
                dve.tensor_tensor(as4(n), as4(n), wide(st(n)), ALU.subtract).then_inc(centred.sem, 1)
                dve.wait_ge(squared.sem, squared.after(n + 1))
                link(dve.tensor_reduce(st(n), Y[:, :, :, :].rearrange("p t e d -> p (t e) d"), AX.X, ALU.add))
            dve.wait_ge(router_in.sem, router_in.after(1))
            full = [P, T, KE, NR]
            link(dve.tensor_tensor(prod[:, :, :, :], R[:, :, D:D + NR].unsqueeze(2).broadcast_to(full),
                                   rw2[:, :, :].unsqueeze(1).broadcast_to(full), ALU.mult))
            link(dve.tensor_reduce(rg[:, :, :], prod[:, :, :, :], AX.X, ALU.add))
            link(dve.tensor_tensor(rg[:, :, :], rg[:, :, :], rb2[:, :].unsqueeze(1).broadcast_to([P, T, KE]), ALU.add))
            link(dve.tensor_reduce(rstat[:, :], rg[:, :, :], AX.X, ALU.max))
            rw = rstat[:, :].unsqueeze(2).broadcast_to([P, T, KE])
            dve.tensor_tensor(rg[:, :, :], rg[:, :, :], rw, ALU.subtract).then_inc(scores_ready.sem, 1)
            dve.tensor_scalar(stat[:, :, :], stat[:, :, :], 1.0 / D, EPS, ALU.mult, ALU.add).then_inc(var_ready.sem, 1)
            dve.wait_ge(exps_ready.sem, exps_ready.after(1))
            link(dve.tensor_reduce(rstat[:, :], rg[:, :, :], AX.X, ALU.add))
            link(dve.reciprocal(rstat[:, :], rstat[:, :]))
            link(dve.tensor_tensor(rg[:, :, :], rg[:, :, :], rw, ALU.mult))
            dve.wait_ge(std_ready.sem, std_ready.after(1))
            link(dve.reciprocal(stat[:, :, :], stat[:, :, :]))
            for n in range(NQ):
                x4 = X[:, 4 * n:4 * n + 4, :]
                link(dve.tensor_tensor(as4(n), as4(n), wide(st(n)), ALU.mult))
                by = lambda w: w[:, :, :].rearrange("p e d -> p (e d)").unsqueeze(1).broadcast_to([P, 4, W1])
                link(dve.tensor_tensor(x4, x4, by(eg), ALU.mult))
                dve.tensor_tensor(x4, x4, by(ebt), ALU.add).then_inc(normed.sem, 1)
            for n in range(NQ):
                dve.wait_ge(gelu_ready.sem, gelu_ready.after(n + 1))
                rgn = rg[:, 4 * n:4 * n + 4, :].rearrange("p t e -> p (t e)")
                dve.tensor_tensor(as4(n), as4(n), wide(rgn), ALU.mult)
            k.dve.end()
    for s in (var_ready, std_ready, router_in, scores_ready, exps_ready):
        s.passed(1)
    for s in (squared, centred, normed, gelu_ready):
        s.passed(NQ)

    G, RG = sb("g_tile", [P, 2, W1]), sb("rg_tile", [P, 2, KE])
    GT, RT = sb("g_tile_t", [C, 2, 2 * KE, P]), sb("rg_tile_t", [KE, 2, P])
    staged = k.count("g_staged")
    turned = k.count("g_turned", 2)
    gt_ready = k.count("gt_ready")
    y_in = k.count("y_in")
    y_added = k.count("y_added", 2)
    with nc.Block() as block:
        @block.gpsimd
        def _(pool):
            with pool.Fori(0, T // 2) as i:
                for p in range(2):
                    pool.wait_ge(turned.sem, 2 * i + turned.room(p + 1))
                    pool.tensor_copy(G[:, p, :], X[:, bass.ds(2 * i + p, 1), :])
                    pool.tensor_copy(RG[:, p, :], rg[:, bass.ds(2 * i + p, 1), :]).then_inc(staged.sem, 1)

        @block.tensor
        def _(pe):
            with pe.Fori(0, T // 2) as i:
                for p in range(2):
                    pe.wait_ge(staged.sem, 2 * i + staged.after(p + 1))
                    for c in range(2 * KE):
                        pe.transpose(ps[0:C, 2 * p + c // 4, (c % 4) * P:(c % 4 + 1) * P], G[:, p, c * C:(c + 1) * C], k.ident[:, :])
                    pe.transpose(ps[0:KE, 2 * p + 1, 3 * P:4 * P], RG[:, p, :], k.ident[:, :]).then_inc(turned.sem, 1)
                for p in range(2):
                    pe.wait_ge(gt_ready.sem, 2 * i + gt_ready.after(p + 1))
                    pe.wait_ge(y_added.sem, 2 * i + y_added.room(p + 1))
                    pe.matmul(ps[:, 4 + p, 0:D], RT[:, p, :], b2[:, :], start=True, stop=False)
                    for c in range(2 * KE):
                        last = pe.matmul(ps[:, 4 + p, 0:D], GT[:, p, c, :], w2[:, c, :], start=False, stop=(c == 2 * KE - 1))
                    last.then_inc(y_in.sem, 1)

        @block.scalar
        def _(act):
            with act.Fori(0, T // 2) as i:
                for p in range(2):
                    act.wait_ge(turned.sem, 2 * i + turned.after(p + 1))
                    act.copy(GT[:, p, 0:4, :], ps[0:C, 2 * p, :])
                    act.copy(GT[:, p, 4:6, :], ps[0:C, 2 * p + 1, 0:2 * P])
                    act.copy(RT[:, p, :], ps[0:KE, 2 * p + 1, 3 * P:4 * P]).then_inc(gt_ready.sem, 1)

        @block.vector
        def _(dve):
            with dve.Fori(0, T // 2) as i:
                k.dve.start(i, 2)
                for p in range(2):
                    h = k.H[:, bass.ds(2 * i + p, 1), :]
                    k.dve(dve, dve.tensor_tensor(h, h, H2[:, bass.ds(2 * i + p, 1), :], ALU.add))
                    dve.wait_ge(y_in.sem, 2 * i + y_in.after(p + 1))
                    dve.tensor_tensor(h, h, ps[:, 4 + p, 0:D], ALU.add).then_inc(y_added.sem, 1)
            k.dve.end(T // 2)
    for s in (staged, turned, gt_ready, y_in, y_added):
        s.passed(T)


def finish(k, out):
    stored = k.count("output_stored")
    with k.nc.Block() as block:
        @block.sync
        def _(sp):
            sp.dma_start(out, k.H[:, :, :]).then_inc(stored.sem, 16)
            sp.wait_ge(stored.sem, stored.after(16))


def build(nc, dram, out):
    with ExitStack() as ctx:
        k = Core(nc, ctx, dram)
        k.all_primed = [k.count(n, c) for n, c in PRIMED.items()]
        begin(k)
        temporal_tokens(k)
        cosine_attention(k)
        moe(k, "f0", 8, 768, "argmax", 1, ACT.Gelu, bias2=True)
        rotary_attention(k)
        causal_mixture(k)
        complex_memory(k)
        moe(k, "f2", 8, 512, "balanced", 2, ACT.Silu)
        transport_attention(k)
        moe(k, "f3", 5, 256, "top", 2, ACT.Silu, gated=True)
        finish(k, out)


def by_chunk(w, bias=None):
    n = w.shape[1]
    a = np.zeros((C + 1, NC, n), np.float32)
    a[:C] = w.reshape(NC, C, n).transpose(1, 0, 2)
    if bias is not None:
        a[C, 0] = bias
    return a


def rows(a):
    a = np.asarray(a)
    return np.ascontiguousarray(np.broadcast_to(a[None], (P,) + a.shape))


def pad_heads(w):
    a = np.zeros(w.shape[:-1] + (HEADS, HP), np.float32)
    a[..., :16] = w.reshape(w.shape[:-1] + (HEADS, 16))
    return a.reshape(w.shape[:-1] + (HW,))


def expert_rows(w):
    E, F, _ = w.shape
    return w.reshape(E, F // P, P, D).transpose(2, 0, 1, 3)


def expert_chunks(w, bias=None):
    return np.stack([by_chunk(w[e], None if bias is None else bias[e]) for e in range(w.shape[0])], 1)


def head_rows(w):
    n = w.shape[1]
    return pad_heads(w.T).T.reshape(3, P, n).transpose(1, 0, 2)


def layouts(i):
    a = {"identity": np.eye(P, dtype=np.float32)}
    for E in (3, 5, 8):
        a[f"lower{E}"] = rows(np.tril(np.ones((E, E), np.float32), -1).reshape(E * E))
    a["f0_router"] = by_chunk(i["L0_ffn_gate_w"], i["L0_ffn_gate_b"])
    a["f0_w1"] = expert_chunks(i["L0_ffn_w1"], i["L0_ffn_b1"])
    a["f0_w2"] = expert_rows(i["L0_ffn_w2"])
    a["f0_b2"] = rows(i["L0_ffn_b2"])
    a["f2_router"] = by_chunk(i["L2_ffn_router_w"].T)
    a["f2_w1"] = expert_chunks(i["L2_ffn_w1"].transpose(0, 2, 1))
    a["f2_w2"] = expert_rows(i["L2_ffn_w2"].transpose(0, 2, 1))
    a["f3_router"] = by_chunk(i["L3_ffn_router_w"].T, i["L3_ffn_router_b"])
    a["f3_w1"] = expert_chunks(i["L3_ffn_gate_w"])
    a["f3_up"] = expert_chunks(i["L3_ffn_up_w"])
    a["f3_w2"] = expert_rows(i["L3_ffn_down_w"])
    w, b = i["L1_attn_qkv_w"].T, i["L1_attn_qkv_b"]
    swap = np.arange(D) ^ 1
    parts = [(0, slice(None)), (0, swap), (1, slice(None)), (1, swap)]
    a["a1_wqk"] = np.stack([by_chunk(pad_heads(w[:, m * D:(m + 1) * D][:, s]), pad_heads(b[m * D:(m + 1) * D][s])) for m, s in parts], 2)
    a["a1_wv"] = by_chunk(pad_heads(w[:, 2 * D:]), pad_heads(b[2 * D:]))
    a["a1_wo"] = head_rows(i["L1_attn_proj_w"].T)
    a["a1_bo"] = i["L1_attn_proj_b"][None]
    freq = (1.0 / np.float32(10000.0) ** (np.arange(0, 16, 2, dtype=np.float32) / 16)).astype(np.float32)
    angle = freq[:, None] * np.arange(32, dtype=np.float32)[None]
    cos, sin = np.zeros((4, 32, 32), np.float32), np.zeros((4, 32, 32), np.float32)
    cos[:, 0:16:2] = cos[:, 1:16:2] = np.cos(angle)
    sin[:, 0:16:2], sin[:, 1:16:2] = -np.sin(angle), np.sin(angle)
    a["a1_turn"] = np.stack([cos.reshape(P, 32), sin.reshape(P, 32)], 1)
    a["f1_wqk"] = by_chunk(i["L1_ffn_Wqk"], i["L1_ffn_bqk"])
    wv = i["L1_ffn_Wv"].transpose(1, 0, 2).reshape(D, D)
    a["f1_wvg"] = by_chunk(np.concatenate([wv, i["L1_ffn_Wg1"]], 1), np.concatenate([i["L1_ffn_bv"].reshape(D), i["L1_ffn_bg1"]]))
    a["f1_wo"] = i["L1_ffn_Wp"].reshape(3, 64, D).transpose(1, 0, 2)
    a["f1_bo"] = i["L1_ffn_bp"][None]
    a["f1_conv"] = np.concatenate([i["L1_ffn_conv_w"][:, 0, :], i["L1_ffn_conv_b"][:, None]], 1)
    query = np.arange(P)[:, None] % 32
    key = np.arange(32)[None]
    a["f1_mask"] = np.repeat(np.where(key > query, np.float32(-1e30), np.float32(0))[:, None], 3, 1)
    pos = np.zeros((P, 3, 32), np.float32)
    pos[:, 2] = np.tile(i["L1_ffn_pos_bias"][:32, :32], (4, 1))
    a["f1_pos"] = pos
    a["f1_wg2"] = rows(i["L1_ffn_Wg2"].T)
    a["f1_bg2"] = rows(i["L1_ffn_bg2"])
    order = np.arange(8).reshape(4, 2).T.reshape(8)
    chunk4 = lambda x: x.reshape((NC, C) + x.shape[1:]).swapaxes(0, 1)
    a["a2_wpz"] = by_chunk(i["L2_attn_pw1"][order].reshape(128, D).T, i["L2_attn_pb1"][order].reshape(128))
    ri = np.concatenate([i["L2_attn_W_real"], i["L2_attn_W_imag"]], 2).transpose(1, 0, 2).reshape(D, 512)
    a["a2_wri"] = by_chunk(ri).reshape(C + 1, NC, 4, P)
    a["a2_pw2"], a["a2_pb2"] = rows(i["L2_attn_pw2"][order]), rows(i["L2_attn_pb2"][order])
    for n, parts in (("a2_m1", ("m_real", "m_imag")), ("a2_m2", ("m_imag", "m_real"))):
        mm = np.concatenate([i[f"L2_attn_{x}"] for x in parts], 2)
        mm = mm.reshape(4, 2 * 64, 64).transpose(1, 0, 2)
        a[n] = np.repeat(mm[:, :, None], 2, 2)
    vals = i["L2_attn_values"][order].reshape(512, D).T
    a["a2_vt"] = chunk4(vals.reshape(D, 4, P))
    a["a2_wout"], a["a2_ob"] = chunk4(i["L2_attn_out_w"].T), i["L2_attn_out_b"][None]
    gw = i["L2_attn_gate_w"].reshape(8, 8, D)[order][:, order]
    a["a2_wgate"] = chunk4(gw.transpose(2, 1, 0).reshape(D, 4, 16))
    a["a2_gb"] = i["L2_attn_gate_b"][order][None]
    a["a2_pair"] = (np.arange(P)[:, None] // 64 == np.arange(2)[None]).astype(np.float32)
    a["a2_wenc"] = chunk4(np.concatenate([i["L2_attn_enc_r_w"], i["L2_attn_enc_i_w"]], 0).T)
    a["a2_wr"], a["a2_rb"] = i["L2_attn_r_out_w"].T, rows(i["L2_attn_r_out_b"])
    a["a2_pc"] = np.stack([i[f"L2_attn_{x}"] for x in ("P_real", "P_imag", "C_real", "C_imag")], 1)
    a["a2_beta"] = np.broadcast_to(i["L2_attn_beta"].reshape(1, 1), (P, 1))
    w1 = i["L2_attn_ew1"].transpose(2, 0, 1).reshape(D, 3 * D)
    b1 = i["L2_attn_eb1"].reshape(3 * D)
    a["a2_w1a"] = by_chunk(w1[:, :2 * D], b1[:2 * D])
    a["a2_w1b"] = by_chunk(np.concatenate([w1[:, 2 * D:], i["L2_attn_rw1"].T], 1), np.concatenate([b1[2 * D:], i["L2_attn_rb1"]]))
    a["a2_eg"], a["a2_ebt"] = rows(i["L2_attn_eg"]), rows(i["L2_attn_ebt"])
    a["a2_w2"] = i["L2_attn_ew2"].transpose(0, 2, 1).reshape(6, C, D).transpose(1, 0, 2)
    a["a2_b2"] = i["L2_attn_eb2"]
    a["a2_rw2"], a["a2_rb2"] = rows(i["L2_attn_rw2"]), rows(i["L2_attn_rb2"])
    a["tok_x"] = by_chunk(i["x"].reshape(4096, D).T)
    a["tok_x"][C, 0] = 1.0
    a["tok_down"] = by_chunk(i["L0_tok_w_down"], i["L0_tok_b_down"])
    a["tok_up"] = i["L0_tok_w_up"]
    a["tok_up_bias"] = rows(i["L0_tok_b_up"])
    a["tok_conv"] = np.concatenate([i["L0_tok_w_conv"][:, 0, :], i["L0_tok_b_conv"][:, None]], 1)
    w, b = i["L0_attn_in_proj_weight"].T, i["L0_attn_in_proj_bias"]
    a["a0_w"] = np.stack([by_chunk(pad_heads(w[:, m * D:(m + 1) * D]), pad_heads(b[m * D:(m + 1) * D])) for m in range(3)], 2)
    a["a0_wo"], a["a0_bo"] = head_rows(i["L0_attn_out_w"].T), i["L0_attn_out_b"][None]
    a["a0_log_scale"] = rows(i["L0_attn_logit_scale"][:, 0, 0])
    a["a0_head_scale"] = rows(i["L0_attn_head_scale"][:, 0, 0])
    w = i["L3_attn_w_qkv"].T
    a["a3_wq"], a["a3_wv"] = by_chunk(pad_heads(w[:, 0:D])), by_chunk(pad_heads(w[:, 2 * D:]))
    a["a3_wo"], a["a3_bo"] = head_rows(i["L3_attn_w_proj"].T), i["L3_attn_b_proj"][None]
    a["eye32"] = (key == query).astype(np.float32)
    a["off32"] = (key != query).astype(np.float32)
    a["blocks32"] = (np.arange(P)[:, None] // 32 == np.arange(P)[None] // 32).astype(np.float32)
    return {n: np.ascontiguousarray(v) for n, v in a.items()}


PRIMED = {"xn_transposed": U, "xt_spread": U, "projection_read": 2, "hidden_ready": 4, "expert_out": 8,
          "expert_added": 4, "gate_ready": 2,
          "scores_out": 2, "probs_ready": 2, "pv_done": 2, "ot_ready": 1, "out_added": 1, "qk_ready": 1,
          "keys_ready": 1, "qn_turned": 2, "qt_ready": 2, "qkv_in": 2, "tile_projected": 2,
          "tile_added": 2, "down_ready": 4, "z_turned": 2, "zt_ready": 2, "up_in": 2, "up_added": 2, "mix_added": 2,
          "h_turned": 2, "h2_ready": 2, "g_turned": 2, "y_added": 2}


def kernel(**inputs):
    from concourse import bacc
    from concourse.bass_utils import run_bass_kernel_spmd

    nc = bacc.Bacc("TRN2", target_bir_lowering=False, num_devices=1)
    arrays = {f"in_{n}": a for n, a in layouts({n: np.asarray(v) for n, v in inputs.items()}).items()}
    dram = {n[3:]: nc.dram_tensor(n, a.shape, F32, kind="ExternalInput").ap() for n, a in arrays.items()}
    dram["scratch"] = nc.dram_tensor("scratch", (C * TOK,), F32, kind="Internal").ap()
    out = nc.dram_tensor("out", (P, T, D), F32, kind="ExternalOutput").ap()
    build(nc, dram, out)
    r = run_bass_kernel_spmd(nc, [arrays], core_ids=[0])
    return np.ascontiguousarray(r.results[0]["out"].transpose(1, 0, 2).reshape(64, 32, D))
```

```python
from contextlib import ExitStack

import numpy as np

import concourse.bass as bass
from concourse import mybir
from concourse.alu_op_type import AluOpType as ALU

F32 = mybir.dt.float32
ACT = mybir.ActivationFunctionType
AX = mybir.AxisListType

P = 128
D = 192
C = 96
NC = D // C
TOK = 2048
T = TOK // P
U = 4
BANK = 512
HEADS = 12
HP = 32
HW = HEADS * HP
EPS = 1e-5


class Count:

    def __init__(self, nc, ctx, name, primed=0):
        self.sem = ctx.enter_context(nc.semaphore(name))
        self.primed, self.base = primed, 0

    def after(self, n):
        return self.base + self.primed + n

    def room(self, n):
        return self.base + n

    def passed(self, n):
        self.base += n


class Chain:

    def __init__(self, nc, ctx, name):
        self.sem = ctx.enter_context(nc.semaphore(name))
        self.base, self.turn, self.per, self.steps = 0, 0, 0, 0

    def start(self, turn=0, per=0):
        self.turn, self.per, self.steps = turn, per, 0

    def __call__(self, eng, ins):
        self.steps += 1
        ins.then_inc(self.sem, 1)
        eng.wait_ge(self.sem, self.turn * self.per + (self.base + self.steps))

    def apart(self, eng, ins):
        self(eng, ins)
        self.steps += 1
        eng.sem_inc(self.sem, 1)

    def end(self, turns=1):
        if turns > 1:
            assert self.steps == self.per, (self.steps, self.per)
        self.base += turns * self.steps


class Core:

    def __init__(self, nc, ctx, dram):
        self.nc, self.ctx, self.dram = nc, ctx, dram
        self.counts = {}
        self.buffers = 0
        self.H = self.keep("residual", [P, T, D])
        self.ident = self.keep("identity", [P, P])
        self.ones = self.keep("ones", [P, P])
        self.ps = ctx.enter_context(nc.psum_tensor("psum", [P, 8, BANK], F32))
        self.dve, self.act, self.pool = (Chain(nc, ctx, f"{e}_step_done") for e in ("vector", "scalar", "gpsimd"))

    def keep(self, name, shape):
        return self.ctx.enter_context(self.nc.sbuf_tensor(name, shape, F32))

    def buffer(self, mem, name, shape):
        self.buffers += 1
        return mem.enter_context(self.nc.sbuf_tensor(f"{name}_{self.buffers}", shape, F32))

    def count(self, name, primed=0):
        if name not in self.counts:
            self.counts[name] = Count(self.nc, self.ctx, name, primed)
        assert self.counts[name].primed == primed
        return self.counts[name]


def load(k, pairs):
    loaded = k.count("weights_loaded")
    with k.nc.Block() as block:
        @block.sync
        def _(sp):
            for n, (dst, name) in enumerate(pairs):
                sp.dma_start(dst, k.dram[name]).then_inc(loaded.sem, 16)
            sp.wait_ge(loaded.sem, loaded.after(16 * len(pairs)))
    loaded.passed(16 * len(pairs))


def begin(k):
    nc = k.nc
    loaded = k.count("weights_loaded")
    with nc.Block() as block:
        @block.sync
        def _(sp):
            sp.dma_start(k.ident[:, :], k.dram["identity"]).then_inc(loaded.sem, 16)
            for s in k.all_primed:
                sp.sem_inc(s.sem, s.primed)
            sp.wait_ge(loaded.sem, loaded.after(16))

        @block.gpsimd
        def _(pool):
            pool.memset(k.ones[:, :], 1.0)
    loaded.passed(16)


def front(k, outs, xt_big=None, xn_big=None, src=None, loads=(), first=0):
    nc, ps = k.nc, k.ps
    norm = src is None
    loaded = k.count("weights_loaded")
    rest_loaded = k.count("rest_loaded")
    xn_ready = k.count("xn_ready")
    var_ready = k.count("var_ready")
    std_ready = k.count("std_ready")
    xn_transposed = k.count("xn_transposed", U)
    xt_ready = k.count("xt_ready")
    xt_spread = k.count("xt_spread", U)
    projected = k.count("projected")
    projection_read = k.count("projection_read", 2)
    with ExitStack() as mem:
        XN = k.buffer(mem, "xn_tiles", [P, U, D])
        XT = k.buffer(mem, "xt_tiles", [C + 1, U, NC, P])
        stats = k.buffer(mem, "bn_stats", [P, T, 6])
        mv = k.buffer(mem, "mean_var", [P, T, 2])
        rstd = k.buffer(mem, "rstd", [P, T])
        spreads = xt_big is not None or xn_big is not None
        with nc.Block() as block:
            @block.sync
            def _(sp):
                for n, (dst, name) in enumerate(loads):
                    sp.dma_start(dst, k.dram[name]).then_inc((loaded if n < first else rest_loaded).sem, 16)
                if first:
                    sp.wait_ge(loaded.sem, loaded.after(16 * first))
                if len(loads) > first:
                    sp.wait_ge(rest_loaded.sem, rest_loaded.after(16 * (len(loads) - first)))

            @block.vector
            def _(dve):
                dve.memset(XT[C:C + 1, :, :, :], 1.0).then_inc(k.dve.sem, 1)
                dve.wait_ge(k.dve.sem, k.dve.base + 1)
                k.dve.base += 1
                if norm:
                    k.dve.start()
                    for t in range(T):
                        last = dve.bn_stats(stats[:, t, :], k.H[:, t, :])
                    k.dve(dve, last)
                    for t in range(T):
                        last = dve.bn_aggr(mv[:, t, :], stats[:, t, :])
                    k.dve(dve, last)
                    dve.tensor_scalar(rstd[:, :], mv[:, :, 1], EPS, None, ALU.add).then_inc(var_ready.sem, 1)
                    dve.wait_ge(std_ready.sem, std_ready.after(1))
                    k.dve(dve, dve.reciprocal(rstd[:, :], rstd[:, :]))
                    k.dve.end()
                with dve.Fori(0, T // U) as i:
                    for u in range(U):
                        dve.wait_ge(xn_transposed.sem, i * U + xn_transposed.room(u + 1))
                        if xn_big is not None:
                            dve.wait_ge(xt_spread.sem, i * U + xt_spread.room(u + 1))
                        x = (k.H if norm else src)[:, bass.ds(i * U + u, 1), :]
                        if norm:
                            last = dve.tensor_scalar(XN[:, u, :], x, mv[:, bass.ds(i * U + u, 1), 0], rstd[:, bass.ds(i * U + u, 1)],
                                                     ALU.subtract, ALU.mult)
                        else:
                            last = dve.tensor_copy(XN[:, u, :], x)
                        last.then_inc(xn_ready.sem, 1)

            @block.tensor
            def _(pe):
                with pe.Fori(0, T // U) as i:
                    for u in range(U):
                        pe.wait_ge(xn_ready.sem, i * U + xn_ready.after(u + 1))
                        for c in range(NC):
                            last = pe.transpose(ps[0:C, u // 2, (2 * (u % 2) + c) * P:(2 * (u % 2) + c + 1) * P],
                                                XN[:, u, c * C:(c + 1) * C], k.ident[:, :])
                        last.then_inc(xn_transposed.sem, 1)
                    if not outs:
                        pe.wait_ge(xt_ready.sem, i * (U // 2) + xt_ready.after(U // 2))
                    for u in range(U):
                        if not outs:
                            break
                        if u == 0 and first:
                            pe.wait_ge(loaded.sem, loaded.after(16 * first))
                        if u % 2 == 0:
                            pe.wait_ge(xt_ready.sem, i * (U // 2) + xt_ready.after(u // 2 + 1))
                        pe.wait_ge(projection_read.sem, i * U + projection_read.room(u + 1))
                        for n, (w, dst) in enumerate(outs):
                            width = dst.shape[2]
                            for c in range(NC):
                                r = C + 1 - c
                                last = pe.matmul(ps[:, 2 + 2 * (u % 2) + n, 0:width], XT[0:r, u, c, :],
                                                 w[0:r, c, :], start=(c == 0), stop=(c == NC - 1))
                        last.then_inc(projected.sem, 1)

            @block.scalar
            def _(act):
                if norm:
                    act.wait_ge(var_ready.sem, var_ready.after(1))
                    act.activation(rstd[:, :], rstd[:, :], ACT.Sqrt).then_inc(std_ready.sem, 1)
                with act.Fori(0, T // U) as i:
                    for h in range(U // 2):
                        act.wait_ge(xn_transposed.sem, i * U + xn_transposed.after(2 * h + 2))
                        if spreads:
                            act.wait_ge(xt_spread.sem, i * U + xt_spread.room(2 * h + 2))
                        act.copy(XT[0:C, 2 * h:2 * h + 2, :, :], ps[0:C, h, :]).then_inc(xt_ready.sem, 1)
                    for u in range(U):
                        if not outs:
                            break
                        act.wait_ge(projected.sem, i * U + projected.after(u + 1))
                        for n, (w, dst) in enumerate(outs):
                            width = dst.shape[2]
                            last = act.copy(dst[:, bass.ds(i * U + u, 1), :], ps[:, 2 + 2 * (u % 2) + n, 0:width])
                        last.then_inc(projection_read.sem, 1)

            @block.gpsimd
            def _(pool):
                if not spreads:
                    return
                if xt_big is not None:
                    k.pool.start()
                    k.pool(pool, pool.memset(xt_big[C:C + 1, :, :], 1.0))
                    k.pool.end()
                with pool.Fori(0, T // U) as i:
                    for u in range(U):
                        if xn_big is not None:
                            pool.wait_ge(xn_ready.sem, i * U + xn_ready.after(u + 1))
                            last = pool.tensor_copy(xn_big[:, bass.ds(i * U + u, 1), :], XN[:, u, :])
                        if xt_big is not None:
                            pool.wait_ge(xt_ready.sem, i * (U // 2) + xt_ready.after(u // 2 + 1))
                            last = pool.tensor_copy(xt_big[0:C, :, bass.ds((i * U + u) * P, P)], XT[0:C, u, :, :])
                        last.then_inc(xt_spread.sem, 1)
    loaded.passed(16 * first)
    rest_loaded.passed(16 * (len(loads) - first))
    if norm:
        var_ready.passed(1)
        std_ready.passed(1)
    xn_ready.passed(T)
    xn_transposed.passed(T)
    xt_ready.passed(T // 2)
    if spreads:
        xt_spread.passed(T)
    if outs:
        projected.passed(T)
        projection_read.passed(T)


class Router:

    def __init__(self, k, L, E, kind, mem, lower=None, top=1, bank=0):
        self.k, self.L, self.E, self.kind, self.lower, self.top, self.bank = k, L, E, kind, lower, top, bank
        self.scores_ready = k.count("scores_ready")
        self.exps_ready = k.count("exps_ready")
        self.load_ready = k.count("load_ready")
        self.load_summed = k.count("load_summed")
        self.load_used = k.count("load_used")
        self.st = k.buffer(mem, "route_stat", [P, T])
        self.beats = k.buffer(mem, "route_beats", [P, T, E, E])
        self.ties = k.buffer(mem, "route_ties", [P, T, E, E])
        self.sel = k.buffer(mem, "route_selected", [P, T, E])
        self.load_e = k.buffer(mem, "route_load", [P, E])
        self.passes = 2 if kind == "softmax_top" else 1

    def vector(self, dve):
        k, L, E, kind, top = self.k, self.L, self.E, self.kind, self.top
        st, beats, ties, sel, load_e = self.st, self.beats, self.ties, self.sel, self.load_e
        per_token = [P, T, E]
        pair = [P, T, E, E]
        row = lambda a: a[:, :].unsqueeze(2).broadcast_to(per_token)
        link = lambda ins: k.dve(dve, ins)
        k.dve.start()

        def normalise(W):
            link(dve.tensor_reduce(st[:, :], W, AX.X, ALU.add))
            link(dve.reciprocal(st[:, :], st[:, :]))
            link(dve.tensor_tensor(W, W, row(st), ALU.mult))

        link(dve.tensor_reduce(st[:, :], L, AX.X, ALU.max))
        dve.tensor_tensor(L, L, row(st), ALU.subtract).then_inc(self.scores_ready.sem, 1)
        dve.wait_ge(self.exps_ready.sem, self.exps_ready.after(1))
        normalise(L)
        if kind == "balanced":
            dve.tensor_reduce(load_e[:, :], L.rearrange("p t e -> p e t"), AX.X, ALU.add).then_inc(self.load_ready.sem, 1)
        link(dve.tensor_tensor(beats[:, :, :, :], L.unsqueeze(2).broadcast_to(pair),
                               L.unsqueeze(3).broadcast_to(pair), ALU.is_gt))
        link(dve.tensor_tensor(ties[:, :, :, :], L.unsqueeze(2).broadcast_to(pair),
                               L.unsqueeze(3).broadcast_to(pair), ALU.is_equal))
        tri = self.lower[:, 0:E * E].rearrange("p (e j) -> p e j", e=E).unsqueeze(1).broadcast_to(pair)
        link(dve.tensor_tensor(ties[:, :, :, :], ties[:, :, :, :], tri, ALU.mult))
        link(dve.tensor_tensor(beats[:, :, :, :], beats[:, :, :, :], ties[:, :, :, :], ALU.add))
        link(dve.tensor_reduce(sel[:, :, :], beats[:, :, :, :], AX.X, ALU.add))
        if kind == "argmax":
            link(dve.tensor_scalar(L, sel[:, :, :], float(top), None, ALU.is_lt))
            return k.dve.end()
        link(dve.tensor_scalar(sel[:, :, :], sel[:, :, :], float(top), None, ALU.is_lt))
        if kind == "balanced":
            dve.wait_ge(self.load_summed.sem, self.load_summed.after(1))
            dve.tensor_scalar(load_e[:, :], self.k.ps[:, self.bank, 0:E], -1.0, 1.0 - 0.9, ALU.add, ALU.mult).then_inc(self.load_used.sem, 1)
            dve.wait_ge(self.load_used.sem, self.load_used.after(1))
            link(dve.tensor_scalar(load_e[:, :], load_e[:, :], 1.0, 0.01, ALU.add, ALU.add))
            link(dve.reciprocal(load_e[:, :], load_e[:, :]))
            link(dve.tensor_tensor(L, L, load_e[:, :].unsqueeze(1).broadcast_to(per_token), ALU.mult))
        if kind == "softmax_top":
            link(dve.tensor_reduce(st[:, :], L, AX.X, ALU.max))
            dve.tensor_tensor(L, L, row(st), ALU.subtract).then_inc(self.scores_ready.sem, 1)
            dve.wait_ge(self.exps_ready.sem, self.exps_ready.after(2))
        link(dve.tensor_tensor(L, L, sel[:, :, :], ALU.mult))
        normalise(L)
        k.dve.end()

    def scalar(self, act):
        for n in range(self.passes):
            act.wait_ge(self.scores_ready.sem, self.scores_ready.after(n + 1))
            act.activation(self.L, self.L, ACT.Exp).then_inc(self.exps_ready.sem, 1)

    def tensor(self, pe):
        if self.kind == "balanced":
            pe.wait_ge(self.load_ready.sem, self.load_ready.after(1))
            pe.matmul(self.k.ps[:, self.bank, 0:self.E], self.k.ones[:, :], self.load_e[:, :], start=True,
                      stop=True).then_inc(self.load_summed.sem, 1)

    def finished(self):
        self.scores_ready.passed(self.passes)
        self.exps_ready.passed(self.passes)
        if self.kind == "balanced":
            for s in (self.load_ready, self.load_summed, self.load_used):
                s.passed(1)


def experts(k, E, F, xt, w1, w2, W, func, router, w1_up=None, b2=None):
    nc, ps = k.nc, k.ps
    NF = F // P
    G = TOK // BANK
    J = BANK // P
    hidden_in = k.count("hidden_in")
    hidden_ready = k.count("hidden_ready", 4)
    expert_out = k.count("expert_out", 2 * J)
    expert_added = k.count("expert_added", J)
    gate_ready = k.count("gate_ready", 2)
    per_chunk = 1 if w1_up is None else 2
    ring = 4 // per_chunk
    with ExitStack() as mem:
        hid = k.buffer(mem, "hidden", [P, 2, NF, BANK])
        gate = k.buffer(mem, "gate", [P, 2, BANK]) if w1_up is not None else None
        with nc.Block() as block:
            @block.tensor
            def _(pe):
                router.tensor(pe)
                with pe.Fori(0, G) as g:
                    def first(e):
                        for f in range(NF):
                            n = e * NF + f
                            pe.wait_ge(hidden_ready.sem, g * (E * NF) + (hidden_ready.base + hidden_ready.primed - ring + n + 1))
                            for m, w in enumerate((w1,) if w1_up is None else (w1, w1_up)):
                                for c in range(NC):
                                    r = C + 1 - c
                                    last = pe.matmul(ps[:, (n % ring) * per_chunk + m, :], w[0:r, e, c, f * P:(f + 1) * P],
                                                     xt[0:r, c, bass.ds(g * BANK, BANK)], start=(c == 0), stop=(c == NC - 1))
                            last.then_inc(hidden_in.sem, 1)

                    def second(e):
                        pe.wait_ge(hidden_ready.sem, g * (E * NF) + hidden_ready.after((e + 1) * NF))
                        for j in range(J):
                            if router.kind == "balanced" and e == 0 and 4 + j == router.bank:
                                pe.wait_ge(router.load_used.sem, router.load_used.after(1))
                            pe.wait_ge(expert_added.sem, g * (E * J) + expert_added.room(e * J + j + 1))
                            for f in range(NF):
                                last = pe.matmul(ps[:, 4 + j, 0:D], hid[:, e % 2, f, j * P:(j + 1) * P], w2[:, e, f, :],
                                                 start=(f == 0), stop=(f == NF - 1))
                            last.then_inc(expert_out.sem, 1)

                    first(0)
                    for e in range(E):
                        if e + 1 < E:
                            first(e + 1)
                        second(e)

            @block.scalar
            def _(act):
                router.scalar(act)
                with act.Fori(0, G) as g:
                    for e in range(E):
                        if w1_up is None:
                            act.wait_ge(expert_out.sem, g * (E * J) + expert_out.room((e + 1) * J))
                        for f in range(NF):
                            n = e * NF + f
                            act.wait_ge(hidden_in.sem, g * (E * NF) + hidden_in.after(n + 1))
                            if w1_up is None:
                                act.activation(hid[:, e % 2, f, :], ps[:, n % ring, :], func).then_inc(hidden_ready.sem, 1)
                            else:
                                act.wait_ge(hidden_ready.sem, g * (E * NF) + (hidden_ready.base + hidden_ready.primed - 2 + n + 1))
                                act.activation(gate[:, n % 2, :], ps[:, (n % ring) * 2, :], func).then_inc(gate_ready.sem, 1)

            @block.vector
            def _(dve):
                router.vector(dve)
                with dve.Fori(0, G) as g:
                    def up(e):
                        dve.wait_ge(expert_out.sem, g * (E * J) + expert_out.room((e + 1) * J))
                        for f in range(NF):
                            n = e * NF + f
                            dve.wait_ge(gate_ready.sem, g * (E * NF) + gate_ready.after(n + 1))
                            dve.tensor_tensor(hid[:, e % 2, f, :], gate[:, n % 2, :], ps[:, (n % ring) * 2 + 1, :],
                                              ALU.mult).then_inc(hidden_ready.sem, 1)

                    def add(e):
                        for j in range(J):
                            t = g * J + j
                            h = k.H[:, bass.ds(t, 1), :]
                            dve.wait_ge(expert_added.sem, g * (E * J) + expert_added.room(e * J + j + 1))
                            if b2 is not None:
                                k.dve(dve, dve.scalar_tensor_tensor(h, b2[:, e, :], W[:, bass.ds(t, 1), e:e + 1], h, ALU.mult, ALU.add))
                            dve.wait_ge(expert_out.sem, g * (E * J) + expert_out.after(e * J + j + 1))
                            dve.scalar_tensor_tensor(h, ps[:, 4 + j, 0:D], W[:, bass.ds(t, 1), e:e + 1], h, ALU.mult,
                                                     ALU.add).then_inc(expert_added.sem, 1)
                    k.dve.start(g, E * J if b2 is not None else 0)
                    if w1_up is not None:
                        up(0)
                    for e in range(E):
                        if w1_up is not None and e + 1 < E:
                            up(e + 1)
                        add(e)
                k.dve.end(G)
    hidden_in.passed(G * E * NF)
    hidden_ready.passed(G * E * NF)
    expert_out.passed(G * E * J)
    expert_added.passed(G * E * J)
    if w1_up is not None:
        gate_ready.passed(G * E * NF)


def moe(k, tag, E, F, kind, top, func, gated=False, bias2=False):
    nc = k.nc
    with ExitStack() as mem:
        sb = lambda name, shape: mem.enter_context(nc.sbuf_tensor(f"{tag}_{name}", shape, F32))
        router, w1, w2 = sb("router", [C + 1, NC, E]), sb("w1", [C + 1, E, NC, F]), sb("w2", [P, E, F // P, D])
        up = sb("up", [C + 1, E, NC, F]) if gated else None
        b2 = sb("b2", [P, E, D]) if bias2 else None
        lower = sb("lower", [P, E * E])
        pairs = [(router[:, :, :], f"{tag}_router"), (w1[:, :, :, :], f"{tag}_w1"), (w2[:, :, :, :], f"{tag}_w2"), (lower[:, :], f"lower{E}")]
        if gated:
            pairs.append((up[:, :, :, :], f"{tag}_up"))
        if bias2:
            pairs.append((b2[:, :, :], f"{tag}_b2"))
        xt = sb("xt", [C + 1, NC, TOK])
        W = sb("weights", [P, T, E])
        front(k, [(router, W)], xt_big=xt, loads=pairs, first=1)
        chooser = Router(k, W[:, :, :], E, kind, mem, lower, top, bank=7)
        experts(k, E, F, xt, w1, w2, W, func, chooser, w1_up=up, b2=b2)
        chooser.finished()


def diagonal_blocks(ps, bank, NJ, L, eng_copy, dst_of, blocks):
    for b in blocks:
        rows = slice(b * L, (b + 1) * L)
        src = ps[rows, bank:bank + NJ, 0:3 * P].rearrange("p j (g m) -> p j g m", m=P)[:, :, :, b * L:(b + 1) * L]
        dst = dst_of(rows)
        if NJ == 1:
            src = src[:, 0, :, :]
        else:
            dst = dst.rearrange("p (j g) m -> p j g m", j=NJ)
        last = eng_copy(dst, src)
    return last


def in_turns(eng, depth, step, link=None, steps=0):
    late = depth - 1

    def call(i, newest, first=False, last=False):
        tiles = [newest - n for n in range(depth)]
        step(i, *(None if (first and n < 0) or (last and n > 1) else n for n in tiles))

    if link:
        link.start()
    for n in range(late):
        call(0, n, first=True)
    if link:
        link.end()
    turns = (T - late) // 2
    with eng.Fori(0, turns) as i:
        if link:
            link.start(i, 2 * steps)
        for n in range(2):
            call(i, late + n)
    if link:
        link.end(turns)
        link.start()
    end = T // 2 - 1
    for n in range(2 * turns + late - 2 * end, 2 + late):
        call(end, n, last=True)
    if link:
        link.end()


class Attention:

    G = 3

    def __init__(self, k, mem, tag, NJ, M, L, scale, values, wo=None, bo=None, ot_big=None, mask=None, head_w=None,
                 score_bank=4, out_bank=0):
        self.k, self.NJ, self.M, self.L, self.scale, self.values = k, NJ, M, L, scale, values
        self.S, self.mask, self.head_w = NJ * self.G, mask, head_w
        self.wo, self.bo, self.ot_big, self.score_bank, self.out_bank = wo, bo, ot_big, score_bank, out_bank
        sb = lambda name, shape: mem.enter_context(k.nc.sbuf_tensor(f"{tag}_{name}", shape, F32))
        S = self.S
        self.SC = sb("scores", [P, 2, S, L])
        self.PT = sb("probs_t", [P, 2, S, P])
        self.V = sb("values", [P, 2, S * M])
        self.OT = sb("out_t", [NJ * M, 2, self.G, P])
        self.stat = sb("row_stat", [P, 2, S])
        self.scores_in = k.count("scores_in")
        self.scores_out = k.count("scores_out", 2)
        self.shifted = k.count("shifted")
        self.exped = k.count("exped")
        self.probs_ready = k.count("probs_ready", 2)
        self.v_staged = k.count("v_staged")
        self.pv_done = k.count("pv_done", 2)
        self.ot_ready = k.count("ot_ready", 1)
        self.out_ready = k.count("out_ready")
        self.out_added = k.count("out_added", 1)

    def finished(self, n=T, scores=True, staged=True):
        for s in (self.exped, self.probs_ready, self.pv_done, self.ot_ready):
            s.passed(n)
        if staged:
            self.v_staged.passed(n)
        if scores:
            self.scores_in.passed(n)
            self.shifted.passed(n)
            self.scores_out.passed(2 * n)
        if self.wo is not None:
            self.out_ready.passed(n)
            self.out_added.passed(n)

    def zero(self, dve):
        self.k.dve.start()
        self.k.dve(dve, dve.memset(self.PT[:, :, :, :], 0.0))
        self.k.dve.end()

    def _blocks(self, eng_copy, p, blocks):
        dst = lambda rows: self.SC[rows, p % 2, :, :]
        diagonal_blocks(self.k.ps, self.score_bank, self.NJ, self.L, eng_copy, dst, blocks).then_inc(self.scores_out.sem, 1)

    def act_extract(self, act, i, p):
        half = range(0, P // self.L // 2)
        act.wait_ge(self.scores_in.sem, 2 * i + self.scores_in.after(p + 1))
        act.wait_ge(self.probs_ready.sem, 2 * i + self.probs_ready.room(p + 1))
        self._blocks(act.copy, p, half)

    def dve_extract(self, dve, i, p):
        half = range(P // self.L // 2, P // self.L)
        dve.wait_ge(self.scores_in.sem, 2 * i + self.scores_in.after(p + 1))
        self._blocks(dve.tensor_copy, p, half)

    SHIFT_STEPS, PROB_STEPS = 1, 3

    def dve_shift(self, dve, i, p):
        k, sc = self.k, self.SC[:, p % 2, :, :]
        dve.wait_ge(self.scores_out.sem, 4 * i + self.scores_out.after(2 * p + 2))
        if self.mask is not None:
            k.dve(dve, dve.scalar_tensor_tensor(sc, sc, self.scale, self.mask[:, :, :], ALU.mult, ALU.add))
        st = self.stat[:, p % 2, :]
        k.dve(dve, dve.tensor_reduce(st, sc, AX.X, ALU.max))
        dve.tensor_tensor(sc, sc, st.unsqueeze(2).broadcast_to([P, self.S, self.L]), ALU.subtract).then_inc(self.shifted.sem, 1)

    def act_exp(self, act, i, p):
        act.wait_ge(self.shifted.sem, 2 * i + self.shifted.after(p + 1))
        sc = self.SC[:, p % 2, :, :]
        act.activation(sc, sc, ACT.Exp, scale=1.0 if self.mask is not None else self.scale).then_inc(self.exped.sem, 1)

    def dve_probs(self, dve, i, p):
        k, L, sc, st = self.k, self.L, self.SC[:, p % 2, :, :], self.stat[:, p % 2, :]
        dve.wait_ge(self.exped.sem, 2 * i + self.exped.after(p + 1))
        k.dve(dve, dve.tensor_reduce(st, sc, AX.X, ALU.add))
        k.dve(dve, dve.reciprocal(st, st))
        if self.head_w is not None:
            k.dve(dve, dve.tensor_tensor(st, st, self.head_w[:, bass.ds(2 * i + p, 1), :], ALU.mult))
        k.dve(dve, dve.tensor_tensor(sc, sc, st.unsqueeze(2).broadcast_to([P, self.S, L]), ALU.mult))
        dve.wait_ge(self.pv_done.sem, 2 * i + self.pv_done.room(p + 1))
        n = L // 32
        for b in range(P // L):
            for r in range(n):
                for c in range(n):
                    rows = slice(b * L + 32 * r, b * L + 32 * r + 32)
                    out_rows = slice(b * L + 32 * c, b * L + 32 * c + 32)
                    last = dve.transpose(self.PT[out_rows, p % 2, :, b * L + 32 * r:b * L + 32 * r + 32],
                                         self.SC[rows, p % 2, :, 32 * c:32 * c + 32])
        last.then_inc(self.probs_ready.sem, 1)

    def pool_values(self, pool, i, p):
        pool.wait_ge(self.pv_done.sem, 2 * i + self.pv_done.room(p + 1))
        pool.tensor_copy(self.V[:, p % 2, :], self.values[:, bass.ds(2 * i + p, 1), :]).then_inc(self.v_staged.sem, 1)

    def pe_values(self, pe, i, p):
        k, M = self.k, self.M
        if self.values is not None:
            pe.wait_ge(self.v_staged.sem, 2 * i + self.v_staged.after(p + 1))
        pe.wait_ge(self.probs_ready.sem, 2 * i + self.probs_ready.after(p + 1))
        pe.wait_ge(self.ot_ready.sem, 2 * i + self.ot_ready.room(p + 1))
        for g in range(self.G):
            for j in range(self.NJ):
                h = self.NJ * g + j
                last = pe.matmul(k.ps[j * M:(j + 1) * M, self.out_bank, g * P:(g + 1) * P], self.V[:, p % 2, h * M:(h + 1) * M],
                                 self.PT[:, p % 2, j * self.G + g, :], start=True, stop=True)
        last.then_inc(self.pv_done.sem, 1)

    def act_out(self, act, i, p):
        act.wait_ge(self.pv_done.sem, 2 * i + self.pv_done.after(p + 1))
        src = self.k.ps[0:self.NJ * self.M, self.out_bank, 0:self.G * P]
        if self.ot_big is not None:
            src = src.rearrange("p (g n l) -> p g n l", g=self.G, l=self.L)
            dst = self.ot_big[:, :, :].rearrange("p g (l n) -> p g n l", l=self.L)
            n = P // self.L
            for g in range(self.G):
                last = act.copy(dst[:, g, bass.ds((2 * i + p) * n, n), :], src[:, g, :, :])
            last.then_inc(self.ot_ready.sem, 1)
            return
        act.copy(self.OT[:, p % 2, :, :], src).then_inc(self.ot_ready.sem, 1)

    def pe_project(self, pe, i, p):
        k = self.k
        pe.wait_ge(self.ot_ready.sem, 2 * i + self.ot_ready.after(p + 1))
        pe.wait_ge(self.out_added.sem, 2 * i + self.out_added.room(p + 1))
        dst = k.ps[:, self.out_bank + 1, 0:D]
        pe.matmul(dst, k.ones[0:1, :], self.bo[0:1, :], start=True, stop=False)
        for g in range(self.G):
            last = pe.matmul(dst, self.OT[:, p % 2, g, :], self.wo[:, g, :], start=False, stop=(g == self.G - 1))
        last.then_inc(self.out_ready.sem, 1)

    def dve_add(self, dve, i, p):
        k = self.k
        h = k.H[:, bass.ds(2 * i + p, 1), :]
        dve.wait_ge(self.out_ready.sem, 2 * i + self.out_ready.after(p + 1))
        dve.tensor_tensor(h, h, k.ps[:, self.out_bank + 1, 0:D], ALU.add).then_inc(self.out_added.sem, 1)


def head_scores(pe, ps, q, kk):
    for g in range(3):
        for j in range(4):
            rows = slice(32 * j, 32 * j + 32)
            cols = slice(g * P, (g + 1) * P)
            last = pe.matmul(ps[:, 4 + j, cols], q[rows, cols], kk[rows, cols], start=True, stop=True)
    return last


def rotary_attention(k):
    nc, ps = k.nc, k.ps
    with ExitStack() as mem:
        sb = lambda name, shape: mem.enter_context(nc.sbuf_tensor(f"a1_{name}", shape, F32))
        wqk, wv = sb("wqk", [C + 1, NC, 4, HW]), sb("wv", [C + 1, NC, HW])
        wo, bo = sb("wo", [P, 3, D]), sb("bo", [1, D])
        turn = sb("turn", [P, 2, 32])
        xt, V = sb("xt", [C + 1, NC, TOK]), sb("v", [P, T, HW])
        front(k, [(wv, V)], xt_big=xt, first=1, loads=[
            (wv[:, :, :], "a1_wv"), (wqk[:, :, :, :], "a1_wqk"), (wo[:, :, :], "a1_wo"), (bo[:, :], "a1_bo"), (turn[:, :, :], "a1_turn")])
        a = Attention(k, mem, "a1", 4, HP, 32, 0.25, V, wo, bo)
        QK = sb("qk", [P, 2, 2, HW])
        by_cos, by_sin = sb("by_cos", [P, 2, HW]), sb("by_sin", [P, 2, HW])
        qk_in = k.count("qk_in")
        qk_ready = k.count("qk_ready", 1)
        with nc.Block() as block:
            @block.tensor
            def _(pe):
                def step(i, new, old):
                    if new is not None:
                        for half in range(2):
                            if old is not None:
                                pe.wait_ge(qk_ready.sem, 4 * i + qk_ready.after(2 * new - 1 + half))
                            for m in range(2 * half, 2 * half + 2):
                                if old is not None and m == 0:
                                    pe.wait_ge(a.ot_ready.sem, 2 * i + a.ot_ready.room(new))
                                if old is not None and m == 1:
                                    pe.wait_ge(a.out_added.sem, 2 * i + a.out_added.room(new))
                                for g in range(3):
                                    for c in range(NC):
                                        r = C + 1 - c
                                        last = pe.matmul(ps[:, m, g * P:(g + 1) * P], wqk[0:r, c, m, g * P:(g + 1) * P],
                                                         xt[0:r, c, bass.ds((2 * i + new) * P, P)], start=(c == 0), stop=(c == NC - 1))
                            last.then_inc(qk_in.sem, 1)
                        pe.wait_ge(qk_ready.sem, 4 * i + qk_ready.after(2 * new + 1))
                    if old is not None:
                        a.pe_values(pe, i, old)
                    if new is not None:
                        pe.wait_ge(qk_ready.sem, 4 * i + qk_ready.after(2 * new + 2))
                        pe.wait_ge(a.scores_out.sem, 4 * i + a.scores_out.room(2 * new + 2))
                        head_scores(pe, ps, QK[:, new % 2, 0, :], QK[:, new % 2, 1, :]).then_inc(a.scores_in.sem, 1)
                    if old is not None:
                        a.pe_project(pe, i, old)

                in_turns(pe, 2, step)

            @block.vector
            def _(dve):
                a.zero(dve)

                def step(i, new, old):
                    if old is not None:
                        a.dve_probs(dve, i, old)
                    if new is not None:
                        for m in range(2):
                            dve.wait_ge(qk_in.sem, 4 * i + qk_in.after(2 * new + m + 1))
                            rep = lambda n: turn[:, n, :].unsqueeze(1).broadcast_to([P, HEADS, 32])
                            part = lambda n: ps[:, 2 * m + n, 0:HW].rearrange("p (h d) -> p h d", d=32)
                            as3 = lambda b: b[:, m, :].rearrange("p (h d) -> p h d", d=32)
                            dve.tensor_tensor(as3(by_cos), part(0), rep(0), ALU.mult)
                            k.dve(dve, dve.tensor_tensor(as3(by_sin), part(1), rep(1), ALU.mult))
                            dve.tensor_tensor(QK[:, new % 2, m, :], by_cos[:, m, :], by_sin[:, m, :], ALU.add).then_inc(qk_ready.sem, 1)
                        a.dve_extract(dve, i, new)
                    if old is not None:
                        a.dve_add(dve, i, old)
                    if new is not None:
                        a.dve_shift(dve, i, new)

                in_turns(dve, 2, step, k.dve, 2 + 1 + 3)

            @block.scalar
            def _(act):
                def step(i, new, old):
                    if old is not None:
                        a.act_out(act, i, old)
                    if new is not None:
                        a.act_extract(act, i, new)
                        a.act_exp(act, i, new)

                in_turns(act, 2, step)

            @block.gpsimd
            def _(pool):
                with pool.Fori(0, T // 2) as i:
                    for p in range(2):
                        a.pool_values(pool, i, p)
        a.finished()
        qk_in.passed(2 * T)
        qk_ready.passed(2 * T)


def causal_mixture(k):
    nc, ps = k.nc, k.ps
    E, HD = 3, 64
    with ExitStack() as mem:
        sb = lambda name, shape: mem.enter_context(nc.sbuf_tensor(f"f1_{name}", shape, F32))
        wqk, wvg = sb("wqk", [C + 1, NC, 2 * D]), sb("wvg", [C + 1, NC, D + 32])
        wo, bo = sb("wo", [HD, E, D]), sb("bo", [1, D])
        conv = sb("conv", [HD, 4])
        mask, pos = sb("mask", [P, E, 32]), sb("pos", [P, E, 32])
        wg2, bg2, lower = sb("wg2", [P, E, 32]), sb("bg2", [P, E]), sb("lower", [P, E * E])
        xt, VG = sb("xt", [C + 1, NC, TOK]), sb("vg", [P, T, D + 32])
        W = sb("w", [P, T, E])
        front(k, [(wvg, VG)], xt_big=xt, first=1, loads=[
            (wvg[:, :, :], "f1_wvg"), (wqk[:, :, :], "f1_wqk"), (wo[:, :, :], "f1_wo"), (bo[:, :], "f1_bo"),
            (conv[:, :], "f1_conv"), (mask[:, :, :], "f1_mask"), (pos[:, :, :], "f1_pos"),
            (wg2[:, :, :], "f1_wg2"), (bg2[:, :], "f1_bg2"), (lower[:, :], "lower3")])
        with ExitStack() as inner:
            prod = inner.enter_context(nc.sbuf_tensor("f1_prod", [P, T, E, 32], F32))
            with nc.Block() as block:
                @block.vector
                def _(dve):
                    link = lambda ins: k.dve(dve, ins)
                    k.dve.start()
                    g1 = VG[:, :, D:D + 32]
                    link(dve.tensor_scalar(g1, g1, 0.0, None, ALU.max))
                    link(dve.tensor_tensor(prod[:, :, :, :], g1.unsqueeze(2).broadcast_to([P, T, E, 32]),
                                           wg2[:, :, :].unsqueeze(1).broadcast_to([P, T, E, 32]), ALU.mult))
                    link(dve.tensor_reduce(W[:, :, :], prod[:, :, :, :], AX.X, ALU.add))
                    link(dve.tensor_tensor(W[:, :, :], W[:, :, :], bg2[:, :].unsqueeze(1).broadcast_to([P, T, E]), ALU.add))
                    link(dve.tensor_tensor(mask[:, :, :], mask[:, :, :], pos[:, :, :], ALU.add))
                    k.dve.end()
            chooser = Router(k, W[:, :, :], E, "softmax_top", inner, lower, 2)
            with nc.Block() as block:
                @block.vector
                def _(dve):
                    chooser.vector(dve)

                @block.scalar
                def _(act):
                    chooser.scalar(act)
            chooser.finished()
        a = Attention(k, mem, "f1", 1, HD, 32, 0.125, VG[:, :, 0:D], wo, bo, mask=mask, head_w=W, out_bank=2)
        Q, K = sb("q", [HD, 2, E, P]), sb("k", [HD, 2, E, P])
        qk_in = k.count("qk_in")
        qk_ready = k.count("qk_ready", 1)
        keys_ready = k.count("keys_ready", 1)
        with nc.Block() as block:
            @block.tensor
            def _(pe):
                def step(i, new, old):
                    if new is not None:
                        pe.wait_ge(qk_ready.sem, 2 * i + qk_ready.room(new + 1))
                        pe.wait_ge(keys_ready.sem, 2 * i + keys_ready.room(new + 1))
                        for m in range(2):
                            for e in range(E):
                                cols = slice(m * D + e * HD, m * D + (e + 1) * HD)
                                for c in range(NC):
                                    r = C + 1 - c
                                    last = pe.matmul(ps[0:HD, m, e * P:(e + 1) * P], wqk[0:r, c, cols],
                                                     xt[0:r, c, bass.ds((2 * i + new) * P, P)], start=(c == 0), stop=(c == NC - 1))
                        last.then_inc(qk_in.sem, 1)
                    if old is not None:
                        a.pe_values(pe, i, old)
                    if new is not None:
                        pe.wait_ge(qk_ready.sem, 2 * i + qk_ready.after(new + 1))
                        pe.wait_ge(keys_ready.sem, 2 * i + keys_ready.after(new + 1))
                        pe.wait_ge(a.scores_out.sem, 4 * i + a.scores_out.room(2 * new + 2))
                        for e in range(E):
                            last = pe.matmul(ps[:, 4, e * P:(e + 1) * P], Q[:, new % 2, e, :], K[:, new % 2, e, :], start=True, stop=True)
                        last.then_inc(a.scores_in.sem, 1)
                    if old is not None:
                        a.pe_project(pe, i, old)

                in_turns(pe, 2, step)

            @block.vector
            def _(dve):
                a.zero(dve)

                def step(i, new, old):
                    if old is not None:
                        a.dve_probs(dve, i, old)
                    if new is not None:
                        dve.wait_ge(qk_in.sem, 2 * i + qk_in.after(new + 1))
                        q, src = Q[:, new % 2, 0, :], ps[0:HD, 0, 0:P]
                        k.dve(dve, dve.tensor_scalar(q, src, conv[:, 1:2], conv[:, 3:4], ALU.mult, ALU.add))
                        seq = lambda x, a0, a1: x.rearrange("p (b s) -> p b s", s=32)[:, :, a0:a1]
                        k.dve(dve, dve.scalar_tensor_tensor(seq(q, 1, 32), seq(src, 0, 31), conv[:, 0:1], seq(q, 1, 32), ALU.mult, ALU.add))
                        dve.scalar_tensor_tensor(seq(q, 0, 31), seq(src, 1, 32), conv[:, 2:3], seq(q, 0, 31), ALU.mult,
                                                 ALU.add).then_inc(qk_ready.sem, 1)
                        a.dve_extract(dve, i, new)
                    if old is not None:
                        a.dve_add(dve, i, old)
                    if new is not None:
                        a.dve_shift(dve, i, new)

                in_turns(dve, 2, step, k.dve, 2 + 2 + 4)

            @block.scalar
            def _(act):
                def step(i, new, old):
                    if new is not None:
                        act.wait_ge(qk_in.sem, 2 * i + qk_in.after(new + 1))
                        act.copy(K[:, new % 2, :, :], ps[0:HD, 1, 0:E * P])
                        act.wait_ge(qk_ready.sem, 2 * i + qk_ready.after(new + 1))
                        act.copy(Q[:, new % 2, 1:E, :], ps[0:HD, 0, P:E * P]).then_inc(keys_ready.sem, 1)
                    if old is not None:
                        a.act_out(act, i, old)
                    if new is not None:
                        a.act_extract(act, i, new)
                        a.act_exp(act, i, new)

                in_turns(act, 2, step)

            @block.gpsimd
            def _(pool):
                with pool.Fori(0, T // 2) as i:
                    for p in range(2):
                        a.pool_values(pool, i, p)
        a.finished()
        for s in (qk_in, qk_ready, keys_ready):
            s.passed(T)


SINKHORN = 10
GT = 4
GW = GT * HW


def transport_attention(k):
    nc, ps = k.nc, k.ps
    with ExitStack() as mem:
        sb = lambda name, shape: mem.enter_context(nc.sbuf_tensor(f"a3_{name}", shape, F32))
        wq, wv = sb("wq", [C + 1, NC, HW]), sb("wv", [C + 1, NC, HW])
        wo, bo = sb("wo", [P, 3, D]), sb("bo", [1, D])
        eye, off, blocks = sb("eye", [P, 32]), sb("off", [P, 32]), sb("blocks", [P, P])
        V, K = sb("v", [P, T, HW]), sb("kernel", [P, T, HEADS, 32])
        with ExitStack() as inner:
            Q = inner.enter_context(nc.sbuf_tensor("a3_q", [P, T, HW], F32))
            front(k, [(wq, Q), (wv, V)], first=2, loads=[
                (wq[:, :, :], "a3_wq"), (wv[:, :, :], "a3_wv"), (wo[:, :, :], "a3_wo"), (bo[:, :], "a3_bo"),
                (eye[:, :], "eye32"), (off[:, :], "off32"), (blocks[:, :], "blocks32")])
            transport_kernel(k, inner, Q, K, off)
        Z = sb("z", [P, T, HEADS, 32])
        with ExitStack() as inner:
            scale_kernel(k, inner, K, Z, blocks, eye)
        a = Attention(k, mem, "a3", 4, HP, 32, 0.25, V, wo, bo)
        with nc.Block() as block:
            @block.tensor
            def _(pe):
                def step(i, new, old):
                    if old is not None:
                        a.pe_project(pe, i, old)
                    if new is not None:
                        a.pe_values(pe, i, new)

                in_turns(pe, 2, step)

            @block.vector
            def _(dve):
                a.zero(dve)

                def step(i, new, old):
                    if new is not None:
                        a.dve_probs(dve, i, new)
                    if old is not None:
                        a.dve_add(dve, i, old)

                in_turns(dve, 2, step, k.dve, 3)

            @block.scalar
            def _(act):
                def step(i, new, old):
                    if new is not None:
                        act.wait_ge(a.probs_ready.sem, 2 * i + a.probs_ready.room(new + 1))
                        act.activation(a.SC[:, new % 2, :, :], Z[:, bass.ds(2 * i + new, 1), :, :], ACT.Exp,
                                       scale=0.25).then_inc(a.exped.sem, 1)
                    if old is not None:
                        a.act_out(act, i, old)

                in_turns(act, 2, step)

            @block.gpsimd
            def _(pool):
                with pool.Fori(0, T // 2) as i:
                    for p in range(2):
                        a.pool_values(pool, i, p)
        a.finished(scores=False)


def transport_kernel(k, mem, Q, K, off):
    nc, ps = k.nc, k.ps
    PARTS = 4
    norm = mem.enter_context(nc.sbuf_tensor("a3_norm", [P, T, HEADS], F32))
    QN = mem.enter_context(nc.sbuf_tensor("a3_qn", [P, 2, HW], F32))
    QT = mem.enter_context(nc.sbuf_tensor("a3_qt", [P, 2, HW], F32))
    ten = mem.enter_context(nc.sbuf_tensor("a3_minus_ten", [P, 1], F32))
    squares_ready = k.count("squares_ready")
    norm2_ready = k.count("norm2_ready")
    norm_ready = k.count("norm_ready")
    qn_ready = k.count("qn_ready")
    qn_turned = k.count("qn_turned", 2)
    qt_ready = k.count("qt_ready", 2)
    scores_in = k.count("scores_in")
    scores_out = k.count("scores_out", 2)
    kernel_ready = k.count("kernel_ready")
    with nc.Block() as block:
        @block.scalar
        def _(act):
            act.activation(K[:, :, :, :], Q[:, :, :], ACT.Square).then_inc(squares_ready.sem, 1)
            act.wait_ge(norm2_ready.sem, norm2_ready.after(1))
            act.activation(norm[:, :, :], norm[:, :, :], ACT.Sqrt).then_inc(norm_ready.sem, 1)

            def step(i, new, old):
                if old is not None:
                    act.wait_ge(scores_in.sem, 2 * i + scores_in.after(old + 1))
                    dst = lambda rows: K[rows, bass.ds(2 * i + old, 1), :, :].rearrange("p t s m -> p (t s) m")
                    diagonal_blocks(ps, 4, 4, 32, act.copy, dst, (0, 1)).then_inc(scores_out.sem, 1)
                if new is not None:
                    act.wait_ge(qn_turned.sem, 2 * i + qn_turned.after(new + 1))
                    act.copy(QT[:, new % 2, :], ps[:, new % 2, 0:HW]).then_inc(qt_ready.sem, 1)

            in_turns(act, 2, step)
            act.wait_ge(scores_out.sem, scores_out.after(2 * T))
            for n in range(PARTS):
                part = K[:, n * T // PARTS:(n + 1) * T // PARTS, :, :]
                act.activation(part, part, ACT.Exp, bias=ten[:, :], scale=10.0).then_inc(kernel_ready.sem, 1)

        @block.vector
        def _(dve):
            k.dve.start()
            dve.memset(ten[:, :], -10.0)
            dve.wait_ge(squares_ready.sem, squares_ready.after(1))
            dve.tensor_reduce(norm[:, :, :], K[:, :, :, :], AX.X, ALU.add).then_inc(norm2_ready.sem, 1)
            dve.wait_ge(norm_ready.sem, norm_ready.after(1))
            k.dve(dve, dve.tensor_scalar(norm[:, :, :], norm[:, :, :], 1e-8, None, ALU.add))
            k.dve(dve, dve.reciprocal(norm[:, :, :], norm[:, :, :]))
            k.dve.end()

            def step(i, new, old):
                if new is not None:
                    p, n = new % 2, 2 * i + new
                    dve.wait_ge(qn_turned.sem, 2 * i + qn_turned.room(new + 1))
                    as3 = lambda x: x.rearrange("p (h d) -> p h d", d=HP)
                    dve.tensor_tensor(as3(QN[:, p, :]), Q[:, bass.ds(n, 1), :].rearrange("p t (h d) -> p (t h) d", d=HP),
                                      norm[:, bass.ds(n, 1), :].rearrange("p t h -> p (t h)").unsqueeze(2).broadcast_to([P, HEADS, HP]),
                                      ALU.mult).then_inc(qn_ready.sem, 1)
                if old is not None:
                    dve.wait_ge(scores_in.sem, 2 * i + scores_in.after(old + 1))
                    dst = lambda rows: K[rows, bass.ds(2 * i + old, 1), :, :].rearrange("p t s m -> p (t s) m")
                    diagonal_blocks(ps, 4, 4, 32, dve.tensor_copy, dst, (2, 3)).then_inc(scores_out.sem, 1)

            in_turns(dve, 2, step)
            for n in range(PARTS):
                dve.wait_ge(kernel_ready.sem, kernel_ready.after(n + 1))
                part = K[:, n * T // PARTS:(n + 1) * T // PARTS, :, :]
                dve.tensor_tensor(part, part, off[:, :].unsqueeze(1).unsqueeze(1).broadcast_to([P, T // PARTS, HEADS, 32]), ALU.mult)

        @block.tensor
        def _(pe):
            def step(i, new, old):
                if old is not None:
                    pe.wait_ge(qt_ready.sem, 2 * i + qt_ready.after(old + 1))
                    pe.wait_ge(scores_out.sem, 4 * i + scores_out.room(2 * old + 2))
                    head_scores(pe, ps, QT[:, old % 2, :], QT[:, old % 2, :]).then_inc(scores_in.sem, 1)
                if new is not None:
                    p = new % 2
                    pe.wait_ge(qn_ready.sem, 2 * i + qn_ready.after(new + 1))
                    pe.wait_ge(qt_ready.sem, 2 * i + qt_ready.room(new + 1))
                    for g in range(3):
                        last = pe.transpose(ps[:, p, g * P:(g + 1) * P], QN[:, p, g * P:(g + 1) * P], k.ident[:, :])
                    last.then_inc(qn_turned.sem, 1)

            in_turns(pe, 2, step)
    for s in (squares_ready, norm2_ready, norm_ready):
        s.passed(1)
    kernel_ready.passed(PARTS)
    for s in (qn_ready, qn_turned, qt_ready, scores_in):
        s.passed(T)
    scores_out.passed(2 * T)


def scale_kernel(k, mem, K, Z, blocks, eye):
    nc, ps = k.nc, k.ps
    NG = T // GT
    STEPS = 2 * SINKHORN - 1
    KV = mem.enter_context(nc.sbuf_tensor("a3_kv", [P, GW], F32))
    KU = mem.enter_context(nc.sbuf_tensor("a3_ku", [P, T, HEADS, 32], F32))
    u = mem.enter_context(nc.sbuf_tensor("a3_u", [P, T * HEADS], F32))
    v = mem.enter_context(nc.sbuf_tensor("a3_v_scale", [P, T * HEADS], F32))
    top = mem.enter_context(nc.sbuf_tensor("a3_top", [P, T * HEADS], F32))
    top_t = mem.enter_context(nc.sbuf_tensor("a3_top_t", [P, T * HEADS], F32))
    seq_top = mem.enter_context(nc.sbuf_tensor("a3_seq_top", [P, T * HEADS // 32], F32))
    scaled = k.count("scaled")
    diagonal_ready = k.count("diagonal_ready")
    vector_spread = k.count("vector_spread")
    ku_ready = k.count("ku_ready")
    n_pairs = GT * HEADS
    pairs = lambda x, g: x[:, g * n_pairs:(g + 1) * n_pairs]
    group = lambda X, g: X[:, g * GT:(g + 1) * GT, :, :].rearrange("p t h m -> p (t h) m")
    flat = lambda X, g: X[:, g * GT:(g + 1) * GT, :, :].rearrange("p t h m -> p (t h m)")
    kv3 = KV[:, :].rearrange("p (q m) -> p q m", m=32)
    slot = lambda g: ps[:, 3 * (g % 2):3 * (g % 2) + 3, :].rearrange("p a b -> p (a b)")
    slot3 = lambda g: slot(g).rearrange("p (q m) -> p q m", m=32)
    with nc.Block() as block:
        @block.vector
        def _(dve):
            link = lambda ins: k.dve(dve, ins)

            def step(n, g, dst):
                dve.wait_ge(vector_spread.sem, n * NG + vector_spread.after(g + 1))
                link(dve.tensor_tensor(kv3, group(K, g), slot3(g), ALU.mult))
                link(dve.tensor_reduce(pairs(dst, g), kv3, AX.X, ALU.add))
                dve.reciprocal(pairs(dst, g), pairs(dst, g)).then_inc(scaled.sem, 1)

            k.dve.start()
            for g in range(NG):
                link(dve.tensor_reduce(pairs(u, g), group(K, g), AX.X, ALU.add))
                dve.reciprocal(pairs(u, g), pairs(u, g)).then_inc(scaled.sem, 1)
            k.dve.end()
            with dve.Fori(0, SINKHORN - 1) as r:
                k.dve.start(r, 2 * 2 * NG)
                for g in range(NG):
                    step(2 * r, g, v)
                for g in range(NG):
                    step(2 * r + 1, g, u)
            k.dve.end(SINKHORN - 1)
            k.dve.start()
            for g in range(NG):
                step(STEPS - 1, g, v)
            for g in range(NG):
                dve.wait_ge(vector_spread.sem, STEPS * NG + vector_spread.after(g + 1))
                dve.wait_ge(ku_ready.sem, ku_ready.after(g + 1))
                dve.tensor_tensor(group(Z, g), group(KU, g), slot3(g), ALU.mult).then_inc(scaled.sem, 1)
            dve.wait_ge(scaled.sem, scaled.after((STEPS + 2) * NG))
            rows3 = lambda X: X[:, :, :, :].rearrange("p t h m -> p (t h) m")
            all_pairs = [P, T * HEADS, 32]
            link(dve.tensor_reduce(top[:, :], rows3(Z), AX.X, ALU.max))
            link(dve.transpose(top_t[:, :], top[:, :]))
            blocks3 = top_t[:, :].rearrange("p (q n) -> p q n", n=32)
            link(dve.tensor_reduce(seq_top[:, :], blocks3, AX.X, ALU.max))
            link(dve.reciprocal(seq_top[:, :], seq_top[:, :]))
            link(dve.tensor_copy(blocks3, seq_top[:, :].unsqueeze(2).broadcast_to([P, T * HEADS // 32, 32])))
            link(dve.transpose(top[:, :], top_t[:, :]))
            link(dve.tensor_tensor(rows3(Z), rows3(Z), top[:, :].unsqueeze(2).broadcast_to(all_pairs), ALU.mult))
            link(dve.tensor_tensor(rows3(Z), rows3(Z), eye[:, :].unsqueeze(1).broadcast_to(all_pairs), ALU.add))
            k.dve.end()

        @block.gpsimd
        def _(pool):
            def diagonals(n, src):
                for g in range(NG):
                    pool.wait_ge(scaled.sem, n * NG + scaled.after(g + 1))
                    pool.tensor_tensor(group(Z, g), eye[:, :].unsqueeze(1).broadcast_to([P, n_pairs, 32]),
                                       pairs(src, g).unsqueeze(2).broadcast_to([P, n_pairs, 32]),
                                       ALU.mult).then_inc(diagonal_ready.sem, 1)

            with pool.Fori(0, SINKHORN - 1) as r:
                diagonals(2 * r, u)
                diagonals(2 * r + 1, v)
            diagonals(STEPS - 1, u)
            diagonals(STEPS, v)
            for g in range(NG):
                pool.tensor_tensor(group(KU, g), group(K, g), pairs(u, g).unsqueeze(2).broadcast_to([P, n_pairs, 32]),
                                   ALU.mult).then_inc(ku_ready.sem, 1)

        @block.tensor
        def _(pe):
            def spread(n):
                for g in range(NG):
                    pe.wait_ge(diagonal_ready.sem, n * NG + diagonal_ready.after(g + 1))
                    pe.wait_ge(scaled.sem, n * NG + scaled.after(NG + g - 1))
                    for b in range(3):
                        last = pe.matmul(ps[:, 3 * (g % 2) + b, :], blocks[:, :], flat(Z, g)[:, b * BANK:(b + 1) * BANK],
                                         start=True, stop=True)
                    last.then_inc(vector_spread.sem, 1)

            with pe.Fori(0, SINKHORN - 1) as r:
                spread(2 * r)
                spread(2 * r + 1)
            spread(STEPS - 1)
            spread(STEPS)
    scaled.passed((STEPS + 2) * NG)
    diagonal_ready.passed((STEPS + 1) * NG)
    vector_spread.passed((STEPS + 1) * NG)
    ku_ready.passed(NG)


def cosine_attention(k):
    nc, ps = k.nc, k.ps
    L = 64
    with ExitStack() as mem:
        sb = lambda name, shape: mem.enter_context(nc.sbuf_tensor(f"a0_{name}", shape, F32))
        w = sb("w", [C + 1, NC, 3, HW])
        wo, bo = sb("wo", [P, 3, D]), sb("bo", [1, D])
        log_scale, head_scale = sb("log_scale", [P, HEADS]), sb("head_scale", [P, HEADS])
        xt = sb("xt", [C + 1, NC, TOK])
        OT = sb("ot", [P, 3, TOK])
        front(k, [], xt_big=xt, loads=[(w[:, :, :, :], "a0_w"), (wo[:, :, :], "a0_wo"), (bo[:, :], "a0_bo"),
                                       (log_scale[:, :], "a0_log_scale"), (head_scale[:, :], "a0_head_scale")])
        with ExitStack() as inner:
            sb2 = lambda name, shape: inner.enter_context(nc.sbuf_tensor(f"a0_{name}", shape, F32))
            a = Attention(k, inner, "a0", 4, HP, L, 1.0, None, ot_big=OT, out_bank=3)
            XT = sb2("xt_tile", [C + 1, 2, NC, P])
            SQ = sb2("squares", [P, 2, 2 * HW])
            norm = sb2("norm", [P, 2, 2, HEADS])
            QN, QT = sb2("qn", [P, 2, 2, HW]), sb2("qt", [P, 2, 2, HW])
            xt_staged = k.count("xt_staged")
            qk_in = k.count("qk_in")
            qkv_in = k.count("qkv_in", 2)
            v_ready = k.count("v_ready")
            squares_ready = k.count("squares_ready")
            norm2_ready = k.count("norm2_ready")
            norm_ready = k.count("norm_ready")
            qn_ready = k.count("qn_ready")
            qn_turned = k.count("qn_turned", 2)
            qt_ready = k.count("qt_ready", 2)
            with nc.Block() as block:
                @block.gpsimd
                def _(pool):
                    with pool.Fori(0, T // 2) as i:
                        for p in range(2):
                            pool.wait_ge(qkv_in.sem, 2 * i + qkv_in.room(p + 1))
                            for c in range(NC):
                                src = xt[:, c, :].rearrange("p (l n) -> p n l", l=L)[:, bass.ds((2 * i + p) * 2, 2), :]
                                last = pool.tensor_copy(XT[:, p, c, :].rearrange("p (n l) -> p n l", l=L), src)
                            last.then_inc(xt_staged.sem, 1)

                @block.tensor
                def _(pe):
                    def step(i, new, mid, old):
                        if mid is not None:
                            pe.wait_ge(qn_ready.sem, 2 * i + qn_ready.after(mid + 1))
                            pe.wait_ge(a.scores_out.sem, 4 * i + a.scores_out.room(2 * mid + 2))
                            for m in range(2):
                                for g in range(3):
                                    cols = slice(g * P, (g + 1) * P)
                                    last = pe.transpose(ps[:, 4 + m, cols], QN[:, mid % 2, m, cols], k.ident[:, :])
                            last.then_inc(qn_turned.sem, 1)
                        if new is not None:
                            pe.wait_ge(xt_staged.sem, 2 * i + xt_staged.after(new + 1))
                            for m in range(3):
                                if m == 2 and mid is not None:
                                    pe.wait_ge(v_ready.sem, 2 * i + v_ready.after(new))
                                for c in range(NC):
                                    r = C + 1 - c
                                    last = pe.matmul(ps[:, m, 0:HW], XT[0:r, new % 2, c, :], w[0:r, c, m, :], start=(c == 0), stop=(c == NC - 1))
                                if m == 1:
                                    last.then_inc(qk_in.sem, 1)
                            last.then_inc(qkv_in.sem, 1)
                        if mid is not None:
                            pe.wait_ge(qt_ready.sem, 2 * i + qt_ready.after(mid + 1))
                            head_scores(pe, ps, QT[:, mid % 2, 0, :], QT[:, mid % 2, 1, :]).then_inc(a.scores_in.sem, 1)
                        if old is not None:
                            a.pe_values(pe, i, old)

                    in_turns(pe, 3, step)

                @block.scalar
                def _(act):
                    act.wait_ge(norm2_ready.sem, norm2_ready.after(1))
                    act.activation(log_scale[:, :], log_scale[:, :], ACT.Exp).then_inc(norm_ready.sem, 1)

                    def step(i, new, mid, old):
                        if mid is not None:
                            act.wait_ge(qn_turned.sem, 2 * i + qn_turned.after(mid + 1))
                            act.copy(QT[:, mid % 2, :, :], ps[:, 4:6, 0:HW]).then_inc(qt_ready.sem, 1)
                        if new is not None:
                            act.wait_ge(qk_in.sem, 2 * i + qk_in.after(new + 1))
                            act.activation(SQ[:, new % 2, :].rearrange("p (m d) -> p m d", m=2), ps[:, 0:2, 0:HW],
                                           ACT.Square).then_inc(squares_ready.sem, 1)
                            act.wait_ge(norm2_ready.sem, 2 * i + norm2_ready.after(new + 2))
                            act.activation(norm[:, new % 2, :, :], norm[:, new % 2, :, :], ACT.Sqrt).then_inc(norm_ready.sem, 1)
                        if mid is not None:
                            a.act_extract(act, i, mid)
                            a.act_exp(act, i, mid)
                        if old is not None:
                            a.act_out(act, i, old)

                    in_turns(act, 3, step)

                @block.vector
                def _(dve):
                    a.zero(dve)
                    dve.tensor_scalar(log_scale[:, :], log_scale[:, :], float(np.log(1.0 / 0.01)), None,
                                      ALU.min).then_inc(norm2_ready.sem, 1)
                    dve.wait_ge(norm_ready.sem, norm_ready.after(1))

                    def step(i, new, mid, old):
                        if old is not None:
                            a.dve_probs(dve, i, old)
                        if new is not None:
                            p = new % 2
                            dve.wait_ge(squares_ready.sem, 2 * i + squares_ready.after(new + 1))
                            nm = norm[:, p, :, :].rearrange("p m h -> p (m h)")
                            dve.tensor_reduce(nm, SQ[:, p, :].rearrange("p (h d) -> p h d", d=HP), AX.X,
                                              ALU.add).then_inc(norm2_ready.sem, 1)
                            dve.wait_ge(norm_ready.sem, 2 * i + norm_ready.after(new + 2))
                            k.dve(dve, dve.tensor_scalar(nm, nm, 1e-12, None, ALU.max))
                            k.dve(dve, dve.reciprocal(nm, nm))
                            k.dve(dve, dve.tensor_tensor(norm[:, p, 0, :], norm[:, p, 0, :], log_scale[:, :], ALU.mult))
                            as4 = lambda x: x.rearrange("p m (h d) -> p m h d", d=HP)
                            dve.tensor_tensor(as4(QN[:, p, :, :]), as4(ps[:, 0:2, 0:HW]),
                                              norm[:, p, :, :].unsqueeze(3).broadcast_to([P, 2, HEADS, HP]), ALU.mult).then_inc(qn_ready.sem, 1)
                        if mid is not None:
                            a.dve_extract(dve, i, mid)
                            a.dve_shift(dve, i, mid)
                        if new is not None:
                            dve.wait_ge(qkv_in.sem, 2 * i + qkv_in.after(new + 1))
                            dve.wait_ge(a.pv_done.sem, 2 * i + a.pv_done.room(new + 1))
                            as3 = lambda x: x.rearrange("p (h d) -> p h d", d=HP)
                            dve.tensor_tensor(as3(a.V[:, p, :]), as3(ps[:, 2, 0:HW]),
                                              head_scale[:, :].unsqueeze(2).broadcast_to([P, HEADS, HP]), ALU.mult).then_inc(v_ready.sem, 1)

                    in_turns(dve, 3, step, k.dve, 3 + 1 + 3)
            a.finished(staged=False)
            for s in (xt_staged, qk_in, qkv_in, squares_ready, qn_ready, qn_turned, qt_ready, v_ready):
                s.passed(T)
            norm2_ready.passed(T + 1)
            norm_ready.passed(T + 1)
        project_tiles(k, mem, OT, wo, bo)


def project_tiles(k, mem, OT, wo, bo):
    nc, ps = k.nc, k.ps
    tile = k.buffer(mem, "ot_tile", [P, 2, 3, P])
    ot_staged = k.count("ot_staged")
    out_ready = k.count("tile_projected", 2)
    out_added = k.count("tile_added", 2)
    with nc.Block() as block:
        @block.gpsimd
        def _(pool):
            with pool.Fori(0, T // 2) as i:
                for p in range(2):
                    pool.wait_ge(out_ready.sem, 2 * i + out_ready.room(p + 1))
                    pool.tensor_copy(tile[:, p, :, :], OT[:, :, bass.ds((2 * i + p) * P, P)]).then_inc(ot_staged.sem, 1)

        @block.tensor
        def _(pe):
            with pe.Fori(0, T // 2) as i:
                for p in range(2):
                    pe.wait_ge(ot_staged.sem, 2 * i + ot_staged.after(p + 1))
                    pe.wait_ge(out_added.sem, 2 * i + out_added.room(p + 1))
                    pe.matmul(ps[:, p, 0:D], k.ones[0:1, :], bo[0:1, :], start=True, stop=False)
                    for g in range(3):
                        last = pe.matmul(ps[:, p, 0:D], tile[:, p, g, :], wo[:, g, :], start=False, stop=(g == 2))
                    last.then_inc(out_ready.sem, 1)

        @block.vector
        def _(dve):
            with dve.Fori(0, T // 2) as i:
                for p in range(2):
                    h = k.H[:, bass.ds(2 * i + p, 1), :]
                    dve.wait_ge(out_ready.sem, 2 * i + out_ready.after(p + 1))
                    dve.tensor_tensor(h, h, ps[:, p, 0:D], ALU.add).then_inc(out_added.sem, 1)
    for s in (ot_staged, out_ready, out_added):
        s.passed(T)


def temporal_tokens(k):
    nc, ps = k.nc, k.ps
    FR, B, N = 16, 4, 64
    SPAN = FR * B * N
    with ExitStack() as mem:
        sb = lambda name, shape: mem.enter_context(nc.sbuf_tensor(f"tok_{name}", shape, F32))
        xf = sb("x", [C + 1, NC, SPAN])
        wd, wu, bu = sb("down", [C + 1, NC, C]), sb("up", [C, D]), sb("up_bias", [P, D])
        conv = sb("conv", [C, 5])
        hd, y, sg = sb("down_out", [C, SPAN]), sb("y", [C, B, FR // 2, N]), sb("sigmoid", [C, TOK])
        z = sb("z", [P, T, C])
        zs, zt = sb("z_tile", [P, 2, C]), sb("z_tile_t", [C, 2, P])
        scratch = k.dram["scratch"]
        loaded = k.count("weights_loaded")
        chunk_loaded = [k.count(f"x_chunk_loaded{n}") for n in range(4)]
        down_in = k.count("down_in")
        down_ready = k.count("down_ready", 4)
        conv_ready = k.count("conv_ready")
        sigmoid_ready = k.count("sigmoid_ready")
        z_ready = k.count("z_ready")
        z_stored = k.count("z_stored")
        z_loaded = k.count("z_loaded")
        NB = SPAN // BANK
        with nc.Block() as block:
            @block.sync
            def _(sp):
                for dst, name in ((wd[:, :, :], "tok_down"), (conv[:, :], "tok_conv"), (wu[:, :], "tok_up"), (bu[:, :], "tok_up_bias")):
                    sp.dma_start(dst, k.dram[name]).then_inc(loaded.sem, 16)
                q = SPAN // 4
                for n in range(4):
                    sp.dma_start(xf[:, :, n * q:(n + 1) * q], k.dram["tok_x"][:, :, n * q:(n + 1) * q]).then_inc(chunk_loaded[n].sem, 16)
                sp.wait_ge(z_ready.sem, z_ready.after(1))
                sp.dma_start(scratch.rearrange("(p n) -> p n", p=C), sg[:, :]).then_inc(z_stored.sem, 16)
                sp.wait_ge(z_stored.sem, z_stored.after(16))
                sp.dma_start(z[:, :, :], scratch.rearrange("(t p f) -> p t f", p=P, f=C)).then_inc(z_loaded.sem, 16)
                sp.wait_ge(z_loaded.sem, z_loaded.after(16))

            @block.tensor
            def _(pe):
                pe.wait_ge(loaded.sem, loaded.after(64))
                for n in range(4):
                    pe.wait_ge(chunk_loaded[n].sem, chunk_loaded[n].after(16))
                    for b in range(NB // 4 * n, NB // 4 * (n + 1)):
                        pe.wait_ge(down_ready.sem, down_ready.room(b + 1))
                        for c in range(NC):
                            r = C + 1 - c
                            last = pe.matmul(ps[0:C, b % 4, :], wd[0:r, c, :], xf[0:r, c, b * BANK:(b + 1) * BANK],
                                             start=(c == 0), stop=(c == NC - 1))
                        last.then_inc(down_in.sem, 1)

            @block.scalar
            def _(act):
                for b in range(NB):
                    act.wait_ge(down_in.sem, down_in.after(b + 1))
                    act.copy(hd[:, b * BANK:(b + 1) * BANK], ps[0:C, b % 4, :]).then_inc(down_ready.sem, 1)
                act.wait_ge(conv_ready.sem, conv_ready.after(1))
                act.activation(sg[:, :], y[:, :, :, :], ACT.Sigmoid, scale=1.702).then_inc(sigmoid_ready.sem, 1)

            @block.vector
            def _(dve):
                link = lambda ins: k.dve(dve, ins)
                k.dve.start()
                dve.wait_ge(down_ready.sem, down_ready.after(NB))
                frames = hd[:, :].rearrange("p (n b t) -> p b t n", n=N, b=B)
                for b in range(B):
                    link(dve.tensor_scalar(y[:, b, :, :], frames[:, b, 0:FR:2, :], conv[:, 1:2], conv[:, 4:5], ALU.mult, ALU.add))
                    link(dve.scalar_tensor_tensor(y[:, b, :, :], frames[:, b, 1:FR:2, :], conv[:, 2:3], y[:, b, :, :], ALU.mult, ALU.add))
                    link(dve.scalar_tensor_tensor(y[:, b, 1:, :], frames[:, b, 1:FR - 2:2, :], conv[:, 0:1], y[:, b, 1:, :], ALU.mult, ALU.add))
                    link(dve.scalar_tensor_tensor(y[:, b, :-1, :], frames[:, b, 2:FR:2, :], conv[:, 3:4], y[:, b, :-1, :], ALU.mult, ALU.add))
                dve.sem_inc(conv_ready.sem, 1)
                dve.wait_ge(sigmoid_ready.sem, sigmoid_ready.after(1))
                dve.tensor_tensor(sg[:, :], sg[:, :], y[:, :, :, :].rearrange("p b f n -> p (b f n)"), ALU.mult).then_inc(z_ready.sem, 1)
                k.dve.end()
        loaded.passed(64)
        for s in chunk_loaded + [z_stored, z_loaded]:
            s.passed(16)
        for s in (conv_ready, sigmoid_ready, z_ready):
            s.passed(1)
        down_in.passed(NB)
        down_ready.passed(NB)

        z_staged = k.count("z_staged")
        z_turned = k.count("z_turned", 2)
        zt_ready = k.count("zt_ready", 2)
        up_in = k.count("up_in", 2)
        up_added = k.count("up_added", 2)
        with nc.Block() as block:
            @block.gpsimd
            def _(pool):
                with pool.Fori(0, T // 2) as i:
                    for p in range(2):
                        pool.wait_ge(z_turned.sem, 2 * i + z_turned.room(p + 1))
                        pool.tensor_copy(zs[:, p, :], z[:, bass.ds(2 * i + p, 1), :]).then_inc(z_staged.sem, 1)

            @block.tensor
            def _(pe):
                with pe.Fori(0, T // 2) as i:
                    for p in range(2):
                        pe.wait_ge(z_staged.sem, 2 * i + z_staged.after(p + 1))
                        pe.wait_ge(zt_ready.sem, 2 * i + zt_ready.room(p + 1))
                        pe.transpose(ps[0:C, p, 0:P], zs[:, p, :], k.ident[:, :]).then_inc(z_turned.sem, 1)
                    for p in range(2):
                        pe.wait_ge(zt_ready.sem, 2 * i + zt_ready.after(p + 1))
                        pe.wait_ge(up_added.sem, 2 * i + up_added.room(p + 1))
                        pe.matmul(ps[:, 2 + p, 0:D], zt[:, p, :], wu[:, :], start=True, stop=True).then_inc(up_in.sem, 1)

            @block.scalar
            def _(act):
                with act.Fori(0, T // 2) as i:
                    for p in range(2):
                        act.wait_ge(z_turned.sem, 2 * i + z_turned.after(p + 1))
                        act.wait_ge(up_in.sem, 2 * i + up_in.room(p + 1))
                        act.copy(zt[:, p, :], ps[0:C, p, 0:P]).then_inc(zt_ready.sem, 1)

            @block.vector
            def _(dve):
                with dve.Fori(0, T // 2) as i:
                    for p in range(2):
                        dve.wait_ge(up_in.sem, 2 * i + up_in.after(p + 1))
                        dve.tensor_tensor(k.H[:, bass.ds(2 * i + p, 1), :], ps[:, 2 + p, 0:D], bu[:, :], ALU.add).then_inc(up_added.sem, 1)
        for s in (z_staged, z_turned, zt_ready, up_in, up_added):
            s.passed(T)


QH, QS, QD = 8, 64, 32
KE = 3


def complex_memory(k):
    nc = k.nc
    with ExitStack() as mem:
        sb = lambda name, shape: mem.enter_context(nc.sbuf_tensor(f"a2_{name}", shape, F32))
        H1 = sb("h1", [P, T, D])
        p_tok = sb("p_tok", [P, T])
        with ExitStack() as inner:
            memory_read(k, inner, H1, p_tok)
        H2 = sb("h2", [P, T, D])
        with ExitStack() as inner:
            reasoning(k, inner, H1, H2, p_tok)
        with ExitStack() as inner:
            routed_experts(k, inner, H2)


def memory_read(k, mem, H1, p_tok):
    nc, ps = k.nc, k.ps
    sb = lambda name, shape: mem.enter_context(nc.sbuf_tensor(f"a2_{name}", shape, F32))
    NG = QH // 2
    wpz = sb("wpz", [C + 1, NC, QH * 16])
    wri = sb("wri", [C + 1, NC, NG, P])
    pw2, pb2 = sb("pw2", [P, QH, 16]), sb("pb2", [P, QH])
    m1, m2 = sb("m1", [P, NG, 2, 64]), sb("m2", [P, NG, 2, 64])
    vt, wout, wgate = sb("vt", [C, NC, 4, P]), sb("wout", [C, NC, D]), sb("wgate", [C, NC, 4, 16])
    ob, gb, pair = sb("ob", [1, D]), sb("gb", [1, QH]), sb("pair", [P, 2])
    xt, PZ = sb("xt", [C + 1, NC, TOK]), sb("pz", [P, T, QH, 16])
    front(k, [(wpz, PZ[:, :, :, :].rearrange("p t h c -> p t (h c)"))], xt_big=xt, xn_big=H1, first=1, loads=[
        (wpz[:, :, :], "a2_wpz"), (wri[:, :, :, :], "a2_wri"), (pw2[:, :, :], "a2_pw2"), (pb2[:, :], "a2_pb2"),
        (m1[:, :, :, :], "a2_m1"), (m2[:, :, :, :], "a2_m2"), (vt[:, :, :, :], "a2_vt"), (wout[:, :, :], "a2_wout"),
        (wgate[:, :, :, :], "a2_wgate"), (ob[:, :], "a2_ob"), (gb[:, :], "a2_gb"), (pair[:, :], "a2_pair")])

    one_minus_p, p_share = sb("one_minus_p", [P, T, QH]), sb("p_share", [P, T, QH])
    mnorm, msq = sb("mnorm", [P, NG]), sb("msq", [P, NG, 64])
    MRI = sb("mri", [P, NG, P])
    VO, VG = sb("vo", [P, 4, D]), sb("vg", [P, 4, QH])
    silu_ready = k.count("silu_ready")
    p_in = k.count("p_in")
    p_ready = k.count("p_ready")
    slots_squared = k.count("slots_squared")
    norm2_ready = k.count("norm2_ready")
    norm_ready = k.count("norm_ready")
    slots_ready = k.count("slots_ready")
    slots_turned = k.count("slots_turned")
    folded = k.count("folded")
    with nc.Block() as block:
        @block.scalar
        def _(act):
            act.activation(PZ[:, :, :, :], PZ[:, :, :, :], ACT.Silu).then_inc(silu_ready.sem, 1)
            act.activation(msq[:, :, :], m1[:, :, 0, :], ACT.Square).then_inc(slots_squared.sem, 1)
            act.wait_ge(p_in.sem, p_in.after(1))
            act.activation(p_share[:, :, :], p_share[:, :, :], ACT.Sigmoid).then_inc(p_ready.sem, 1)
            act.wait_ge(norm2_ready.sem, norm2_ready.after(1))
            act.activation(mnorm[:, :], mnorm[:, :], ACT.Sqrt).then_inc(norm_ready.sem, 1)
            act.wait_ge(folded.sem, folded.after(1))
            for n in range(4):
                act.copy(VO[:, n, :], ps[:, 2 + n // 2, (n % 2) * D:(n % 2 + 1) * D])
            gates = ps[:, 4, 0:64].rearrange("p (n j g) -> p n j g", n=4, j=2)
            for j in range(2):
                act.copy(VG[64 * j:64 * j + 64, :, :], gates[64 * j:64 * j + 64, :, j, :])

        @block.vector
        def _(dve):
            link = lambda ins: k.dve(dve, ins)
            k.dve.start()
            dve.wait_ge(silu_ready.sem, silu_ready.after(1))
            link(dve.tensor_tensor(PZ[:, :, :, :], PZ[:, :, :, :], pw2[:, :, :].unsqueeze(1).broadcast_to([P, T, QH, 16]), ALU.mult))
            link(dve.tensor_reduce(p_share[:, :, :], PZ[:, :, :, :], AX.X, ALU.add))
            dve.tensor_tensor(p_share[:, :, :], p_share[:, :, :], pb2[:, :].unsqueeze(1).broadcast_to([P, T, QH]), ALU.add).then_inc(p_in.sem, 1)
            dve.wait_ge(slots_squared.sem, slots_squared.after(1))
            dve.tensor_reduce(mnorm[:, :], msq[:, :, :], AX.X, ALU.add).then_inc(norm2_ready.sem, 1)
            dve.wait_ge(p_ready.sem, p_ready.after(1))
            link(dve.tensor_scalar(p_share[:, :, :], p_share[:, :, :], 0.95, None, ALU.mult))
            link(dve.tensor_scalar(one_minus_p[:, :, :], p_share[:, :, :], -1.0, 1.0, ALU.mult, ALU.add))
            link(dve.tensor_reduce(p_tok[:, :], p_share[:, :, :], AX.X, ALU.add))
            link(dve.tensor_scalar(p_tok[:, :], p_tok[:, :], 1.0 / QH, None, ALU.mult))
            link(dve.tensor_scalar(p_share[:, :, :], p_share[:, :, :], 1.0 / QD, None, ALU.mult))
            dve.wait_ge(norm_ready.sem, norm_ready.after(1))
            link(dve.tensor_scalar(mnorm[:, :], mnorm[:, :], 1e-12, None, ALU.max))
            link(dve.reciprocal(mnorm[:, :], mnorm[:, :]))
            for m in (m1, m2):
                flat = m[:, :, :, :].rearrange("p g a d -> p g (a d)")
                link(dve.tensor_tensor(flat, flat, mnorm[:, :].unsqueeze(2).broadcast_to([P, NG, P]), ALU.mult))
            neg = m2[:, :, :, 0:QD]
            dve.tensor_scalar(neg, neg, -1.0, None, ALU.mult).then_inc(slots_ready.sem, 1)
            dve.wait_ge(slots_turned.sem, slots_turned.after(1))
            for n in range(2):
                for j in range(2):
                    rows = slice(64 * j, 64 * j + 64)
                    src = ps[rows, n, :].rearrange("p (g s) -> p g s", g=NG)[:, :, rows]
                    dve.tensor_copy(MRI[rows, :, 64 * n:64 * n + 64], src)
            k.dve.end()

        @block.tensor
        def _(pe):
            for n in range(4):
                for c in range(NC):
                    pe.matmul(ps[:, 2 + n // 2, (n % 2) * D:(n % 2 + 1) * D], vt[:, c, n, :], wout[:, c, :], start=(c == 0), stop=(c == NC - 1))
                for c in range(NC):
                    last = pe.matmul(ps[:, 4, 16 * n:16 * n + 16], vt[:, c, n, :], wgate[:, c, n, :], start=(c == 0), stop=(c == NC - 1))
            last.then_inc(folded.sem, 1)
            pe.wait_ge(slots_ready.sem, slots_ready.after(1))
            for n, m in enumerate((m1, m2)):
                for g in range(NG):
                    last = pe.transpose(ps[:, n, g * P:(g + 1) * P], m[:, g, :, :].rearrange("p a d -> p (a d)"), k.ident[:, :])
            last.then_inc(slots_turned.sem, 1)
    for s in (silu_ready, p_in, p_ready, slots_squared, norm2_ready, norm_ready, slots_ready, slots_turned, folded):
        s.passed(1)

    PP, SQ = sb("pp", [P, 2, NG, P]), sb("pp_squares", [P, 2, NG, P])
    OV = sb("overlap", [P, 2, QH, 2, QS])
    AT, ATT = sb("attn", [P, 2, QH, QS]), sb("attn_t", [P, 2, 4, P])
    al, rs, gt = sb("alpha", [P, 2, QH]), sb("row_sum", [P, 2, QH]), sb("gates", [P, 2, QH])
    st = sb("gate_stat", [P, 2])
    proj_in = k.count("proj_in")
    proj_ready = k.count("proj_ready")
    overlap_in = k.count("overlap_in")
    overlap_ready = k.count("overlap_ready")
    attn_ready = k.count("attn_ready")
    attn_turned = k.count("attn_turned")
    attn_t_ready = k.count("attn_t_ready")
    gated_ready = k.count("gated_ready")
    gated_turned = k.count("gated_turned")
    gated_t_ready = k.count("gated_t_ready")
    logits_in = k.count("logits_in")
    logits_shifted = k.count("logits_shifted")
    gates_exped = k.count("gates_exped")
    mix_in = k.count("mix_in")
    mix_added = k.count("mix_added", 2)
    with nc.Block() as block:
        @block.tensor
        def _(pe):
            def turn(i, n, bank, ready, turned):
                pe.wait_ge(ready.sem, 2 * i + ready.after(n + 1))
                flat = AT[:, n % 2, :, :].rearrange("p h s -> p (h s)")
                for c in range(4):
                    last = pe.transpose(ps[:, bank, c * P:(c + 1) * P], flat[:, c * P:(c + 1) * P], k.ident[:, :])
                last.then_inc(turned.sem, 1)

            def step(i, new, mid, old):
                if new is not None:
                    for g in range(NG):
                        for c in range(NC):
                            last = pe.matmul(ps[:, 0, g * P:(g + 1) * P], wri[0:C, c, g, :], xt[0:C, c, bass.ds((2 * i + new) * P, P)],
                                             start=(c == 0), stop=(c == NC - 1))
                    last.then_inc(proj_in.sem, 1)
                if old is not None:
                    turn(i, old, 2, gated_ready, gated_turned)
                if mid is not None:
                    turn(i, mid, 1, attn_ready, attn_turned)
                if new is not None:
                    p = new % 2
                    pe.wait_ge(proj_ready.sem, 2 * i + proj_ready.after(new + 1))
                    for g in range(NG):
                        for j in range(2):
                            rows = slice(64 * j, 64 * j + 64)
                            pe.matmul(ps[:, 3 + j, g * P:(g + 1) * P], PP[rows, p, g, :], MRI[rows, g, :], start=True, stop=True)
                    for g in range(NG):
                        last = pe.matmul(ps[:, 5, 2 * g:2 * g + 2], SQ[:, p, g, :], pair[:, :], start=True, stop=True)
                    last.then_inc(overlap_in.sem, 1)
                if mid is not None:
                    pe.wait_ge(attn_t_ready.sem, 2 * i + attn_t_ready.after(mid + 1))
                    pe.matmul(ps[:, 6, 0:QH], k.ones[0:1, :], gb[0:1, :], start=True, stop=False)
                    for n in range(4):
                        last = pe.matmul(ps[:, 6, 0:QH], ATT[:, mid % 2, n, :], VG[:, n, :], start=False, stop=(n == 3))
                    last.then_inc(logits_in.sem, 1)
                if old is not None:
                    pe.wait_ge(gated_t_ready.sem, 2 * i + gated_t_ready.after(old + 1))
                    pe.wait_ge(mix_added.sem, 2 * i + mix_added.after(old))
                    pe.matmul(ps[:, 7, 0:D], k.ones[0:1, :], ob[0:1, :], start=True, stop=False)
                    for n in range(4):
                        last = pe.matmul(ps[:, 7, 0:D], ATT[:, old % 2, n, :], VO[:, n, :], start=False, stop=(n == 3))
                    last.then_inc(mix_in.sem, 1)

            in_turns(pe, 3, step)

        @block.scalar
        def _(act):
            def step(i, new, mid, old):
                if new is not None:
                    act.wait_ge(proj_in.sem, 2 * i + proj_in.after(new + 1))
                    act.copy(PP[:, new % 2, :, :], ps[:, 0, :])
                    act.activation(SQ[:, new % 2, :, :], ps[:, 0, :], ACT.Square).then_inc(proj_ready.sem, 1)
                if old is not None:
                    act.wait_ge(gated_turned.sem, 2 * i + gated_turned.after(old + 1))
                    act.copy(ATT[:, old % 2, :, :], ps[:, 2, :]).then_inc(gated_t_ready.sem, 1)
                if mid is not None:
                    act.wait_ge(attn_turned.sem, 2 * i + attn_turned.after(mid + 1))
                    act.copy(ATT[:, mid % 2, :, :], ps[:, 1, :]).then_inc(attn_t_ready.sem, 1)
                if new is not None:
                    act.wait_ge(overlap_in.sem, 2 * i + overlap_in.after(new + 1))
                    act.activation(OV[:, new % 2, :, :, :].rearrange("p (j g) a s -> p j (g a s)", j=2), ps[:, 3:5, :],
                                   ACT.Square).then_inc(overlap_ready.sem, 1)
                if mid is not None:
                    act.wait_ge(logits_shifted.sem, 2 * i + logits_shifted.after(mid + 1))
                    act.activation(gt[:, mid % 2, :], gt[:, mid % 2, :], ACT.Exp).then_inc(gates_exped.sem, 1)

            in_turns(act, 3, step)

        @block.vector
        def _(dve):
            link = lambda ins: k.dve(dve, ins)
            wide = lambda x: x.unsqueeze(2).broadcast_to([P, QH, QS])

            def step(i, new, mid, old):
                tile = lambda X, n: X[:, bass.ds(2 * i + n, 1), :].rearrange("p t h -> p (t h)")
                if new is not None:
                    dve.wait_ge(overlap_in.sem, 2 * i + overlap_in.after(new + 1))
                    a, at, r = al[:, new % 2, :], AT[:, new % 2, :, :], rs[:, new % 2, :]
                    n2 = ps[:, 5, 0:8].rearrange("p (g j) -> p j g", j=2)
                    link(dve.tensor_scalar(a.rearrange("p (j g) -> p j g", j=2), n2, 1e-24, None, ALU.max))
                    link(dve.reciprocal(a, a))
                    link(dve.tensor_tensor(a, a, tile(one_minus_p, new), ALU.mult))
                if mid is not None:
                    m = mid % 2
                    dve.wait_ge(logits_in.sem, 2 * i + logits_in.after(mid + 1))
                    link(dve.tensor_reduce(st[:, m:m + 1], ps[:, 6, 0:QH], AX.X, ALU.max))
                    dve.tensor_scalar(gt[:, m, :], ps[:, 6, 0:QH], st[:, m:m + 1], None, ALU.subtract).then_inc(logits_shifted.sem, 1)
                if new is not None:
                    dve.wait_ge(overlap_ready.sem, 2 * i + overlap_ready.after(new + 1))
                    ov = OV[:, new % 2, :, :, :]
                    link(dve.tensor_tensor(at, ov[:, :, 0, :], ov[:, :, 1, :], ALU.add))
                    link(dve.tensor_tensor(at, at, wide(a), ALU.mult))
                    link(dve.tensor_tensor(at, at, wide(tile(p_share, new)), ALU.add))
                    link(dve.tensor_reduce(r, at, AX.X, ALU.add))
                    link(dve.tensor_scalar(r, r, 1e-8, None, ALU.add))
                    link(dve.reciprocal(r, r))
                    dve.tensor_tensor(at, at, wide(r), ALU.mult).then_inc(attn_ready.sem, 1)
                if mid is not None:
                    dve.wait_ge(gates_exped.sem, 2 * i + gates_exped.after(mid + 1))
                    link(dve.tensor_reduce(st[:, m:m + 1], gt[:, m, :], AX.X, ALU.add))
                    link(dve.reciprocal(st[:, m:m + 1], st[:, m:m + 1]))
                    link(dve.tensor_scalar(gt[:, m, :], gt[:, m, :], st[:, m:m + 1], None, ALU.mult))
                    gated = AT[:, m, :, :]
                    dve.tensor_tensor(gated, gated, wide(gt[:, m, :]), ALU.mult).then_inc(gated_ready.sem, 1)
                if old is not None:
                    h = H1[:, bass.ds(2 * i + old, 1), :]
                    dve.wait_ge(mix_in.sem, 2 * i + mix_in.after(old + 1))
                    dve.tensor_tensor(h, h, ps[:, 7, 0:D], ALU.add).then_inc(mix_added.sem, 1)

            in_turns(dve, 3, step, k.dve, 3 + 6 + 1 + 3)
    for s in (proj_in, proj_ready, overlap_in, overlap_ready, logits_in, logits_shifted, gates_exped, mix_in, mix_added,
              attn_ready, attn_turned, attn_t_ready, gated_ready, gated_turned, gated_t_ready):
        s.passed(T)


def reasoning(k, mem, H1, H2, p_tok):
    nc, ps = k.nc, k.ps
    sb = lambda name, shape: mem.enter_context(nc.sbuf_tensor(f"a2_{name}", shape, F32))
    wenc, wr, rb = sb("wenc", [C, NC, 64]), sb("wr", [64, D]), sb("rb", [P, D])
    PC, beta = sb("pc", [32, 4, 32]), sb("beta", [P, 1])
    sq, nrm, prod = sb("pc_sq", [32, 4, 32]), sb("pc_norm", [32, 2]), sb("pc_prod", [32, 4, 32])
    g_ = sb("g", [32, 4])
    A4, AB = sb("a4", [32, 4, 2, 32]), sb("ab", [64, P])
    q_tok = sb("q_tok", [P, T])
    load(k, [(wenc[:, :, :], "a2_wenc"), (wr[:, :], "a2_wr"), (rb[:, :], "a2_rb"), (PC[:, :, :], "a2_pc"), (beta[:, :], "a2_beta")])
    sigmoid_ready = k.count("sigmoid_ready")
    norm2_ready, norm_ready = k.count("norm2_ready"), k.count("norm_ready")
    with nc.Block() as block:
        @block.scalar
        def _(act):
            act.activation(beta[:, :], beta[:, :], ACT.Sigmoid).then_inc(sigmoid_ready.sem, 1)
            act.wait_ge(norm2_ready.sem, norm2_ready.after(1))
            act.activation(nrm[:, :], nrm[:, :], ACT.Sqrt).then_inc(norm_ready.sem, 1)

        @block.vector
        def _(dve):
            link = lambda ins: k.dve(dve, ins)
            k.dve.start()
            dve.tensor_scalar(q_tok[:, :], p_tok[:, :], -1.0, 1.0, ALU.mult, ALU.add)
            link(dve.tensor_tensor(sq[:, :, :], PC[:, :, :], PC[:, :, :], ALU.mult))
            dve.tensor_reduce(nrm[:, :], sq[:, :, :].rearrange("p (x a) d -> p x (a d)", x=2), AX.X, ALU.add).then_inc(norm2_ready.sem, 1)
            dve.wait_ge(norm_ready.sem, norm_ready.after(1))
            link(dve.tensor_scalar(nrm[:, :], nrm[:, :], 1e-12, None, ALU.max))
            link(dve.reciprocal(nrm[:, :], nrm[:, :]))
            both = PC[:, :, :].rearrange("p (x a) d -> p x (a d)", x=2)
            link(dve.tensor_tensor(both, both, nrm[:, :].unsqueeze(2).broadcast_to([32, 2, 64]), ALU.mult))
            Pr, Pi, Cr, Ci = (PC[:, n, :] for n in range(4))
            for n, (a, b) in enumerate(((Pr, Cr), (Pi, Ci), (Pr, Ci), (Pi, Cr))):
                link(dve.tensor_tensor(prod[:, n, :], a, b, ALU.mult))
            link(dve.tensor_reduce(g_[:, :], prod[:, :, :], AX.X, ALU.add))
            link(dve.tensor_tensor(g_[:, 0:1], g_[:, 0:1], g_[:, 1:2], ALU.add))
            link(dve.tensor_tensor(g_[:, 1:2], g_[:, 2:3], g_[:, 3:4], ALU.subtract))
            g_re, g_im = g_[:, 0:1], g_[:, 1:2]
            X, Y = A4[:, 0, 0, :], A4[:, 0, 1, :]
            link(dve.tensor_scalar(prod[:, 0, :], Pi, g_im, None, ALU.mult))
            link(dve.tensor_scalar(prod[:, 1, :], Pr, g_im, None, ALU.mult))
            link(dve.scalar_tensor_tensor(X, Pr, g_re, prod[:, 0, :], ALU.mult, ALU.subtract))
            link(dve.scalar_tensor_tensor(Y, Pi, g_re, prod[:, 1, :], ALU.mult, ALU.add))
            link(dve.tensor_copy(A4[:, 1, 0, :], Y))
            link(dve.tensor_scalar(A4[:, 1, 1, :], X, -1.0, None, ALU.mult))
            link(dve.tensor_copy(A4[:, 2, 0, :], Cr))
            link(dve.tensor_copy(A4[:, 2, 1, :], Ci))
            link(dve.tensor_copy(A4[:, 3, 0, :], Ci))
            link(dve.tensor_scalar(A4[:, 3, 1, :], Cr, -1.0, None, ALU.mult))
            for half in range(2):
                link(dve.transpose(AB[32 * half:32 * half + 32, :].rearrange("p (v s) -> p v s", v=4), A4[:, :, half, :]))
            k.dve.end()
            dve.wait_ge(sigmoid_ready.sem, sigmoid_ready.after(1))
    for s in (sigmoid_ready, norm2_ready, norm_ready):
        s.passed(1)

    Hs, HT = sb("h_tile", [P, 2, D]), sb("h_tile_t", [C, 2, NC, P])
    E, ES = sb("enc", [64, 2, P]), sb("enc_sq", [64, 2, P])
    CP, CT, cs = sb("coupling", [P, 2, 32]), sb("coupling_t", [P, 2, P]), sb("coupling_stat", [P, 2, 8])
    R, F, M, FT = sb("r", [P, 2, P]), sb("feats", [P, 2, P]), sb("feat_products", [P, 2, P]), sb("feats_t", [64, 2, P])
    RE = sb("reason", [P, 2, D])
    h_staged = k.count("h_staged")
    h_turned = k.count("h_turned", 2)
    ht_ready = k.count("ht_ready")
    coupled = k.count("coupled")
    enc_ready = k.count("enc_ready")
    shifted = k.count("coupling_shifted")
    exped = k.count("coupling_exped")
    ct_ready = k.count("coupling_t_ready")
    sums_in = k.count("sums_in")
    r_ready = k.count("r_ready")
    feats_ready = k.count("feats_ready")
    feats_turned = k.count("feats_turned")
    ft_ready = k.count("ft_ready")
    reason_in = k.count("reason_in")
    h2_ready = k.count("h2_ready", 2)
    with nc.Block() as block:
        @block.gpsimd
        def _(pool):
            with pool.Fori(0, T // 2) as i:
                for p in range(2):
                    pool.wait_ge(h_turned.sem, 2 * i + h_turned.room(p + 1))
                    pool.tensor_copy(Hs[:, p, :], H1[:, bass.ds(2 * i + p, 1), :]).then_inc(h_staged.sem, 1)

        @block.tensor
        def _(pe):
            def step(i, new, mid, old):
                if new is not None:
                    p = new % 2
                    pe.wait_ge(h_staged.sem, 2 * i + h_staged.after(new + 1))
                    for c in range(NC):
                        last = pe.transpose(ps[0:C, 0, c * P:(c + 1) * P], Hs[:, p, c * C:(c + 1) * C], k.ident[:, :])
                    last.then_inc(h_turned.sem, 1)
                if old is not None:
                    pe.wait_ge(feats_ready.sem, 2 * i + feats_ready.after(old + 1))
                    pe.transpose(ps[:, 4, 0:P], F[:, old % 2, :], k.ident[:, :]).then_inc(feats_turned.sem, 1)
                if mid is not None:
                    m = mid % 2
                    pe.wait_ge(enc_ready.sem, 2 * i + enc_ready.after(mid + 1))
                    pe.wait_ge(ct_ready.sem, 2 * i + ct_ready.after(mid + 1))
                    pe.matmul(ps[:, 3, 0:P], E[:, m, :], AB[:, :], start=True, stop=True)
                    pe.matmul(ps[:, 3, P:P + 1], ES[:, m, :], k.ones[0:64, 0:1], start=True, stop=True)
                    pe.matmul(ps[:, 3, P + 1:P + 2], CT[:, m, :], q_tok[:, bass.ds(2 * i + mid, 1)],
                              start=True, stop=True).then_inc(sums_in.sem, 1)
                if new is not None:
                    pe.wait_ge(ht_ready.sem, 2 * i + ht_ready.after(new + 1))
                    for c in range(NC):
                        pe.matmul(ps[:, 1, 0:P], HT[:, p, c, :], HT[:, p, c, :], start=(c == 0), stop=(c == NC - 1))
                    for c in range(NC):
                        last = pe.matmul(ps[0:64, 2, 0:P], wenc[:, c, :], HT[:, p, c, :], start=(c == 0), stop=(c == NC - 1))
                    last.then_inc(coupled.sem, 1)
                if old is not None:
                    pe.wait_ge(ft_ready.sem, 2 * i + ft_ready.after(old + 1))
                    pe.wait_ge(h2_ready.sem, 2 * i + h2_ready.after(old))
                    pe.matmul(ps[:, 5, 0:D], FT[:, old % 2, :], wr[:, :], start=True, stop=True).then_inc(reason_in.sem, 1)

            in_turns(pe, 3, step)

        @block.scalar
        def _(act):
            def step(i, new, mid, old):
                if new is not None:
                    p = new % 2
                    act.wait_ge(h_turned.sem, 2 * i + h_turned.after(new + 1))
                    act.copy(HT[:, p, :, :], ps[0:C, 0, 0:2 * P]).then_inc(ht_ready.sem, 1)
                if old is not None:
                    act.wait_ge(feats_turned.sem, 2 * i + feats_turned.after(old + 1))
                    act.copy(FT[:, old % 2, :], ps[0:64, 4, 0:P]).then_inc(ft_ready.sem, 1)
                if mid is not None:
                    act.wait_ge(sums_in.sem, 2 * i + sums_in.after(mid + 1))
                    act.copy(R[:, mid % 2, :], ps[:, 3, 0:P])
                    act.copy(cs[:, mid % 2, 4:6], ps[:, 3, P:P + 2]).then_inc(r_ready.sem, 1)
                if new is not None:
                    act.wait_ge(coupled.sem, 2 * i + coupled.after(new + 1))
                    act.copy(E[:, p, :], ps[0:64, 2, 0:P])
                    act.activation(ES[:, p, :], ps[0:64, 2, 0:P], ACT.Square).then_inc(enc_ready.sem, 1)
                    act.wait_ge(shifted.sem, 2 * i + shifted.after(new + 1))
                    act.activation(CP[:, p, :], CP[:, p, :], ACT.Exp, scale=float(D) ** -0.5).then_inc(exped.sem, 1)

            in_turns(act, 3, step)

        @block.vector
        def _(dve):
            link = lambda ins: k.dve(dve, ins)
            k.dve.start()
            dve.memset(F[:, :, 64:P], 0.0)
            link(dve.memset(CT[:, :, :], 0.0))
            k.dve.end()

            def step(i, new, mid, old):
                if mid is not None:
                    m = mid % 2
                    dve.wait_ge(r_ready.sem, 2 * i + r_ready.after(mid + 1))
                    c_ = lambda n: cs[:, m, n:n + 1]
                    link(dve.reciprocal(c_(1), c_(1)))
                    link(dve.tensor_scalar(c_(2), c_(5), c_(1), beta[:, :], ALU.mult, ALU.mult))
                    link(dve.tensor_scalar(c_(2), c_(2), -1.0, 1.0, ALU.mult, ALU.add))
                    link(dve.tensor_tensor(c_(2), c_(2), p_tok[:, bass.ds(2 * i + mid, 1)], ALU.mult))
                    link(dve.tensor_scalar(c_(2), c_(2), 0.0, 0.95, ALU.max, ALU.min))
                    link(dve.tensor_scalar(c_(2), c_(2), -1.0, 1.0, ALU.mult, ALU.add))
                    link(dve.tensor_scalar(c_(3), c_(4), 1e-24, None, ALU.max))
                    link(dve.reciprocal(c_(3), c_(3)))
                    t = R[:, m, 0:64].rearrange("p (v s) -> p v s", v=2)
                    by = lambda n: R[:, m, 32 * n:32 * n + 32].unsqueeze(1).broadcast_to([P, 2, 32])
                    mm = lambda n: M[:, m, 64 * n:64 * n + 64].rearrange("p (v s) -> p v s", v=2)
                    dve.tensor_tensor(mm(0), t, by(2), ALU.mult)
                    link(dve.tensor_tensor(mm(1), t, by(3), ALU.mult))
                    dve.tensor_tensor(F[:, m, 0:32], M[:, m, 0:32], M[:, m, 96:128], ALU.add)
                    dve.tensor_tensor(F[:, m, 32:64], M[:, m, 32:64], M[:, m, 64:96], ALU.subtract).then_inc(feats_ready.sem, 1)
                if new is not None:
                    p = new % 2
                    dve.wait_ge(coupled.sem, 2 * i + coupled.after(new + 1))
                    cp = CP[:, p, :]
                    for b in range(4):
                        rows = slice(32 * b, 32 * b + 32)
                        last = dve.tensor_copy(CP[rows, p, :], ps[rows, 1, rows])
                    link(last)
                    link(dve.tensor_reduce(cs[:, p, 0:1], cp, AX.X, ALU.max))
                    dve.tensor_scalar(cp, cp, cs[:, p, 0:1], None, ALU.subtract).then_inc(shifted.sem, 1)
                if old is not None:
                    dve.wait_ge(reason_in.sem, 2 * i + reason_in.after(old + 1))
                    o = old % 2
                    re = RE[:, o, :]
                    link(dve.scalar_tensor_tensor(re, ps[:, 5, 0:D], cs[:, o, 3:4], rb[:, :], ALU.mult, ALU.add))
                    link(dve.tensor_scalar(re, re, cs[:, o, 2:3], None, ALU.mult))
                    t = 2 * i + old
                    dve.tensor_tensor(H2[:, bass.ds(t, 1), :], re, H1[:, bass.ds(t, 1), :], ALU.add).then_inc(h2_ready.sem, 1)
                if new is not None:
                    dve.wait_ge(exped.sem, 2 * i + exped.after(new + 1))
                    link(dve.tensor_reduce(cs[:, p, 1:2], CP[:, p, :], AX.X, ALU.add))
                    for b in range(4):
                        rows = slice(32 * b, 32 * b + 32)
                        last = dve.transpose(CT[rows, p, rows], CP[rows, p, :])
                    last.then_inc(ct_ready.sem, 1)

            in_turns(dve, 3, step, k.dve, 2 + 1 + 9 + 2)
    for s in (h_staged, h_turned, ht_ready, coupled, enc_ready, shifted, exped, ct_ready, sums_in, r_ready, feats_ready,
              feats_turned, ft_ready, reason_in, h2_ready):
        s.passed(T)


def routed_experts(k, mem, H2):
    nc, ps = k.nc, k.ps
    sb = lambda name, shape: mem.enter_context(nc.sbuf_tensor(f"a2_{name}", shape, F32))
    W1 = KE * D
    NR = 16
    cut = 2 * D
    w1a, w1b = sb("w1a", [C + 1, NC, cut]), sb("w1b", [C + 1, NC, D + NR])
    eg, ebt = sb("eg", [P, KE, D]), sb("ebt", [P, KE, D])
    w2, b2 = sb("ew2", [C, 2 * KE, D]), sb("eb2", [KE, D])
    rw2, rb2 = sb("rw2", [P, KE, NR]), sb("rb2", [P, KE])
    X, R = sb("x", [P, T, W1]), sb("router_in", [P, T, D + NR])
    front(k, [(w1a, X[:, :, 0:cut]), (w1b, R[:, :, :])], src=H2, first=2, loads=[
        (w1a[:, :, :], "a2_w1a"), (w1b[:, :, :], "a2_w1b"), (eg[:, :, :], "a2_eg"), (ebt[:, :, :], "a2_ebt"),
        (w2[:, :, :], "a2_w2"), (b2[:, :], "a2_b2"), (rw2[:, :, :], "a2_rw2"), (rb2[:, :], "a2_rb2")])
    rg, rstat = sb("rg", [P, T, KE]), sb("rstat", [P, T])
    prod = sb("rprod", [P, T, KE, NR])
    stats, mv, rstd = sb("e_bn_stats", [P, T, KE, 6]), sb("e_mean_var", [P, T, KE, 2]), sb("e_rstd", [P, T, KE])
    G, RG = sb("g_tile", [P, 2, W1]), sb("rg_tile", [P, 2, KE])
    GT, RT = sb("g_tile_t", [C, 2, 2 * KE, P]), sb("rg_tile_t", [KE, 2, P])
    third_ready = k.count("third_ready")
    var_ready, std_ready = k.count("var_ready"), k.count("std_ready")
    normed = k.count("x_normed")
    gelu_ready = k.count("gelu_ready")
    router_in = k.count("router_ready")
    scores_ready, exps_ready = k.count("scores_ready"), k.count("exps_ready")
    staged = k.count("g_staged")
    turned = k.count("g_turned", 2)
    gt_ready = k.count("gt_ready")
    y_in = k.count("y_in")
    y_added = k.count("y_added", 2)
    NT = T // 2
    with nc.Block() as block:
        @block.scalar
        def _(act):
            def gelu(i, ahead):
                act.wait_ge(normed.sem, i + normed.after(ahead + 1))
                x = X[:, bass.ds(2 * (i + ahead), 2), :]
                act.activation(x, x, ACT.Gelu).then_inc(gelu_ready.sem, 1)

            def turned_out(i):
                for p in range(2):
                    act.wait_ge(turned.sem, 2 * i + turned.after(p + 1))
                    act.copy(GT[:, p, 0:4, :], ps[0:C, 2 * p, :])
                    act.copy(GT[:, p, 4:6, :], ps[0:C, 2 * p + 1, 0:2 * P])
                    act.copy(RT[:, p, :], ps[0:KE, 2 * p + 1, 3 * P:4 * P]).then_inc(gt_ready.sem, 1)

            act.activation(R[:, :, D:D + NR], R[:, :, D:D + NR], ACT.Gelu).then_inc(router_in.sem, 1)
            act.wait_ge(scores_ready.sem, scores_ready.after(1))
            act.activation(rg[:, :, :], rg[:, :, :], ACT.Exp).then_inc(exps_ready.sem, 1)
            act.wait_ge(var_ready.sem, var_ready.after(1))
            act.activation(rstd[:, :, :], rstd[:, :, :], ACT.Sqrt).then_inc(std_ready.sem, 1)
            gelu(0, 0)
            gelu(0, 1)
            with act.Fori(0, NT - 2) as i:
                turned_out(i)
                gelu(i, 2)
            turned_out(NT - 2)
            turned_out(NT - 1)

        @block.vector
        def _(dve):
            link = lambda ins: k.dve(dve, ins)

            def normalise(i, ahead):
                for p in range(2):
                    t = 2 * (i + ahead) + p
                    for e in range(KE):
                        x = X[:, bass.ds(t, 1), e * D:(e + 1) * D]
                        last = dve.tensor_scalar(x, x, mv[:, bass.ds(t, 1), e, 0], rstd[:, bass.ds(t, 1), e], ALU.subtract, ALU.mult)
                link(last)
                x2 = X[:, bass.ds(2 * (i + ahead), 2), :]
                by = lambda w: w[:, :, :].rearrange("p e d -> p (e d)").unsqueeze(1).broadcast_to([P, 2, W1])
                link(dve.tensor_tensor(x2, x2, by(eg), ALU.mult))
                dve.tensor_tensor(x2, x2, by(ebt), ALU.add).then_inc(normed.sem, 1)

            def add(i):
                for p in range(2):
                    h = k.H[:, bass.ds(2 * i + p, 1), :]
                    link(dve.tensor_tensor(h, h, H2[:, bass.ds(2 * i + p, 1), :], ALU.add))
                    dve.wait_ge(y_in.sem, 2 * i + y_in.after(p + 1))
                    dve.tensor_tensor(h, h, ps[:, 4 + p, 0:D], ALU.add).then_inc(y_added.sem, 1)

            k.dve.start()
            for e in range(KE):
                if e == KE - 1:
                    dve.wait_ge(third_ready.sem, third_ready.after(1))
                for t in range(T):
                    last = dve.bn_stats(stats[:, t, e, :], X[:, t, e * D:(e + 1) * D])
            link(last)
            dve.wait_ge(router_in.sem, router_in.after(1))
            full = [P, T, KE, NR]
            link(dve.tensor_tensor(prod[:, :, :, :], R[:, :, D:D + NR].unsqueeze(2).broadcast_to(full),
                                   rw2[:, :, :].unsqueeze(1).broadcast_to(full), ALU.mult))
            link(dve.tensor_reduce(rg[:, :, :], prod[:, :, :, :], AX.X, ALU.add))
            link(dve.tensor_tensor(rg[:, :, :], rg[:, :, :], rb2[:, :].unsqueeze(1).broadcast_to([P, T, KE]), ALU.add))
            link(dve.tensor_reduce(rstat[:, :], rg[:, :, :], AX.X, ALU.max))
            rw = rstat[:, :].unsqueeze(2).broadcast_to([P, T, KE])
            dve.tensor_tensor(rg[:, :, :], rg[:, :, :], rw, ALU.subtract).then_inc(scores_ready.sem, 1)
            for t in range(T):
                for e in range(KE):
                    last = dve.bn_aggr(mv[:, t, e, :], stats[:, t, e, :])
            link(last)
            dve.tensor_scalar(rstd[:, :, :], mv[:, :, :, 1], EPS, None, ALU.add).then_inc(var_ready.sem, 1)
            dve.wait_ge(exps_ready.sem, exps_ready.after(1))
            link(dve.tensor_reduce(rstat[:, :], rg[:, :, :], AX.X, ALU.add))
            link(dve.reciprocal(rstat[:, :], rstat[:, :]))
            link(dve.tensor_tensor(rg[:, :, :], rg[:, :, :], rw, ALU.mult))
            dve.wait_ge(std_ready.sem, std_ready.after(1))
            link(dve.reciprocal(rstd[:, :, :], rstd[:, :, :]))
            normalise(0, 0)
            normalise(0, 1)
            k.dve.end()
            with dve.Fori(0, NT - 2) as i:
                k.dve.start(i, 2 + 2)
                normalise(i, 2)
                add(i)
            k.dve.end(NT - 2)
            k.dve.start()
            add(NT - 2)
            add(NT - 1)
            k.dve.end()

        @block.gpsimd
        def _(pool):
            pool.tensor_copy(X[:, :, cut:W1], R[:, :, 0:D]).then_inc(third_ready.sem, 1)
            with pool.Fori(0, NT) as i:
                pool.wait_ge(gelu_ready.sem, i + gelu_ready.after(1))
                for p in range(2):
                    t = 2 * i + p
                    pool.wait_ge(turned.sem, 2 * i + turned.room(p + 1))
                    pool.tensor_tensor(G[:, p, :].rearrange("p (e d) -> p e d", e=KE),
                                       X[:, bass.ds(t, 1), :].rearrange("p t (e d) -> p (t e) d", e=KE),
                                       rg[:, bass.ds(t, 1), :].rearrange("p t e -> p (t e)").unsqueeze(2).broadcast_to([P, KE, D]), ALU.mult)
                    pool.tensor_copy(RG[:, p, :], rg[:, bass.ds(t, 1), :]).then_inc(staged.sem, 1)

        @block.tensor
        def _(pe):
            with pe.Fori(0, NT) as i:
                for p in range(2):
                    pe.wait_ge(staged.sem, 2 * i + staged.after(p + 1))
                    for c in range(2 * KE):
                        pe.transpose(ps[0:C, 2 * p + c // 4, (c % 4) * P:(c % 4 + 1) * P], G[:, p, c * C:(c + 1) * C], k.ident[:, :])
                    pe.transpose(ps[0:KE, 2 * p + 1, 3 * P:4 * P], RG[:, p, :], k.ident[:, :]).then_inc(turned.sem, 1)
                for p in range(2):
                    pe.wait_ge(gt_ready.sem, 2 * i + gt_ready.after(p + 1))
                    pe.wait_ge(y_added.sem, 2 * i + y_added.room(p + 1))
                    pe.matmul(ps[:, 4 + p, 0:D], RT[:, p, :], b2[:, :], start=True, stop=False)
                    for c in range(2 * KE):
                        last = pe.matmul(ps[:, 4 + p, 0:D], GT[:, p, c, :], w2[:, c, :], start=False, stop=(c == 2 * KE - 1))
                    last.then_inc(y_in.sem, 1)
    for s in (third_ready, var_ready, std_ready, router_in, scores_ready, exps_ready):
        s.passed(1)
    for s in (normed, gelu_ready):
        s.passed(NT)
    for s in (staged, turned, gt_ready, y_in, y_added):
        s.passed(T)


def finish(k, out):
    stored = k.count("output_stored")
    with k.nc.Block() as block:
        @block.sync
        def _(sp):
            sp.dma_start(out, k.H[:, :, :]).then_inc(stored.sem, 16)
            sp.wait_ge(stored.sem, stored.after(16))


def build(nc, dram, out):
    with ExitStack() as ctx:
        k = Core(nc, ctx, dram)
        k.all_primed = [k.count(n, c) for n, c in PRIMED.items()]
        begin(k)
        temporal_tokens(k)
        cosine_attention(k)
        moe(k, "f0", 8, 768, "argmax", 1, ACT.Gelu, bias2=True)
        rotary_attention(k)
        causal_mixture(k)
        complex_memory(k)
        moe(k, "f2", 8, 512, "balanced", 2, ACT.Silu)
        transport_attention(k)
        moe(k, "f3", 5, 256, "top", 2, ACT.Silu, gated=True)
        finish(k, out)


def by_chunk(w, bias=None):
    n = w.shape[1]
    a = np.zeros((C + 1, NC, n), np.float32)
    a[:C] = w.reshape(NC, C, n).transpose(1, 0, 2)
    if bias is not None:
        a[C, 0] = bias
    return a


def rows(a):
    a = np.asarray(a)
    return np.ascontiguousarray(np.broadcast_to(a[None], (P,) + a.shape))


def pad_heads(w):
    a = np.zeros(w.shape[:-1] + (HEADS, HP), np.float32)
    a[..., :16] = w.reshape(w.shape[:-1] + (HEADS, 16))
    return a.reshape(w.shape[:-1] + (HW,))


def expert_rows(w):
    E, F, _ = w.shape
    return w.reshape(E, F // P, P, D).transpose(2, 0, 1, 3)


def expert_chunks(w, bias=None):
    return np.stack([by_chunk(w[e], None if bias is None else bias[e]) for e in range(w.shape[0])], 1)


def head_rows(w):
    n = w.shape[1]
    return pad_heads(w.T).T.reshape(3, P, n).transpose(1, 0, 2)


def layouts(i):
    a = {"identity": np.eye(P, dtype=np.float32)}
    for E in (3, 5, 8):
        a[f"lower{E}"] = rows(np.tril(np.ones((E, E), np.float32), -1).reshape(E * E))
    a["f0_router"] = by_chunk(i["L0_ffn_gate_w"], i["L0_ffn_gate_b"])
    a["f0_w1"] = expert_chunks(i["L0_ffn_w1"], i["L0_ffn_b1"])
    a["f0_w2"] = expert_rows(i["L0_ffn_w2"])
    a["f0_b2"] = rows(i["L0_ffn_b2"])
    a["f2_router"] = by_chunk(i["L2_ffn_router_w"].T)
    a["f2_w1"] = expert_chunks(i["L2_ffn_w1"].transpose(0, 2, 1))
    a["f2_w2"] = expert_rows(i["L2_ffn_w2"].transpose(0, 2, 1))
    a["f3_router"] = by_chunk(i["L3_ffn_router_w"].T, i["L3_ffn_router_b"])
    a["f3_w1"] = expert_chunks(i["L3_ffn_gate_w"])
    a["f3_up"] = expert_chunks(i["L3_ffn_up_w"])
    a["f3_w2"] = expert_rows(i["L3_ffn_down_w"])
    w, b = i["L1_attn_qkv_w"].T, i["L1_attn_qkv_b"]
    swap = np.arange(D) ^ 1
    parts = [(0, slice(None)), (0, swap), (1, slice(None)), (1, swap)]
    a["a1_wqk"] = np.stack([by_chunk(pad_heads(w[:, m * D:(m + 1) * D][:, s]), pad_heads(b[m * D:(m + 1) * D][s])) for m, s in parts], 2)
    a["a1_wv"] = by_chunk(pad_heads(w[:, 2 * D:]), pad_heads(b[2 * D:]))
    a["a1_wo"] = head_rows(i["L1_attn_proj_w"].T)
    a["a1_bo"] = i["L1_attn_proj_b"][None]
    freq = (1.0 / np.float32(10000.0) ** (np.arange(0, 16, 2, dtype=np.float32) / 16)).astype(np.float32)
    angle = freq[:, None] * np.arange(32, dtype=np.float32)[None]
    cos, sin = np.zeros((4, 32, 32), np.float32), np.zeros((4, 32, 32), np.float32)
    cos[:, 0:16:2] = cos[:, 1:16:2] = np.cos(angle)
    sin[:, 0:16:2], sin[:, 1:16:2] = -np.sin(angle), np.sin(angle)
    a["a1_turn"] = np.stack([cos.reshape(P, 32), sin.reshape(P, 32)], 1)
    a["f1_wqk"] = by_chunk(i["L1_ffn_Wqk"], i["L1_ffn_bqk"])
    wv = i["L1_ffn_Wv"].transpose(1, 0, 2).reshape(D, D)
    a["f1_wvg"] = by_chunk(np.concatenate([wv, i["L1_ffn_Wg1"]], 1), np.concatenate([i["L1_ffn_bv"].reshape(D), i["L1_ffn_bg1"]]))
    a["f1_wo"] = i["L1_ffn_Wp"].reshape(3, 64, D).transpose(1, 0, 2)
    a["f1_bo"] = i["L1_ffn_bp"][None]
    a["f1_conv"] = np.concatenate([i["L1_ffn_conv_w"][:, 0, :], i["L1_ffn_conv_b"][:, None]], 1)
    query = np.arange(P)[:, None] % 32
    key = np.arange(32)[None]
    a["f1_mask"] = np.repeat(np.where(key > query, np.float32(-1e30), np.float32(0))[:, None], 3, 1)
    pos = np.zeros((P, 3, 32), np.float32)
    pos[:, 2] = np.tile(i["L1_ffn_pos_bias"][:32, :32], (4, 1))
    a["f1_pos"] = pos
    a["f1_wg2"] = rows(i["L1_ffn_Wg2"].T)
    a["f1_bg2"] = rows(i["L1_ffn_bg2"])
    order = np.arange(8).reshape(4, 2).T.reshape(8)
    chunk4 = lambda x: x.reshape((NC, C) + x.shape[1:]).swapaxes(0, 1)
    a["a2_wpz"] = by_chunk(i["L2_attn_pw1"][order].reshape(128, D).T, i["L2_attn_pb1"][order].reshape(128))
    ri = np.concatenate([i["L2_attn_W_real"], i["L2_attn_W_imag"]], 2).transpose(1, 0, 2).reshape(D, 512)
    a["a2_wri"] = by_chunk(ri).reshape(C + 1, NC, 4, P)
    a["a2_pw2"], a["a2_pb2"] = rows(i["L2_attn_pw2"][order]), rows(i["L2_attn_pb2"][order])
    for n, parts in (("a2_m1", ("m_real", "m_imag")), ("a2_m2", ("m_imag", "m_real"))):
        mm = np.concatenate([i[f"L2_attn_{x}"] for x in parts], 2)
        mm = mm.reshape(4, 2 * 64, 64).transpose(1, 0, 2)
        a[n] = np.repeat(mm[:, :, None], 2, 2)
    vals = i["L2_attn_values"][order].reshape(512, D).T
    a["a2_vt"] = chunk4(vals.reshape(D, 4, P))
    a["a2_wout"], a["a2_ob"] = chunk4(i["L2_attn_out_w"].T), i["L2_attn_out_b"][None]
    gw = i["L2_attn_gate_w"].reshape(8, 8, D)[order][:, order]
    a["a2_wgate"] = chunk4(gw.transpose(2, 1, 0).reshape(D, 4, 16))
    a["a2_gb"] = i["L2_attn_gate_b"][order][None]
    a["a2_pair"] = (np.arange(P)[:, None] // 64 == np.arange(2)[None]).astype(np.float32)
    a["a2_wenc"] = chunk4(np.concatenate([i["L2_attn_enc_r_w"], i["L2_attn_enc_i_w"]], 0).T)
    a["a2_wr"], a["a2_rb"] = i["L2_attn_r_out_w"].T, rows(i["L2_attn_r_out_b"])
    a["a2_pc"] = np.stack([i[f"L2_attn_{x}"] for x in ("P_real", "P_imag", "C_real", "C_imag")], 1)
    a["a2_beta"] = np.broadcast_to(i["L2_attn_beta"].reshape(1, 1), (P, 1))
    w1 = i["L2_attn_ew1"].transpose(2, 0, 1).reshape(D, 3 * D)
    b1 = i["L2_attn_eb1"].reshape(3 * D)
    a["a2_w1a"] = by_chunk(w1[:, :2 * D], b1[:2 * D])
    a["a2_w1b"] = by_chunk(np.concatenate([w1[:, 2 * D:], i["L2_attn_rw1"].T], 1), np.concatenate([b1[2 * D:], i["L2_attn_rb1"]]))
    a["a2_eg"], a["a2_ebt"] = rows(i["L2_attn_eg"]), rows(i["L2_attn_ebt"])
    a["a2_w2"] = i["L2_attn_ew2"].transpose(0, 2, 1).reshape(6, C, D).transpose(1, 0, 2)
    a["a2_b2"] = i["L2_attn_eb2"]
    a["a2_rw2"], a["a2_rb2"] = rows(i["L2_attn_rw2"]), rows(i["L2_attn_rb2"])
    a["tok_x"] = by_chunk(i["x"].reshape(4096, D).T)
    a["tok_x"][C, 0] = 1.0
    a["tok_down"] = by_chunk(i["L0_tok_w_down"], i["L0_tok_b_down"])
    a["tok_up"] = i["L0_tok_w_up"]
    a["tok_up_bias"] = rows(i["L0_tok_b_up"])
    a["tok_conv"] = np.concatenate([i["L0_tok_w_conv"][:, 0, :], i["L0_tok_b_conv"][:, None]], 1)
    w, b = i["L0_attn_in_proj_weight"].T, i["L0_attn_in_proj_bias"]
    a["a0_w"] = np.stack([by_chunk(pad_heads(w[:, m * D:(m + 1) * D]), pad_heads(b[m * D:(m + 1) * D])) for m in range(3)], 2)
    a["a0_wo"], a["a0_bo"] = head_rows(i["L0_attn_out_w"].T), i["L0_attn_out_b"][None]
    a["a0_log_scale"] = rows(i["L0_attn_logit_scale"][:, 0, 0])
    a["a0_head_scale"] = rows(i["L0_attn_head_scale"][:, 0, 0])
    w = i["L3_attn_w_qkv"].T
    a["a3_wq"], a["a3_wv"] = by_chunk(pad_heads(w[:, 0:D])), by_chunk(pad_heads(w[:, 2 * D:]))
    a["a3_wo"], a["a3_bo"] = head_rows(i["L3_attn_w_proj"].T), i["L3_attn_b_proj"][None]
    a["eye32"] = (key == query).astype(np.float32)
    a["off32"] = (key != query).astype(np.float32)
    a["blocks32"] = (np.arange(P)[:, None] // 32 == np.arange(P)[None] // 32).astype(np.float32)
    return {n: np.ascontiguousarray(v) for n, v in a.items()}


PRIMED = {"xn_transposed": U, "xt_spread": U, "projection_read": 2, "hidden_ready": 4, "expert_out": 8,
          "expert_added": 4, "gate_ready": 2,
          "scores_out": 2, "probs_ready": 2, "pv_done": 2, "ot_ready": 1, "out_added": 1, "qk_ready": 1,
          "keys_ready": 1, "qn_turned": 2, "qt_ready": 2, "qkv_in": 2, "tile_projected": 2,
          "tile_added": 2, "down_ready": 4, "z_turned": 2, "zt_ready": 2, "up_in": 2, "up_added": 2, "mix_added": 2,
          "h_turned": 2, "h2_ready": 2, "g_turned": 2, "y_added": 2}


def kernel(**inputs):
    from concourse import bacc
    from concourse.bass_utils import run_bass_kernel_spmd

    nc = bacc.Bacc("TRN2", target_bir_lowering=False, num_devices=1)
    arrays = {f"in_{n}": a for n, a in layouts({n: np.asarray(v) for n, v in inputs.items()}).items()}
    dram = {n[3:]: nc.dram_tensor(n, a.shape, F32, kind="ExternalInput").ap() for n, a in arrays.items()}
    dram["scratch"] = nc.dram_tensor("scratch", (C * TOK,), F32, kind="Internal").ap()
    out = nc.dram_tensor("out", (P, T, D), F32, kind="ExternalOutput").ap()
    build(nc, dram, out)
    r = run_bass_kernel_spmd(nc, [arrays], core_ids=[0])
    return np.ascontiguousarray(r.results[0]["out"].transpose(1, 0, 2).reshape(64, 32, D))
```
